# Optimizing a Trainium2 kernel written in Bass

```python
import numpy as np
import jax
import jax.numpy as jnp

def _softmax(x, axis=-1):
    return jax.nn.softmax(x, axis=axis)

def _gelu(x):
    return jax.nn.gelu(x, approximate=True)

def _silu(x):
    return jax.nn.silu(x)

def _sigmoid(x):
    return jax.nn.sigmoid(x)

def _layernorm(x, axis=-1, eps=1e-05):
    m = jnp.mean(x, axis=axis, keepdims=True)
    v = jnp.var(x, axis=axis, keepdims=True)
    return (x - m) / jnp.sqrt(v + eps)

def _scatter_add(tgt, idx, src, axis=0):
    return tgt.at[idx].add(src)

def _segment_sum(src, seg, n):
    return jax.ops.segment_sum(src, seg, n)
kernel_name = 'mk_gnn_ffn_d4_gnn_r32_2a7b87'

def setup_inputs(seed: int=0):
    np.random.seed(seed)
    _w = jnp.asarray

    def _rec_inputs():
        import jax
        import jax.numpy as jnp
        _gk = jax.random.key(seed)
        x = -5.39e-05 + 0.9998 * jax.random.normal(jax.random.fold_in(_gk, 1), (3125, 256), jnp.float32)
        src = jax.random.randint(jax.random.fold_in(_gk, 2), (50000,), 0, 3125, jnp.int32)
        dst = jax.random.randint(jax.random.fold_in(_gk, 3), (50000,), 0, 3125, jnp.int32)
        _o = jnp.argsort(dst, stable=True)
        src = src[_o]
        dst = dst[_o]
        edge_type_8 = jax.random.randint(jax.random.fold_in(_gk, 13), (50000,), 0, 8, jnp.int32)
        edge_weight = jax.random.uniform(jax.random.fold_in(_gk, 14), (50000,), jnp.float32, 0.0, 1)
        node_type_4 = jax.random.randint(jax.random.fold_in(_gk, 15), (3125,), 0, 4, jnp.int32)
        return (x, src, dst, edge_type_8, edge_weight, node_type_4)
    x, src, dst, edge_type_8, edge_weight, node_type_4 = _rec_inputs()

    def _L0_gnn_setup():
        import jax, jax.numpy as jnp
        import numpy as np
        NUM_NODES = 3125
        IN_CH = 256
        HIDDEN = 128
        OUT_CH = 256
        NUM_EDGES = 100000

        def gcn_conv(x, W, b, src, dst, num_nodes):
            h = x @ W
            loop = jnp.arange(num_nodes, dtype=src.dtype)
            s = jnp.concatenate([src, loop])
            d = jnp.concatenate([dst, loop])
            deg = jax.ops.segment_sum(jnp.ones_like(d, dtype=h.dtype), d, num_segments=num_nodes)
            dinv = jnp.where(deg > 0, jax.lax.rsqrt(deg), 0.0)
            norm = dinv[s] * dinv[d]
            msg = h[s] * norm[:, None]
            out = jax.ops.segment_sum(msg, d, num_segments=num_nodes)
            return out + b
        key = jax.random.key(seed)
        k1, k2, k3, k4 = jax.random.split(key, 4)
        edge_index = jax.random.randint(k1, (2, NUM_EDGES), 0, NUM_NODES, dtype=jnp.int64)
        node_features = jax.random.normal(k2, (NUM_NODES, IN_CH), dtype=jnp.float32)
        W1 = jax.random.normal(k3, (IN_CH, HIDDEN), dtype=jnp.float32) * (1.0 / np.sqrt(IN_CH))
        b1 = jnp.zeros((HIDDEN,), dtype=jnp.float32)
        W2 = jax.random.normal(k4, (HIDDEN, OUT_CH), dtype=jnp.float32) * (1.0 / np.sqrt(HIDDEN))
        b2 = jnp.zeros((OUT_CH,), dtype=jnp.float32)
        return {'node_features': node_features, 'W1': W1, 'b1': b1, 'W2': W2, 'b2': b2, 'edge_index': edge_index}
    _L0_gnn_all = _L0_gnn_setup()
    _L0_gnn_in = {k: v for k, v in _L0_gnn_all.items() if k in ('W1', 'b1', 'W2', 'b2')}
    del _L0_gnn_all

    def _L0_ffn_setup():
        import jax, jax.numpy as jnp
        import numpy as np
        B, N, D = (16, 128, 256)
        NUM_EXPERTS, TOP_K, HEADS = (4, 2, 4)
        N_EDGES = 32768
        LN_EPS = 1e-05

        def _layernorm(x, g, b):
            mu = x.mean(-1, keepdims=True)
            var = ((x - mu) ** 2).mean(-1, keepdims=True)
            return (x - mu) * jax.lax.rsqrt(var + LN_EPS) * g + b

        def _forward(x, edge_index, W_gat, att_src, att_dst, b_gat, ln_gamma, ln_beta, W1, b1, W2, b2):
            Bc, Nc, Dc = x.shape
            M = Bc * Nc
            x_flat = x.reshape(M, Dc)
            h = (x_flat @ W_gat).reshape(M, HEADS, NUM_EXPERTS)
            loops = jnp.arange(M, dtype=edge_index.dtype)
            src = jnp.concatenate([edge_index[0], loops])
            dst = jnp.concatenate([edge_index[1], loops])
            a_src = (h * att_src).sum(-1)
            a_dst = (h * att_dst).sum(-1)
            e = jax.nn.leaky_relu(a_src[src] + a_dst[dst], negative_slope=0.2)
            e_max = jax.ops.segment_max(e, dst, num_segments=M)
            ee = jnp.exp(e - e_max[dst])
            denom = jax.ops.segment_sum(ee, dst, num_segments=M)
            alpha = ee / (denom[dst] + 1e-16)
            msg = h[src] * alpha[:, :, None]
            agg = jax.ops.segment_sum(msg, dst, num_segments=M).reshape(M, HEADS * NUM_EXPERTS) + b_gat
            scores = _layernorm(agg, ln_gamma, ln_beta).reshape(M, HEADS, NUM_EXPERTS).mean(1)
            scores = scores.reshape(Bc, Nc, NUM_EXPERTS)
            topk_s, topk_i = jax.lax.top_k(scores, TOP_K)
            w = jax.nn.softmax(topk_s, axis=-1)
            out = jnp.zeros_like(x)
            for ei in range(NUM_EXPERTS):
                g = jnp.where(topk_i == ei, w, 0.0).sum(-1)
                hh = jax.nn.gelu(x @ W1[ei] + b1[ei], approximate=False)
                out = out + g[..., None] * (hh @ W2[ei] + b2[ei])
            return out
        key = jax.random.key(seed)
        ks = jax.random.split(key, 8)
        s = 0.05
        return {'x': jax.random.normal(ks[0], (B, N, D), jnp.float32), 'W_gat': jax.random.normal(ks[1], (D, HEADS * NUM_EXPERTS), jnp.float32) * s, 'att_src': jax.random.normal(ks[2], (HEADS, NUM_EXPERTS), jnp.float32) * s, 'att_dst': jax.random.normal(ks[3], (HEADS, NUM_EXPERTS), jnp.float32) * s, 'b_gat': jnp.zeros((HEADS * NUM_EXPERTS,), jnp.float32), 'ln_gamma': jnp.ones((HEADS * NUM_EXPERTS,), jnp.float32), 'ln_beta': jnp.zeros((HEADS * NUM_EXPERTS,), jnp.float32), 'W1': jax.random.normal(ks[4], (NUM_EXPERTS, D, 2 * D), jnp.float32) * s, 'b1': jnp.zeros((NUM_EXPERTS, 2 * D), jnp.float32), 'W2': jax.random.normal(ks[5], (NUM_EXPERTS, 2 * D, D), jnp.float32) * s, 'b2': jnp.zeros((NUM_EXPERTS, D), jnp.float32), 'edge_index': jax.random.randint(ks[6], (2, N_EDGES), 0, B * N, jnp.int32)}
    _L0_ffn_all = _L0_ffn_setup()
    _L0_ffn_in = {k: v for k, v in _L0_ffn_all.items() if k in ('W_gat', 'att_src', 'att_dst', 'b_gat', 'ln_gamma', 'ln_beta', 'W1', 'b1', 'W2', 'b2', 'edge_index')}
    del _L0_ffn_all

    def _L1_gnn_setup():
        import jax, jax.numpy as jnp
        import numpy as np
        N_NODES = 625
        N_EDGES = 10000
        IN_DIM = 256
        OUT_DIM = 256
        N_HEADS = 4
        D_K = OUT_DIM // N_HEADS
        N_NTYPES = 4
        N_RELS = 8
        SQRT_DK = float(np.sqrt(D_K))

        def _typed_matmul(x, W, node_type):
            all_t = jnp.einsum('ni,tio->tno', x, W)
            return all_t[node_type, jnp.arange(x.shape[0])]
        key = jax.random.key(seed)
        ks = jax.random.split(key, 12)
        xav = lambda k, shape, fan: jax.random.normal(k, shape, jnp.float32) * (1.0 / np.sqrt(fan))
        return {'h': jax.random.normal(ks[0], (N_NODES, IN_DIM), jnp.float32), 'k_linears': xav(ks[1], (N_NTYPES, IN_DIM, OUT_DIM), IN_DIM), 'q_linears': xav(ks[2], (N_NTYPES, IN_DIM, OUT_DIM), IN_DIM), 'v_linears': xav(ks[3], (N_NTYPES, IN_DIM, OUT_DIM), IN_DIM), 'a_linears': xav(ks[4], (N_NTYPES, OUT_DIM, OUT_DIM), OUT_DIM), 'relation_att': xav(ks[5], (N_RELS, N_HEADS, D_K, D_K), D_K), 'relation_msg': xav(ks[6], (N_RELS, N_HEADS, D_K, D_K), D_K), 'relation_pri': jnp.ones((N_RELS, N_HEADS), jnp.float32), 'skip': jnp.ones((N_NTYPES,), jnp.float32), 'node_type': jax.random.randint(ks[7], (N_NODES,), 0, N_NTYPES), 'etype': jnp.sort(jax.random.randint(ks[8], (N_EDGES,), 0, N_RELS)), 'row_idx': jax.random.randint(ks[9], (N_EDGES,), 0, N_NODES), 'col_idx': jax.random.randint(ks[10], (N_EDGES,), 0, N_NODES)}
    _L1_gnn_all = _L1_gnn_setup()
    _L1_gnn_in = {k: v for k, v in _L1_gnn_all.items() if k in ('k_linears', 'q_linears', 'v_linears', 'a_linears', 'relation_att', 'relation_msg', 'relation_pri', 'skip')}
    del _L1_gnn_all

    def _L1_ffn_setup():
        import jax, jax.numpy as jnp
        import numpy as np
        BN_EPS = 0.001

        def _bn(h, g, b, m, v):
            return g * (h - m) * jax.lax.rsqrt(v + BN_EPS) + b
        key = jax.random.key(seed)
        ks = jax.random.split(key, 8)
        B, F, Df = (256, 64, 256)
        E, H, D = (8, 256, 256)
        s1 = 1.0 / np.sqrt(Df)
        s2 = 1.0 / np.sqrt(H)
        return {'x': jax.random.normal(ks[0], (B, F, Df), jnp.float32), 'Wr': jax.random.normal(ks[1], (Df, E), jnp.float32) * s1, 'br': jnp.zeros((E,), jnp.float32), 'W1': jax.random.normal(ks[2], (E, Df, H), jnp.float32) * s1, 'b1': jnp.zeros((E, H), jnp.float32), 'g1': jnp.ones((E, H), jnp.float32), 'be1': jnp.zeros((E, H), jnp.float32), 'm1': jnp.zeros((E, H), jnp.float32), 'v1': jnp.ones((E, H), jnp.float32), 'W2': jax.random.normal(ks[3], (E, H, H), jnp.float32) * s2, 'b2': jnp.zeros((E, H), jnp.float32), 'g2': jnp.ones((E, H), jnp.float32), 'be2': jnp.zeros((E, H), jnp.float32), 'm2': jnp.zeros((E, H), jnp.float32), 'v2': jnp.ones((E, H), jnp.float32), 'Wo': jax.random.normal(ks[4], (E, H, D), jnp.float32) * s2, 'bo': jnp.zeros((E, D), jnp.float32)}
    _L1_ffn_all = _L1_ffn_setup()
    _L1_ffn_in = {k: v for k, v in _L1_ffn_all.items() if k in ('Wr', 'br', 'W1', 'b1', 'g1', 'be1', 'm1', 'v1', 'W2', 'b2', 'g2', 'be2', 'm2', 'v2', 'Wo', 'bo')}
    del _L1_ffn_all

    def _L2_gnn_setup():
        import jax, jax.numpy as jnp
        import numpy as np
        N_NODES = 50000
        N_EDGES = 25000
        IN_CH = 256
        HID_CH = 256
        OUT_CH = 256
        N_LAYERS = 3
        key = jax.random.key(seed)
        ks = jax.random.split(key, 8)
        s_in = 1.0 / np.sqrt(IN_CH)
        s_h = 1.0 / np.sqrt(HID_CH)
        return {'x': jax.random.normal(ks[0], (N_NODES, IN_CH), dtype=jnp.float32), 'W_in': jax.random.normal(ks[1], (IN_CH, HID_CH), dtype=jnp.float32) * s_in, 'b_in': jnp.zeros((HID_CH,), dtype=jnp.float32), 'W_agg': jax.random.normal(ks[2], (N_LAYERS, HID_CH, HID_CH), dtype=jnp.float32) * s_h, 'W_self': jax.random.normal(ks[3], (N_LAYERS, HID_CH, HID_CH), dtype=jnp.float32) * s_h, 'b_hid': jnp.zeros((N_LAYERS, HID_CH), dtype=jnp.float32), 'W_out': jax.random.normal(ks[4], (HID_CH, OUT_CH), dtype=jnp.float32) * s_h, 'b_out': jnp.zeros((OUT_CH,), dtype=jnp.float32), 'edge_index': jax.random.randint(ks[5], (2, N_EDGES), 0, N_NODES, dtype=jnp.int64)}
    _L2_gnn_all = _L2_gnn_setup()
    _L2_gnn_in = {k: v for k, v in _L2_gnn_all.items() if k in ('W_in', 'b_in', 'W_agg', 'W_self', 'b_hid', 'W_out', 'b_out')}
    del _L2_gnn_all

    def _L2_ffn_setup():
        import math
        import jax, jax.numpy as jnp
        import numpy as np
        CAPACITY_FACTOR = 1.25
        key = jax.random.key(seed)
        ks = jax.random.split(key, 5)
        B, L, D, F, E = (8, 256, 256, 1024, 8)
        h = jax.random.normal(ks[0], (B, L, D), dtype=jnp.float32)
        gate_w = jax.random.normal(ks[1], (D, E), dtype=jnp.float32) * 0.02
        gate_b = jnp.zeros((E,), dtype=jnp.float32)
        w1 = jax.random.normal(ks[2], (E, D, F), dtype=jnp.float32) * (1.0 / math.sqrt(D))
        b1 = jnp.zeros((E, F), dtype=jnp.float32)
        w2 = jax.random.normal(ks[3], (E, F, D), dtype=jnp.float32) * (1.0 / math.sqrt(F))
        b2 = jnp.zeros((E, D), dtype=jnp.float32)
        return {'h': h, 'gate_w': gate_w, 'gate_b': gate_b, 'w1': w1, 'b1': b1, 'w2': w2, 'b2': b2}
    _L2_ffn_all = _L2_ffn_setup()
    _L2_ffn_in = {k: v for k, v in _L2_ffn_all.items() if k in ('gate_w', 'gate_b', 'w1', 'b1', 'w2', 'b2')}
    del _L2_ffn_all

    def _L3_gnn_setup():
        import jax, jax.numpy as jnp
        import numpy as np
        N, D, E = (3125, 256, 100000)
        key = jax.random.key(seed)
        ks = jax.random.split(key, 8)
        return {'x': jax.random.normal(ks[0], (N, D), dtype=jnp.float32), 'edge_weight': jax.random.uniform(ks[1], (E,), dtype=jnp.float32), 'ln_w': jnp.ones((D,), jnp.float32), 'ln_b': jnp.zeros((D,), jnp.float32), 'W': jax.random.normal(ks[2], (D, D), dtype=jnp.float32) * (1.0 / np.sqrt(D)), 'b': jax.random.normal(ks[3], (D,), dtype=jnp.float32) * 0.01, 'gamma': jax.random.normal(ks[4], (D,), dtype=jnp.float32), 'beta': jax.random.normal(ks[5], (D,), dtype=jnp.float32), 'edge_row': jax.random.randint(ks[6], (E,), 0, N, dtype=jnp.int32), 'edge_col': jax.random.randint(ks[7], (E,), 0, N, dtype=jnp.int32)}
    _L3_gnn_all = _L3_gnn_setup()
    _L3_gnn_in = {k: v for k, v in _L3_gnn_all.items() if k in ('ln_w', 'ln_b', 'W', 'b', 'gamma', 'beta')}
    del _L3_gnn_all

    def _L3_ffn_setup():
        import math
        import jax, jax.numpy as jnp
        import numpy as np
        CAPACITY_FACTOR = 1.25
        TOP_K = 2
        LN_EPS = 1e-05

        def _layer_norm(x, gamma, beta):
            mu = jnp.mean(x, axis=-1, keepdims=True)
            var = jnp.var(x, axis=-1, keepdims=True)
            return (x - mu) * jax.lax.rsqrt(var + LN_EPS) * gamma + beta
        key = jax.random.key(seed)
        ks = jax.random.split(key, 4)
        B, S, D, F, E = (8, 128, 256, 512, 8)
        x = jax.random.normal(ks[0], (B, S, D), dtype=jnp.float32)
        Wr = jax.random.normal(ks[1], (D, E), dtype=jnp.float32) / np.sqrt(D)
        br = jnp.zeros((E,), jnp.float32)
        W1 = jax.random.normal(ks[2], (E, D, F), dtype=jnp.float32) / np.sqrt(D)
        b1 = jnp.zeros((E, F), jnp.float32)
        W2 = jax.random.normal(ks[3], (E, F, D), dtype=jnp.float32) / np.sqrt(F)
        b2 = jnp.zeros((E, D), jnp.float32)
        gamma = jnp.ones((D,), jnp.float32)
        beta = jnp.zeros((D,), jnp.float32)
        return {'x': x, 'Wr': Wr, 'br': br, 'W1': W1, 'b1': b1, 'W2': W2, 'b2': b2, 'gamma': gamma, 'beta': beta}
    _L3_ffn_all = _L3_ffn_setup()
    _L3_ffn_in = {k: v for k, v in _L3_ffn_all.items() if k in ('Wr', 'br', 'W1', 'b1', 'W2', 'b2', 'gamma', 'beta')}
    del _L3_ffn_all
    return {'x': x, 'src': src, 'dst': dst, 'edge_type_8': edge_type_8, 'edge_weight': edge_weight, 'node_type_4': node_type_4, 'L0_gnn_W1': _L0_gnn_in['W1'], 'L0_gnn_b1': _L0_gnn_in['b1'], 'L0_gnn_W2': _L0_gnn_in['W2'], 'L0_gnn_b2': _L0_gnn_in['b2'], 'L0_ffn_W_gat': _L0_ffn_in['W_gat'], 'L0_ffn_att_src': _L0_ffn_in['att_src'], 'L0_ffn_att_dst': _L0_ffn_in['att_dst'], 'L0_ffn_b_gat': _L0_ffn_in['b_gat'], 'L0_ffn_ln_gamma': _L0_ffn_in['ln_gamma'], 'L0_ffn_ln_beta': _L0_ffn_in['ln_beta'], 'L0_ffn_W1': _L0_ffn_in['W1'], 'L0_ffn_b1': _L0_ffn_in['b1'], 'L0_ffn_W2': _L0_ffn_in['W2'], 'L0_ffn_b2': _L0_ffn_in['b2'], 'L0_ffn_edge_index': _L0_ffn_in['edge_index'], 'L1_gnn_k_linears': _L1_gnn_in['k_linears'], 'L1_gnn_q_linears': _L1_gnn_in['q_linears'], 'L1_gnn_v_linears': _L1_gnn_in['v_linears'], 'L1_gnn_a_linears': _L1_gnn_in['a_linears'], 'L1_gnn_relation_att': _L1_gnn_in['relation_att'], 'L1_gnn_relation_msg': _L1_gnn_in['relation_msg'], 'L1_gnn_relation_pri': _L1_gnn_in['relation_pri'], 'L1_gnn_skip': _L1_gnn_in['skip'], 'L1_ffn_Wr': _L1_ffn_in['Wr'], 'L1_ffn_br': _L1_ffn_in['br'], 'L1_ffn_W1': _L1_ffn_in['W1'], 'L1_ffn_b1': _L1_ffn_in['b1'], 'L1_ffn_g1': _L1_ffn_in['g1'], 'L1_ffn_be1': _L1_ffn_in['be1'], 'L1_ffn_m1': _L1_ffn_in['m1'], 'L1_ffn_v1': _L1_ffn_in['v1'], 'L1_ffn_W2': _L1_ffn_in['W2'], 'L1_ffn_b2': _L1_ffn_in['b2'], 'L1_ffn_g2': _L1_ffn_in['g2'], 'L1_ffn_be2': _L1_ffn_in['be2'], 'L1_ffn_m2': _L1_ffn_in['m2'], 'L1_ffn_v2': _L1_ffn_in['v2'], 'L1_ffn_Wo': _L1_ffn_in['Wo'], 'L1_ffn_bo': _L1_ffn_in['bo'], 'L2_gnn_W_in': _L2_gnn_in['W_in'], 'L2_gnn_b_in': _L2_gnn_in['b_in'], 'L2_gnn_W_agg': _L2_gnn_in['W_agg'], 'L2_gnn_W_self': _L2_gnn_in['W_self'], 'L2_gnn_b_hid': _L2_gnn_in['b_hid'], 'L2_gnn_W_out': _L2_gnn_in['W_out'], 'L2_gnn_b_out': _L2_gnn_in['b_out'], 'L2_ffn_gate_w': _L2_ffn_in['gate_w'], 'L2_ffn_gate_b': _L2_ffn_in['gate_b'], 'L2_ffn_w1': _L2_ffn_in['w1'], 'L2_ffn_b1': _L2_ffn_in['b1'], 'L2_ffn_w2': _L2_ffn_in['w2'], 'L2_ffn_b2': _L2_ffn_in['b2'], 'L3_gnn_ln_w': _L3_gnn_in['ln_w'], 'L3_gnn_ln_b': _L3_gnn_in['ln_b'], 'L3_gnn_W': _L3_gnn_in['W'], 'L3_gnn_b': _L3_gnn_in['b'], 'L3_gnn_gamma': _L3_gnn_in['gamma'], 'L3_gnn_beta': _L3_gnn_in['beta'], 'L3_ffn_Wr': _L3_ffn_in['Wr'], 'L3_ffn_br': _L3_ffn_in['br'], 'L3_ffn_W1': _L3_ffn_in['W1'], 'L3_ffn_b1': _L3_ffn_in['b1'], 'L3_ffn_W2': _L3_ffn_in['W2'], 'L3_ffn_b2': _L3_ffn_in['b2'], 'L3_ffn_gamma': _L3_ffn_in['gamma'], 'L3_ffn_beta': _L3_ffn_in['beta']}

def reference(x, src, dst, edge_type_8, edge_weight, node_type_4, L0_gnn_W1, L0_gnn_b1, L0_gnn_W2, L0_gnn_b2, L0_ffn_W_gat, L0_ffn_att_src, L0_ffn_att_dst, L0_ffn_b_gat, L0_ffn_ln_gamma, L0_ffn_ln_beta, L0_ffn_W1, L0_ffn_b1, L0_ffn_W2, L0_ffn_b2, L0_ffn_edge_index, L1_gnn_k_linears, L1_gnn_q_linears, L1_gnn_v_linears, L1_gnn_a_linears, L1_gnn_relation_att, L1_gnn_relation_msg, L1_gnn_relation_pri, L1_gnn_skip, L1_ffn_Wr, L1_ffn_br, L1_ffn_W1, L1_ffn_b1, L1_ffn_g1, L1_ffn_be1, L1_ffn_m1, L1_ffn_v1, L1_ffn_W2, L1_ffn_b2, L1_ffn_g2, L1_ffn_be2, L1_ffn_m2, L1_ffn_v2, L1_ffn_Wo, L1_ffn_bo, L2_gnn_W_in, L2_gnn_b_in, L2_gnn_W_agg, L2_gnn_W_self, L2_gnn_b_hid, L2_gnn_W_out, L2_gnn_b_out, L2_ffn_gate_w, L2_ffn_gate_b, L2_ffn_w1, L2_ffn_b1, L2_ffn_w2, L2_ffn_b2, L3_gnn_ln_w, L3_gnn_ln_b, L3_gnn_W, L3_gnn_b, L3_gnn_gamma, L3_gnn_beta, L3_ffn_Wr, L3_ffn_br, L3_ffn_W1, L3_ffn_b1, L3_ffn_W2, L3_ffn_b2, L3_ffn_gamma, L3_ffn_beta):
    import jax
    import jax.numpy as jnp

    def _L0_gnn_ref(node_features, W1, b1, W2, b2, edge_index):
        import jax, jax.numpy as jnp
        import numpy as np
        NUM_NODES = 3125
        IN_CH = 256
        HIDDEN = 128
        OUT_CH = 256
        NUM_EDGES = 100000

        def gcn_conv(x, W, b, src, dst, num_nodes):
            h = x @ W
            loop = jnp.arange(num_nodes, dtype=src.dtype)
            s = jnp.concatenate([src, loop])
            d = jnp.concatenate([dst, loop])
            deg = jax.ops.segment_sum(jnp.ones_like(d, dtype=h.dtype), d, num_segments=num_nodes)
            dinv = jnp.where(deg > 0, jax.lax.rsqrt(deg), 0.0)
            norm = dinv[s] * dinv[d]
            msg = h[s] * norm[:, None]
            out = jax.ops.segment_sum(msg, d, num_segments=num_nodes)
            return out + b
        src, dst = (edge_index[0], edge_index[1])
        x = gcn_conv(node_features, W1, b1, src, dst, NUM_NODES)
        x = jax.nn.relu(x)
        x = gcn_conv(x, W2, b2, src, dst, NUM_NODES)
        return x

    def _L0_ffn_ref(x, W_gat, att_src, att_dst, b_gat, ln_gamma, ln_beta, W1, b1, W2, b2, edge_index):
        import jax, jax.numpy as jnp
        import numpy as np
        B, N, D = (16, 128, 256)
        NUM_EXPERTS, TOP_K, HEADS = (4, 2, 4)
        N_EDGES = 32768
        LN_EPS = 1e-05

        def _layernorm(x, g, b):
            mu = x.mean(-1, keepdims=True)
            var = ((x - mu) ** 2).mean(-1, keepdims=True)
            return (x - mu) * jax.lax.rsqrt(var + LN_EPS) * g + b

        def _forward(x, edge_index, W_gat, att_src, att_dst, b_gat, ln_gamma, ln_beta, W1, b1, W2, b2):
            Bc, Nc, Dc = x.shape
            M = Bc * Nc
            x_flat = x.reshape(M, Dc)
            h = (x_flat @ W_gat).reshape(M, HEADS, NUM_EXPERTS)
            loops = jnp.arange(M, dtype=edge_index.dtype)
            src = jnp.concatenate([edge_index[0], loops])
            dst = jnp.concatenate([edge_index[1], loops])
            a_src = (h * att_src).sum(-1)
            a_dst = (h * att_dst).sum(-1)
            e = jax.nn.leaky_relu(a_src[src] + a_dst[dst], negative_slope=0.2)
            e_max = jax.ops.segment_max(e, dst, num_segments=M)
            ee = jnp.exp(e - e_max[dst])
            denom = jax.ops.segment_sum(ee, dst, num_segments=M)
            alpha = ee / (denom[dst] + 1e-16)
            msg = h[src] * alpha[:, :, None]
            agg = jax.ops.segment_sum(msg, dst, num_segments=M).reshape(M, HEADS * NUM_EXPERTS) + b_gat
            scores = _layernorm(agg, ln_gamma, ln_beta).reshape(M, HEADS, NUM_EXPERTS).mean(1)
            scores = scores.reshape(Bc, Nc, NUM_EXPERTS)
            topk_s, topk_i = jax.lax.top_k(scores, TOP_K)
            w = jax.nn.softmax(topk_s, axis=-1)
            out = jnp.zeros_like(x)
            for ei in range(NUM_EXPERTS):
                g = jnp.where(topk_i == ei, w, 0.0).sum(-1)
                hh = jax.nn.gelu(x @ W1[ei] + b1[ei], approximate=False)
                out = out + g[..., None] * (hh @ W2[ei] + b2[ei])
            return out
        return _forward(x, edge_index, W_gat, att_src, att_dst, b_gat, ln_gamma, ln_beta, W1, b1, W2, b2)

    def _L1_gnn_ref(h, k_linears, q_linears, v_linears, a_linears, relation_att, relation_msg, relation_pri, skip, node_type, etype, row_idx, col_idx):
        import jax, jax.numpy as jnp
        import numpy as np
        N_NODES = 625
        N_EDGES = 10000
        IN_DIM = 256
        OUT_DIM = 256
        N_HEADS = 4
        D_K = OUT_DIM // N_HEADS
        N_NTYPES = 4
        N_RELS = 8
        SQRT_DK = float(np.sqrt(D_K))

        def _typed_matmul(x, W, node_type):
            all_t = jnp.einsum('ni,tio->tno', x, W)
            return all_t[node_type, jnp.arange(x.shape[0])]
        n = h.shape[0]
        k = _typed_matmul(h, k_linears, node_type).reshape(n, N_HEADS, D_K)
        q = _typed_matmul(h, q_linears, node_type).reshape(n, N_HEADS, D_K)
        v = _typed_matmul(h, v_linears, node_type).reshape(n, N_HEADS, D_K)
        q_att = jnp.einsum('nhd,rhde->rnhe', q, relation_att)
        v_msg = jnp.einsum('nhd,rhde->rnhe', v, relation_msg)
        aw_q_edge = q_att[etype, col_idx]
        msg_edge = v_msg[etype, row_idx]
        attn_score = jnp.sum(aw_q_edge * k[row_idx], axis=-1)
        score = attn_score * (relation_pri[etype] / SQRT_DK)
        m = jax.ops.segment_max(score, col_idx, num_segments=n)
        ex = jnp.exp(score - m[col_idx])
        denom = jax.ops.segment_sum(ex, col_idx, num_segments=n)
        alpha = ex / denom[col_idx]
        agg = jax.ops.segment_sum(alpha[..., None] * msg_edge, col_idx, num_segments=n)
        agg = agg.reshape(n, OUT_DIM)
        out = _typed_matmul(agg, a_linears, node_type)
        out = jax.nn.sigmoid(skip)[node_type][:, None] * out
        return out

    def _L1_ffn_ref(x, Wr, br, W1, b1, g1, be1, m1, v1, W2, b2, g2, be2, m2, v2, Wo, bo):
        import jax, jax.numpy as jnp
        import numpy as np
        BN_EPS = 0.001

        def _bn(h, g, b, m, v):
            return g * (h - m) * jax.lax.rsqrt(v + BN_EPS) + b
        feat = jnp.mean(x, axis=0)
        w = jax.nn.softmax(feat @ Wr + br, axis=-1)
        h = jnp.einsum('bfd,edh->bfeh', x, W1) + b1
        h = jax.nn.relu(_bn(h, g1, be1, m1, v1))
        h = jnp.einsum('bfeh,ehk->bfek', h, W2) + b2
        h = jax.nn.relu(_bn(h, g2, be2, m2, v2))
        y = jnp.einsum('bfeh,ehd->bfed', h, Wo) + bo
        return jnp.einsum('bfed,fe->bfd', y, w)

    def _L2_gnn_ref(x, W_in, b_in, W_agg, W_self, b_hid, W_out, b_out, edge_index):
        import jax, jax.numpy as jnp
        import numpy as np
        N_NODES = 50000
        N_EDGES = 25000
        IN_CH = 256
        HID_CH = 256
        OUT_CH = 256
        N_LAYERS = 3
        n = x.shape[0]
        dst = edge_index[0]
        src = edge_index[1]
        n_layers = W_agg.shape[0]
        h = x @ W_in + b_in
        deg = jax.ops.segment_sum(jnp.ones_like(dst, dtype=h.dtype), dst, num_segments=n)
        deg = jnp.maximum(deg, 1.0)[:, None]
        for l in range(n_layers):
            agg = jax.ops.segment_sum(h[src], dst, num_segments=n) / deg
            h = jax.nn.relu(agg @ W_agg[l] + h @ W_self[l] + b_hid[l])
        return h @ W_out + b_out

    def _L2_ffn_ref(h, gate_w, gate_b, w1, b1, w2, b2):
        import math
        import jax, jax.numpy as jnp
        import numpy as np
        CAPACITY_FACTOR = 1.25
        B, L, D = h.shape
        E = gate_w.shape[1]
        T = B * L
        C = max(1, math.ceil(CAPACITY_FACTOR * T / E))
        x = h.reshape(T, D)
        logits = x @ gate_w + gate_b
        probs = jax.nn.softmax(logits, axis=-1)
        idx = jnp.argmax(probs, axis=-1)
        prb = jnp.take_along_axis(probs, idx[:, None], axis=1)[:, 0]
        one_hot = jax.nn.one_hot(idx, E, dtype=jnp.float32)
        pos = (jnp.cumsum(one_hot, axis=0) * one_hot).sum(-1).astype(jnp.int32) - 1
        kept = pos < C
        pos_safe = jnp.where(kept, pos, C)
        buf = jnp.zeros((E, C, D), dtype=h.dtype).at[idx, pos_safe].set(x, mode='drop')
        hmid = jax.nn.relu(jnp.einsum('ecd,edf->ecf', buf, w1) + b1[:, None, :])
        ybuf = jnp.einsum('ecf,efd->ecd', hmid, w2) + b2[:, None, :]
        pos_g = jnp.minimum(pos, C - 1)
        y_tok = ybuf[idx, pos_g] * (prb * kept)[:, None]
        y = y_tok.reshape(B, L, D)
        y = jnp.nan_to_num(y, nan=0.0, posinf=10000.0, neginf=-10000.0)
        return y

    def _L3_gnn_ref(x, edge_weight, ln_w, ln_b, W, b, gamma, beta, edge_row, edge_col):
        import jax, jax.numpy as jnp
        import numpy as np
        N, D, E = (3125, 256, 100000)
        n_nodes = x.shape[0]
        mu = jnp.mean(x, axis=-1, keepdims=True)
        var = jnp.var(x, axis=-1, keepdims=True)
        h = (x - mu) * jax.lax.rsqrt(var + 1e-05) * ln_w + ln_b
        h = h * jax.nn.sigmoid(h)
        msg = edge_weight[:, None] * h[edge_col]
        z = jax.ops.segment_sum(msg, edge_row, num_segments=n_nodes)
        h = z @ W.T + b
        h = h * gamma + beta
        return x + h

    def _L3_ffn_ref(x, Wr, br, W1, b1, W2, b2, gamma, beta):
        import math
        import jax, jax.numpy as jnp
        import numpy as np
        CAPACITY_FACTOR = 1.25
        TOP_K = 2
        LN_EPS = 1e-05

        def _layer_norm(x, gamma, beta):
            mu = jnp.mean(x, axis=-1, keepdims=True)
            var = jnp.var(x, axis=-1, keepdims=True)
            return (x - mu) * jax.lax.rsqrt(var + LN_EPS) * gamma + beta
        B, S, D = x.shape
        E = Wr.shape[1]
        N = B * S
        K = TOP_K
        logits = jnp.mean(x, axis=1) @ Wr + br
        routing_weights = jax.nn.softmax(logits, axis=-1)
        capacity = float(math.ceil(N * CAPACITY_FACTOR / E))
        expected_loads = routing_weights.sum(axis=0) * (N / B)
        scale = jnp.where(expected_loads > capacity, capacity / expected_loads, 1.0)
        routing_weights = jax.nn.softmax(routing_weights * scale, axis=-1)
        rw_tok = jnp.broadcast_to(routing_weights[:, None, :], (B, S, E)).reshape(N, E)
        top_w, top_i = jax.lax.top_k(rw_tok, K)
        top_w = jax.nn.softmax(top_w, axis=-1)
        xf = x.reshape(N, D)
        h = jax.nn.gelu(jnp.einsum('nd,edf->enf', xf, W1) + b1[:, None, :], approximate=False)
        y = jnp.einsum('enf,efd->end', h, W2) + b2[:, None, :]
        w_dense = jnp.zeros((N, E), x.dtype).at[jnp.arange(N)[:, None], top_i].add(top_w)
        out = jnp.einsum('ne,end->nd', w_dense, y).reshape(B, S, D)
        out = _layer_norm(out + x, gamma, beta)
        return out
    edge_index = jnp.stack([src, dst])
    x = x + _L0_gnn_ref(_layernorm(x, axis=-1), L0_gnn_W1, L0_gnn_b1, L0_gnn_W2, L0_gnn_b2, edge_index)
    x = x + _L0_ffn_ref(_layernorm(x, axis=-1)[None], L0_ffn_W_gat, L0_ffn_att_src, L0_ffn_att_dst, L0_ffn_b_gat, L0_ffn_ln_gamma, L0_ffn_ln_beta, L0_ffn_W1, L0_ffn_b1, L0_ffn_W2, L0_ffn_b2, L0_ffn_edge_index)[0]
    x = x + _L1_gnn_ref(_layernorm(x, axis=-1), L1_gnn_k_linears, L1_gnn_q_linears, L1_gnn_v_linears, L1_gnn_a_linears, L1_gnn_relation_att, L1_gnn_relation_msg, L1_gnn_relation_pri, L1_gnn_skip, node_type_4, edge_type_8, src, dst)
    x = x + _L1_ffn_ref(_layernorm(x, axis=-1)[None], L1_ffn_Wr, L1_ffn_br, L1_ffn_W1, L1_ffn_b1, L1_ffn_g1, L1_ffn_be1, L1_ffn_m1, L1_ffn_v1, L1_ffn_W2, L1_ffn_b2, L1_ffn_g2, L1_ffn_be2, L1_ffn_m2, L1_ffn_v2, L1_ffn_Wo, L1_ffn_bo)[0]
    x = x + _L2_gnn_ref(_layernorm(x, axis=-1), L2_gnn_W_in, L2_gnn_b_in, L2_gnn_W_agg, L2_gnn_W_self, L2_gnn_b_hid, L2_gnn_W_out, L2_gnn_b_out, edge_index)
    x = x + _L2_ffn_ref(_layernorm(x, axis=-1)[None], L2_ffn_gate_w, L2_ffn_gate_b, L2_ffn_w1, L2_ffn_b1, L2_ffn_w2, L2_ffn_b2)[0]
    x = x + _L3_gnn_ref(_layernorm(x, axis=-1), edge_weight, L3_gnn_ln_w, L3_gnn_ln_b, L3_gnn_W, L3_gnn_b, L3_gnn_gamma, L3_gnn_beta, src, dst)
    x = x + _L3_ffn_ref(_layernorm(x, axis=-1)[None], L3_ffn_Wr, L3_ffn_br, L3_ffn_W1, L3_ffn_b1, L3_ffn_W2, L3_ffn_b2, L3_ffn_gamma, L3_ffn_beta)[0]
    return x

_drawn_inputs = setup_inputs


def setup_inputs(seed=0):
    import zlib

    import numpy as np

    out = dict(_drawn_inputs(seed))
    spreads = {'L0_gnn_b1': (0.0, 0.1),
     'L0_gnn_b2': (0.0, 0.1),
     'L0_ffn_b_gat': (0.0, 0.1),
     'L0_ffn_ln_gamma': (1.0, 0.2),
     'L0_ffn_ln_beta': (0.0, 0.1),
     'L0_ffn_b1': (0.0, 0.1),
     'L0_ffn_b2': (0.0, 0.1),
     'L1_gnn_relation_pri': (1.0, 0.2),
     'L1_gnn_skip': (1.0, 0.6),
     'L1_ffn_br': (0.0, 0.521),
     'L1_ffn_b1': (0.0, 0.383),
     'L1_ffn_g1': (1.0, 0.2),
     'L1_ffn_be1': (0.0, 0.434),
     'L1_ffn_m1': (0.0, 0.401),
     'L1_ffn_v1': (1.0, 0.6),
     'L1_ffn_b2': (0.0, 0.274),
     'L1_ffn_g2': (1.0, 0.2),
     'L1_ffn_be2': (0.0, 0.293),
     'L1_ffn_m2': (0.0, 0.1),
     'L1_ffn_v2': (1.0, 0.6),
     'L1_ffn_bo': (0.0, 0.1),
     'L2_gnn_b_in': (0.0, 0.1),
     'L2_gnn_b_hid': (0.0, 0.1),
     'L2_gnn_b_out': (0.0, 0.1),
     'L2_ffn_gate_b': (0.0, 0.1),
     'L2_ffn_b1': (0.0, 0.8),
     'L2_ffn_b2': (0.0, 0.8),
     'L3_gnn_ln_w': (1.0, 0.2),
     'L3_gnn_ln_b': (0.0, 0.1),
     'L3_ffn_br': (0.0, 0.1),
     'L3_ffn_b1': (0.0, 0.8),
     'L3_ffn_b2': (0.0, 0.588),
     'L3_ffn_gamma': (1.0, 0.2),
     'L3_ffn_beta': (0.0, 0.398)}
    factors = {'L3_gnn_b': 23.416}
    for name, (base, spread) in spreads.items():
        noise = np.random.default_rng([zlib.crc32(name.encode()), seed]).standard_normal(out[name].shape)
        drawn = base * np.exp(spread * noise) if base else spread * noise
        out[name] = jnp.asarray(drawn.astype(out[name].dtype))
    for name, factor in factors.items():
        out[name] = (out[name] * factor).astype(out[name].dtype)
    return out
```

```python
from contextlib import ExitStack


import concourse.bass as bass
from concourse import mybir

F32 = mybir.dt.float32
BF16 = mybir.dt.bfloat16
I32 = mybir.dt.int32
ALU = mybir.AluOpType
ACT = mybir.ActivationFunctionType
AX_X = mybir.AxisListType.X
ds = bass.ds

P = 128
N = 3125
D = 256
NT = -(-N // P)
NP = NT * P
U = 5
ROUNDS = NT // U
LAST = N - (NT - 1) * P
EPS = 1e-5
CHUNK = 320
G = 8


class Kit:
    pass


def sems(nc, ctx, stage, names):
    taken = [nc.alloc_semaphore(f"{stage}_{n}") for n in names.split()]

    def give_back():
        for sem in taken:
            nc.gpsimd.sem_clear(sem)
            nc.release_semaphore(sem)
    ctx.callback(give_back)
    return taken


def gather_sems(nc, stage, what, n):
    return [nc.alloc_semaphore(f"{stage}_{what}{u}") for u in range(n)]


def wait_alone(eng, sem, value):
    eng.wait_ge(sem, value)
    eng.nop(nofuse=True)


def link_on(eng, sem):
    count = {"base": 0, "k": 0}

    def link(ins):
        count["k"] += 1
        ins.then_inc(sem, 1)
        eng.wait_ge(sem, count["base"] + count["k"])

    def begin(i, n):
        count["start"], count["n"] = count["base"] + count["k"], n
        count["base"], count["k"] = count["start"] + i * n, 0

    def end(rounds):
        assert count["k"] == count["n"], (count["k"], count["n"])
        count["base"], count["k"] = count["start"] + rounds * count["n"], 0

    def plain():
        return count["base"] + count["k"]

    link.begin, link.end, link.value = begin, end, plain
    return link


def nat(buf):
    return buf[:, :].rearrange("p (t d) -> p t d", t=NT)


def tr(buf, k=2):
    return buf[:, 0:k * NP].rearrange("p (k n) -> p k n", k=k)


def row_to_all(ap1d, n=P):
    return bass.AP(tensor=ap1d.tensor, offset=ap1d.offset, ap=[[0, n], list(ap1d.ap[0])])


def make_constants(nc, ctx, kit):
    def sb(name, shape, dt=F32):
        return ctx.enter_context(nc.sbuf_tensor(name, shape, dt))
    kit.ident = sb("ident", [P, P])
    kit.tri = sb("tri_strict", [P, P])
    kit.ones = sb("ones", [P, P])
    kit.iota = sb("iota_row", [P, P])
    kit.iota_t = sb("iota_tiles", [1, 424])
    kit.node = sb("node_number", [P, NT])
    with ExitStack() as c:
        made, = sems(nc, c, "const", "made")
        ints = c.enter_context(nc.sbuf_tensor("iota_int", [P, P], I32))
        ints_t = c.enter_context(nc.sbuf_tensor("iota_t_int", [1, 424], I32))
        node_i = c.enter_context(nc.sbuf_tensor("node_int", [P, NT], I32))
        with nc.Block() as block:
            @block.gpsimd
            def _(pool):
                link = link_on(pool, made)
                link(nc.gpsimd.memset(kit.ident[:], 0.0))
                link(nc.gpsimd.affine_select(out=kit.ident[:], in_=kit.ident[:], compare_op=ALU.not_equal,
                                             fill=1.0, base=0, pattern=[[-1, P]], channel_multiplier=1))
                link(nc.gpsimd.memset(kit.ones[:], 1.0))
                link(nc.gpsimd.affine_select(out=kit.tri[:], in_=kit.ones[:], compare_op=ALU.is_gt,
                                             fill=0.0, base=0, pattern=[[1, P]], channel_multiplier=-1))
                link(nc.gpsimd.iota(ints[:], pattern=[[1, P]], base=0, channel_multiplier=0))
                link(nc.gpsimd.tensor_copy(kit.iota[:], ints[:]))
                link(nc.gpsimd.iota(ints_t[:], pattern=[[1, 424]], base=0, channel_multiplier=0))
                link(nc.gpsimd.tensor_copy(kit.iota_t[:], ints_t[:]))
                link(nc.gpsimd.iota(node_i[:], pattern=[[P, NT]], base=0, channel_multiplier=1))
                link(nc.gpsimd.tensor_copy(kit.node[:], node_i[:]))


class EdgeList:
    pass


def alloc_edges(nc, ctx, name, groups):
    e = EdgeList()
    e.name, e.groups = name, groups
    e.rec = ctx.enter_context(nc.sbuf_tensor(f"{name}_rec", [P, groups + G, 4], F32))
    e.src = ctx.enter_context(nc.sbuf_tensor(f"{name}_src", [P, groups + G], I32))
    e.key = ctx.enter_context(nc.sbuf_tensor(f"{name}_key", [P, groups + G], I32))
    e.blk = ctx.enter_context(nc.sbuf_tensor(f"{name}_blk", [1, groups], I32))
    e.dram = nc.dram_tensor(f"{name}_sorted", (P * groups, 4), F32).ap()
    return e


def sort_edges(nc, kit, e, rows, src, dst, etype=None, weight=None, first=0):
    C = dst.shape[0] // rows
    S = 8
    groups = e.groups
    view = lambda a: a.rearrange("(p c) -> p c", p=rows)
    nm = e.name
    with ExitStack() as c:
        def sb(name, shape, dt=F32):
            return c.enter_context(nc.sbuf_tensor(f"{nm}_{name}", shape, dt))
        dst_i, src_i, type_i, work_i = (sb(x, [rows, C], I32) for x in ("dsti", "srci", "typei", "worki"))
        hi, eq, inc, pos, ones_row, wt = (sb(x, [rows, C]) for x in ("hi", "eq", "inc", "pos", "ones_row", "wt"))
        rec = sb("in_rec", [rows, C, 4])
        adr = sb("adr", [rows, C], I32)
        col = sb("col", [rows, C], I32)
        tot, before = sb("tot", [rows, NT]), sb("before", [rows, NT])
        n_grp, end = sb("n_grp", [P, NT]), sb("end", [P, NT])
        n_int = sb("n_int", [P, NT], I32)
        bf, bf2 = sb("bf", [1, groups]), sb("bf2", [1, groups])
        empty = sb("empty", [P, groups, 4])
        st_rec = [sb(f"st_rec{u}", [rows, 4]) for u in range(S)]
        st_adr = [sb(f"st_adr{u}", [rows, 1], I32) for u in range(S)]
        ps = c.enter_context(nc.psum_tensor(f"{nm}_ps", [P, 512], F32))
        loaded, cleared, emptied, step, counted, summed, addressed, staged = sems(
            nc, c, nm, "loaded cleared emptied step counted summed addressed staged")
        sent = gather_sems(nc, nm, "sent", S)
        back, = sems(nc, c, nm, "back")
        n_loads = 2 + (etype is not None) + (weight is not None)
        with nc.Block() as block:
            @block.sync
            def _(sp):
                sp.dma_start(dst_i[:], view(dst)).then_inc(loaded, 16)
                sp.dma_start(src_i[:], view(src)).then_inc(loaded, 16)
                if etype is not None:
                    sp.dma_start(type_i[:], view(etype)).then_inc(loaded, 16)
                if weight is not None:
                    sp.dma_start(wt[:], view(weight)).then_inc(loaded, 16)
                sp.wait_ge(cleared, 4)
                sp.dma_start(e.dram.rearrange("(p g) w -> p (g w)", p=P),
                             empty[:].rearrange("p g w -> p (g w)")).then_inc(emptied, 16)
                for u in range(S):
                    sp.wait_ge(sent[u], 16 * (C // S))
                sp.dma_start(e.rec[:, 0:groups, :],
                             e.dram.rearrange("(p g) w -> p g w", p=P)).then_inc(back, 16)

            @block.vector
            def _(dve):
                nc.vector.memset(empty[:], 0.0).then_inc(cleared, 1)
                dve.wait_ge(cleared, 1)
                nc.vector.memset(empty[:, :, 1:2], 999.0).then_inc(cleared, 1)
                nc.vector.memset(e.rec[:, groups:, :], 0.0).then_inc(cleared, 1)
                nc.vector.memset(bf[:], 0.0).then_inc(cleared, 1)
                dve.wait_ge(cleared, 4)
                dve.wait_ge(loaded, 16 * n_loads)
                link = link_on(dve, step)
                link(nc.vector.tensor_scalar(work_i[:], dst_i[:], 7, None, ALU.arith_shift_right))
                link(nc.vector.tensor_copy(hi[:], work_i[:]))
                link(nc.vector.tensor_scalar(col[:], dst_i[:], 127, None, ALU.bitwise_and))
                link(nc.vector.tensor_copy(rec[:, :, 1], col[:]))
                link(nc.vector.tensor_copy(rec[:, :, 0], src_i[:]))
                if weight is not None:
                    link(nc.vector.tensor_copy(rec[:, :, 2], wt[:]))
                else:
                    link(nc.vector.memset(rec[:, :, 2], 1.0))
                if etype is not None:
                    link(nc.vector.scalar_tensor_tensor(out=rec[:, :, 3], in0=type_i[:], scalar=float(NP),
                                                        in1=src_i[:], op0=ALU.mult, op1=ALU.add))
                else:
                    link(nc.vector.tensor_copy(rec[:, :, 3], src_i[:]))
                link(nc.vector.memset(pos[:], float(first * P - 1)))
                with dve.Fori(0, NT) as b:
                    link.begin(b, 2)
                    link(nc.vector.tensor_scalar(eq[:], hi[:], kit.iota[0:rows, ds(b, 1)], None, ALU.is_equal))
                    link(nc.vector.tensor_reduce(tot[:, ds(b, 1)], eq[:], AX_X, ALU.add))
                link.end(NT)
                nc.vector.memset(ones_row[:], 1.0).then_inc(counted, 1)
                dve.wait_ge(counted, 1)
                dve.wait_ge(summed, 1)
                link(nc.vector.tensor_scalar(n_int[:], ps[:, 64:64 + NT], 127.0, None, ALU.add))
                link(nc.vector.tensor_scalar(n_int[:], n_int[:], 7, None, ALU.arith_shift_right))
                link(nc.vector.tensor_copy(n_grp[:], n_int[:]))
                link(nc.vector.tensor_tensor_scan(end[:], kit.ones[:, 0:NT], n_grp[:], 0.0, ALU.mult, ALU.add))
                link(nc.vector.tensor_tensor(n_grp[:], end[:], n_grp[:], ALU.subtract))
                link(nc.vector.scalar_tensor_tensor(out=before[:], in0=n_grp[0:rows, :], scalar=128.0,
                                                    in1=ps[0:rows, 0:NT], op0=ALU.mult, op1=ALU.add))
                with dve.Fori(0, NT) as b:
                    link.begin(b, 4)
                    link(nc.vector.tensor_scalar(eq[:], hi[:], kit.iota[0:rows, ds(b, 1)], None, ALU.is_equal))
                    link(nc.vector.tensor_tensor_scan(inc[:], ones_row[:], eq[:], 0.0, ALU.mult, ALU.add))
                    link(nc.vector.scalar_tensor_tensor(out=wt[:], in0=inc[:], scalar=before[:, ds(b, 1)],
                                                        in1=eq[:], op0=ALU.add, op1=ALU.mult))
                    link(nc.vector.tensor_tensor(pos[:], pos[:], wt[:], ALU.add))
                link.end(NT)
                link(nc.vector.tensor_copy(work_i[:], pos[:]))
                link(nc.vector.tensor_scalar(col[:], work_i[:], 127, None, ALU.bitwise_and))
                link(nc.vector.tensor_scalar(work_i[:], work_i[:], 7, None, ALU.arith_shift_right))
                link(nc.vector.scalar_tensor_tensor(out=adr[:], in0=col[:], scalar=float(groups), in1=work_i[:],
                                                    op0=ALU.mult, op1=ALU.add))
                with dve.Fori(0, NT) as b:
                    link.begin(b, 1)
                    link(nc.vector.scalar_tensor_tensor(out=bf[:], in0=kit.iota_t[:, 0:groups],
                                                        scalar=end[0:1, ds(b, 1)], in1=bf[:],
                                                        op0=ALU.is_ge, op1=ALU.add))
                link.end(NT)
                if first:
                    link(nc.vector.tensor_copy(bf2[:, first:groups], bf[:, 0:groups - first]))
                    link(nc.vector.tensor_copy(bf[:, first:groups], bf2[:, first:groups]))
                    link(nc.vector.tensor_copy(bf[:, 0:first], kit.iota_t[:, 0:first]))
                link(nc.vector.tensor_scalar(e.blk[:], bf[:], float(NT - 1), None, ALU.min))
                dve.wait_ge(emptied, 16)
                for i, u in [(0, u) for u in range(S)]:
                    nc.vector.tensor_copy(st_rec[u][:], rec[:, u, :])
                    nc.vector.tensor_copy(st_adr[u][:], adr[:, u:u + 1]).then_inc(staged, 1)
                with dve.Fori(1, C // S) as i:
                    for u in range(S):
                        dve.wait_ge(sent[u], i * 16)
                        nc.vector.tensor_copy(st_rec[u][:], rec[:, ds(i * S + u, 1), :].rearrange("p o w -> p (o w)"))
                        nc.vector.tensor_copy(st_adr[u][:], adr[:, ds(i * S + u, 1)]).then_inc(staged, 1)
                dve.wait_ge(back, 16)
                if first:
                    link(nc.vector.tensor_copy(e.rec[:, 0:first, 0], kit.node[:]))
                    link(nc.vector.tensor_copy(e.rec[:, 0:first, 3], kit.node[:]))
                    link(nc.vector.tensor_copy(e.rec[:, 0:first, 1], kit.node[:, 0:1].broadcast_to([P, first])))
                nc.vector.tensor_copy(e.src[:], e.rec[:, :, 0]).then_inc(addressed, 1)
                nc.vector.tensor_copy(e.key[:], e.rec[:, :, 3]).then_inc(addressed, 1)
                dve.wait_ge(addressed, 2)

            @block.tensor
            def _(pe):
                pe.wait_ge(counted, 1)
                nc.tensor.matmul(ps[0:rows, 0:NT], kit.tri[0:rows, 0:rows], tot[:], start=True, stop=True)
                nc.tensor.matmul(ps[:, 64:64 + NT], kit.ones[0:rows, :], tot[:], start=True, stop=True)\
                    .then_inc(summed, 1)

            @block.gpsimd
            def _(pool):
                with pool.Fori(0, C // S) as i:
                    for u in range(S):
                        wait_alone(pool, staged, i * S + u + 1)
                        nc.gpsimd.indirect_dma_start(e.dram, bass.IndirectOffsetOnAxis(ap=st_adr[u][:, :1], axis=0),
                                                     st_rec[u][:], None).then_inc(sent[u], 16)


def layer_norm(nc, kit, nm, x, xn, xt=None):
    with ExitStack() as c:
        st = [c.enter_context(nc.sbuf_tensor(f"{nm}_st{u}", [P, D], F32)) for u in range(U)]
        stats = c.enter_context(nc.sbuf_tensor(f"{nm}_stats", [P, NT, 6], F32))
        mean, var, tmp, std, rstd, shift = (c.enter_context(nc.sbuf_tensor(f"{nm}_{x_}", [P, NT], F32))
                                            for x_ in ("mean", "var", "tmp", "std", "rstd", "shift"))
        ps = [c.enter_context(nc.psum_tensor(f"{nm}_ps{u}", [P, 512], F32)) for u in range(U)]
        measured, step, rooted, normed, turned, kept = sems(nc, c, nm, "measured step rooted normed turned kept")
        with nc.Block() as block:
            @block.vector
            def _(dve):
                with dve.Fori(0, NT) as t:
                    nc.vector.bn_stats(stats[:, ds(t, 1), :].rearrange("p o s -> p (o s)"),
                                       nat(x)[:, ds(t, 1), :].rearrange("p o d -> p (o d)")).then_inc(measured, 1)
                dve.wait_ge(measured, NT)
                link = link_on(dve, step)
                link(nc.vector.tensor_tensor(mean[:], stats[:, :, 1], stats[:, :, 4], ALU.add))
                link(nc.vector.tensor_scalar(mean[:], mean[:], 0.5, None, ALU.mult))
                link(nc.vector.tensor_tensor(tmp[:], stats[:, :, 1], stats[:, :, 4], ALU.subtract))
                link(nc.vector.tensor_tensor(tmp[:], tmp[:], tmp[:], ALU.mult))
                link(nc.vector.tensor_tensor(var[:], stats[:, :, 2], stats[:, :, 5], ALU.add))
                link(nc.vector.tensor_scalar(var[:], var[:], 1.0 / D, EPS, ALU.mult, ALU.add))
                link(nc.vector.scalar_tensor_tensor(out=var[:], in0=tmp[:], scalar=0.25, in1=var[:],
                                                    op0=ALU.mult, op1=ALU.add))
                dve.wait_ge(rooted, 1)
                link(nc.vector.reciprocal(rstd[:], std[:]))
                link(nc.vector.scalar_tensor_tensor(out=shift[:], in0=mean[:], scalar=-1.0, in1=rstd[:],
                                                    op0=ALU.mult, op1=ALU.mult))
                with dve.Fori(0, ROUNDS) as i:
                    for u in range(U):
                        t = i * U + u
                        dve.wait_ge(kept, i * U + u + 1)
                        nc.vector.tensor_scalar(st[u][:], nat(x)[:, ds(t, 1), :].rearrange("p o d -> p (o d)"),
                                                rstd[:, ds(t, 1)], shift[:, ds(t, 1)],
                                                ALU.mult, ALU.add).then_inc(normed, 1)

            @block.scalar
            def _(act):
                act.wait_ge(step, 7)
                nc.scalar.activation(std[:], var[:], ACT.Sqrt).then_inc(rooted, 1)
                act.sem_inc(kept, U)
                with act.Fori(0, ROUNDS) as i:
                    for u in range(U):
                        t = i * U + u
                        act.wait_ge(turned, i * U + u + 1)
                        kept_xn = nc.scalar.copy(nat(xn)[:, ds(t, 1), :].rearrange("p o d -> p (o d)"), st[u][:])
                        if xt is None:
                            kept_xn.then_inc(kept, 1)
                            continue
                        nc.scalar.copy(tr(xt)[:, :, ds(t * P, P)],
                                       ps[u][:, 0:D].rearrange("p (k n) -> p k n", k=2)).then_inc(kept, 1)

            @block.tensor
            def _(pe):
                with pe.Fori(0, ROUNDS) as i:
                    for u in range(U):
                        pe.wait_ge(normed, i * U + u + 1)
                        if xt is None:
                            pe.nop(nofuse=True).then_inc(turned, 1)
                            continue
                        nc.tensor.transpose(ps[u][:, 0:P], st[u][:, 0:P], kit.ident[:])
                        nc.tensor.transpose(ps[u][:, P:D], st[u][:, P:D], kit.ident[:]).then_inc(turned, 1)


def project_t(nc, nm, sources, dst, fc, func=ACT.Identity, bias=None):
    terms = [(src, kc, w, k) for src, kc, w in sources for k in range(kc)]
    with ExitStack() as c:
        ps = [[c.enter_context(nc.psum_tensor(f"{nm}_ps{h}{f}", [P, 512], F32)) for f in range(fc)] for h in range(2)]
        multiplied, read = sems(nc, c, nm, "multiplied read")
        with nc.Block() as block:
            @block.tensor
            def _(pe):
                with pe.Fori(0, NP // CHUNK // 2) as i:
                    for h in range(2):
                        for f in range(fc):
                            pe.wait_ge(read, (i * 2 + h) * fc + f + 1)
                            for n, (src, kc, w, k) in enumerate(terms):
                                mm = nc.tensor.matmul(ps[h][f][:, 0:CHUNK], w[:, k, f * P:(f + 1) * P],
                                                      tr(src, kc)[:, k, ds((i * 2 + h) * CHUNK, CHUNK)],
                                                      start=(n == 0), stop=(n == len(terms) - 1))
                            mm.then_inc(multiplied, 1)

            @block.scalar
            def _(act):
                act.sem_inc(read, 2 * fc)
                with act.Fori(0, NP // CHUNK // 2) as i:
                    for h in range(2):
                        for f in range(fc):
                            act.wait_ge(multiplied, (i * 2 + h) * fc + f + 1)
                            nc.scalar.activation(tr(dst, fc)[:, f, ds((i * 2 + h) * CHUNK, CHUNK)],
                                                 ps[h][f][:, 0:CHUNK], func,
                                                 bias=(bias[:, f:f + 1] if bias is not None else 0.0)).then_inc(read, 1)


def write_table(nc, kit, nm, src, kc, scratch, table):
    W = kc * P
    rows = scratch[:, 0:NT * W].rearrange("p (t d) -> p t d", t=NT)
    with ExitStack() as c:
        st = [c.enter_context(nc.sbuf_tensor(f"{nm}_st{u}", [P, kc, P], F32)) for u in range(U)]
        ps = [c.enter_context(nc.psum_tensor(f"{nm}_ps{u}", [P, 512], F32)) for u in range(U)]
        staged, turned, copied, stored = sems(nc, c, nm, "staged turned copied stored")
        with nc.Block() as block:
            @block.vector
            def _(dve):
                with dve.Fori(0, ROUNDS) as i:
                    for u in range(U):
                        dve.wait_ge(turned, i * U + u + 1)
                        nc.vector.tensor_copy(st[u][:], tr(src, kc)[:, :, ds((i * U + u) * P, P)]).then_inc(staged, 1)

            @block.tensor
            def _(pe):
                pe.sem_inc(turned, U)
                with pe.Fori(0, ROUNDS) as i:
                    for u in range(U):
                        pe.wait_ge(staged, i * U + u + 1)
                        pe.wait_ge(copied, i * U + u + 1)
                        for k in range(kc):
                            mm = nc.tensor.transpose(ps[u][:, k * P:(k + 1) * P], st[u][:, k, :], kit.ident[:])
                        mm.then_inc(turned, 1)

            @block.scalar
            def _(act):
                act.sem_inc(copied, U)
                with act.Fori(0, ROUNDS) as i:
                    for u in range(U):
                        act.wait_ge(turned, i * U + u + 1 + U)
                        nc.scalar.copy(rows[:, ds(i * U + u, 1), :].rearrange("p o d -> p (o d)"),
                                       ps[u][:, 0:W]).then_inc(copied, 1)

            @block.sync
            def _(sp):
                with sp.Fori(0, ROUNDS) as i:
                    sp.wait_ge(copied, i * U + 2 * U)
                    sp.dma_start(table.rearrange("(t p) d -> p t d", p=P)[:, ds(i * U, U), :],
                                 rows[:, ds(i * U, U), :]).then_inc(stored, 16)
                sp.wait_ge(stored, 16 * ROUNDS)


def aggregate_t(nc, kit, nm, e, table, kc, acc, weighted=False):
    W = kc * P
    with ExitStack() as c:
        idx = [c.enter_context(nc.sbuf_tensor(f"{nm}_idx{u}", [P, 1], I32)) for u in range(G)]
        rows = [c.enter_context(nc.sbuf_tensor(f"{nm}_rows{u}", [P, W], F32)) for u in range(G)]
        hot = [c.enter_context(nc.sbuf_tensor(f"{nm}_hot{u}", [P, P], F32)) for u in range(G)]
        ps = [c.enter_context(nc.psum_tensor(f"{nm}_ps{u}", [P, 512], F32)) for u in range(G)]
        indexed, matched, multiplied, added = sems(nc, c, nm, "indexed matched multiplied added")
        gathered = gather_sems(nc, nm, "gathered", G)
        rounds = e.groups // G
        with nc.Block() as block:
            @block.scalar
            def _(act):
                with act.Fori(0, rounds) as i:
                    for u in range(G):
                        act.wait_ge(multiplied, i * G + u + 1)
                        nc.scalar.copy(idx[u][:], e.src[:, ds(i * G + u, 1)]).then_inc(indexed, 1)

            @block.gpsimd
            def _(pool):
                with pool.Fori(0, rounds) as i:
                    for u in range(G):
                        wait_alone(pool, indexed, i * G + u + 1)
                        nc.gpsimd.indirect_dma_start(rows[u][:], None, table,
                                                     bass.IndirectOffsetOnAxis(ap=idx[u][:, :1], axis=0)
                                                     ).then_inc(gathered[u], 16)

            @block.tensor
            def _(pe):
                pe.sem_inc(multiplied, G)
                with pe.Fori(0, rounds) as i:
                    for u in range(G):
                        pe.wait_ge(gathered[u], i * 16 + 16)
                        pe.wait_ge(matched, i * G + u + 1)
                        pe.wait_ge(added, i * G + u + 1)
                        for k in range(kc):
                            mm = nc.tensor.matmul(ps[u][:, k * P:(k + 1) * P], rows[u][:, k * P:(k + 1) * P],
                                                  hot[u][:], start=True, stop=True)
                        mm.then_inc(multiplied, 1)

            @block.vector
            def _(dve):
                def match(t, u):
                    nc.vector.tensor_scalar(hot[u][:], kit.iota[:], e.rec[:, ds(t, 1), 1:2].rearrange("p o w -> p (o w)"),
                                            e.rec[:, ds(t, 1), 2:3].rearrange("p o w -> p (o w)") if weighted else None,
                                            ALU.is_equal, *([ALU.mult] if weighted else [])).then_inc(matched, 1)
                for u in range(G):
                    match(u, u)
                nc.vector.memset(acc[:, 0:kc * NP], 0.0).then_inc(added, G)
                with dve.Fori(0, rounds) as i:
                    for u in range(G):
                        t = i * G + u
                        blk = dve.value_load(e.blk[0:1, ds(t, 1)], min_val=0, max_val=NT - 1)
                        dve.wait_ge(multiplied, i * G + u + 1 + G)
                        dve.wait_ge(added, i * G + u + G)
                        to = tr(acc, kc)[:, :, ds(blk * P, P)]
                        nc.vector.tensor_tensor(to, to, ps[u][:, 0:W].rearrange("p (k n) -> p k n", k=kc),
                                                ALU.add).then_inc(added, 1)
                        match(t + G, u)


def turn(nc, kit, nm, src, dst):
    with ExitStack() as c:
        st = [c.enter_context(nc.sbuf_tensor(f"{nm}_st{u}", [P, D], F32)) for u in range(U)]
        ps = [c.enter_context(nc.psum_tensor(f"{nm}_ps{u}", [P, 512], F32)) for u in range(U)]
        staged, turned, copied = sems(nc, c, nm, "staged turned copied")
        with nc.Block() as block:
            @block.vector
            def _(dve):
                with dve.Fori(0, ROUNDS) as i:
                    for u in range(U):
                        dve.wait_ge(turned, i * U + u + 1)
                        nc.vector.tensor_copy(st[u][:], src[:, ds(i * U + u, 1), :].rearrange("p o d -> p (o d)")
                                              ).then_inc(staged, 1)

            @block.tensor
            def _(pe):
                pe.sem_inc(turned, U)
                with pe.Fori(0, ROUNDS) as i:
                    for u in range(U):
                        pe.wait_ge(staged, i * U + u + 1)
                        pe.wait_ge(copied, i * U + u + 1)
                        nc.tensor.transpose(ps[u][:, 0:P], st[u][:, 0:P], kit.ident[:])
                        nc.tensor.transpose(ps[u][:, P:D], st[u][:, P:D], kit.ident[:]).then_inc(turned, 1)

            @block.scalar
            def _(act):
                act.sem_inc(copied, U)
                with act.Fori(0, ROUNDS) as i:
                    for u in range(U):
                        wait_alone(act, turned, i * U + u + 1 + U)
                        nc.scalar.copy(dst[:, :, ds((i * U + u) * P, P)],
                                       ps[u][:, 0:D].rearrange("p (k n) -> p k n", k=2)).then_inc(copied, 1)


def add_projection(nc, nm, src, w, to, bias=None, fresh=False, gate=None):
    kc, width = w.shape[1], w.shape[2]
    with ExitStack() as c:
        st = [c.enter_context(nc.sbuf_tensor(f"{nm}_st{u}", [P, kc, P], F32)) for u in range(U)]
        ps = [c.enter_context(nc.psum_tensor(f"{nm}_ps{u}", [P, 512], F32)) for u in range(U)]
        staged, multiplied, added, biased = sems(nc, c, nm, "staged multiplied added biased")
        with nc.Block() as block:
            @block.scalar
            def _(act):
                with act.Fori(0, ROUNDS) as i:
                    for u in range(U):
                        act.wait_ge(multiplied, i * U + u + 1)
                        nc.scalar.copy(st[u][:], tr(src, kc)[:, :, ds((i * U + u) * P, P)]).then_inc(staged, 1)

            @block.tensor
            def _(pe):
                pe.sem_inc(multiplied, U)
                with pe.Fori(0, ROUNDS) as i:
                    for u in range(U):
                        pe.wait_ge(staged, i * U + u + 1)
                        pe.wait_ge(added, i * U + u + 1)
                        for k in range(kc):
                            mm = nc.tensor.matmul(ps[u][:, 0:width], st[u][:, k, :], w[:, k, :],
                                                  start=(k == 0), stop=(k == kc - 1))
                        mm.then_inc(multiplied, 1)

            @block.vector
            def _(dve):
                if fresh and bias is None:
                    nc.vector.memset(to, 0.0).then_inc(biased, 1)
                elif fresh:
                    nc.vector.tensor_copy(to, bias[:, None, :].broadcast_to([P, NT, width])).then_inc(biased, 1)
                elif bias is not None:
                    nc.vector.tensor_tensor(to, to, bias[:, None, :].broadcast_to([P, NT, width]),
                                            ALU.add).then_inc(biased, 1)
                if fresh or bias is not None:
                    dve.wait_ge(biased, 1)
                dve.sem_inc(added, U)
                with dve.Fori(0, ROUNDS) as i:
                    for u in range(U):
                        dve.wait_ge(multiplied, i * U + u + 1 + U)
                        part = to[:, ds(i * U + u, 1), :].rearrange("p o d -> p (o d)")
                        if gate is None:
                            nc.vector.tensor_tensor(part, part, ps[u][:, 0:width], ALU.add).then_inc(added, 1)
                        else:
                            nc.vector.scalar_tensor_tensor(out=part, in0=ps[u][:, 0:width],
                                                           scalar=gate[:, ds(i * U + u, 1)], in1=part,
                                                           op0=ALU.mult, op1=ALU.add).then_inc(added, 1)


def in_degrees(nc, kit, nm, dst, rows, deg):
    C = dst.shape[0] // rows
    B = 16
    with ExitStack() as c:
        def sb(name, shape, dt=F32):
            return c.enter_context(nc.sbuf_tensor(f"{nm}_{name}", shape, dt))
        dst_i, work_i = sb("dst", [rows, C], I32), sb("work", [rows, C], I32)
        lo, hi = sb("lo", [rows, C]), sb("hi", [rows, C])
        is_lo = [sb(f"is_lo{h}", [rows, B, P], BF16) for h in range(2)]
        is_hi = [sb(f"is_hi{h}", [rows, B, NT], BF16) for h in range(2)]
        ps = c.enter_context(nc.psum_tensor(f"{nm}_ps", [P, 512], F32))
        zero = sb("zero", [P, P])
        loaded, step, matched, used = sems(nc, c, nm, "loaded step matched used")
        rounds = C // B
        with nc.Block() as block:
            @block.sync
            def _(sp):
                sp.dma_start(dst_i[:], dst.rearrange("(p c) -> p c", p=rows)).then_inc(loaded, 16)

            @block.vector
            def _(dve):
                dve.wait_ge(loaded, 16)
                link = link_on(dve, step)
                link(nc.vector.memset(zero[:], 0.0))
                link(nc.vector.tensor_scalar(work_i[:], dst_i[:], 7, None, ALU.arith_shift_right))
                link(nc.vector.tensor_copy(hi[:], work_i[:]))
                link(nc.vector.tensor_scalar(work_i[:], dst_i[:], 127, None, ALU.bitwise_and))
                link(nc.vector.tensor_copy(lo[:], work_i[:]))

                def match(i, h):
                    for part, n, to in ((lo, P, is_lo[h]), (hi, NT, is_hi[h])):
                        ins = nc.vector.tensor_tensor(to[:], part[:, ds(i * B, B)][:, :, None].broadcast_to([rows, B, n]),
                                                      kit.iota[0:rows, None, 0:n].broadcast_to([rows, B, n]),
                                                      ALU.is_equal)
                    ins.then_inc(matched, 1)
                match(0, 0)
                with dve.Fori(0, (rounds - 1) // 2) as i:
                    for h in (1, 0):
                        j = i * 2 + (2 - h)
                        dve.wait_ge(used, j)
                        match(j, h)
                dve.wait_ge(used, rounds + 1)
                nc.vector.tensor_copy(deg[:], ps[:, 0:NT]).then_inc(step, 1)
                dve.wait_ge(step, 6)

            @block.tensor
            def _(pe):
                pe.sem_inc(used, 1)
                pe.wait_ge(step, 1)
                nc.tensor.matmul(ps[:, 0:NT], zero[:], zero[:, 0:NT], start=True, stop=False)

                def count(i, h, last=False):
                    pe.wait_ge(matched, i + 1)
                    for b in range(B):
                        mm = nc.tensor.matmul(ps[:, 0:NT], is_lo[h][:, b, :], is_hi[h][:, b, :], start=False,
                                              stop=(last and b == B - 1))
                    mm.then_inc(used, 1)
                with pe.Fori(0, (rounds - 1) // 2) as i:
                    for h in range(2):
                        count(i * 2 + h, h)
                count(rounds - 1, 0, last=True)
        assert rounds % 2 == 1


def rows_to_all(nc, kit, nm, col, out):
    with ExitStack() as c:
        diag = [c.enter_context(nc.sbuf_tensor(f"{nm}_diag{u}", [P, P], F32)) for u in range(U)]
        ps = [c.enter_context(nc.psum_tensor(f"{nm}_ps{u}", [P, 512], F32)) for u in range(U)]
        made, multiplied, copied = sems(nc, c, nm, "made multiplied copied")
        with nc.Block() as block:
            @block.vector
            def _(dve):
                with dve.Fori(0, ROUNDS) as i:
                    for u in range(U):
                        dve.wait_ge(multiplied, i * U + u + 1)
                        nc.vector.tensor_scalar(diag[u][:], kit.ident[:], col[:, ds(i * U + u, 1)], None,
                                                ALU.mult).then_inc(made, 1)

            @block.tensor
            def _(pe):
                pe.sem_inc(multiplied, U)
                with pe.Fori(0, ROUNDS) as i:
                    for u in range(U):
                        pe.wait_ge(made, i * U + u + 1)
                        pe.wait_ge(copied, i * U + u + 1)
                        nc.tensor.matmul(ps[u][:, 0:P], kit.ones[:], diag[u][:], start=True,
                                         stop=True).then_inc(multiplied, 1)

            @block.scalar
            def _(act):
                act.sem_inc(copied, U)
                with act.Fori(0, ROUNDS) as i:
                    for u in range(U):
                        act.wait_ge(multiplied, i * U + u + 1 + U)
                        nc.scalar.copy(out[:, ds((i * U + u) * P, P)], ps[u][:, 0:P]).then_inc(copied, 1)


def load(nc, nm, pairs):
    with ExitStack() as c:
        loaded, = sems(nc, c, nm, "loaded")
        with nc.Block() as block:
            @block.sync
            def _(sp):
                for to, src in pairs:
                    sp.dma_start(to, src).then_inc(loaded, 16)
                sp.wait_ge(loaded, 16 * len(pairs))


def on_vector(nc, nm, steps):
    with ExitStack() as c:
        step, = sems(nc, c, nm, "step")
        with nc.Block() as block:
            @block.vector
            def _(dve):
                steps(link_on(dve, step))


def chunks(ap):
    return ap.rearrange("(k p) n -> p k n", p=P)


def gcn_stage(nc, kit, A, x, bufs, e, table):
    b1, b2, b3, b4 = bufs
    with ExitStack() as c:
        def sb(name, shape, dt=F32):
            return c.enter_context(nc.sbuf_tensor(f"gcn_{name}", shape, dt))
        w1, w2 = sb("w1", [P, 2, P]), sb("w2", [P, 1, D])
        bias1, bias2 = sb("b1", [P, 1]), sb("b2", [P, D])
        deg, dinv, dall = kit.deg, sb("dinv", [P, NT]), sb("dall", [P, NP])
        load(nc, "gcn_load", [(w1[:], chunks(A["L0_gnn_W1"])), (w2[:], chunks(A["L0_gnn_W2"])),
                              (bias1[:], A["L0_gnn_b1"].rearrange("(p o) -> p o", o=1)),
                              (bias2[:], row_to_all(A["L0_gnn_b2"]))])
        layer_norm(nc, kit, "gcn_ln", x, b1, b2)
        in_degrees(nc, kit, "gcn_deg", A["dst"], 125, deg)
        with ExitStack() as cc:
            step, rooted = sems(nc, cc, "gcn_dinv", "step rooted")
            with nc.Block() as block:
                @block.vector
                def _(dve):
                    nc.vector.tensor_scalar(dinv[:], deg[:], 1.0, None, ALU.add).then_inc(step, 1)
                    dve.wait_ge(rooted, 1)
                    nc.vector.reciprocal(dinv[:], dinv[:]).then_inc(step, 1)
                    dve.wait_ge(step, 2)

                @block.scalar
                def _(act):
                    act.wait_ge(step, 1)
                    nc.scalar.activation(dinv[:], dinv[:], ACT.Sqrt).then_inc(rooted, 1)
        rows_to_all(nc, kit, "gcn_dall", dinv, dall)
        one, agg = b3[:, 0:NP], b4[:, 0:NP]
        project_t(nc, "gcn_h", [(b2, 2, w1)], b3, 1)
        on_vector(nc, "gcn_v1", lambda link: link(nc.vector.tensor_tensor(one, one, dall[:], ALU.mult)))
        write_table(nc, kit, "gcn_t1", b3, 1, b4, table)
        aggregate_t(nc, kit, "gcn_a1", e, table, 1, b4)

        def between(link):
            link(nc.vector.tensor_tensor(one, one, agg, ALU.add))
            link(nc.vector.tensor_tensor(one, one, dall[:], ALU.mult))
            link(nc.vector.tensor_scalar(one, one, bias1[:], 0.0, ALU.add, ALU.max))
            link(nc.vector.tensor_tensor(one, one, dall[:], ALU.mult))
        on_vector(nc, "gcn_v2", between)
        write_table(nc, kit, "gcn_t2", b3, 1, b4, table)
        aggregate_t(nc, kit, "gcn_a2", e, table, 1, b4)

        def after(link):
            link(nc.vector.tensor_tensor(one, one, agg, ALU.add))
            link(nc.vector.tensor_tensor(one, one, dall[:], ALU.mult))
        on_vector(nc, "gcn_v3", after)
        add_projection(nc, "gcn_out", b3, w2, nat(x), bias2)


def per_node(ap, n):
    return ap[:, :, None].broadcast_to([P, ap.shape[1], n])


def softmax_rows(nc, nm, z, n):
    tiles = z.shape[1]
    with ExitStack() as c:
        m, s = (c.enter_context(nc.sbuf_tensor(f"{nm}_{x}", [P, tiles], F32)) for x in "ms")
        step, raised = sems(nc, c, nm, "step raised")
        with nc.Block() as block:
            @block.vector
            def _(dve):
                link = link_on(dve, step)
                link(nc.vector.tensor_reduce(m[:], z, AX_X, ALU.max))
                link(nc.vector.tensor_tensor(z, z, per_node(m[:], n), ALU.subtract))
                dve.wait_ge(raised, 1)
                link(nc.vector.tensor_reduce(s[:], z, AX_X, ALU.add))
                link(nc.vector.reciprocal(s[:], s[:]))
                link(nc.vector.tensor_tensor(z, z, per_node(s[:], n), ALU.mult))

            @block.scalar
            def _(act):
                act.wait_ge(step, 2)
                nc.scalar.activation(z, z, ACT.Exp).then_inc(raised, 1)


def add_gated_bias(nc, kit, nm, gates, b, x):
    E = b.shape[0]
    with ExitStack() as c:
        gt = [c.enter_context(nc.sbuf_tensor(f"{nm}_gt{u}", [E, P], F32)) for u in range(U)]
        st = [c.enter_context(nc.sbuf_tensor(f"{nm}_st{u}", [P, E], F32)) for u in range(U)]
        ps = [c.enter_context(nc.psum_tensor(f"{nm}_ps{u}", [P, 512], F32)) for u in range(U)]
        staged, turned, copied, multiplied, added = sems(nc, c, nm, "staged turned copied multiplied added")
        with nc.Block() as block:
            @block.vector
            def _(dve):
                dve.sem_inc(added, U)
                with dve.Fori(0, ROUNDS) as i:
                    for u in range(U):
                        dve.wait_ge(multiplied, i * U + u + 1)
                        nc.vector.tensor_copy(st[u][:], gates[:, ds(i * U + u, 1), :].rearrange("p o e -> p (o e)")
                                              ).then_inc(staged, 1)
                    for u in range(U):
                        dve.wait_ge(multiplied, i * U + u + 1 + U)
                        part = nat(x)[:, ds(i * U + u, 1), :].rearrange("p o d -> p (o d)")
                        nc.vector.tensor_tensor(part, part, ps[u][:, 0:D], ALU.add).then_inc(added, 1)

            @block.tensor
            def _(pe):
                pe.sem_inc(multiplied, U)
                with pe.Fori(0, ROUNDS) as i:
                    for u in range(U):
                        pe.wait_ge(staged, i * U + u + 1)
                        pe.wait_ge(added, i * U + u + 1)
                        nc.tensor.transpose(ps[u][0:E, D:D + P], st[u][:], kit.ident[:]).then_inc(turned, 1)
                    for u in range(U):
                        pe.wait_ge(copied, i * U + u + 1)
                        nc.tensor.matmul(ps[u][:, 0:D], gt[u][:], b, start=True, stop=True).then_inc(multiplied, 1)

            @block.scalar
            def _(act):
                with act.Fori(0, ROUNDS) as i:
                    for u in range(U):
                        act.wait_ge(turned, i * U + u + 1)
                        nc.scalar.copy(gt[u][:], ps[u][0:E, D:D + P]).then_inc(copied, 1)


class Mid:

    def __init__(self, w, kc, fc, func, bias, scale=None):
        self.w, self.kc, self.fc, self.func, self.bias, self.scale = w, kc, fc, func, bias, scale


def expert_mlps(nc, nm, src, experts, mids, last, gates, x, pick=None):
    SPAN = U * P
    kl = mids[-1].fc
    groups = sum(2 * m.fc for m in mids)
    RING = 4
    assert groups % RING == 0
    with ExitStack() as c:
        wm = [[c.enter_context(nc.sbuf_tensor(f"{nm}_w{n}_{q}", [P, m.kc, m.fc * P], F32)) for n, m in enumerate(mids)]
              for q in range(2)]
        wl = [c.enter_context(nc.sbuf_tensor(f"{nm}_wl_{q}", [P, kl, D], F32)) for q in range(2)]
        h = [c.enter_context(nc.sbuf_tensor(f"{nm}_h{n}", [P, m.fc, SPAN], F32)) for n, m in enumerate(mids)]
        ps = [c.enter_context(nc.psum_tensor(f"{nm}_ps{r}", [P, 512], F32)) for r in range(RING)]
        py = [c.enter_context(nc.psum_tensor(f"{nm}_py{r}", [P, 512], F32)) for r in range(4)]
        out_ps = [py[u % 4][:, 0:D] for u in range(U)]
        loaded = sems(nc, c, nm, "loaded0 loaded1")
        multiplied, read, finished, added, left = sems(nc, c, nm, "multiplied read finished added left")

        def experts_loop(eng, body):
            if experts == 2:
                for q in range(2):
                    body(0, q)
            else:
                with eng.Fori(0, experts // 2) as i:
                    for q in range(2):
                        body(i, q)

        with nc.Block() as block:
            @block.sync
            def _(sp):
                def body(i, q):
                    e = i * 2 + q
                    at = pick(sp, e) if pick else e
                    sp.wait_ge(left, e + 1)
                    for n, m in enumerate(mids):
                        sp.dma_start(wm[q][n][:], m.w(at).rearrange("o (k p) f -> p (o k) f", p=P)).then_inc(loaded[q], 16)
                    sp.dma_start(wl[q][:], last(at).rearrange("o (k p) f -> p (o k) f", p=P)).then_inc(loaded[q], 16)
                experts_loop(sp, body)

            @block.tensor
            def _(pe):
                pe.sem_inc(left, 2)

                def body(i, q):
                    wait_alone(pe, loaded[q], (i + 1) * 16 * (len(mids) + 1))
                    with pe.Fori(0, ROUNDS) as j:
                        r = (i * 2 + q) * ROUNDS + j
                        g = 0
                        for n, m in enumerate(mids):
                            for half in range(2):
                                if n:
                                    pe.wait_ge(read, r * groups + RING + g0 + (half + 1) * mids[n - 1].fc)
                                for f in range(m.fc):
                                    pe.wait_ge(read, r * groups + g + 1)
                                    for k in range(m.kc):
                                        rhs = (tr(src)[:, k, ds((j * 2 + half) * CHUNK, CHUNK)] if n == 0
                                               else h[n - 1][:, k, half * CHUNK:(half + 1) * CHUNK])
                                        mm = nc.tensor.matmul(ps[g % RING][:, 0:CHUNK],
                                                              wm[q][n][:, k, f * P:(f + 1) * P], rhs,
                                                              start=(k == 0), stop=(k == m.kc - 1))
                                    mm.then_inc(multiplied, 1)
                                    g += 1
                            g0 = g - 2 * m.fc
                        for u in range(U):
                            half = 0 if (u + 1) * P <= CHUNK else 1
                            pe.wait_ge(read, r * groups + RING + g0 + (half + 1) * kl)
                            pe.wait_ge(added, r * U + (U if u == 0 else U + 1 if u == 4 else u + 1))
                            for k in range(kl):
                                mm = nc.tensor.matmul(out_ps[u], h[-1][:, k, u * P:(u + 1) * P], wl[q][:, k, :],
                                                      start=(k == 0), stop=(k == kl - 1))
                            mm.then_inc(finished, 1)
                    pe.drain().then_inc(left, 1)
                experts_loop(pe, body)

            @block.scalar
            def _(act):
                act.sem_inc(read, RING)

                def body(i, q):
                    with act.Fori(0, ROUNDS) as j:
                        r = (i * 2 + q) * ROUNDS + j
                        g = 0
                        for n, m in enumerate(mids):
                            for half in range(2):
                                for f in range(m.fc):
                                    wait_alone(act, multiplied, r * groups + g + 1)
                                    e = i * 2 + q
                                    bias = m.bias[:, ds(e, 1), f:f + 1].rearrange("p o f -> p (o f)")
                                    scale = (m.scale[:, ds(e, 1), f:f + 1].rearrange("p o f -> p (o f)")
                                             if m.scale is not None else 1.0)
                                    nc.scalar.activation(h[n][:, f, half * CHUNK:(half + 1) * CHUNK],
                                                         ps[g % RING][:, 0:CHUNK], m.func, bias=bias,
                                                         scale=scale).then_inc(read, 1)
                                    g += 1
                experts_loop(act, body)

            @block.vector
            def _(dve):
                dve.sem_inc(added, U)

                def body(i, q):
                    with dve.Fori(0, ROUNDS) as j:
                        r = (i * 2 + q) * ROUNDS + j
                        e = i * 2 + q
                        for u in range(U):
                            t = j * U + u
                            dve.wait_ge(finished, r * U + u + 1)
                            dve.wait_ge(added, r * U + u + 1)
                            part = nat(x)[:, ds(t, 1), :].rearrange("p o d -> p (o d)")
                            gate = gates[:, ds(t, 1), ds(e, 1)].rearrange("p o e -> p (o e)")
                            nc.vector.scalar_tensor_tensor(out=part, in0=out_ps[u], scalar=gate, in1=part,
                                                           op0=ALU.mult, op1=ALU.add).then_inc(added, 1)
                experts_loop(dve, body)


def expert_columns(ap2d, fc):
    return ap2d.rearrange("e (f p) -> p e f", f=fc)


def soft_moe_stage(nc, kit, A, x, bufs):
    b1, b2, b3, b4 = bufs
    E, F = A["L1_ffn_b1"].shape
    fc = F // P
    BN_EPS = 0.001
    with ExitStack() as c:
        def sb(name, shape, dt=F32):
            return c.enter_context(nc.sbuf_tensor(f"soft_{name}", shape, dt))
        wr, br, bo = sb("wr", [P, 2, E]), sb("br", [P, E]), sb("bo", [E, D])
        gates = sb("gates", [P, NT, E])
        par = {n: sb(n, [P, E, fc]) for n in "b1 g1 be1 m1 v1 b2 g2 be2 m2 v2".split()}
        layer_norm(nc, kit, "soft_ln", x, b1, b2)
        with nc.allow_non_contiguous_dma(reason="short columns"):
            load(nc, "soft_load",
                 [(wr[:], chunks(A["L1_ffn_Wr"])), (br[:], row_to_all(A["L1_ffn_br"])), (bo[:], A["L1_ffn_bo"])]
                 + [(t[:, e, :], column(A[f"L1_ffn_{n}"][e], fc)) for n, t in par.items() for e in range(E)])
        with ExitStack() as cc:
            step, rooted = sems(nc, cc, "soft_bn", "step rooted")
            with nc.Block() as block:
                @block.vector
                def _(dve):
                    link = link_on(dve, step)
                    for n in "12":
                        v = par["v" + n]
                        link(nc.vector.tensor_scalar(v[:], v[:], BN_EPS, None, ALU.add))
                    dve.wait_ge(rooted, 2)
                    for n in "12":
                        v, g, b, m, be = (par[k + n] for k in ("v", "g", "b", "m", "be"))
                        link(nc.vector.reciprocal(v[:], v[:]))
                        link(nc.vector.tensor_tensor(v[:], v[:], g[:], ALU.mult))
                        link(nc.vector.tensor_tensor(b[:], b[:], m[:], ALU.subtract))
                        link(nc.vector.tensor_tensor(b[:], b[:], v[:], ALU.mult))
                        link(nc.vector.tensor_tensor(b[:], b[:], be[:], ALU.add))

                @block.scalar
                def _(act):
                    for k, n in enumerate("12"):
                        act.wait_ge(step, k + 1)
                        nc.scalar.activation(par["v" + n][:], par["v" + n][:], ACT.Sqrt).then_inc(rooted, 1)
        add_projection(nc, "soft_gate", b2, wr, gates[:], br, fresh=True)
        softmax_rows(nc, "soft_sm", gates[:], E)
        add_gated_bias(nc, kit, "soft_bo", gates, bo[:], x)
        of = lambda name: lambda e: A[name][ds(e, 1), :, :]
        expert_mlps(nc, "soft", b2, E, [Mid(of("L1_ffn_W1"), 2, fc, ACT.Relu, par["b1"], par["v1"]),
                                        Mid(of("L1_ffn_W2"), fc, fc, ACT.Relu, par["b2"], par["v2"])],
                    of("L1_ffn_Wo"), gates, x)


BIG = 1e30
R = 4


class EdgeAttention:

    def __init__(self, edges, index, keys, values, q, heads, dv, dots, score_at=0):
        self.edges, self.index, self.keys, self.values, self.q = edges, index, keys, values, q
        self.heads, self.dv, self.dots, self.score_at = heads, dv, dots, score_at


def two_by_two(eng, step, rounds):
    for a in range(2):
        step(0, a, a, True, False)
    with eng.Fori(1, rounds // 2) as i:
        for a in range(2):
            step(i, a, i * 2 + a, True, True)
    for a in range(2):
        step(rounds // 2, a, rounds + a, False, True)


def edge_scores(nc, kit, nm, at, scores, top):
    e, H = at.edges, at.heads
    WQ, WK = at.q.shape[2], at.keys.shape[1]
    rounds = e.groups // R
    with ExitStack() as c:
        def two(name, shape, dt=F32):
            return [c.enter_context(nc.sbuf_tensor(f"{nm}_{name}{a}", shape, dt)) for a in range(2)]
        idx, rows = two("idx", [P, R], I32), two("rows", [P, R, WK])
        hot, hot_t, off = two("hot", [P, R, P]), two("hot_t", [P, R, P]), two("off", [P, R, P], BF16)
        sc = two("sc", [P, R, H])
        tmp = c.enter_context(nc.sbuf_tensor(f"{nm}_tmp", [P, R, WQ], F32))
        big = c.enter_context(nc.sbuf_tensor(f"{nm}_big", [P, H, P], BF16))
        tm = c.enter_context(nc.sbuf_tensor(f"{nm}_tm", [P, R, H], F32))
        pt = c.enter_context(nc.psum_tensor(f"{nm}_pt", [P, 512], F32))
        pq = c.enter_context(nc.psum_tensor(f"{nm}_pq", [P, max(512, R * WQ)], F32))
        pm = [c.enter_context(nc.psum_tensor(f"{nm}_pm{u}", [P, 512], F32)) for u in range(R)]
        pq_v = pq[:, 0:R * WQ].rearrange("p (r w) -> p r w", r=R)
        (indexed, matched, turned, copied, shifted, spread, part, scored, kept, broadcast, reduced, raised,
         chain) = sems(nc, c, nm, "indexed matched turned copied shifted spread part scored kept broadcast reduced "
                       "raised chain")
        gathered = gather_sems(nc, nm, "gathered", 2)
        with nc.Block() as block:
            @block.scalar
            def _(act):
                nc.scalar.copy(idx[0][:], at.index[:, 0:R]).then_inc(indexed, 1)

                def step(i, a, r, now, late):
                    if now:
                        act.wait_ge(turned, r + 1)
                        nc.scalar.copy(hot_t[a][:], pt[:].rearrange("p (r n) -> p r n", r=R)).then_inc(copied, 1)
                        if late:
                            act.wait_ge(broadcast, r - 1)
                        nc.scalar.activation(off[a][:], hot[a][:], ACT.Copy, bias=-1.0).then_inc(shifted, 1)
                    if late or a:
                        if not now and a:
                            return
                        wait_alone(act, scored, r)
                        nc.scalar.copy(scores[:, ds((i * 2 + a - 1) * R, R), :], sc[1 - a][:]).then_inc(kept, 1)
                    if now:
                        nc.scalar.copy(idx[1 - a][:], at.index[:, ds((r + 1) * R, R)]).then_inc(indexed, 1)
                two_by_two(act, step, rounds)

            @block.gpsimd
            def _(pool):
                def step(i, a, r, now, late):
                    if now:
                        wait_alone(pool, indexed, r + 1)
                        for u in range(R):
                            nc.gpsimd.indirect_dma_start(rows[a][:, u, :], None, at.keys,
                                                         bass.IndirectOffsetOnAxis(ap=idx[a][:, u:u + 1], axis=0)
                                                         ).then_inc(gathered[a], 16)
                two_by_two(pool, step, rounds)

            @block.tensor
            def _(pe):
                def step(i, a, r, now, late):
                    if now:
                        pe.wait_ge(matched, r + 1)
                        if late or a:
                            pe.wait_ge(copied, r)
                        for u in range(R):
                            mm = nc.tensor.transpose(pt[:, u * P:(u + 1) * P], hot[a][:, u, :], kit.ident[:])
                        mm.then_inc(turned, 1)
                    if late:
                        pe.wait_ge(scored, r - 1)
                        pe.wait_ge(shifted, r - 1)
                        pe.wait_ge(reduced, r - 1)
                        for u in range(R):
                            nc.tensor.matmul(pm[u][:, 0:H * P], off[a][:, u, :], big[:].rearrange("p h n -> p (h n)"),
                                             start=True, stop=False)
                            for h in range(H):
                                mm = nc.tensor.matmul(pm[u][:, h * P:(h + 1) * P],
                                                      sc[a][:, u, h:h + 1].broadcast_to([P, P]), kit.ident[:],
                                                      start=False, stop=(h == H - 1))
                        mm.then_inc(broadcast, 1)
                    if now:
                        pe.wait_ge(copied, r + 1)
                        if late or a:
                            pe.wait_ge(scored, r)
                        for u in range(R):
                            blk = pe.value_load(e.blk[0:1, ds(r * R + u, 1)], min_val=0, max_val=NT - 1)
                            mm = nc.tensor.matmul(pq_v[:, u, :], hot_t[a][:, u, :],
                                                  at.q[:, ds(blk, 1), :].rearrange("p o w -> p (o w)"),
                                                  start=True, stop=True)
                        mm.then_inc(spread, 1)
                two_by_two(pe, step, rounds)

            @block.vector
            def _(dve):
                link = link_on(dve, chain)

                def match(r, a):
                    nc.vector.tensor_tensor(hot[a][:], kit.iota[:, None, :].broadcast_to([P, R, P]),
                                            e.rec[:, ds(r * R, R), 1:2].broadcast_to([P, R, P]),
                                            ALU.is_equal).then_inc(matched, 1)
                for h in range(H):
                    link(nc.vector.tensor_scalar(big[:, h, :], kit.ident[:], BIG, None, ALU.mult))
                nc.vector.memset(top, -3e38).then_inc(raised, 1)
                nc.vector.memset(tm[:], 0.0).then_inc(reduced, 1)
                match(0, 0)

                def step(i, a, r, now, late):
                    if now:
                        if late or a:
                            dve.wait_ge(shifted, r)
                            dve.wait_ge(turned, r)
                        match(r + 1, 1 - a)
                    if late:
                        dve.wait_ge(broadcast, r - 1)
                        dve.wait_ge(raised, (r - 2) * R + 1)
                        for u in range(R):
                            ins = nc.vector.tensor_reduce(tm[:, u, :], pm[u][:, 0:H * P].rearrange(
                                "p (h n) -> p h n", h=H), AX_X, ALU.max)
                        ins.then_inc(reduced, 1)
                        dve.wait_ge(reduced, r)
                        for u in range(R):
                            blk = dve.value_load(e.blk[0:1, ds((r - 2) * R + u, 1)], min_val=0, max_val=NT - 1)
                            to = top[:, ds(blk, 1), :].rearrange("p o h -> p (o h)")
                            dve.wait_ge(raised, (r - 2) * R + u + 1)
                            nc.vector.tensor_tensor(to, to, tm[:, u, :], ALU.max).then_inc(raised, 1)
                    if now:
                        dve.wait_ge(spread, r + 1)
                        dve.wait_ge(gathered[a], (i + 1) * 16 * R)
                        if late:
                            dve.wait_ge(kept, r - 1)
                        if late or a:
                            dve.wait_ge(scored, r)
                        if at.dots:
                            nc.vector.tensor_tensor(tmp[:], rows[a][:], pq_v, ALU.mult).then_inc(part, 1)
                            dve.wait_ge(part, r + 1)
                            nc.vector.tensor_reduce(sc[a][:], tmp[:].rearrange("p r (h d) -> p r h d", h=H), AX_X,
                                                    ALU.add).then_inc(scored, 1)
                        else:
                            nc.vector.tensor_tensor(tmp[:], rows[a][:, :, at.score_at:at.score_at + H], pq_v,
                                                    ALU.add).then_inc(part, 1)
                            dve.wait_ge(part, r + 1)
                            nc.vector.scalar_tensor_tensor(out=sc[a][:], in0=tmp[:], scalar=0.2, in1=tmp[:],
                                                           op0=ALU.mult, op1=ALU.max).then_inc(scored, 1)
                two_by_two(dve, step, rounds)


def edge_sums(nc, kit, nm, at, scores, top, acc):
    e, H, dv = at.edges, at.heads, at.dv
    WV = at.values.shape[1]
    W = H + H * dv
    rounds = e.groups // R
    with ExitStack() as c:
        def two(name, shape, dt=F32):
            return [c.enter_context(nc.sbuf_tensor(f"{nm}_{name}{a}", shape, dt)) for a in range(2)]
        idx, rows = two("idx", [P, R], I32), two("rows", [P, R, WV])
        hot, hot_t = two("hot", [P, R, P]), two("hot_t", [P, R, P])
        z, val = two("z", [P, R, H]), two("val", [P, R, W])
        pt = c.enter_context(nc.psum_tensor(f"{nm}_pt", [P, 512], F32))
        pd = c.enter_context(nc.psum_tensor(f"{nm}_pd", [P, 512], F32))
        pa = [c.enter_context(nc.psum_tensor(f"{nm}_pa{u}", [P, 512], F32)) for u in range(R)]
        pd_v = pd[:, 0:R * H].rearrange("p (r h) -> p r h", r=R)
        (indexed, matched, turned, copied, spread, part, shifted, raised, weighted, multiplied, added) = sems(
            nc, c, nm, "indexed matched turned copied spread part shifted raised weighted multiplied added")
        gathered = gather_sems(nc, nm, "gathered", 2)

        def one_by_one(eng, step):
            step(0, 0, 0, True, False)
            step(0, 1, 1, True, True)
            with eng.Fori(1, rounds // 2) as i:
                for a in range(2):
                    step(i, a, i * 2 + a, True, True)
            step(rounds // 2, 0, rounds, False, True)

        with nc.Block() as block:
            @block.scalar
            def _(act):
                nc.scalar.copy(idx[0][:], at.index[:, 0:R]).then_inc(indexed, 1)

                def step(i, a, r, now, late):
                    if now:
                        if late:
                            wait_alone(act, weighted, r)
                        nc.scalar.copy(idx[1 - a][:], at.index[:, ds((r + 1) * R, R)]).then_inc(indexed, 1)
                        act.wait_ge(turned, r + 1)
                        nc.scalar.copy(hot_t[a][:], pt[:].rearrange("p (r n) -> p r n", r=R)).then_inc(copied, 1)
                        act.wait_ge(shifted, r + 1)
                        nc.scalar.activation(val[a][:, :, 0:H], z[a][:], ACT.Exp).then_inc(raised, 1)
                one_by_one(act, step)

            @block.gpsimd
            def _(pool):
                def step(i, a, r, now, late):
                    if now:
                        wait_alone(pool, indexed, r + 1)
                        for u in range(R):
                            nc.gpsimd.indirect_dma_start(rows[a][:, u, :], None, at.values,
                                                         bass.IndirectOffsetOnAxis(ap=idx[a][:, u:u + 1], axis=0)
                                                         ).then_inc(gathered[a], 16)
                one_by_one(pool, step)

            @block.tensor
            def _(pe):
                def step(i, a, r, now, late):
                    if now:
                        pe.wait_ge(matched, r + 1)
                        if late:
                            pe.wait_ge(copied, r)
                        for u in range(R):
                            mm = nc.tensor.transpose(pt[:, u * P:(u + 1) * P], hot[a][:, u, :], kit.ident[:])
                        mm.then_inc(turned, 1)
                        pe.wait_ge(copied, r + 1)
                        if late:
                            pe.wait_ge(shifted, r)
                        for u in range(R):
                            blk = pe.value_load(e.blk[0:1, ds(r * R + u, 1)], min_val=0, max_val=NT - 1)
                            mm = nc.tensor.matmul(pd_v[:, u, :], hot_t[a][:, u, :],
                                                  top[:, ds(blk, 1), :].rearrange("p o w -> p (o w)"),
                                                  start=True, stop=True)
                        mm.then_inc(spread, 1)
                    if late:
                        pe.wait_ge(weighted, r)
                        for u in range(R):
                            pe.wait_ge(added, (r - 1) * R + u + 1)
                            nc.tensor.matmul(pa[u][:, 0:W], hot[1 - a][:, u, :], val[1 - a][:, u, :],
                                             start=True, stop=True).then_inc(multiplied, 1)
                one_by_one(pe, step)

            @block.vector
            def _(dve):
                def match(r, a):
                    nc.vector.tensor_tensor(hot[a][:], kit.iota[:, None, :].broadcast_to([P, R, P]),
                                            e.rec[:, ds(r * R, R), 1:2].broadcast_to([P, R, P]),
                                            ALU.is_equal).then_inc(matched, 1)
                nc.vector.memset(acc, 0.0).then_inc(added, R)
                match(0, 0)

                def step(i, a, r, now, late):
                    if now:
                        dve.wait_ge(spread, r + 1)
                        nc.vector.tensor_tensor(z[a][:], scores[:, ds(r * R, R), :], pd_v, ALU.subtract).then_inc(part, 1)
                        dve.wait_ge(part, r + 1)
                        nc.vector.tensor_scalar(z[a][:], z[a][:], 0.0, None, ALU.min).then_inc(shifted, 1)
                    if late:
                        for u in range(R):
                            blk = dve.value_load(e.blk[0:1, ds((r - 1) * R + u, 1)], min_val=0, max_val=NT - 1)
                            to = acc[:, ds(blk, 1), :].rearrange("p o w -> p (o w)")
                            dve.wait_ge(multiplied, (r - 1) * R + u + 1)
                            dve.wait_ge(added, r * R + u)
                            nc.vector.tensor_tensor(to, to, pa[u][:, 0:W], ALU.add).then_inc(added, 1)
                    if now:
                        match(r + 1, 1 - a)
                        dve.wait_ge(gathered[a], (i + 1) * 16 * R)
                        dve.wait_ge(raised, r + 1)
                        for u in range(R):
                            ins = nc.vector.tensor_tensor(
                                val[a][:, u, H:].rearrange("p (h d) -> p h d", h=H),
                                rows[a][:, u, 0:H * dv].rearrange("p (h d) -> p h d", h=H),
                                val[a][:, u, 0:H][:, :, None].broadcast_to([P, H, dv]), ALU.mult)
                        ins.then_inc(weighted, 1)
                one_by_one(dve, step)


def gat_moe_stage(nc, kit, A, x, bufs):
    b1, b2, b3, b4 = bufs
    E, F = A["L0_ffn_b1"].shape
    H = A["L0_ffn_att_src"].shape[0]
    fc, HE = F // P, H * E
    rows = dict(src=A["L0_ffn_edge_index"][0], dst=A["L0_ffn_edge_index"][1])
    n_edges = rows["src"].shape[0]
    groups = -(-(NT + (n_edges + NT * (P - 1)) // P) // 8) * 8
    table = nc.dram_tensor("gat_table", (NP, HE + 2 * H), F32).ap()
    with ExitStack() as c:
        def sb(name, shape, dt=F32):
            return c.enter_context(nc.sbuf_tensor(f"gat_{name}", shape, dt))
        gates = sb("gates", [P, NT, E])
        b1s, b2s = sb("b1s", [P, E, fc]), sb("b2s", [E, D])
        layer_norm(nc, kit, "gat_ln", x, b1, b2)
        with ExitStack() as cc:
            def sb2(name, shape, dt=F32):
                return cc.enter_context(nc.sbuf_tensor(f"gat_{name}", shape, dt))
            own = alloc_edges(nc, cc, "own", groups)
            sort_edges(nc, kit, own, P, first=NT, **rows)
            w = sb2("w", [P, 2, HE])
            rows_in = {n: sb2(n, [P, HE]) for n in ("att_src", "att_dst", "b_gat", "ln_gamma", "ln_beta")}
            h = sb2("h", [P, NT, HE + 2 * H])
            tmp, score = sb2("tmp", [P, NT, HE]), sb2("score", [P, NT, E])
            scores, top = sb2("scores", [P, groups, H]), sb2("top", [P, NT, H])
            acc = sb2("acc", [P, NT, H + HE])
            mean, var, std = sb2("mean", [P, NT]), sb2("var", [P, NT]), sb2("std", [P, NT])
            above, same = sb2("above", [P, NT, E, E]), sb2("same", [P, NT, E, E])
            lower, rank = sb2("lower", [P, E, E]), sb2("rank", [P, NT, E])

            def flat(a):
                return a if len(a.shape) == 1 else a.rearrange("h e -> (h e)")
            with nc.allow_non_contiguous_dma(reason="short columns"):
                load(nc, "gat_load", [(w[:], chunks(A["L0_ffn_W_gat"])), (b2s[:], A["L0_ffn_b2"])]
                     + [(b1s[:, e, :], column(A["L0_ffn_b1"][e], fc)) for e in range(E)]
                     + [(t[:], row_to_all(flat(A[f"L0_ffn_{n}"]))) for n, t in rows_in.items()])
            add_projection(nc, "gat_h", b2, w, tmp[:], fresh=True)

            def node_scores(link):
                link(nc.vector.tensor_copy(h[:, :, 0:HE], tmp[:]))
                for n, at in (("att_src", HE), ("att_dst", HE + H)):
                    link(nc.vector.tensor_tensor(tmp[:], h[:, :, 0:HE],
                                                 rows_in[n][:, None, :].broadcast_to([P, NT, HE]), ALU.mult))
                    link(nc.vector.tensor_reduce(h[:, :, at:at + H], tmp[:].rearrange("p t (h e) -> p t h e", h=H),
                                                 AX_X, ALU.add))
                link(nc.vector.tensor_copy(top[:], h[:, :, HE + H:]))
            on_vector(nc, "gat_v1", node_scores)
            load(nc, "gat_store", [(table.rearrange("(t p) w -> p t w", p=P), h[:])])
            own_dst = sb2("own_dst", [P, NT, H])
            on_vector(nc, "gat_v2", lambda link: link(nc.vector.tensor_copy(own_dst[:], top[:])))
            at = EdgeAttention(own, own.src, table, table, own_dst, H, E, dots=False, score_at=HE)
            edge_scores(nc, kit, "gat_s", at, scores, top[:])
            edge_sums(nc, kit, "gat_a", at, scores, top[:], acc[:])
            with ExitStack() as c3:
                step, ready, rooted = sems(nc, c3, "gat_score", "step ready rooted")
                with nc.Block() as block:
                    @block.vector
                    def _(dve):
                        link = link_on(dve, step)
                        agg, den = acc[:, :, H:], acc[:, :, 0:H]
                        agg_h = agg.rearrange("p t (h e) -> p t h e", h=H)
                        link(nc.vector.tensor_scalar(den, den, 1e-16, None, ALU.add))
                        link(nc.vector.reciprocal(den, den))
                        link(nc.vector.tensor_tensor(agg_h, agg_h, den[:, :, :, None].broadcast_to([P, NT, H, E]),
                                                     ALU.mult))
                        link(nc.vector.tensor_tensor(tmp[:], agg, rows_in["b_gat"][:, None, :].broadcast_to([P, NT, HE]),
                                                     ALU.add))
                        link(nc.vector.tensor_reduce(mean[:], tmp[:], AX_X, ALU.add))
                        link(nc.vector.tensor_scalar(mean[:], mean[:], 1.0 / HE, None, ALU.mult))
                        link(nc.vector.tensor_tensor(tmp[:], tmp[:], per_node(mean[:], HE), ALU.subtract))
                        link(nc.vector.tensor_tensor(agg, tmp[:], tmp[:], ALU.mult))
                        link(nc.vector.tensor_reduce(var[:], agg, AX_X, ALU.add))
                        nc.vector.tensor_scalar(var[:], var[:], 1.0 / HE, EPS, ALU.mult, ALU.add).then_inc(ready, 1)
                        dve.wait_ge(rooted, 1)
                        link(nc.vector.reciprocal(std[:], std[:]))
                        link(nc.vector.tensor_tensor(tmp[:], tmp[:], per_node(std[:], HE), ALU.mult))
                        for n, op in (("ln_gamma", ALU.mult), ("ln_beta", ALU.add)):
                            link(nc.vector.tensor_tensor(tmp[:], tmp[:],
                                                         rows_in[n][:, None, :].broadcast_to([P, NT, HE]), op))
                        link(nc.vector.tensor_reduce(score[:], tmp[:].rearrange("p t (h e) -> p t e h", h=H), AX_X,
                                                     ALU.add))
                        link(nc.vector.tensor_scalar(score[:], score[:], 1.0 / H, None, ALU.mult))
                        rank_rows(nc, kit, link, score[:], E, above[:], same[:], lower[:], rank[:])
                        link(nc.vector.tensor_scalar(rank[:], rank[:], 2.0, None, ALU.is_lt))
                        link(nc.vector.tensor_tensor(gates[:], score[:], rank[:], ALU.mult))
                        link(nc.vector.tensor_scalar(rank[:], rank[:], 1.0, BIG, ALU.subtract, ALU.mult))
                        link(nc.vector.tensor_tensor(gates[:], gates[:], rank[:], ALU.add))

                    @block.scalar
                    def _(act):
                        act.wait_ge(ready, 1)
                        nc.scalar.activation(std[:], var[:], ACT.Sqrt).then_inc(rooted, 1)
            softmax_rows(nc, "gat_sm", gates[:], E)
        add_gated_bias(nc, kit, "gat_b2", gates, b2s[:], x)
        of = lambda name: lambda e: A[name][ds(e, 1), :, :]
        expert_mlps(nc, "gatx", b2, E, [Mid(of("L0_ffn_W1"), 2, fc, ACT.Gelu, b1s)], of("L0_ffn_W2"), gates, x)


def hgt_stage(nc, kit, A, x, bufs, e):
    b1, b2, b3, b4 = bufs
    TYPES = A["L1_gnn_k_linears"].shape[0]
    RELS, H, DK, _ = A["L1_gnn_relation_att"].shape
    KC = TYPES * 2
    HP = H // 2
    keys = nc.dram_tensor("hgt_keys", (RELS * NP, D), F32).ap()
    values = nc.dram_tensor("hgt_values", (RELS * NP, D), F32).ap()
    q = nat(b2)
    w_k, w_q, w_v = (b3[:, n * KC * D:(n + 1) * KC * D].rearrange("p (k n) -> p k n", k=KC) for n in range(3))
    raw, rel_k, rel_v = (b4[:, n * HP * RELS * P:(n + 1) * HP * RELS * P].rearrange("p (h r n) -> p h r n", h=HP, r=RELS)
                         for n in range(3))
    with ExitStack() as c:
        def sb(name, shape, dt=F32):
            return c.enter_context(nc.sbuf_tensor(f"hgt_{name}", shape, dt))
        kind_i, kind, is_kind = sb("kind_i", [P, NT], I32), sb("kind", [P, NT]), sb("is_kind", [P, TYPES, NT])
        skip = sb("skip", [P, TYPES])
        layer_norm(nc, kit, "hgt_ln", x, b1)
        with ExitStack() as cc:
            pri = cc.enter_context(nc.sbuf_tensor("hgt_pri", [P, RELS, H], F32))
            step, zeroed, loaded, turned, squashed = sems(nc, cc, "hgt_w", "step zeroed loaded turned squashed")
            pt = cc.enter_context(nc.psum_tensor("hgt_pt", [P, HP * RELS * P], F32))
            with nc.Block() as block, nc.allow_non_contiguous_dma(reason="short rows"):
                @block.sync
                def _(sp):
                    for t, n in ((w_k, "k"), (w_q, "q"), (w_v, "v")):
                        sp.dma_start(t, A[f"L1_gnn_{n}_linears"].rearrange("t (k p) n -> p (t k) n", p=P)).then_inc(loaded, 16)
                    sp.dma_start(skip[:], row_to_all(A["L1_gnn_skip"])).then_inc(loaded, 16)
                    sp.dma_start(pri[:].rearrange("p r h -> p (r h)"),
                                 row_to_all(A["L1_gnn_relation_pri"].rearrange("r h -> (r h)"))).then_inc(loaded, 16)
                    sp.wait_ge(zeroed, 3)
                    sp.dma_start(kind_i[:, 0:NT - 1],
                                 A["node_type_4"][0:(NT - 1) * P].rearrange("(t p) -> p t", p=P)).then_inc(loaded, 16)
                    sp.dma_start(kind_i[0:LAST, NT - 1:NT],
                                 A["node_type_4"][(NT - 1) * P:N].rearrange("(p o) -> p o", o=1)).then_inc(loaded, 16)
                    for t, n in ((raw, "att"), (rel_v, "msg")):
                        for hp in range(HP):
                            for h2 in range(2):
                                at = slice(h2 * DK, (h2 + 1) * DK)
                                sp.dma_start(t[at, hp, :, at],
                                             A[f"L1_gnn_relation_{n}"][:, hp * 2 + h2, :, :].rearrange("r d e -> d r e")
                                             ).then_inc(loaded, 16)
                    sp.wait_ge(loaded, 16 * (7 + 2 * HP * 2))

                @block.vector
                def _(dve):
                    nc.vector.memset(raw, 0.0).then_inc(zeroed, 1)
                    nc.vector.memset(rel_v, 0.0).then_inc(zeroed, 1)
                    nc.vector.memset(kind_i[:], 0).then_inc(zeroed, 1)
                    dve.wait_ge(loaded, 16 * (7 + 2 * HP * 2))
                    link = link_on(dve, step)
                    link(nc.vector.tensor_copy(kind[:], kind_i[:]))
                    for t in range(TYPES):
                        link(nc.vector.tensor_scalar(is_kind[:, t, :], kind[:], float(t), None, ALU.is_equal))
                    link(nc.vector.tensor_scalar(pri[:], pri[:], 1.0 / DK ** 0.5, None, ALU.mult))
                    dve.wait_ge(turned, 1)
                    pt_v = pt[:].rearrange("p (h r n) -> p h r n", h=HP, r=RELS)
                    for hp in range(HP):
                        for h2 in range(2):
                            at = slice(h2 * DK, (h2 + 1) * DK)
                            link(nc.vector.tensor_tensor(rel_k[:, hp, :, at], pt_v[:, hp, :, at],
                                                         pri[:, :, hp * 2 + h2:hp * 2 + h2 + 1].broadcast_to([P, RELS, DK]),
                                                         ALU.mult))

                @block.tensor
                def _(pe):
                    pe.wait_ge(loaded, 16 * (7 + 2 * HP * 2))
                    for hp in range(HP):
                        for r in range(RELS):
                            n = hp * RELS + r
                            mm = nc.tensor.transpose(pt[:, n * P:(n + 1) * P], raw[:, hp, r, :], kit.ident[:])
                    mm.then_inc(turned, 1)

                @block.scalar
                def _(act):
                    act.wait_ge(loaded, 16 * (7 + 2 * HP * 2))
                    nc.scalar.activation(skip[:], skip[:], ACT.Sigmoid).then_inc(squashed, 1)
                    act.wait_ge(squashed, 1)
        hgt_tables(nc, kit, nat(b1), is_kind, w_k, w_q, w_v, rel_k, rel_v, q, keys, values, TYPES, RELS, HP)
        with ExitStack() as cc:
            groups = e.groups
            scores = cc.enter_context(nc.sbuf_tensor("hgt_scores", [P, groups, H], F32))
            top = cc.enter_context(nc.sbuf_tensor("hgt_top", [P, NT, H], F32))
            acc = cc.enter_context(nc.sbuf_tensor("hgt_acc", [P, NT, H + D], F32))
            at = EdgeAttention(e, e.key, keys, values, q, H, DK, dots=True)
            edge_scores(nc, kit, "hgt_s", at, scores, top[:])
            edge_sums(nc, kit, "hgt_a", at, scores, top[:], acc[:])

            def divide(link):
                link(nc.vector.tensor_scalar(acc[:, :, 0:H], acc[:, :, 0:H], 1e-30, None, ALU.max))
                link(nc.vector.reciprocal(acc[:, :, 0:H], acc[:, :, 0:H]))
                link(nc.vector.tensor_tensor(nat(b1).rearrange("p t (h d) -> p t h d", h=H),
                                             acc[:, :, H:].rearrange("p t (h d) -> p t h d", h=H),
                                             acc[:, :, 0:H][:, :, :, None].broadcast_to([P, NT, H, DK]), ALU.mult))
                for t in range(TYPES):
                    link(nc.vector.tensor_scalar(is_kind[:, t, :], is_kind[:, t, :], skip[:, t:t + 1], None, ALU.mult))
            on_vector(nc, "hgt_v1", divide)
        turn(nc, kit, "hgt_turn", nat(b1), tr(b2))
        load(nc, "hgt_load_a", [(w_k, A["L1_gnn_a_linears"].rearrange("t (k p) n -> p (t k) n", p=P))])
        for t in range(TYPES):
            add_projection(nc, f"hgt_out{t}", b2, w_k[:, 2 * t:2 * t + 2, :], nat(x), gate=is_kind[:, t, :])


def hgt_tables(nc, kit, xn, is_kind, w_k, w_q, w_v, rel_k, rel_v, q, keys, values, TYPES, RELS, HP):
    KC = TYPES * 2
    with ExitStack() as c:
        def sb(name, shape, dt=F32):
            return c.enter_context(nc.sbuf_tensor(f"hgtt_{name}", shape, dt))
        xm, xmt, kvt = sb("xm", [P, TYPES, D]), sb("xmt", [P, KC, P]), sb("kvt", [P, 2 * HP, P])
        out_k, out_v = sb("out_k", [P, RELS, D]), sb("out_v", [P, RELS, D])
        pt = c.enter_context(nc.psum_tensor("hgtt_pt", [P, KC * P], F32))
        pkv = c.enter_context(nc.psum_tensor("hgtt_pkv", [P, 512], F32))
        pq = c.enter_context(nc.psum_tensor("hgtt_pq", [P, 512], F32))
        pr = [c.enter_context(nc.psum_tensor(f"hgtt_pr{n}", [P, 512], F32)) for n in range(4)]
        (masked, turned, copied, projected, kv_copied, q_copied, related, out_k_ready, out_v_ready, k_free,
         v_free) = sems(nc, c, "hgtt", "masked turned copied projected kv_copied q_copied related out_k_ready "
                        "out_v_ready k_free v_free")
        stored_k, stored_v = sems(nc, c, "hgtt", "stored_k stored_v")
        half = RELS // 2
        parts = [(v, g, hp) for g in range(2) for hp in range(HP) for v in range(2)]

        def tiles(eng, step):
            with eng.Fori(0, NT - 1) as t:
                step(t, True)
            step(NT - 1, False)

        with nc.Block() as block:
            @block.vector
            def _(dve):
                def mask(t):
                    for k in range(TYPES):
                        ins = nc.vector.tensor_scalar(xm[:, k, :], xn[:, ds(t, 1), :].rearrange("p o d -> p (o d)"),
                                                      is_kind[:, k, ds(t, 1)], None, ALU.mult)
                    ins.then_inc(masked, 1)
                mask(0)
                dve.sem_inc(kv_copied, 1)
                dve.sem_inc(out_v_ready, 2)

                def step(t, more):
                    if more:
                        dve.wait_ge(turned, t + 1)
                        mask(t + 1)
                    dve.wait_ge(projected, t + 1)
                    dve.wait_ge(related, t * 8 + 8)
                    nc.vector.tensor_copy(kvt[:], pkv[:].rearrange("p (c n) -> p c n", n=P)).then_inc(kv_copied, 1)
                    dve.wait_ge(v_free, t + 1)
                    for n, (v, g, hp) in enumerate(parts):
                        if v:
                            dve.wait_ge(related, t * 8 + 8 + n + 1)
                            nc.vector.tensor_copy(out_v[:, g * half:(g + 1) * half, hp * P:(hp + 1) * P],
                                                  pr[n % 4][:].rearrange("p (r n) -> p r n", r=half)).then_inc(out_v_ready, 1)
                tiles(dve, step)

            @block.tensor
            def _(pe):
                pe.sem_inc(related, 8)

                def turn_masked():
                    for k in range(KC):
                        mm = nc.tensor.transpose(pt[:, k * P:(k + 1) * P], xm[:, k // 2, (k % 2) * P:(k % 2 + 1) * P],
                                                 kit.ident[:])
                    mm.then_inc(turned, 1)
                pe.wait_ge(masked, 1)
                turn_masked()

                def step(t, more):
                    pe.wait_ge(copied, t + 1)
                    pe.wait_ge(kv_copied, t + 1)
                    for n, w in enumerate((w_k, w_v)):
                        for f in range(HP):
                            for k in range(KC):
                                nc.tensor.matmul(pkv[:, (n * HP + f) * P:(n * HP + f + 1) * P], w[:, k, f * P:(f + 1) * P],
                                                 xmt[:, k, :], start=(k == 0), stop=(k == KC - 1))
                    pe.wait_ge(q_copied, t + 1)
                    for k in range(KC):
                        mm = nc.tensor.matmul(pq[:, 0:D], xmt[:, k, :], w_q[:, k, :], start=(k == 0), stop=(k == KC - 1))
                    mm.then_inc(projected, 1)
                    if more:
                        pe.wait_ge(masked, t + 2)
                        turn_masked()
                    pe.wait_ge(kv_copied, t + 2)
                    for n, (v, g, hp) in enumerate(parts):
                        pe.wait_ge(out_v_ready if v else out_k_ready, t * 4 + n // 2 + 1)
                        nc.tensor.matmul(pr[n % 4][:], kvt[:, v * HP + hp, :],
                                         (rel_v if v else rel_k)[:, hp, g * half:(g + 1) * half, :].rearrange(
                                             "p r n -> p (r n)"), start=True, stop=True).then_inc(related, 1)
                tiles(pe, step)

            @block.scalar
            def _(act):
                act.sem_inc(q_copied, 1)
                act.sem_inc(out_k_ready, 2)

                def copy_turned(t):
                    act.wait_ge(turned, t + 1)
                    nc.scalar.copy(xmt[:], pt[:].rearrange("p (k n) -> p k n", k=KC)).then_inc(copied, 1)
                copy_turned(0)

                def step(t, more):
                    wait_alone(act, projected, t + 1)
                    nc.scalar.copy(q[:, ds(t, 1), :].rearrange("p o d -> p (o d)"), pq[:, 0:D]).then_inc(q_copied, 1)
                    if more:
                        copy_turned(t + 1)
                    act.wait_ge(k_free, t + 1)
                    for n, (v, g, hp) in enumerate(parts):
                        if not v:
                            act.wait_ge(related, t * 8 + 8 + n + 1)
                            nc.scalar.copy(out_k[:, g * half:(g + 1) * half, hp * P:(hp + 1) * P],
                                           pr[n % 4][:].rearrange("p (r n) -> p r n", r=half)).then_inc(out_k_ready, 1)
                tiles(act, step)

            @block.sync
            def _(sp):
                sp.sem_inc(k_free, 1)
                sp.sem_inc(v_free, 1)
                by_node = [a.rearrange("(r t p) d -> t p r d", r=RELS, p=P) for a in (keys, values)]
                with sp.Fori(0, NT) as t:
                    for ready, out, table, stored in ((out_k_ready, out_k, by_node[0], stored_k),
                                                      (out_v_ready, out_v, by_node[1], stored_v)):
                        sp.wait_ge(ready, t * 4 + 2 + 4)
                        sp.dma_start(table[ds(t, 1), :, :, :].rearrange("o p r d -> p (o r) d"), out[:]).then_inc(stored, 16)
                    sp.wait_ge(stored_k, t * 16 + 16)
                    sp.sem_inc(k_free, 1)
                    sp.wait_ge(stored_v, t * 16 + 16)
                    sp.sem_inc(v_free, 1)


def column(ap1d, k):
    return ap1d.rearrange("(k p) -> p k", k=k)


def sage_stage(nc, kit, A, x, bufs, e, table):
    b1, b2, b3, b4 = bufs
    with ExitStack() as c:
        def sb(name, shape, dt=F32):
            return c.enter_context(nc.sbuf_tensor(f"sage_{name}", shape, dt))
        layers = A["L2_gnn_W_agg"].shape[0]
        w_in, w_out = sb("w_in", [P, 2, D]), sb("w_out", [P, 2, D])
        w_agg = [sb(f"w_agg{i}", [P, 2, D]) for i in range(layers)]
        w_self = [sb(f"w_self{i}", [P, 2, D]) for i in range(layers)]
        bias_in, bias_out = sb("b_in", [P, 2]), sb("b_out", [P, D])
        bias = [sb(f"b_hid{i}", [P, 2]) for i in range(layers)]
        rdeg, rall = sb("rdeg", [P, NT]), sb("rall", [P, NP])
        with nc.allow_non_contiguous_dma(reason="short bias columns"):
            load(nc, "sage_load",
                 [(w_in[:], chunks(A["L2_gnn_W_in"])), (w_out[:], chunks(A["L2_gnn_W_out"])),
                  (bias_in[:], column(A["L2_gnn_b_in"], 2)), (bias_out[:], row_to_all(A["L2_gnn_b_out"]))]
                 + [(w_agg[i][:], chunks(A["L2_gnn_W_agg"][i])) for i in range(layers)]
                 + [(w_self[i][:], chunks(A["L2_gnn_W_self"][i])) for i in range(layers)]
                 + [(bias[i][:], column(A["L2_gnn_b_hid"][i], 2)) for i in range(layers)])
        layer_norm(nc, kit, "sage_ln", x, b1, b2)

        def mean_factor(link):
            link(nc.vector.tensor_scalar(rdeg[:], kit.deg[:], 1.0, None, ALU.max))
            link(nc.vector.reciprocal(rdeg[:], rdeg[:]))
        on_vector(nc, "sage_v0", mean_factor)
        rows_to_all(nc, kit, "sage_rall", rdeg, rall)
        project_t(nc, "sage_in", [(b2, 2, w_in)], b3, 2, bias=bias_in)
        h, free = b3, b2
        for i in range(layers):
            write_table(nc, kit, f"sage_t{i}", h, 2, b1, table)
            aggregate_t(nc, kit, f"sage_a{i}", e, table, 2, b4)
            on_vector(nc, f"sage_v{i + 1}", lambda link: link(nc.vector.tensor_tensor(
                tr(b4), tr(b4), rall[:, None, :].broadcast_to([P, 2, NP]), ALU.mult)))
            project_t(nc, f"sage_p{i}", [(b4, 2, w_agg[i]), (h, 2, w_self[i])], free, 2, ACT.Relu, bias[i])
            h, free = free, h
        add_projection(nc, "sage_out", h, w_out, nat(x), bias_out)


def weighted_stage(nc, kit, A, x, bufs, e, table):
    b1, b2, b3, b4 = bufs
    with ExitStack() as c:
        def sb(name, shape, dt=F32):
            return c.enter_context(nc.sbuf_tensor(f"wsum_{name}", shape, dt))
        w, wt = sb("w", [P, 2, D]), sb("wt", [P, 2, D])
        ln_w, ln_b = sb("ln_w", [P, 2]), sb("ln_b", [P, 2])
        bias, gamma, beta = sb("b", [P, D]), sb("gamma", [P, D]), sb("beta", [P, D])
        with nc.allow_non_contiguous_dma(reason="short columns"):
            load(nc, "wsum_load",
                 [(w[:], chunks(A["L3_gnn_W"])), (ln_w[:], column(A["L3_gnn_ln_w"], 2)),
                  (ln_b[:], column(A["L3_gnn_ln_b"], 2)), (bias[:], row_to_all(A["L3_gnn_b"])),
                  (gamma[:], row_to_all(A["L3_gnn_gamma"])), (beta[:], row_to_all(A["L3_gnn_beta"]))])
        layer_norm(nc, kit, "wsum_ln", x, b1, b2)
        layer_norm(nc, kit, "wsum_ln2", b1, b3, b2)
        with ExitStack() as cc:
            step, squashed, turned = sems(nc, cc, "wsum_silu", "step squashed turned")
            ps = cc.enter_context(nc.psum_tensor("wsum_ps", [P, 512], F32))
            with nc.Block() as block:
                @block.tensor
                def _(pe):
                    for k in range(2):
                        for o in range(2):
                            mm = nc.tensor.transpose(ps[:, k * D + o * P:k * D + (o + 1) * P],
                                                     w[:, o, k * P:(k + 1) * P], kit.ident[:])
                    mm.then_inc(turned, 1)

                @block.vector
                def _(dve):
                    link = link_on(dve, step)
                    for k in range(2):
                        link(nc.vector.tensor_scalar(tr(b2)[:, k, :], tr(b2)[:, k, :], ln_w[:, k:k + 1],
                                                     ln_b[:, k:k + 1], ALU.mult, ALU.add))
                    dve.wait_ge(turned, 1)
                    link(nc.vector.tensor_tensor(wt[:], ps[:].rearrange("p (k n) -> p k n", k=2),
                                                 gamma[:, None, :].broadcast_to([P, 2, D]), ALU.mult))
                    link(nc.vector.tensor_tensor(bias[:], bias[:], gamma[:], ALU.mult))
                    link(nc.vector.tensor_tensor(bias[:], bias[:], beta[:], ALU.add))
                    link(nc.vector.tensor_tensor(x[:], x[:], b1[:], ALU.add))
                    for k in range(2):
                        dve.wait_ge(squashed, k + 1)
                        link(nc.vector.tensor_tensor(tr(b2)[:, k, :], tr(b2)[:, k, :], tr(b4)[:, k, :], ALU.mult))

                @block.scalar
                def _(act):
                    for k in range(2):
                        act.wait_ge(step, k + 1)
                        nc.scalar.activation(tr(b4)[:, k, :], tr(b2)[:, k, :], ACT.Sigmoid).then_inc(squashed, 1)
        write_table(nc, kit, "wsum_t", b2, 2, b3, table)
        aggregate_t(nc, kit, "wsum_a", e, table, 2, b4, weighted=True)
        add_projection(nc, "wsum_out", b4, wt, nat(x), bias)


def rank_rows(nc, kit, link, z, n, above, same, lower, rank):
    T = z.shape[1]
    each = z[:, :, :, None].broadcast_to([P, T, n, n])
    other = z[:, :, None, :].broadcast_to([P, T, n, n])
    link(nc.vector.tensor_tensor(lower, kit.iota[:, None, 0:n].broadcast_to([P, n, n]),
                                 kit.iota[:, 0:n, None].broadcast_to([P, n, n]), ALU.is_lt))
    link(nc.vector.tensor_tensor(above, other, each, ALU.is_gt))
    link(nc.vector.tensor_tensor(same, other, each, ALU.is_equal))
    link(nc.vector.tensor_tensor(same, same, lower[:, None, :, :].broadcast_to([P, T, n, n]), ALU.mult))
    link(nc.vector.tensor_tensor(above, above, same, ALU.add))
    link(nc.vector.tensor_reduce(rank, above, AX_X, ALU.add))


def shared_moe_stage(nc, kit, A, x, bufs):
    b1, b2, b3, b4 = bufs
    E, F = A["L3_ffn_b1"].shape
    fc = F // P
    K = 2
    CAPACITY = float(-(-N * 5 // (4 * E)))
    with ExitStack() as c:
        def sb(name, shape, dt=F32):
            return c.enter_context(nc.sbuf_tensor(f"shared_{name}", shape, dt))
        wr, br = sb("wr", [P, 2, E]), sb("br", [P, E])
        gamma, beta = sb("gamma", [P, D]), sb("beta", [P, D])
        mean, mean_all = sb("mean", [P, 2]), sb("mean_all", [P, 2, P])
        z, load_, pick_w = sb("z", [P, 1, E]), sb("load", [P, 1, E]), sb("pick_w", [P, 1, K])
        above, same, lower = sb("above", [P, 1, E, E]), sb("same", [P, 1, E, E]), sb("lower", [P, E, E])
        rank, is_r, pick_f = sb("rank", [P, 1, E]), sb("is_r", [P, 1, E]), sb("pick_f", [P, K])
        pick_i = sb("pick_i", [P, K], I32)
        gates = sb("gates", [P, NT, K])
        b1s, b2s = sb("b1s", [P, K, fc]), sb("b2s", [K, D])
        layer_norm(nc, kit, "shared_ln", x, b1, b2)
        load(nc, "shared_load", [(wr[:], chunks(A["L3_ffn_Wr"])), (br[:], row_to_all(A["L3_ffn_br"])),
                                 (gamma[:], row_to_all(A["L3_ffn_gamma"])), (beta[:], row_to_all(A["L3_ffn_beta"]))])
        with ExitStack() as cc:
            step, multiplied = sems(nc, cc, "shared_logit", "step multiplied")
            ps = cc.enter_context(nc.psum_tensor("shared_ps", [P, 512], F32))
            with nc.Block() as block:
                @block.vector
                def _(dve):
                    link = link_on(dve, step)
                    link(nc.vector.tensor_reduce(mean[:], tr(b2)[:, :, 0:N], AX_X, ALU.add))
                    link(nc.vector.tensor_scalar(mean[:], mean[:], 1.0 / N, None, ALU.mult))
                    link(nc.vector.tensor_copy(mean_all[:], mean[:, :, None].broadcast_to([P, 2, P])))
                    link(nc.vector.tensor_copy(b3[:], b1[:]))
                    dve.wait_ge(multiplied, 1)
                    link(nc.vector.tensor_tensor(z[:, 0, :], ps[:, 0:E], br[:], ALU.add))

                @block.tensor
                def _(pe):
                    pe.wait_ge(step, 3)
                    for k in range(2):
                        mm = nc.tensor.matmul(ps[:, 0:E], mean_all[:, k, :], wr[:, k, :], start=(k == 0), stop=(k == 1))
                    mm.then_inc(multiplied, 1)
        softmax_rows(nc, "shared_sm1", z[:], E)

        def scale_loads(link):
            link(nc.vector.tensor_scalar(load_[:], z[:], float(N), 1.0, ALU.mult, ALU.max))
            link(nc.vector.reciprocal(load_[:], load_[:]))
            link(nc.vector.tensor_scalar(load_[:], load_[:], CAPACITY, 1.0, ALU.mult, ALU.min))
            link(nc.vector.tensor_tensor(z[:], z[:], load_[:], ALU.mult))
        on_vector(nc, "shared_v1", scale_loads)
        softmax_rows(nc, "shared_sm2", z[:], E)

        def choose(link):
            rank_rows(nc, kit, link, z[:], E, above[:], same[:], lower[:], rank[:])
            for r in range(K):
                link(nc.vector.tensor_scalar(is_r[:], rank[:], float(r), None, ALU.is_equal))
                link(nc.vector.tensor_tensor(load_[:], is_r[:], kit.iota[:, None, 0:E], ALU.mult))
                link(nc.vector.tensor_reduce(pick_f[:, r:r + 1], load_[:], AX_X, ALU.add))
                link(nc.vector.tensor_tensor(load_[:], is_r[:], z[:], ALU.mult))
                link(nc.vector.tensor_reduce(pick_w[:, :, r:r + 1], load_[:], AX_X, ALU.add))
            link(nc.vector.tensor_copy(pick_i[:], pick_f[:]))
        on_vector(nc, "shared_v2", choose)
        softmax_rows(nc, "shared_sm3", pick_w[:], K)
        on_vector(nc, "shared_v3", lambda link: link(nc.vector.tensor_copy(
            gates[:], pick_w[:].broadcast_to([P, NT, K]))))
        pick = lambda eng, e: eng.value_load(pick_i[0:1, ds(e, 1)], min_val=0, max_val=E - 1)
        with ExitStack() as cc:
            loaded, = sems(nc, cc, "shared_b", "loaded")
            with nc.Block() as block:
                @block.sync
                def _(sp):
                    for r in range(K):
                        at = pick(sp, r)
                        for f in range(fc):
                            sp.dma_start(b1s[:, r, f:f + 1],
                                         A["L3_ffn_b1"][ds(at, 1), f * P:(f + 1) * P].rearrange("o p -> p o")
                                         ).then_inc(loaded, 16)
                        sp.dma_start(b2s[r:r + 1, :], A["L3_ffn_b2"][ds(at, 1), :]).then_inc(loaded, 16)
                    sp.wait_ge(loaded, 16 * K * (fc + 1))
        add_gated_bias(nc, kit, "shared_b2", gates, b2s[:], b3)
        of = lambda name: lambda e: A[name][ds(e, 1), :, :]
        expert_mlps(nc, "shared", b2, K, [Mid(of("L3_ffn_W1"), 2, fc, ACT.Gelu, b1s)], of("L3_ffn_W2"), gates, b3, pick)
        layer_norm(nc, kit, "shared_ln2", b3, b4)

        def after(link):
            link(nc.vector.tensor_tensor(nat(b4), nat(b4), gamma[:, None, :].broadcast_to([P, NT, D]), ALU.mult))
            link(nc.vector.tensor_tensor(nat(b4), nat(b4), beta[:, None, :].broadcast_to([P, NT, D]), ALU.add))
            link(nc.vector.tensor_tensor(x[:], x[:], b4[:], ALU.add))
        on_vector(nc, "shared_v4", after)


FLT_MAX = 3.4028234663852886e38


def switch_stage(nc, kit, A, x, bufs):
    b1, b2, b3, b4 = bufs
    E, F = A["L2_ffn_b1"].shape
    fc = F // P
    C = -(-N * 5 // (4 * E))
    ST = -(-C // P)
    S = ST * P
    slots = nc.dram_tensor("switch_slots", (E * S + NP, D), F32).ap()
    answers = nc.dram_tensor("switch_answers", (E * S, D), F32).ap()
    with ExitStack() as c:
        def sb(name, shape, dt=F32):
            return c.enter_context(nc.sbuf_tensor(f"switch_{name}", shape, dt))
        slot_i, back_i = sb("slot_i", [P, NT], I32), sb("back_i", [P, NT], I32)
        factor = sb("factor", [P, NT])
        layer_norm(nc, kit, "switch_ln", x, b1, b2)
        with ExitStack() as cc:
            def sb2(name, shape, dt=F32):
                return cc.enter_context(nc.sbuf_tensor(f"switch_{name}", shape, dt))
            gw, gb, z = sb2("gw", [P, 2, E]), sb2("gb", [P, E]), sb2("z", [P, NT, E])
            above, same = sb2("above", [P, NT, E, E]), sb2("same", [P, NT, E, E])
            lower, rank = sb2("lower", [P, E, E]), sb2("rank", [P, NT, E])
            hot, ahead, total = sb2("hot", [P, NT, E]), sb2("ahead", [P, NT, E]), sb2("total", [P, NT, E])
            pos, kept, first, valid, spare = (sb2(n, [P, NT]) for n in ("pos", "kept", "first", "valid", "spare"))
            load(nc, "switch_load", [(gw[:], chunks(A["L2_ffn_gate_w"])), (gb[:], row_to_all(A["L2_ffn_gate_b"]))])
            add_projection(nc, "switch_gate", b2, gw, z[:], gb, fresh=True)
            softmax_rows(nc, "switch_sm", z[:], E)
            step, chosen, summed, placed, zeroed = sems(nc, cc, "switch_route", "step chosen summed placed zeroed")
            sent, = gather_sems(nc, "switch_route", "sent", 1)
            ps = cc.enter_context(nc.psum_tensor("switch_ps", [P, 512], F32))
            with nc.Block() as block:
                @block.vector
                def _(dve):
                    link = link_on(dve, step)
                    link(nc.vector.memset(b3[:, 0:E * S * D // P // 2], 0.0))
                    link(nc.vector.tensor_reduce(factor[:], z[:], AX_X, ALU.max))
                    rank_rows(nc, kit, link, z[:], E, above[:], same[:], lower[:], rank[:])
                    link(nc.vector.tensor_scalar(valid[:], kit.node[:], float(N), None, ALU.is_lt))
                    link(nc.vector.tensor_scalar(hot[:], rank[:], 0.0, None, ALU.is_equal))
                    nc.vector.tensor_tensor(hot[:], hot[:], per_node(valid[:], E), ALU.mult).then_inc(chosen, 1)
                    dve.wait_ge(summed, 1)
                    link(nc.vector.tensor_copy(ahead[:], ps[:, 0:NT * E].rearrange("p (t e) -> p t e", e=E)))
                    link(nc.vector.tensor_copy(total[:], ps[:, 256:256 + NT * E].rearrange("p (t e) -> p t e", e=E)))
                    for e in range(E):
                        link(nc.vector.tensor_tensor_scan(rank[:, :, e], kit.ones[:, 0:NT], total[:, :, e], 0.0,
                                                          ALU.mult, ALU.add))
                    link(nc.vector.tensor_tensor(ahead[:], ahead[:], rank[:], ALU.add))
                    link(nc.vector.tensor_tensor(ahead[:], ahead[:], total[:], ALU.subtract))
                    link(nc.vector.tensor_tensor(ahead[:], ahead[:], hot[:], ALU.mult))
                    link(nc.vector.tensor_reduce(pos[:], ahead[:], AX_X, ALU.add))
                    link(nc.vector.tensor_tensor(total[:], hot[:], kit.iota[:, None, 0:E].broadcast_to([P, NT, E]),
                                                 ALU.mult))
                    link(nc.vector.tensor_reduce(first[:], total[:], AX_X, ALU.add))
                    link(nc.vector.tensor_scalar(first[:], first[:], float(S), None, ALU.mult))
                    link(nc.vector.tensor_scalar(kept[:], pos[:], float(C), None, ALU.is_lt))
                    link(nc.vector.tensor_tensor(kept[:], kept[:], valid[:], ALU.mult))
                    link(nc.vector.tensor_tensor(factor[:], factor[:], kept[:], ALU.mult))
                    link(nc.vector.scalar_tensor_tensor(out=spare[:], in0=pos[:], scalar=float(C - 1), in1=first[:],
                                                        op0=ALU.min, op1=ALU.add))
                    link(nc.vector.tensor_copy(back_i[:], spare[:]))
                    link(nc.vector.tensor_scalar(valid[:], kit.node[:], float(E * S), None, ALU.add))
                    link(nc.vector.tensor_tensor(spare[:], spare[:], valid[:], ALU.subtract))
                    link(nc.vector.tensor_tensor(spare[:], spare[:], kept[:], ALU.mult))
                    link(nc.vector.tensor_tensor(spare[:], spare[:], valid[:], ALU.add))
                    nc.vector.tensor_copy(slot_i[:], spare[:]).then_inc(placed, 1)

                @block.tensor
                def _(pe):
                    pe.wait_ge(chosen, 1)
                    flat = hot[:].rearrange("p t e -> p (t e)")
                    nc.tensor.matmul(ps[:, 0:NT * E], kit.tri[:], flat, start=True, stop=True)
                    nc.tensor.matmul(ps[:, 256:256 + NT * E], kit.ones[:], flat, start=True, stop=True).then_inc(summed, 1)

                @block.sync
                def _(sp):
                    half = E * S // 2
                    sp.wait_ge(step, 1)
                    for n in range(2):
                        sp.dma_start(slots[n * half:(n + 1) * half, :].rearrange("(p r) d -> p (r d)", p=P),
                                     b3[:, 0:half * D // P]).then_inc(zeroed, 16)

                @block.gpsimd
                def _(pool):
                    pool.wait_ge(zeroed, 32)
                    pool.wait_ge(placed, 1)
                    for t in range(NT):
                        nc.gpsimd.indirect_dma_start(slots, bass.IndirectOffsetOnAxis(ap=slot_i[:, t:t + 1], axis=0),
                                                     nat(b1)[:, t, :], None).then_inc(sent, 16)
                    pool.wait_ge(sent, 16 * NT)
        switch_experts(nc, kit, A, slots, answers, E, fc, ST, bufs)
        with ExitStack() as cc:
            fetched = gather_sems(nc, "switch_back", "fetched", ROUNDS)
            scaled, step = sems(nc, cc, "switch_back", "scaled step")
            limit = [cc.enter_context(nc.sbuf_tensor(f"switch_limit{n}", [P, 1], F32)) for n in range(3)]
            with nc.Block() as block:
                @block.gpsimd
                def _(pool):
                    for t in range(NT):
                        nc.gpsimd.indirect_dma_start(nat(b3)[:, t, :], None, answers,
                                                     bass.IndirectOffsetOnAxis(ap=back_i[:, t:t + 1], axis=0)
                                                     ).then_inc(fetched[t // U], 16)

                @block.vector
                def _(dve):
                    for r in range(ROUNDS):
                        dve.wait_ge(fetched[r], 16 * U)
                        part = nat(b3)[:, r * U:(r + 1) * U, :]
                        nc.vector.tensor_tensor(part, part, per_node(factor[:, r * U:(r + 1) * U], D),
                                                ALU.mult).then_inc(scaled, 1)
                    dve.wait_ge(scaled, ROUNDS)
                    link = link_on(dve, step)
                    mask = b4[:].bitcast(I32)
                    for n, (to, op, than) in enumerate(((1e4, ALU.is_gt, FLT_MAX), (-1e4, ALU.is_lt, -FLT_MAX),
                                                        (0.0, ALU.not_equal, None))):
                        link(nc.vector.memset(limit[n][:], to))
                        link(nc.vector.tensor_scalar(mask, b3[:], than, None, op) if than is not None
                             else nc.vector.tensor_tensor(mask, b3[:], b3[:], op))
                        link(nc.vector.copy_predicated(b3[:], mask, limit[n][:].broadcast_to([P, NT * D])))
                    link(nc.vector.tensor_tensor(x[:], x[:], b3[:], ALU.add))


def switch_experts(nc, kit, A, slots, answers, E, fc, ST, big):
    S = ST * P
    with ExitStack() as c:
        def sb(name, shape, dt=F32):
            return c.enter_context(nc.sbuf_tensor(f"swx_{name}", shape, dt))
        b1s = sb("b1s", [P, E, fc])

        def carve(buf, *shapes):
            at, parts = 0, []
            for n, m in shapes:
                parts.append(buf[:, at:at + n * m].rearrange("p (n m) -> p n m", n=n))
                at += n * m
            return parts
        h, = carve(big[0], (fc, S))
        w1_0, w1_1, w2_0 = carve(big[1], (2, fc * P), (2, fc * P), (fc, D))
        w2_1, rows_0, rows_1, y_0, y_1 = carve(big[2], (fc, D), (ST, D), (ST, D), (ST, D), (ST, D))
        b2s, xt = carve(big[3], (E, D), (2, S))
        w1, w2, rows, y = (w1_0, w1_1), (w2_0, w2_1), (rows_0, rows_1), (y_0, y_1)
        with nc.allow_non_contiguous_dma(reason="short columns"):
            load(nc, "swx_load", [(b1s[:, e, :], column(A["L2_ffn_b1"][e], fc)) for e in range(E)]
                 + [(b2s[:, e, :], row_to_all(A["L2_ffn_b2"][e])) for e in range(E)])
        ps = [c.enter_context(nc.psum_tensor(f"swx_ps{r}", [P, 512], F32)) for r in range(4)]
        py = [c.enter_context(nc.psum_tensor(f"swx_py{r}", [P, 512], F32)) for r in range(4)]
        loaded = sems(nc, c, "swx", "loaded0 loaded1")
        stored = gather_sems(nc, "swx", "stored", 2)
        turned, copied, multiplied, read, finished, added, left, y_free = sems(
            nc, c, "swx", "turned copied multiplied read finished added left y_free")
        with nc.Block() as block:
            def pairs(eng, body):
                with eng.Fori(0, E // 2) as i:
                    for q in range(2):
                        body(i, q, i * 2 + q)

            @block.sync
            def _(sp):
                def body(i, q, e):
                    sp.wait_ge(left, e + 1)
                    sp.dma_start(rows[q], slots[ds(e * S, S), :].rearrange("(s p) d -> p s d", p=P)).then_inc(loaded[q], 16)
                    sp.dma_start(w1[q], A["L2_ffn_w1"][ds(e, 1), :, :].rearrange("o (k p) f -> p (o k) f", p=P)
                                 ).then_inc(loaded[q], 16)
                    sp.dma_start(w2[q], A["L2_ffn_w2"][ds(e, 1), :, :].rearrange("o (k p) f -> p (o k) f", p=P)
                                 ).then_inc(loaded[q], 16)
                pairs(sp, body)

            @block.tensor
            def _(pe):
                pe.sem_inc(left, 2)

                def body(i, q, e):
                    wait_alone(pe, loaded[q], i * 48 + 48)
                    for k in range(2):
                        pe.wait_ge(read, e * fc + 4)
                        for s in range(ST):
                            mm = nc.tensor.transpose(ps[k][:, s * P:(s + 1) * P], rows[q][:, s, k * P:(k + 1) * P],
                                                     kit.ident[:])
                        mm.then_inc(turned, 1)
                    for g in range(fc):
                        pe.wait_ge(copied, e * 2 + 2)
                        pe.wait_ge(read, e * fc + g + 1)
                        for k in range(2):
                            mm = nc.tensor.matmul(ps[g % 4][:, 0:S], w1[q][:, k, g * P:(g + 1) * P], xt[:, k, :],
                                                  start=(k == 0), stop=(k == 1))
                        mm.then_inc(multiplied, 1)
                    pe.wait_ge(read, e * fc + fc + 4)
                    for s in range(ST):
                        pe.wait_ge(added, e * ST + s + 1)
                        for k in range(fc):
                            mm = nc.tensor.matmul(py[s][:, 0:D], h[:, k, s * P:(s + 1) * P], w2[q][:, k, :],
                                                  start=(k == 0), stop=(k == fc - 1))
                        mm.then_inc(finished, 1)
                    pe.drain().then_inc(left, 1)
                pairs(pe, body)

            @block.scalar
            def _(act):
                act.sem_inc(read, 4)

                def body(i, q, e):
                    for k in range(2):
                        act.wait_ge(turned, e * 2 + k + 1)
                        nc.scalar.copy(xt[:, k, :], ps[k][:, 0:S]).then_inc(copied, 1)
                    for g in range(fc):
                        wait_alone(act, multiplied, e * fc + g + 1)
                        nc.scalar.activation(h[:, g, :], ps[g % 4][:, 0:S], ACT.Relu,
                                             bias=b1s[:, ds(e, 1), g:g + 1].rearrange("p o f -> p (o f)")
                                             ).then_inc(read, 1)
                pairs(act, body)

            @block.vector
            def _(dve):
                dve.sem_inc(added, ST)

                def body(i, q, e):
                    dve.wait_ge(y_free, e + 1)
                    for s in range(ST):
                        dve.wait_ge(finished, e * ST + s + 1)
                        nc.vector.tensor_tensor(y[q][:, s, :], py[s][:, 0:D],
                                                b2s[:, ds(e, 1), :].rearrange("p o d -> p (o d)"), ALU.add).then_inc(added, 1)
                pairs(dve, body)

            @block.gpsimd
            def _(pool):
                pool.sem_inc(y_free, 2)

                def body(i, q, e):
                    wait_alone(pool, added, e * ST + ST + ST)
                    nc.gpsimd.dma_start(answers[ds(e * S, S), :].rearrange("(s p) d -> p s d", p=P), y[q]
                                        ).then_inc(stored[q], 16)
                    wait_alone(pool, stored[q], i * 16 + 16)
                    pool.sem_inc(y_free, 1)
                pairs(pool, body)


def program(nc, A, out, stages=range(8)):
    with ExitStack() as ctx:
        kit = Kit()
        make_constants(nc, ctx, kit)
        x, *bufs = [ctx.enter_context(nc.sbuf_tensor(n, [P, NT * D], F32)) for n in ("x", "big1", "big2", "big3", "big4")]
        kit.deg = ctx.enter_context(nc.sbuf_tensor("deg", [P, NT], F32))
        table = nc.dram_tensor("table", (NP, D), F32).ap()
        table_half = nc.dram_tensor("table_half", (NP, P), F32).ap()
        load_x(nc, A["x"], x)
        edges = alloc_edges(nc, ctx, "edge", 416)
        if 0 in stages or 2 in stages:
            sort_edges(nc, kit, edges, 125, A["src"], A["dst"], etype=A["edge_type_8"])
        if 0 in stages:
            gcn_stage(nc, kit, A, x, bufs, edges, table_half)
        if 1 in stages:
            gat_moe_stage(nc, kit, A, x, bufs)
        if 2 in stages:
            hgt_stage(nc, kit, A, x, bufs, edges)
        if 3 in stages:
            soft_moe_stage(nc, kit, A, x, bufs)
        if 4 in stages or 6 in stages:
            edges.name = "back"
            sort_edges(nc, kit, edges, 125, A["dst"], A["src"], weight=A["edge_weight"])
        if 4 in stages:
            in_degrees(nc, kit, "deg", A["src"], 125, kit.deg)
            sage_stage(nc, kit, A, x, bufs, edges, table)
        if 5 in stages:
            switch_stage(nc, kit, A, x, bufs)
        if 6 in stages:
            weighted_stage(nc, kit, A, x, bufs, edges, table)
        if 7 in stages:
            shared_moe_stage(nc, kit, A, x, bufs)
        store_x(nc, x, out)


def load_x(nc, src, x):
    with ExitStack() as c:
        loaded, cleared = sems(nc, c, "load_x", "loaded cleared")
        with nc.Block() as block:
            @block.vector
            def _(dve):
                nc.vector.memset(nat(x)[:, NT - 1, :], 0.0).then_inc(cleared, 1)

            @block.sync
            def _(sp):
                sp.dma_start(nat(x)[:, 0:NT - 1, :],
                             src[0:(NT - 1) * P, :].rearrange("(t p) d -> p t d", p=P)).then_inc(loaded, 16)
                sp.wait_ge(cleared, 1)
                sp.dma_start(nat(x)[0:LAST, NT - 1, :], src[(NT - 1) * P:N, :]).then_inc(loaded, 16)
                sp.wait_ge(loaded, 32)


def store_x(nc, x, out):
    with ExitStack() as c:
        stored, = sems(nc, c, "store_x", "stored")
        with nc.Block() as block:
            @block.sync
            def _(sp):
                sp.dma_start(out[0:(NT - 1) * P, :].rearrange("(t p) d -> p t d", p=P),
                             nat(x)[:, 0:NT - 1, :]).then_inc(stored, 16)
                sp.dma_start(out[(NT - 1) * P:N, :], nat(x)[0:LAST, NT - 1, :]).then_inc(stored, 16)
                sp.wait_ge(stored, 32)


_INS = ['x', 'src', 'dst', 'edge_type_8', 'edge_weight', 'node_type_4', 'L0_gnn_W1', 'L0_gnn_b1',
        'L0_gnn_W2', 'L0_gnn_b2', 'L0_ffn_W_gat', 'L0_ffn_att_src', 'L0_ffn_att_dst',
        'L0_ffn_b_gat', 'L0_ffn_ln_gamma', 'L0_ffn_ln_beta', 'L0_ffn_W1', 'L0_ffn_b1', 'L0_ffn_W2',
        'L0_ffn_b2', 'L0_ffn_edge_index', 'L1_gnn_k_linears', 'L1_gnn_q_linears',
        'L1_gnn_v_linears', 'L1_gnn_a_linears', 'L1_gnn_relation_att', 'L1_gnn_relation_msg',
        'L1_gnn_relation_pri', 'L1_gnn_skip', 'L1_ffn_Wr', 'L1_ffn_br', 'L1_ffn_W1', 'L1_ffn_b1',
        'L1_ffn_g1', 'L1_ffn_be1', 'L1_ffn_m1', 'L1_ffn_v1', 'L1_ffn_W2', 'L1_ffn_b2', 'L1_ffn_g2',
        'L1_ffn_be2', 'L1_ffn_m2', 'L1_ffn_v2', 'L1_ffn_Wo', 'L1_ffn_bo', 'L2_gnn_W_in',
        'L2_gnn_b_in', 'L2_gnn_W_agg', 'L2_gnn_W_self', 'L2_gnn_b_hid', 'L2_gnn_W_out',
        'L2_gnn_b_out', 'L2_ffn_gate_w', 'L2_ffn_gate_b', 'L2_ffn_w1', 'L2_ffn_b1', 'L2_ffn_w2',
        'L2_ffn_b2', 'L3_gnn_ln_w', 'L3_gnn_ln_b', 'L3_gnn_W', 'L3_gnn_b', 'L3_gnn_gamma',
        'L3_gnn_beta', 'L3_ffn_Wr', 'L3_ffn_br', 'L3_ffn_W1', 'L3_ffn_b1', 'L3_ffn_W2', 'L3_ffn_b2',
        'L3_ffn_gamma', 'L3_ffn_beta']
_OUTS = [((3125, 256), 'float32')]


def kernel(**inputs):
    import numpy as _np
    import concourse.bacc as _bacc
    from concourse import mybir as _mybir
    from concourse.bass_utils import run_bass_kernel_spmd as _run

    nc = _bacc.Bacc("TRN2", target_bir_lowering=False, num_devices=1)
    arrays, named = {}, {}
    for name in _INS:
        a = _np.ascontiguousarray(inputs[name])
        arrays[f"in_{name}_dram"] = a
        named[name] = nc.dram_tensor(f"in_{name}_dram", a.shape, _mybir.dt.from_np(a.dtype), kind="ExternalInput").ap()
    shape, dtype = _OUTS[0]
    out = nc.dram_tensor("out_0_dram", shape, _mybir.dt.from_np(_np.dtype(dtype)), kind="ExternalOutput").ap()
    program(nc, named, out)
    r = _run(nc, [arrays], core_ids=[0])
    return r.results[0]["out_0_dram"]
```

```python
from contextlib import ExitStack


import concourse.bass as bass
from concourse import mybir

F32 = mybir.dt.float32
BF16 = mybir.dt.bfloat16
I32 = mybir.dt.int32
ALU = mybir.AluOpType
ACT = mybir.ActivationFunctionType
AX_X = mybir.AxisListType.X
ds = bass.ds

P = 128
N = 3125
D = 256
NT = -(-N // P)
NP = NT * P
U = 5
ROUNDS = NT // U
LAST = N - (NT - 1) * P
EPS = 1e-5
CHUNK = 320
G = 8


class Kit:
    pass


def sems(nc, ctx, stage, names):
    taken = [nc.alloc_semaphore(f"{stage}_{n}") for n in names.split()]

    def give_back():
        for sem in taken:
            nc.gpsimd.sem_clear(sem)
            nc.release_semaphore(sem)
    ctx.callback(give_back)
    return taken


def gather_sems(nc, stage, what, n):
    return [nc.alloc_semaphore(f"{stage}_{what}{u}") for u in range(n)]


def wait_alone(eng, sem, value):
    eng.wait_ge(sem, value)
    eng.nop(nofuse=True)


def link_on(eng, sem):
    count = {"base": 0, "k": 0}

    def link(ins):
        count["k"] += 1
        ins.then_inc(sem, 1)
        eng.wait_ge(sem, count["base"] + count["k"])

    def begin(i, n):
        count["start"], count["n"] = count["base"] + count["k"], n
        count["base"], count["k"] = count["start"] + i * n, 0

    def end(rounds):
        assert count["k"] == count["n"], (count["k"], count["n"])
        count["base"], count["k"] = count["start"] + rounds * count["n"], 0

    def plain():
        return count["base"] + count["k"]

    link.begin, link.end, link.value = begin, end, plain
    return link


def nat(buf):
    return buf[:, :].rearrange("p (t d) -> p t d", t=NT)


def tr(buf, k=2):
    return buf[:, 0:k * NP].rearrange("p (k n) -> p k n", k=k)


def row_to_all(ap1d, n=P):
    return bass.AP(tensor=ap1d.tensor, offset=ap1d.offset, ap=[[0, n], list(ap1d.ap[0])])


def make_constants(nc, ctx, kit):
    def sb(name, shape, dt=F32):
        return ctx.enter_context(nc.sbuf_tensor(name, shape, dt))
    kit.ident = sb("ident", [P, P])
    kit.tri = sb("tri_strict", [P, P])
    kit.ones = sb("ones", [P, P])
    kit.iota = sb("iota_row", [P, P])
    kit.iota_t = sb("iota_tiles", [P, 424])
    kit.node = sb("node_number", [P, NT])
    with ExitStack() as c:
        made, = sems(nc, c, "const", "made")
        ints = c.enter_context(nc.sbuf_tensor("iota_int", [P, P], I32))
        ints_t = c.enter_context(nc.sbuf_tensor("iota_t_int", [P, 424], I32))
        node_i = c.enter_context(nc.sbuf_tensor("node_int", [P, NT], I32))
        with nc.Block() as block:
            @block.gpsimd
            def _(pool):
                link = link_on(pool, made)
                link(nc.gpsimd.memset(kit.ident[:], 0.0))
                link(nc.gpsimd.affine_select(out=kit.ident[:], in_=kit.ident[:], compare_op=ALU.not_equal,
                                             fill=1.0, base=0, pattern=[[-1, P]], channel_multiplier=1))
                link(nc.gpsimd.memset(kit.ones[:], 1.0))
                link(nc.gpsimd.affine_select(out=kit.tri[:], in_=kit.ones[:], compare_op=ALU.is_gt,
                                             fill=0.0, base=0, pattern=[[1, P]], channel_multiplier=-1))
                link(nc.gpsimd.iota(ints[:], pattern=[[1, P]], base=0, channel_multiplier=0))
                link(nc.gpsimd.tensor_copy(kit.iota[:], ints[:]))
                link(nc.gpsimd.iota(ints_t[:], pattern=[[1, 424]], base=0, channel_multiplier=0))
                link(nc.gpsimd.tensor_copy(kit.iota_t[:], ints_t[:]))
                link(nc.gpsimd.iota(node_i[:], pattern=[[P, NT]], base=0, channel_multiplier=1))
                link(nc.gpsimd.tensor_copy(kit.node[:], node_i[:]))


class EdgeList:
    pass


def alloc_edges(nc, ctx, name, groups):
    e = EdgeList()
    e.name, e.groups = name, groups
    e.rec = ctx.enter_context(nc.sbuf_tensor(f"{name}_rec", [P, groups + G, 4], F32))
    e.src = ctx.enter_context(nc.sbuf_tensor(f"{name}_src", [P, groups + G], I32))
    e.key = ctx.enter_context(nc.sbuf_tensor(f"{name}_key", [P, groups + G], I32))
    e.tile = ctx.enter_context(nc.sbuf_tensor(f"{name}_tile", [P, groups], F32))
    e.blk = ctx.enter_context(nc.sbuf_tensor(f"{name}_blk", [1, groups], I32))
    e.dram = nc.dram_tensor(f"{name}_sorted", (P * groups, 4), F32).ap()
    return e


def sort_edges(nc, kit, e, rows, src, dst, etype=None, weight=None, first=0):
    C = dst.shape[0] // rows
    S = 8
    groups = e.groups
    view = lambda a: a.rearrange("(p c) -> p c", p=rows)
    nm = e.name
    with ExitStack() as c:
        def sb(name, shape, dt=F32):
            return c.enter_context(nc.sbuf_tensor(f"{nm}_{name}", shape, dt))
        dst_i, src_i, type_i, work_i = (sb(x, [rows, C], I32) for x in ("dsti", "srci", "typei", "worki"))
        hi, eq, inc, pos, ones_row, wt = (sb(x, [rows, C]) for x in ("hi", "eq", "inc", "pos", "ones_row", "wt"))
        rec = sb("in_rec", [rows, C, 4])
        adr = sb("adr", [rows, C], I32)
        col = sb("col", [rows, C], I32)
        tot, before = sb("tot", [rows, NT]), sb("before", [rows, NT])
        n_grp, end = sb("n_grp", [P, NT]), sb("end", [P, NT])
        n_int = sb("n_int", [P, NT], I32)
        tile, shifted = e.tile, sb("shifted", [P, groups])
        empty = sb("empty", [P, groups, 4])
        st_rec = [sb(f"st_rec{u}", [rows, 4]) for u in range(S)]
        st_adr = [sb(f"st_adr{u}", [rows, 1], I32) for u in range(S)]
        ps = c.enter_context(nc.psum_tensor(f"{nm}_ps", [P, 512], F32))
        loaded, cleared, emptied, step, counted, summed, addressed, staged = sems(
            nc, c, nm, "loaded cleared emptied step counted summed addressed staged")
        sent = gather_sems(nc, nm, "sent", S)
        back, = sems(nc, c, nm, "back")
        n_loads = 2 + (etype is not None) + (weight is not None)
        with nc.Block() as block:
            @block.sync
            def _(sp):
                sp.dma_start(dst_i[:], view(dst)).then_inc(loaded, 16)
                sp.dma_start(src_i[:], view(src)).then_inc(loaded, 16)
                if etype is not None:
                    sp.dma_start(type_i[:], view(etype)).then_inc(loaded, 16)
                if weight is not None:
                    sp.dma_start(wt[:], view(weight)).then_inc(loaded, 16)
                sp.wait_ge(cleared, 4)
                sp.dma_start(e.dram.rearrange("(p g) w -> p (g w)", p=P),
                             empty[:].rearrange("p g w -> p (g w)")).then_inc(emptied, 16)
                for u in range(S):
                    sp.wait_ge(sent[u], 16 * (C // S))
                sp.dma_start(e.rec[:, 0:groups, :],
                             e.dram.rearrange("(p g) w -> p g w", p=P)).then_inc(back, 16)

            @block.vector
            def _(dve):
                nc.vector.memset(empty[:], 0.0).then_inc(cleared, 1)
                dve.wait_ge(cleared, 1)
                nc.vector.memset(empty[:, :, 1:2], 999.0).then_inc(cleared, 1)
                nc.vector.memset(e.rec[:, groups:, :], 0.0).then_inc(cleared, 1)
                nc.vector.memset(tile[:], 0.0).then_inc(cleared, 1)
                dve.wait_ge(cleared, 4)
                dve.wait_ge(loaded, 16 * n_loads)
                link = link_on(dve, step)
                link(nc.vector.tensor_scalar(work_i[:], dst_i[:], 7, None, ALU.arith_shift_right))
                link(nc.vector.tensor_copy(hi[:], work_i[:]))
                link(nc.vector.tensor_scalar(col[:], dst_i[:], 127, None, ALU.bitwise_and))
                link(nc.vector.tensor_copy(rec[:, :, 1], col[:]))
                link(nc.vector.tensor_copy(rec[:, :, 0], src_i[:]))
                if weight is not None:
                    link(nc.vector.tensor_copy(rec[:, :, 2], wt[:]))
                else:
                    link(nc.vector.memset(rec[:, :, 2], 1.0))
                if etype is not None:
                    link(nc.vector.scalar_tensor_tensor(out=rec[:, :, 3], in0=type_i[:], scalar=float(NP),
                                                        in1=src_i[:], op0=ALU.mult, op1=ALU.add))
                else:
                    link(nc.vector.tensor_copy(rec[:, :, 3], src_i[:]))
                link(nc.vector.memset(pos[:], float(first * P - 1)))
                with dve.Fori(0, NT) as b:
                    link.begin(b, 2)
                    link(nc.vector.tensor_scalar(eq[:], hi[:], kit.iota[0:rows, ds(b, 1)], None, ALU.is_equal))
                    link(nc.vector.tensor_reduce(tot[:, ds(b, 1)], eq[:], AX_X, ALU.add))
                link.end(NT)
                nc.vector.memset(ones_row[:], 1.0).then_inc(counted, 1)
                dve.wait_ge(counted, 1)
                dve.wait_ge(summed, 1)
                link(nc.vector.tensor_scalar(n_int[:], ps[:, 64:64 + NT], 127.0, None, ALU.add))
                link(nc.vector.tensor_scalar(n_int[:], n_int[:], 7, None, ALU.arith_shift_right))
                link(nc.vector.tensor_copy(n_grp[:], n_int[:]))
                link(nc.vector.tensor_tensor_scan(end[:], kit.ones[:, 0:NT], n_grp[:], 0.0, ALU.mult, ALU.add))
                link(nc.vector.tensor_tensor(n_grp[:], end[:], n_grp[:], ALU.subtract))
                link(nc.vector.scalar_tensor_tensor(out=before[:], in0=n_grp[0:rows, :], scalar=128.0,
                                                    in1=ps[0:rows, 0:NT], op0=ALU.mult, op1=ALU.add))
                with dve.Fori(0, NT) as b:
                    link.begin(b, 4)
                    link(nc.vector.tensor_scalar(eq[:], hi[:], kit.iota[0:rows, ds(b, 1)], None, ALU.is_equal))
                    link(nc.vector.tensor_tensor_scan(inc[:], ones_row[:], eq[:], 0.0, ALU.mult, ALU.add))
                    link(nc.vector.scalar_tensor_tensor(out=wt[:], in0=inc[:], scalar=before[:, ds(b, 1)],
                                                        in1=eq[:], op0=ALU.add, op1=ALU.mult))
                    link(nc.vector.tensor_tensor(pos[:], pos[:], wt[:], ALU.add))
                link.end(NT)
                link(nc.vector.tensor_copy(work_i[:], pos[:]))
                link(nc.vector.tensor_scalar(col[:], work_i[:], 127, None, ALU.bitwise_and))
                link(nc.vector.tensor_scalar(work_i[:], work_i[:], 7, None, ALU.arith_shift_right))
                link(nc.vector.scalar_tensor_tensor(out=adr[:], in0=col[:], scalar=float(groups), in1=work_i[:],
                                                    op0=ALU.mult, op1=ALU.add))
                with dve.Fori(0, NT) as b:
                    link.begin(b, 1)
                    link(nc.vector.scalar_tensor_tensor(out=tile[:], in0=kit.iota_t[:, 0:groups],
                                                        scalar=end[:, ds(b, 1)], in1=tile[:],
                                                        op0=ALU.is_ge, op1=ALU.add))
                link.end(NT)
                if first:
                    link(nc.vector.tensor_copy(shifted[:, first:groups], tile[:, 0:groups - first]))
                    link(nc.vector.tensor_copy(tile[:, first:groups], shifted[:, first:groups]))
                    link(nc.vector.tensor_copy(tile[:, 0:first], kit.iota_t[:, 0:first]))
                link(nc.vector.tensor_scalar(tile[:], tile[:], float(NT - 1), None, ALU.min))
                link(nc.vector.tensor_copy(e.blk[:], tile[0:1, :]))
                dve.wait_ge(emptied, 16)
                for i, u in [(0, u) for u in range(S)]:
                    nc.vector.tensor_copy(st_rec[u][:], rec[:, u, :])
                    nc.vector.tensor_copy(st_adr[u][:], adr[:, u:u + 1]).then_inc(staged, 1)
                with dve.Fori(1, C // S) as i:
                    for u in range(S):
                        dve.wait_ge(sent[u], i * 16)
                        nc.vector.tensor_copy(st_rec[u][:], rec[:, ds(i * S + u, 1), :].rearrange("p o w -> p (o w)"))
                        nc.vector.tensor_copy(st_adr[u][:], adr[:, ds(i * S + u, 1)]).then_inc(staged, 1)
                dve.wait_ge(back, 16)
                if first:
                    link(nc.vector.tensor_copy(e.rec[:, 0:first, 0], kit.node[:]))
                    link(nc.vector.tensor_copy(e.rec[:, 0:first, 3], kit.node[:]))
                    link(nc.vector.tensor_copy(e.rec[:, 0:first, 1], kit.node[:, 0:1].broadcast_to([P, first])))
                nc.vector.tensor_copy(e.src[:], e.rec[:, :, 0]).then_inc(addressed, 1)
                nc.vector.tensor_copy(e.key[:], e.rec[:, :, 3]).then_inc(addressed, 1)
                dve.wait_ge(addressed, 2)

            @block.tensor
            def _(pe):
                pe.wait_ge(counted, 1)
                nc.tensor.matmul(ps[0:rows, 0:NT], kit.tri[0:rows, 0:rows], tot[:], start=True, stop=True)
                nc.tensor.matmul(ps[:, 64:64 + NT], kit.ones[0:rows, :], tot[:], start=True, stop=True)\
                    .then_inc(summed, 1)

            @block.gpsimd
            def _(pool):
                with pool.Fori(0, C // S) as i:
                    for u in range(S):
                        wait_alone(pool, staged, i * S + u + 1)
                        nc.gpsimd.indirect_dma_start(e.dram, bass.IndirectOffsetOnAxis(ap=st_adr[u][:, :1], axis=0),
                                                     st_rec[u][:], None).then_inc(sent[u], 16)


def layer_norm(nc, kit, nm, x, xn, xt=None):
    with ExitStack() as c:
        st = [c.enter_context(nc.sbuf_tensor(f"{nm}_st{u}", [P, D], F32)) for u in range(U)]
        stats = c.enter_context(nc.sbuf_tensor(f"{nm}_stats", [P, NT, 6], F32))
        mean, var, tmp, std, rstd, shift = (c.enter_context(nc.sbuf_tensor(f"{nm}_{x_}", [P, NT], F32))
                                            for x_ in ("mean", "var", "tmp", "std", "rstd", "shift"))
        ps = [c.enter_context(nc.psum_tensor(f"{nm}_ps{u}", [P, 512], F32)) for u in range(U)]
        measured, step, rooted, normed, turned, kept = sems(nc, c, nm, "measured step rooted normed turned kept")
        with nc.Block() as block:
            @block.vector
            def _(dve):
                with dve.Fori(0, NT) as t:
                    nc.vector.bn_stats(stats[:, ds(t, 1), :].rearrange("p o s -> p (o s)"),
                                       nat(x)[:, ds(t, 1), :].rearrange("p o d -> p (o d)")).then_inc(measured, 1)
                dve.wait_ge(measured, NT)
                link = link_on(dve, step)
                link(nc.vector.tensor_tensor(mean[:], stats[:, :, 1], stats[:, :, 4], ALU.add))
                link(nc.vector.tensor_scalar(mean[:], mean[:], 0.5, None, ALU.mult))
                link(nc.vector.tensor_tensor(tmp[:], stats[:, :, 1], stats[:, :, 4], ALU.subtract))
                link(nc.vector.tensor_tensor(tmp[:], tmp[:], tmp[:], ALU.mult))
                link(nc.vector.tensor_tensor(var[:], stats[:, :, 2], stats[:, :, 5], ALU.add))
                link(nc.vector.tensor_scalar(var[:], var[:], 1.0 / D, EPS, ALU.mult, ALU.add))
                link(nc.vector.scalar_tensor_tensor(out=var[:], in0=tmp[:], scalar=0.25, in1=var[:],
                                                    op0=ALU.mult, op1=ALU.add))
                dve.wait_ge(rooted, 1)
                link(nc.vector.reciprocal(rstd[:], std[:]))
                link(nc.vector.scalar_tensor_tensor(out=shift[:], in0=mean[:], scalar=-1.0, in1=rstd[:],
                                                    op0=ALU.mult, op1=ALU.mult))
                with dve.Fori(0, ROUNDS) as i:
                    for u in range(U):
                        t = i * U + u
                        dve.wait_ge(kept, i * U + u + 1)
                        nc.vector.tensor_scalar(st[u][:], nat(x)[:, ds(t, 1), :].rearrange("p o d -> p (o d)"),
                                                rstd[:, ds(t, 1)], shift[:, ds(t, 1)],
                                                ALU.mult, ALU.add).then_inc(normed, 1)

            @block.scalar
            def _(act):
                act.wait_ge(step, 7)
                nc.scalar.activation(std[:], var[:], ACT.Sqrt).then_inc(rooted, 1)
                act.sem_inc(kept, U)
                with act.Fori(0, ROUNDS) as i:
                    for u in range(U):
                        t = i * U + u
                        act.wait_ge(turned, i * U + u + 1)
                        kept_xn = nc.scalar.copy(nat(xn)[:, ds(t, 1), :].rearrange("p o d -> p (o d)"), st[u][:])
                        if xt is None:
                            kept_xn.then_inc(kept, 1)
                            continue
                        nc.scalar.copy(tr(xt)[:, :, ds(t * P, P)],
                                       ps[u][:, 0:D].rearrange("p (k n) -> p k n", k=2)).then_inc(kept, 1)

            @block.tensor
            def _(pe):
                with pe.Fori(0, ROUNDS) as i:
                    for u in range(U):
                        pe.wait_ge(normed, i * U + u + 1)
                        if xt is None:
                            pe.nop(nofuse=True).then_inc(turned, 1)
                            continue
                        nc.tensor.transpose(ps[u][:, 0:P], st[u][:, 0:P], kit.ident[:])
                        nc.tensor.transpose(ps[u][:, P:D], st[u][:, P:D], kit.ident[:]).then_inc(turned, 1)


def project_t(nc, nm, sources, dst, fc, func=ACT.Identity, bias=None):
    terms = [(src, kc, w, k) for src, kc, w in sources for k in range(kc)]
    with ExitStack() as c:
        ps = [[c.enter_context(nc.psum_tensor(f"{nm}_ps{h}{f}", [P, 512], F32)) for f in range(fc)] for h in range(2)]
        multiplied, read = sems(nc, c, nm, "multiplied read")
        with nc.Block() as block:
            @block.tensor
            def _(pe):
                with pe.Fori(0, NP // CHUNK // 2) as i:
                    for h in range(2):
                        for f in range(fc):
                            pe.wait_ge(read, (i * 2 + h) * fc + f + 1)
                            for n, (src, kc, w, k) in enumerate(terms):
                                mm = nc.tensor.matmul(ps[h][f][:, 0:CHUNK], w[:, k, f * P:(f + 1) * P],
                                                      tr(src, kc)[:, k, ds((i * 2 + h) * CHUNK, CHUNK)],
                                                      start=(n == 0), stop=(n == len(terms) - 1))
                            mm.then_inc(multiplied, 1)

            @block.scalar
            def _(act):
                act.sem_inc(read, 2 * fc)
                with act.Fori(0, NP // CHUNK // 2) as i:
                    for h in range(2):
                        for f in range(fc):
                            act.wait_ge(multiplied, (i * 2 + h) * fc + f + 1)
                            nc.scalar.activation(tr(dst, fc)[:, f, ds((i * 2 + h) * CHUNK, CHUNK)],
                                                 ps[h][f][:, 0:CHUNK], func,
                                                 bias=(bias[:, f:f + 1] if bias is not None else 0.0)).then_inc(read, 1)


def write_table(nc, kit, nm, src, kc, scratch, table):
    W = kc * P
    rows = scratch[:, 0:NT * W].rearrange("p (t d) -> p t d", t=NT)
    with ExitStack() as c:
        st = [c.enter_context(nc.sbuf_tensor(f"{nm}_st{u}", [P, kc, P], F32)) for u in range(U)]
        ps = [c.enter_context(nc.psum_tensor(f"{nm}_ps{u}", [P, 512], F32)) for u in range(U)]
        staged, turned, copied, stored = sems(nc, c, nm, "staged turned copied stored")
        with nc.Block() as block:
            @block.vector
            def _(dve):
                with dve.Fori(0, ROUNDS) as i:
                    for u in range(U):
                        dve.wait_ge(turned, i * U + u + 1)
                        nc.vector.tensor_copy(st[u][:], tr(src, kc)[:, :, ds((i * U + u) * P, P)]).then_inc(staged, 1)

            @block.tensor
            def _(pe):
                pe.sem_inc(turned, U)
                with pe.Fori(0, ROUNDS) as i:
                    for u in range(U):
                        pe.wait_ge(staged, i * U + u + 1)
                        pe.wait_ge(copied, i * U + u + 1)
                        for k in range(kc):
                            mm = nc.tensor.transpose(ps[u][:, k * P:(k + 1) * P], st[u][:, k, :], kit.ident[:])
                        mm.then_inc(turned, 1)

            @block.scalar
            def _(act):
                act.sem_inc(copied, U)
                with act.Fori(0, ROUNDS) as i:
                    for u in range(U):
                        act.wait_ge(turned, i * U + u + 1 + U)
                        nc.scalar.copy(rows[:, ds(i * U + u, 1), :].rearrange("p o d -> p (o d)"),
                                       ps[u][:, 0:W]).then_inc(copied, 1)

            @block.sync
            def _(sp):
                with sp.Fori(0, ROUNDS) as i:
                    sp.wait_ge(copied, i * U + 2 * U)
                    sp.dma_start(table.rearrange("(t p) d -> p t d", p=P)[:, ds(i * U, U), :],
                                 rows[:, ds(i * U, U), :]).then_inc(stored, 16)
                sp.wait_ge(stored, 16 * ROUNDS)


def aggregate_t(nc, kit, nm, e, table, kc, acc, weighted=False):
    W = kc * P
    with ExitStack() as c:
        idx = [c.enter_context(nc.sbuf_tensor(f"{nm}_idx{u}", [P, 1], I32)) for u in range(G)]
        rows = [c.enter_context(nc.sbuf_tensor(f"{nm}_rows{u}", [P, W], F32)) for u in range(G)]
        hot = [c.enter_context(nc.sbuf_tensor(f"{nm}_hot{u}", [P, P], F32)) for u in range(G)]
        ps = [c.enter_context(nc.psum_tensor(f"{nm}_ps{u}", [P, 512], F32)) for u in range(G)]
        indexed, matched, multiplied, added = sems(nc, c, nm, "indexed matched multiplied added")
        gathered = gather_sems(nc, nm, "gathered", G)
        rounds = e.groups // G
        with nc.Block() as block:
            @block.scalar
            def _(act):
                with act.Fori(0, rounds) as i:
                    for u in range(G):
                        act.wait_ge(multiplied, i * G + u + 1)
                        nc.scalar.copy(idx[u][:], e.src[:, ds(i * G + u, 1)]).then_inc(indexed, 1)

            @block.gpsimd
            def _(pool):
                with pool.Fori(0, rounds) as i:
                    for u in range(G):
                        wait_alone(pool, indexed, i * G + u + 1)
                        nc.gpsimd.indirect_dma_start(rows[u][:], None, table,
                                                     bass.IndirectOffsetOnAxis(ap=idx[u][:, :1], axis=0)
                                                     ).then_inc(gathered[u], 16)

            @block.tensor
            def _(pe):
                pe.sem_inc(multiplied, G)
                with pe.Fori(0, rounds) as i:
                    for u in range(G):
                        pe.wait_ge(gathered[u], i * 16 + 16)
                        pe.wait_ge(matched, i * G + u + 1)
                        pe.wait_ge(added, i * G + u + 1)
                        for k in range(kc):
                            mm = nc.tensor.matmul(ps[u][:, k * P:(k + 1) * P], rows[u][:, k * P:(k + 1) * P],
                                                  hot[u][:], start=True, stop=True)
                        mm.then_inc(multiplied, 1)

            @block.vector
            def _(dve):
                def match(t, u):
                    nc.vector.tensor_scalar(hot[u][:], kit.iota[:], e.rec[:, ds(t, 1), 1:2].rearrange("p o w -> p (o w)"),
                                            e.rec[:, ds(t, 1), 2:3].rearrange("p o w -> p (o w)") if weighted else None,
                                            ALU.is_equal, *([ALU.mult] if weighted else [])).then_inc(matched, 1)
                for u in range(G):
                    match(u, u)
                nc.vector.memset(acc[:, 0:kc * NP], 0.0).then_inc(added, G)
                with dve.Fori(0, rounds) as i:
                    for u in range(G):
                        t = i * G + u
                        blk = dve.value_load(e.blk[0:1, ds(t, 1)], min_val=0, max_val=NT - 1)
                        dve.wait_ge(multiplied, i * G + u + 1 + G)
                        dve.wait_ge(added, i * G + u + G)
                        to = tr(acc, kc)[:, :, ds(blk * P, P)]
                        nc.vector.tensor_tensor(to, to, ps[u][:, 0:W].rearrange("p (k n) -> p k n", k=kc),
                                                ALU.add).then_inc(added, 1)
                        match(t + G, u)


def turn(nc, kit, nm, src, dst):
    with ExitStack() as c:
        st = [c.enter_context(nc.sbuf_tensor(f"{nm}_st{u}", [P, D], F32)) for u in range(U)]
        ps = [c.enter_context(nc.psum_tensor(f"{nm}_ps{u}", [P, 512], F32)) for u in range(U)]
        staged, turned, copied = sems(nc, c, nm, "staged turned copied")
        with nc.Block() as block:
            @block.vector
            def _(dve):
                with dve.Fori(0, ROUNDS) as i:
                    for u in range(U):
                        dve.wait_ge(turned, i * U + u + 1)
                        nc.vector.tensor_copy(st[u][:], src[:, ds(i * U + u, 1), :].rearrange("p o d -> p (o d)")
                                              ).then_inc(staged, 1)

            @block.tensor
            def _(pe):
                pe.sem_inc(turned, U)
                with pe.Fori(0, ROUNDS) as i:
                    for u in range(U):
                        pe.wait_ge(staged, i * U + u + 1)
                        pe.wait_ge(copied, i * U + u + 1)
                        nc.tensor.transpose(ps[u][:, 0:P], st[u][:, 0:P], kit.ident[:])
                        nc.tensor.transpose(ps[u][:, P:D], st[u][:, P:D], kit.ident[:]).then_inc(turned, 1)

            @block.scalar
            def _(act):
                act.sem_inc(copied, U)
                with act.Fori(0, ROUNDS) as i:
                    for u in range(U):
                        wait_alone(act, turned, i * U + u + 1 + U)
                        nc.scalar.copy(dst[:, :, ds((i * U + u) * P, P)],
                                       ps[u][:, 0:D].rearrange("p (k n) -> p k n", k=2)).then_inc(copied, 1)


def add_projection(nc, nm, src, w, to, bias=None, fresh=False, gate=None):
    kc, width = w.shape[1], w.shape[2]
    with ExitStack() as c:
        st = [c.enter_context(nc.sbuf_tensor(f"{nm}_st{u}", [P, kc, P], F32)) for u in range(U)]
        ps = [c.enter_context(nc.psum_tensor(f"{nm}_ps{u}", [P, 512], F32)) for u in range(U)]
        staged, multiplied, added, biased = sems(nc, c, nm, "staged multiplied added biased")
        with nc.Block() as block:
            @block.scalar
            def _(act):
                with act.Fori(0, ROUNDS) as i:
                    for u in range(U):
                        act.wait_ge(multiplied, i * U + u + 1)
                        nc.scalar.copy(st[u][:], tr(src, kc)[:, :, ds((i * U + u) * P, P)]).then_inc(staged, 1)

            @block.tensor
            def _(pe):
                pe.sem_inc(multiplied, U)
                with pe.Fori(0, ROUNDS) as i:
                    for u in range(U):
                        pe.wait_ge(staged, i * U + u + 1)
                        pe.wait_ge(added, i * U + u + 1)
                        for k in range(kc):
                            mm = nc.tensor.matmul(ps[u][:, 0:width], st[u][:, k, :], w[:, k, :],
                                                  start=(k == 0), stop=(k == kc - 1))
                        mm.then_inc(multiplied, 1)

            @block.vector
            def _(dve):
                if fresh and bias is None:
                    nc.vector.memset(to, 0.0).then_inc(biased, 1)
                elif fresh:
                    nc.vector.tensor_copy(to, bias[:, None, :].broadcast_to([P, NT, width])).then_inc(biased, 1)
                elif bias is not None:
                    nc.vector.tensor_tensor(to, to, bias[:, None, :].broadcast_to([P, NT, width]),
                                            ALU.add).then_inc(biased, 1)
                if fresh or bias is not None:
                    dve.wait_ge(biased, 1)
                dve.sem_inc(added, U)
                with dve.Fori(0, ROUNDS) as i:
                    for u in range(U):
                        dve.wait_ge(multiplied, i * U + u + 1 + U)
                        part = to[:, ds(i * U + u, 1), :].rearrange("p o d -> p (o d)")
                        if gate is None:
                            nc.vector.tensor_tensor(part, part, ps[u][:, 0:width], ALU.add).then_inc(added, 1)
                        else:
                            nc.vector.scalar_tensor_tensor(out=part, in0=ps[u][:, 0:width],
                                                           scalar=gate[:, ds(i * U + u, 1)], in1=part,
                                                           op0=ALU.mult, op1=ALU.add).then_inc(added, 1)


def in_degrees(nc, kit, nm, dst, rows, deg):
    C = dst.shape[0] // rows
    B = 16
    with ExitStack() as c:
        def sb(name, shape, dt=F32):
            return c.enter_context(nc.sbuf_tensor(f"{nm}_{name}", shape, dt))
        dst_i, work_i = sb("dst", [rows, C], I32), sb("work", [rows, C], I32)
        lo, hi = sb("lo", [rows, C]), sb("hi", [rows, C])
        is_lo = [sb(f"is_lo{h}", [rows, B, P], BF16) for h in range(2)]
        is_hi = [sb(f"is_hi{h}", [rows, B, NT], BF16) for h in range(2)]
        ps = c.enter_context(nc.psum_tensor(f"{nm}_ps", [P, 512], F32))
        zero = sb("zero", [P, P])
        loaded, step, matched, used = sems(nc, c, nm, "loaded step matched used")
        rounds = C // B
        with nc.Block() as block:
            @block.sync
            def _(sp):
                sp.dma_start(dst_i[:], dst.rearrange("(p c) -> p c", p=rows)).then_inc(loaded, 16)

            @block.vector
            def _(dve):
                dve.wait_ge(loaded, 16)
                link = link_on(dve, step)
                link(nc.vector.memset(zero[:], 0.0))
                link(nc.vector.tensor_scalar(work_i[:], dst_i[:], 7, None, ALU.arith_shift_right))
                link(nc.vector.tensor_copy(hi[:], work_i[:]))
                link(nc.vector.tensor_scalar(work_i[:], dst_i[:], 127, None, ALU.bitwise_and))
                link(nc.vector.tensor_copy(lo[:], work_i[:]))

                def match(i, h):
                    for part, n, to in ((lo, P, is_lo[h]), (hi, NT, is_hi[h])):
                        ins = nc.vector.tensor_tensor(to[:], part[:, ds(i * B, B)][:, :, None].broadcast_to([rows, B, n]),
                                                      kit.iota[0:rows, None, 0:n].broadcast_to([rows, B, n]),
                                                      ALU.is_equal)
                    ins.then_inc(matched, 1)
                match(0, 0)
                with dve.Fori(0, (rounds - 1) // 2) as i:
                    for h in (1, 0):
                        j = i * 2 + (2 - h)
                        dve.wait_ge(used, j)
                        match(j, h)
                dve.wait_ge(used, rounds + 1)
                nc.vector.tensor_copy(deg[:], ps[:, 0:NT]).then_inc(step, 1)
                dve.wait_ge(step, 6)

            @block.tensor
            def _(pe):
                pe.sem_inc(used, 1)
                pe.wait_ge(step, 1)
                nc.tensor.matmul(ps[:, 0:NT], zero[:], zero[:, 0:NT], start=True, stop=False)

                def count(i, h, last=False):
                    pe.wait_ge(matched, i + 1)
                    for b in range(B):
                        mm = nc.tensor.matmul(ps[:, 0:NT], is_lo[h][:, b, :], is_hi[h][:, b, :], start=False,
                                              stop=(last and b == B - 1))
                    mm.then_inc(used, 1)
                with pe.Fori(0, (rounds - 1) // 2) as i:
                    for h in range(2):
                        count(i * 2 + h, h)
                count(rounds - 1, 0, last=True)
        assert rounds % 2 == 1


def rows_to_all(nc, kit, nm, col, out):
    with ExitStack() as c:
        diag = [c.enter_context(nc.sbuf_tensor(f"{nm}_diag{u}", [P, P], F32)) for u in range(U)]
        ps = [c.enter_context(nc.psum_tensor(f"{nm}_ps{u}", [P, 512], F32)) for u in range(U)]
        made, multiplied, copied = sems(nc, c, nm, "made multiplied copied")
        with nc.Block() as block:
            @block.vector
            def _(dve):
                with dve.Fori(0, ROUNDS) as i:
                    for u in range(U):
                        dve.wait_ge(multiplied, i * U + u + 1)
                        nc.vector.tensor_scalar(diag[u][:], kit.ident[:], col[:, ds(i * U + u, 1)], None,
                                                ALU.mult).then_inc(made, 1)

            @block.tensor
            def _(pe):
                pe.sem_inc(multiplied, U)
                with pe.Fori(0, ROUNDS) as i:
                    for u in range(U):
                        pe.wait_ge(made, i * U + u + 1)
                        pe.wait_ge(copied, i * U + u + 1)
                        nc.tensor.matmul(ps[u][:, 0:P], kit.ones[:], diag[u][:], start=True,
                                         stop=True).then_inc(multiplied, 1)

            @block.scalar
            def _(act):
                act.sem_inc(copied, U)
                with act.Fori(0, ROUNDS) as i:
                    for u in range(U):
                        act.wait_ge(multiplied, i * U + u + 1 + U)
                        nc.scalar.copy(out[:, ds((i * U + u) * P, P)], ps[u][:, 0:P]).then_inc(copied, 1)


def load(nc, nm, pairs):
    with ExitStack() as c:
        loaded, = sems(nc, c, nm, "loaded")
        with nc.Block() as block:
            @block.sync
            def _(sp):
                for to, src in pairs:
                    sp.dma_start(to, src).then_inc(loaded, 16)
                sp.wait_ge(loaded, 16 * len(pairs))


def on_vector(nc, nm, steps):
    with ExitStack() as c:
        step, = sems(nc, c, nm, "step")
        with nc.Block() as block:
            @block.vector
            def _(dve):
                steps(link_on(dve, step))


def chunks(ap):
    return ap.rearrange("(k p) n -> p k n", p=P)


def gcn_stage(nc, kit, A, x, bufs, e, table):
    b1, b2, b3, b4 = bufs
    with ExitStack() as c:
        def sb(name, shape, dt=F32):
            return c.enter_context(nc.sbuf_tensor(f"gcn_{name}", shape, dt))
        w1, w2 = sb("w1", [P, 2, P]), sb("w2", [P, 1, D])
        bias1, bias2 = sb("b1", [P, 1]), sb("b2", [P, D])
        deg, dinv, dall = kit.deg, sb("dinv", [P, NT]), sb("dall", [P, NP])
        load(nc, "gcn_load", [(w1[:], chunks(A["L0_gnn_W1"])), (w2[:], chunks(A["L0_gnn_W2"])),
                              (bias1[:], A["L0_gnn_b1"].rearrange("(p o) -> p o", o=1)),
                              (bias2[:], row_to_all(A["L0_gnn_b2"]))])
        layer_norm(nc, kit, "gcn_ln", x, b1, b2)
        in_degrees(nc, kit, "gcn_deg", A["dst"], 125, deg)
        with ExitStack() as cc:
            step, rooted = sems(nc, cc, "gcn_dinv", "step rooted")
            with nc.Block() as block:
                @block.vector
                def _(dve):
                    nc.vector.tensor_scalar(dinv[:], deg[:], 1.0, None, ALU.add).then_inc(step, 1)
                    dve.wait_ge(rooted, 1)
                    nc.vector.reciprocal(dinv[:], dinv[:]).then_inc(step, 1)
                    dve.wait_ge(step, 2)

                @block.scalar
                def _(act):
                    act.wait_ge(step, 1)
                    nc.scalar.activation(dinv[:], dinv[:], ACT.Sqrt).then_inc(rooted, 1)
        rows_to_all(nc, kit, "gcn_dall", dinv, dall)
        one, agg = b3[:, 0:NP], b4[:, 0:NP]
        project_t(nc, "gcn_h", [(b2, 2, w1)], b3, 1)
        on_vector(nc, "gcn_v1", lambda link: link(nc.vector.tensor_tensor(one, one, dall[:], ALU.mult)))
        write_table(nc, kit, "gcn_t1", b3, 1, b4, table)
        aggregate_t(nc, kit, "gcn_a1", e, table, 1, b4)

        def between(link):
            link(nc.vector.tensor_tensor(one, one, agg, ALU.add))
            link(nc.vector.tensor_tensor(one, one, dall[:], ALU.mult))
            link(nc.vector.tensor_scalar(one, one, bias1[:], 0.0, ALU.add, ALU.max))
            link(nc.vector.tensor_tensor(one, one, dall[:], ALU.mult))
        on_vector(nc, "gcn_v2", between)
        write_table(nc, kit, "gcn_t2", b3, 1, b4, table)
        aggregate_t(nc, kit, "gcn_a2", e, table, 1, b4)

        def after(link):
            link(nc.vector.tensor_tensor(one, one, agg, ALU.add))
            link(nc.vector.tensor_tensor(one, one, dall[:], ALU.mult))
        on_vector(nc, "gcn_v3", after)
        add_projection(nc, "gcn_out", b3, w2, nat(x), bias2)


def per_node(ap, n):
    return ap[:, :, None].broadcast_to([P, ap.shape[1], n])


def softmax_rows(nc, nm, z, n):
    tiles = z.shape[1]
    with ExitStack() as c:
        m, s = (c.enter_context(nc.sbuf_tensor(f"{nm}_{x}", [P, tiles], F32)) for x in "ms")
        step, raised = sems(nc, c, nm, "step raised")
        with nc.Block() as block:
            @block.vector
            def _(dve):
                link = link_on(dve, step)
                link(nc.vector.tensor_reduce(m[:], z, AX_X, ALU.max))
                link(nc.vector.tensor_tensor(z, z, per_node(m[:], n), ALU.subtract))
                dve.wait_ge(raised, 1)
                link(nc.vector.tensor_reduce(s[:], z, AX_X, ALU.add))
                link(nc.vector.reciprocal(s[:], s[:]))
                link(nc.vector.tensor_tensor(z, z, per_node(s[:], n), ALU.mult))

            @block.scalar
            def _(act):
                act.wait_ge(step, 2)
                nc.scalar.activation(z, z, ACT.Exp).then_inc(raised, 1)


def add_gated_bias(nc, kit, nm, gates, b, x):
    E = b.shape[0]
    with ExitStack() as c:
        gt = [c.enter_context(nc.sbuf_tensor(f"{nm}_gt{u}", [E, P], F32)) for u in range(U)]
        st = [c.enter_context(nc.sbuf_tensor(f"{nm}_st{u}", [P, E], F32)) for u in range(U)]
        ps = [c.enter_context(nc.psum_tensor(f"{nm}_ps{u}", [P, 512], F32)) for u in range(U)]
        staged, turned, copied, multiplied, added = sems(nc, c, nm, "staged turned copied multiplied added")
        with nc.Block() as block:
            @block.vector
            def _(dve):
                dve.sem_inc(added, U)
                with dve.Fori(0, ROUNDS) as i:
                    for u in range(U):
                        dve.wait_ge(multiplied, i * U + u + 1)
                        nc.vector.tensor_copy(st[u][:], gates[:, ds(i * U + u, 1), :].rearrange("p o e -> p (o e)")
                                              ).then_inc(staged, 1)
                    for u in range(U):
                        dve.wait_ge(multiplied, i * U + u + 1 + U)
                        part = nat(x)[:, ds(i * U + u, 1), :].rearrange("p o d -> p (o d)")
                        nc.vector.tensor_tensor(part, part, ps[u][:, 0:D], ALU.add).then_inc(added, 1)

            @block.tensor
            def _(pe):
                pe.sem_inc(multiplied, U)
                with pe.Fori(0, ROUNDS) as i:
                    for u in range(U):
                        pe.wait_ge(staged, i * U + u + 1)
                        pe.wait_ge(added, i * U + u + 1)
                        nc.tensor.transpose(ps[u][0:E, D:D + P], st[u][:], kit.ident[:]).then_inc(turned, 1)
                    for u in range(U):
                        pe.wait_ge(copied, i * U + u + 1)
                        nc.tensor.matmul(ps[u][:, 0:D], gt[u][:], b, start=True, stop=True).then_inc(multiplied, 1)

            @block.scalar
            def _(act):
                with act.Fori(0, ROUNDS) as i:
                    for u in range(U):
                        act.wait_ge(turned, i * U + u + 1)
                        nc.scalar.copy(gt[u][:], ps[u][0:E, D:D + P]).then_inc(copied, 1)


class Mid:

    def __init__(self, w, kc, fc, func, bias, scale=None):
        self.w, self.kc, self.fc, self.func, self.bias, self.scale = w, kc, fc, func, bias, scale


def expert_mlps(nc, nm, src, experts, mids, last, gates, x, pick=None):
    SPAN = U * P
    kl = mids[-1].fc
    groups = sum(2 * m.fc for m in mids)
    RING = 4
    assert groups % RING == 0
    with ExitStack() as c:
        wm = [[c.enter_context(nc.sbuf_tensor(f"{nm}_w{n}_{q}", [P, m.kc, m.fc * P], F32)) for n, m in enumerate(mids)]
              for q in range(2)]
        wl = [c.enter_context(nc.sbuf_tensor(f"{nm}_wl_{q}", [P, kl, D], F32)) for q in range(2)]
        h = [c.enter_context(nc.sbuf_tensor(f"{nm}_h{n}", [P, m.fc, SPAN], F32)) for n, m in enumerate(mids)]
        ps = [c.enter_context(nc.psum_tensor(f"{nm}_ps{r}", [P, 512], F32)) for r in range(RING)]
        py = [c.enter_context(nc.psum_tensor(f"{nm}_py{r}", [P, 512], F32)) for r in range(4)]
        out_ps = [py[u % 4][:, 0:D] for u in range(U)]
        loaded = sems(nc, c, nm, "loaded0 loaded1")
        multiplied, read, finished, added, left = sems(nc, c, nm, "multiplied read finished added left")

        def experts_loop(eng, body):
            if experts == 2:
                for q in range(2):
                    body(0, q)
            else:
                with eng.Fori(0, experts // 2) as i:
                    for q in range(2):
                        body(i, q)

        with nc.Block() as block:
            @block.sync
            def _(sp):
                def body(i, q):
                    e = i * 2 + q
                    at = pick(sp, e) if pick else e
                    sp.wait_ge(left, e + 1)
                    for n, m in enumerate(mids):
                        sp.dma_start(wm[q][n][:], m.w(at).rearrange("o (k p) f -> p (o k) f", p=P)).then_inc(loaded[q], 16)
                    sp.dma_start(wl[q][:], last(at).rearrange("o (k p) f -> p (o k) f", p=P)).then_inc(loaded[q], 16)
                experts_loop(sp, body)

            @block.tensor
            def _(pe):
                pe.sem_inc(left, 2)

                def body(i, q):
                    wait_alone(pe, loaded[q], (i + 1) * 16 * (len(mids) + 1))
                    with pe.Fori(0, ROUNDS) as j:
                        r = (i * 2 + q) * ROUNDS + j
                        g = 0
                        for n, m in enumerate(mids):
                            for half in range(2):
                                if n:
                                    pe.wait_ge(read, r * groups + RING + g0 + (half + 1) * mids[n - 1].fc)
                                for f in range(m.fc):
                                    pe.wait_ge(read, r * groups + g + 1)
                                    for k in range(m.kc):
                                        rhs = (tr(src)[:, k, ds((j * 2 + half) * CHUNK, CHUNK)] if n == 0
                                               else h[n - 1][:, k, half * CHUNK:(half + 1) * CHUNK])
                                        mm = nc.tensor.matmul(ps[g % RING][:, 0:CHUNK],
                                                              wm[q][n][:, k, f * P:(f + 1) * P], rhs,
                                                              start=(k == 0), stop=(k == m.kc - 1))
                                    mm.then_inc(multiplied, 1)
                                    g += 1
                            g0 = g - 2 * m.fc
                        for u in range(U):
                            half = 0 if (u + 1) * P <= CHUNK else 1
                            pe.wait_ge(read, r * groups + RING + g0 + (half + 1) * kl)
                            pe.wait_ge(added, r * U + (U if u == 0 else U + 1 if u == 4 else u + 1))
                            for k in range(kl):
                                mm = nc.tensor.matmul(out_ps[u], h[-1][:, k, u * P:(u + 1) * P], wl[q][:, k, :],
                                                      start=(k == 0), stop=(k == kl - 1))
                            mm.then_inc(finished, 1)
                    pe.drain().then_inc(left, 1)
                experts_loop(pe, body)

            @block.scalar
            def _(act):
                act.sem_inc(read, RING)

                def body(i, q):
                    with act.Fori(0, ROUNDS) as j:
                        r = (i * 2 + q) * ROUNDS + j
                        g = 0
                        for n, m in enumerate(mids):
                            for half in range(2):
                                for f in range(m.fc):
                                    wait_alone(act, multiplied, r * groups + g + 1)
                                    e = i * 2 + q
                                    bias = m.bias[:, ds(e, 1), f:f + 1].rearrange("p o f -> p (o f)")
                                    scale = (m.scale[:, ds(e, 1), f:f + 1].rearrange("p o f -> p (o f)")
                                             if m.scale is not None else 1.0)
                                    nc.scalar.activation(h[n][:, f, half * CHUNK:(half + 1) * CHUNK],
                                                         ps[g % RING][:, 0:CHUNK], m.func, bias=bias,
                                                         scale=scale).then_inc(read, 1)
                                    g += 1
                experts_loop(act, body)

            @block.vector
            def _(dve):
                dve.sem_inc(added, U)

                def body(i, q):
                    with dve.Fori(0, ROUNDS) as j:
                        r = (i * 2 + q) * ROUNDS + j
                        e = i * 2 + q
                        for u in range(U):
                            t = j * U + u
                            dve.wait_ge(finished, r * U + u + 1)
                            dve.wait_ge(added, r * U + u + 1)
                            part = nat(x)[:, ds(t, 1), :].rearrange("p o d -> p (o d)")
                            gate = gates[:, ds(t, 1), ds(e, 1)].rearrange("p o e -> p (o e)")
                            nc.vector.scalar_tensor_tensor(out=part, in0=out_ps[u], scalar=gate, in1=part,
                                                           op0=ALU.mult, op1=ALU.add).then_inc(added, 1)
                experts_loop(dve, body)


def expert_columns(ap2d, fc):
    return ap2d.rearrange("e (f p) -> p e f", f=fc)


def soft_moe_stage(nc, kit, A, x, bufs):
    b1, b2, b3, b4 = bufs
    E, F = A["L1_ffn_b1"].shape
    fc = F // P
    BN_EPS = 0.001
    with ExitStack() as c:
        def sb(name, shape, dt=F32):
            return c.enter_context(nc.sbuf_tensor(f"soft_{name}", shape, dt))
        wr, br, bo = sb("wr", [P, 2, E]), sb("br", [P, E]), sb("bo", [E, D])
        gates = sb("gates", [P, NT, E])
        par = {n: sb(n, [P, E, fc]) for n in "b1 g1 be1 m1 v1 b2 g2 be2 m2 v2".split()}
        layer_norm(nc, kit, "soft_ln", x, b1, b2)
        with nc.allow_non_contiguous_dma(reason="short columns"):
            load(nc, "soft_load",
                 [(wr[:], chunks(A["L1_ffn_Wr"])), (br[:], row_to_all(A["L1_ffn_br"])), (bo[:], A["L1_ffn_bo"])]
                 + [(t[:, e, :], column(A[f"L1_ffn_{n}"][e], fc)) for n, t in par.items() for e in range(E)])
        with ExitStack() as cc:
            step, rooted = sems(nc, cc, "soft_bn", "step rooted")
            with nc.Block() as block:
                @block.vector
                def _(dve):
                    link = link_on(dve, step)
                    for n in "12":
                        v = par["v" + n]
                        link(nc.vector.tensor_scalar(v[:], v[:], BN_EPS, None, ALU.add))
                    dve.wait_ge(rooted, 2)
                    for n in "12":
                        v, g, b, m, be = (par[k + n] for k in ("v", "g", "b", "m", "be"))
                        link(nc.vector.reciprocal(v[:], v[:]))
                        link(nc.vector.tensor_tensor(v[:], v[:], g[:], ALU.mult))
                        link(nc.vector.tensor_tensor(b[:], b[:], m[:], ALU.subtract))
                        link(nc.vector.tensor_tensor(b[:], b[:], v[:], ALU.mult))
                        link(nc.vector.tensor_tensor(b[:], b[:], be[:], ALU.add))

                @block.scalar
                def _(act):
                    for k, n in enumerate("12"):
                        act.wait_ge(step, k + 1)
                        nc.scalar.activation(par["v" + n][:], par["v" + n][:], ACT.Sqrt).then_inc(rooted, 1)
        add_projection(nc, "soft_gate", b2, wr, gates[:], br, fresh=True)
        softmax_rows(nc, "soft_sm", gates[:], E)
        add_gated_bias(nc, kit, "soft_bo", gates, bo[:], x)
        of = lambda name: lambda e: A[name][ds(e, 1), :, :]
        expert_mlps(nc, "soft", b2, E, [Mid(of("L1_ffn_W1"), 2, fc, ACT.Relu, par["b1"], par["v1"]),
                                        Mid(of("L1_ffn_W2"), fc, fc, ACT.Relu, par["b2"], par["v2"])],
                    of("L1_ffn_Wo"), gates, x)


BIG = 1e30
R = 4
DEEP = 4


class EdgeAttention:

    def __init__(self, edges, index, keys, values, q, heads, dv, dots, spare, score_at=0, held=None):
        self.edges, self.index, self.keys, self.values, self.q = edges, index, keys, values, q
        self.heads, self.dv, self.dots, self.score_at, self.held = heads, dv, dots, score_at, held
        self.spare = spare

    def rows(self, width):
        return [self.spare[:, a * R * width:(a + 1) * R * width].rearrange("p (r w) -> p r w", r=R)
                for a in range(DEEP)]


class Round:

    def __init__(self, j, c, rounds, looped):
        self.j, self.c, self.rounds, self.looped = j, c, rounds, looped
        self.n, self.slot, self.turn = j * DEEP + c, c % DEEP, j + c // DEEP
        self.there = looped or 0 <= c < rounds

    def off(self, o):
        return Round(self.j, self.c + o, self.rounds, self.looped)


def rolling(eng, step, rounds):
    for c in range(-2, 3):
        step(Round(0, c, rounds, False))
    with eng.Fori(0, rounds // DEEP - 2) as j:
        for k in range(DEEP):
            step(Round(j, 3 + k, rounds, True))
    for c in range(rounds - 5, rounds + 3):
        step(Round(0, c, rounds, False))


def edge_scores(nc, kit, nm, at, scores, top):
    e, H, dv = at.edges, at.heads, at.dv
    WQ, WK = at.q.shape[2], at.keys.shape[1]
    rounds = e.groups // R
    assert rounds % DEEP == 0
    with ExitStack() as c:
        def many(count, name, shape, dt=F32):
            return [c.enter_context(nc.sbuf_tensor(f"{nm}_{name}{a}", shape, dt)) for a in range(count)]
        idx, rows = many(DEEP, "idx", [P, R], I32), at.rows(WK)
        hot, hot_t = many(DEEP, "hot", [P, R, P]), many(2, "hot_t", [P, R, P])
        off, sc = many(DEEP, "off", [P, R, P], BF16), many(DEEP, "sc", [P, R, H])
        qs, tmp = many(2, "qs", [P, R, WQ]), many(2, "tmp", [P, R, WQ])
        big, = many(1, "big", [P, H, P], BF16)
        row_max, = many(1, "row_max", [P, R, H])
        is_tile, = many(1, "is_tile", [P, R, NT])
        by_tile, = many(1, "by_tile", [P, NT, H, R])
        round_max, = many(1, "round_max", [P, NT, H])
        pt = [c.enter_context(nc.psum_tensor(f"{nm}_pt{a}", [P, 512], F32)) for a in range(2)]
        pq = c.enter_context(nc.psum_tensor(f"{nm}_pq", [P, max(512, R * WQ)], F32))
        pm = [c.enter_context(nc.psum_tensor(f"{nm}_pm{u}", [P, 512], F32)) for u in range(R)]
        pq_v = pq[:, 0:R * WQ].rearrange("p (r w) -> p r w", r=R)
        (indexed, matched, turned, copied, shifted, spread, q_copied, part, scored, kept, broadcast, reduced, selected,
         limited, clipped, folded, raised, chain) = sems(
             nc, c, nm, "indexed matched turned copied shifted spread q_copied part scored kept broadcast reduced "
             "selected limited clipped folded raised chain")
        gathered = gather_sems(nc, nm, "gathered", DEEP)
        with nc.Block() as block:
            @block.scalar
            def _(act):
                act.sem_inc(kept, DEEP)

                def step(r):
                    m = r.off(-1)
                    if m.there:
                        act.wait_ge(spread, m.n + 1)
                        nc.scalar.activation(qs[m.slot % 2][:], pq_v, ACT.Copy).then_inc(q_copied, 1)
                    m = r.off(1)
                    if m.there:
                        act.wait_ge(turned, DEEP + m.n + 1)
                        nc.scalar.copy(hot_t[m.slot % 2][:], pt[m.slot % 2][:].rearrange("p (r n) -> p r n", r=R)
                                       ).then_inc(copied, 1)
                        act.wait_ge(broadcast, (m.n + 1) * R)
                        nc.scalar.activation(off[m.slot][:], hot[m.slot][:], ACT.Copy, bias=-1.0
                                             ).then_inc(shifted, 1)
                    m = r.off(-2)
                    if m.there:
                        wait_alone(act, scored, m.n + 1)
                        if at.held is not None:
                            nc.scalar.copy(at.held[:, ds(m.n * R, R), :], rows[m.slot][:, :, 0:H * dv])
                        nc.scalar.copy(scores[:, ds(m.n * R, R), :], sc[m.slot][:]).then_inc(kept, 1)
                    m = r.off(2)
                    if m.there:
                        nc.scalar.copy(idx[m.slot][:], at.index[:, ds(m.n * R, R)]).then_inc(indexed, 1)
                rolling(act, step, rounds)

            @block.gpsimd
            def _(pool):
                def step(r):
                    m = r.off(2)
                    if m.there:
                        wait_alone(pool, indexed, m.n + 1)
                        if at.held is not None:
                            wait_alone(pool, kept, m.n + 1)
                        for u in range(R):
                            nc.gpsimd.indirect_dma_start(rows[m.slot][:, u, :], None, at.keys,
                                                         bass.IndirectOffsetOnAxis(ap=idx[m.slot][:, u:u + 1], axis=0)
                                                         ).then_inc(gathered[m.slot], 16)
                rolling(pool, step, rounds)

            @block.tensor
            def _(pe):
                pe.sem_inc(turned, DEEP)
                pe.sem_inc(broadcast, DEEP * R)

                def step(r):
                    nxt, old = r.off(1), r.off(-2)
                    if nxt.there:
                        pe.wait_ge(matched, nxt.n + 1)
                        for u in range(R):
                            mm = nc.tensor.transpose(pt[nxt.slot % 2][:, u * P:(u + 1) * P], hot[nxt.slot][:, u, :],
                                                     kit.ident[:])
                        mm.then_inc(turned, 1)
                    for u in range(R):
                        if r.there:
                            blk = pe.value_load(e.blk[0:1, ds(r.n * R + u, 1)], min_val=0, max_val=NT - 1)
                        if old.there:
                            if u == 0:
                                pe.wait_ge(scored, old.n + 1)
                                pe.wait_ge(shifted, old.n + 1)
                            pe.wait_ge(reduced, old.n * R + u + 1)
                            nc.tensor.matmul(pm[u][:, 0:H * P], off[old.slot][:, u, :],
                                             big[:].rearrange("p h n -> p (h n)"), start=True, stop=False)
                            for h in range(H):
                                mm = nc.tensor.matmul(pm[u][:, h * P:(h + 1) * P],
                                                      sc[old.slot][:, u, h:h + 1].broadcast_to([P, P]), kit.ident[:],
                                                      start=False, stop=(h == H - 1))
                            mm.then_inc(broadcast, 1)
                        if r.there:
                            if u == 0:
                                pe.wait_ge(copied, r.n + 1)
                                pe.wait_ge(q_copied, r.n + 1)
                            mm = nc.tensor.matmul(pq_v[:, u, :], hot_t[r.slot % 2][:, u, :],
                                                  at.q[:, ds(blk, 1), :].rearrange("p o w -> p (o w)"),
                                                  start=True, stop=True)
                            if u == R - 1:
                                mm.then_inc(spread, 1)
                rolling(pe, step, rounds)

            @block.vector
            def _(dve):
                link = link_on(dve, chain)
                for h in range(H):
                    link(nc.vector.tensor_scalar(big[:, h, :], kit.ident[:], BIG, None, ALU.mult))
                nc.vector.memset(top, -3e38).then_inc(raised, 1)
                dve.sem_inc(reduced, R)
                dve.sem_inc(q_copied, 1)

                def step(r):
                    old, cur, far = r.off(-3), r.off(-1), r.off(2)

                    def combine(us):
                        for u in us:
                            q = qs[cur.slot % 2][:, u, :]
                            if at.dots:
                                ins = nc.vector.tensor_tensor(tmp[cur.slot % 2][:, u, :], rows[cur.slot][:, u, :], q,
                                                              ALU.mult)
                            else:
                                ins = nc.vector.tensor_tensor(tmp[cur.slot % 2][:, u, :],
                                                              rows[cur.slot][:, u, at.score_at:at.score_at + H], q,
                                                              ALU.add)
                        return ins
                    if old.there:
                        if old.looped or old.c >= 1:
                            dve.wait_ge(clipped, old.n)
                        nc.vector.tensor_tensor(is_tile[:], kit.iota[:, None, 0:NT].broadcast_to([P, R, NT]),
                                                e.tile[:, ds(old.n * R, R), None].broadcast_to([P, R, NT]),
                                                ALU.is_equal).then_inc(selected, 1)
                        for u in range(R):
                            dve.wait_ge(broadcast, (DEEP + old.n) * R + u + 1)
                            nc.vector.tensor_reduce(row_max[:, u, :], pm[u][:, 0:H * P].rearrange(
                                "p (h n) -> p h n", h=H), AX_X, ALU.max).then_inc(reduced, 1)
                        dve.wait_ge(selected, old.n + 1)
                        nc.vector.tensor_scalar(is_tile[:], is_tile[:], 2 * BIG, BIG, ALU.mult, ALU.subtract
                                                ).then_inc(limited, 1)
                    if cur.there:
                        dve.wait_ge(q_copied, cur.n + 2)
                        dve.wait_ge(gathered[cur.slot], (cur.turn + 1) * 16 * R)
                        if cur.looped or cur.c >= 2:
                            dve.wait_ge(scored, cur.n - 1)
                        combine(range(R // 2))
                    if old.there:
                        dve.wait_ge(reduced, (old.n + 2) * R)
                        dve.wait_ge(limited, old.n + 1)
                        nc.vector.tensor_tensor(
                            by_tile[:], row_max[:].rearrange("p r h -> p h r")[:, None, :, :].broadcast_to([P, NT, H, R]),
                            is_tile[:].rearrange("p r t -> p t r")[:, :, None, :].broadcast_to([P, NT, H, R]),
                            ALU.min).then_inc(clipped, 1)
                    if cur.there:
                        combine(range(R // 2, R)).then_inc(part, 1)
                    if old.there:
                        dve.wait_ge(clipped, old.n + 1)
                        dve.wait_ge(raised, old.n + 1)
                        nc.vector.tensor_reduce(round_max[:], by_tile[:], AX_X, ALU.max).then_inc(folded, 1)
                    if far.there:
                        dve.wait_ge(turned, far.n + 1)
                        if far.looped or far.c >= DEEP:
                            dve.wait_ge(shifted, far.n + 1 - DEEP)
                        nc.vector.tensor_tensor(hot[far.slot][:], kit.iota[:, None, :].broadcast_to([P, R, P]),
                                                e.rec[:, ds(far.n * R, R), 1:2].broadcast_to([P, R, P]),
                                                ALU.is_equal).then_inc(matched, 1)
                    if old.there:
                        dve.wait_ge(folded, old.n + 1)
                        nc.vector.tensor_tensor(top, top, round_max[:], ALU.max).then_inc(raised, 1)
                    if cur.there:
                        dve.wait_ge(part, cur.n + 1)
                        dve.wait_ge(kept, cur.n + 1)
                        if at.dots:
                            nc.vector.tensor_reduce(sc[cur.slot][:], tmp[cur.slot % 2][:].rearrange(
                                "p r (h d) -> p r h d", h=H), AX_X, ALU.add).then_inc(scored, 1)
                        else:
                            nc.vector.scalar_tensor_tensor(out=sc[cur.slot][:], in0=tmp[cur.slot % 2][:], scalar=0.2,
                                                           in1=tmp[cur.slot % 2][:], op0=ALU.mult, op1=ALU.max
                                                           ).then_inc(scored, 1)
                rolling(dve, step, rounds)


def edge_sums(nc, kit, nm, at, scores, top, acc):
    e, H, dv = at.edges, at.heads, at.dv
    WV = at.values.shape[1]
    W = H + H * dv
    rounds = e.groups // R
    with ExitStack() as c:
        def many(count, name, shape, dt=F32):
            return [c.enter_context(nc.sbuf_tensor(f"{nm}_{name}{a}", shape, dt)) for a in range(count)]
        if at.held is None:
            idx, rows = many(DEEP, "idx", [P, R], I32), at.rows(WV)
            gathered = gather_sems(nc, nm, "gathered", DEEP)
        hot, hot_t = many(DEEP, "hot", [P, R, P]), many(2, "hot_t", [P, R, P])
        z, val = many(2, "z", [P, R, H]), many(2, "val", [P, R, W])
        pt = [c.enter_context(nc.psum_tensor(f"{nm}_pt{a}", [P, 512], F32)) for a in range(2)]
        pd = [c.enter_context(nc.psum_tensor(f"{nm}_pd{a}", [P, 512], F32)) for a in range(2)]
        pa = [c.enter_context(nc.psum_tensor(f"{nm}_pa{u}", [P, 512], F32)) for u in range(R)]
        pd_v = [p[:, 0:R * H].rearrange("p (r h) -> p r h", r=R) for p in pd]
        (indexed, matched, turned, copied, spread, part, shifted, raised, weighted, multiplied, added) = sems(
            nc, c, nm, "indexed matched turned copied spread part shifted raised weighted multiplied added")

        with nc.Block() as block:
            @block.scalar
            def _(act):
                def step(r):
                    m = r.off(-1)
                    if m.there:
                        act.wait_ge(shifted, m.n + 1)
                        nc.scalar.activation(val[m.slot % 2][:, :, 0:H], z[m.slot % 2][:], ACT.Exp).then_inc(raised, 1)
                    m = r.off(2)
                    if m.there and at.held is None:
                        if m.looped or m.c >= DEEP:
                            wait_alone(act, weighted, (m.n + 1 - DEEP) * R)
                        nc.scalar.copy(idx[m.slot][:], at.index[:, ds(m.n * R, R)]).then_inc(indexed, 1)
                    m = r.off(1)
                    if m.there:
                        act.wait_ge(turned, m.n + 1)
                        nc.scalar.copy(hot_t[m.slot % 2][:], pt[m.slot % 2][:].rearrange("p (r n) -> p r n", r=R)
                                       ).then_inc(copied, 1)
                rolling(act, step, rounds)

            if at.held is None:
                @block.gpsimd
                def _(pool):
                    def step(r):
                        m = r.off(2)
                        if m.there:
                            wait_alone(pool, indexed, m.n + 1)
                            for u in range(R):
                                nc.gpsimd.indirect_dma_start(
                                    rows[m.slot][:, u, :], None, at.values,
                                    bass.IndirectOffsetOnAxis(ap=idx[m.slot][:, u:u + 1], axis=0)
                                ).then_inc(gathered[m.slot], 16)
                    rolling(pool, step, rounds)

            @block.tensor
            def _(pe):
                def step(r):
                    old, nxt = r.off(-2), r.off(1)
                    for u in range(R):
                        if r.there:
                            blk = pe.value_load(e.blk[0:1, ds(r.n * R + u, 1)], min_val=0, max_val=NT - 1)
                        if old.there:
                            pe.wait_ge(weighted, old.n * R + u + 1)
                            pe.wait_ge(added, old.n * R + u + 1)
                            nc.tensor.matmul(pa[u][:, 0:W], hot[old.slot][:, u, :], val[old.slot % 2][:, u, :],
                                             start=True, stop=True).then_inc(multiplied, 1)
                        if r.there:
                            if u == 0:
                                pe.wait_ge(copied, r.n + 1)
                                if r.looped or r.c >= 2:
                                    pe.wait_ge(shifted, r.n - 1)
                            mm = nc.tensor.matmul(pd_v[r.slot % 2][:, u, :], hot_t[r.slot % 2][:, u, :],
                                                  top[:, ds(blk, 1), :].rearrange("p o w -> p (o w)"),
                                                  start=True, stop=True)
                            if u == R - 1:
                                mm.then_inc(spread, 1)
                    if nxt.there:
                        pe.wait_ge(matched, nxt.n + 1)
                        for u in range(R):
                            mm = nc.tensor.transpose(pt[nxt.slot % 2][:, u * P:(u + 1) * P], hot[nxt.slot][:, u, :],
                                                     kit.ident[:])
                        mm.then_inc(turned, 1)
                rolling(pe, step, rounds)

            @block.vector
            def _(dve):
                nc.vector.memset(acc, 0.0).then_inc(added, R)

                def step(r):
                    cur, mid, old, nxt = r.off(-1), r.off(-2), r.off(-3), r.off(1)
                    if cur.there:
                        dve.wait_ge(spread, cur.n + 1)
                        nc.vector.tensor_tensor(z[cur.slot % 2][:], scores[:, ds(cur.n * R, R), :], pd_v[cur.slot % 2],
                                                ALU.subtract).then_inc(part, 1)
                    for u in range(R):
                        if old.there:
                            blk = dve.value_load(e.blk[0:1, ds(old.n * R + u, 1)], min_val=0, max_val=NT - 1)
                        if mid.there:
                            if u == 0:
                                if at.held is None:
                                    dve.wait_ge(gathered[mid.slot], (mid.turn + 1) * 16 * R)
                                dve.wait_ge(raised, mid.n + 1)
                            v = (rows[mid.slot][:, u, 0:H * dv] if at.held is None
                                 else at.held[:, ds(mid.n * R + u, 1), :].rearrange("p o w -> p (o w)"))
                            nc.vector.tensor_tensor(
                                val[mid.slot % 2][:, u, H:].rearrange("p (h d) -> p h d", h=H),
                                v.rearrange("p (h d) -> p h d", h=H),
                                val[mid.slot % 2][:, u, 0:H][:, :, None].broadcast_to([P, H, dv]), ALU.mult
                            ).then_inc(weighted, 1)
                        if old.there:
                            to = acc[:, ds(blk, 1), :].rearrange("p o w -> p (o w)")
                            dve.wait_ge(multiplied, old.n * R + u + 1)
                            dve.wait_ge(added, (old.n + 1) * R + u)
                            nc.vector.tensor_tensor(to, to, pa[u][:, 0:W], ALU.add).then_inc(added, 1)
                    if cur.there:
                        dve.wait_ge(part, cur.n + 1)
                        nc.vector.tensor_scalar(z[cur.slot % 2][:], z[cur.slot % 2][:], 0.0, None, ALU.min
                                                ).then_inc(shifted, 1)
                    if nxt.there:
                        nc.vector.tensor_tensor(hot[nxt.slot][:], kit.iota[:, None, :].broadcast_to([P, R, P]),
                                                e.rec[:, ds(nxt.n * R, R), 1:2].broadcast_to([P, R, P]),
                                                ALU.is_equal).then_inc(matched, 1)
                rolling(dve, step, rounds)


def gat_moe_stage(nc, kit, A, x, bufs):
    b1, b2, b3, b4 = bufs
    E, F = A["L0_ffn_b1"].shape
    H = A["L0_ffn_att_src"].shape[0]
    fc, HE = F // P, H * E
    rows = dict(src=A["L0_ffn_edge_index"][0], dst=A["L0_ffn_edge_index"][1])
    n_edges = rows["src"].shape[0]
    groups = -(-(NT + (n_edges + NT * (P - 1)) // P) // (R * DEEP)) * R * DEEP
    table = nc.dram_tensor("gat_table", (NP, HE + 2 * H), F32).ap()
    with ExitStack() as c:
        def sb(name, shape, dt=F32):
            return c.enter_context(nc.sbuf_tensor(f"gat_{name}", shape, dt))
        gates = sb("gates", [P, NT, E])
        b1s, b2s = sb("b1s", [P, E, fc]), sb("b2s", [E, D])
        layer_norm(nc, kit, "gat_ln", x, b1, b2)
        with ExitStack() as cc:
            def sb2(name, shape, dt=F32):
                return cc.enter_context(nc.sbuf_tensor(f"gat_{name}", shape, dt))
            own = alloc_edges(nc, cc, "own", groups)
            sort_edges(nc, kit, own, P, first=NT, **rows)
            w = sb2("w", [P, 2, HE])
            rows_in = {n: sb2(n, [P, HE]) for n in ("att_src", "att_dst", "b_gat", "ln_gamma", "ln_beta")}
            h = sb2("h", [P, NT, HE + 2 * H])
            tmp, score = sb2("tmp", [P, NT, HE]), sb2("score", [P, NT, E])
            scores, top = sb2("scores", [P, groups, H]), sb2("top", [P, NT, H])
            acc = sb2("acc", [P, NT, H + HE])
            held = b4[:, 0:groups * HE].rearrange("p (g w) -> p g w", g=groups)
            mean, var, std = sb2("mean", [P, NT]), sb2("var", [P, NT]), sb2("std", [P, NT])
            above, same = sb2("above", [P, NT, E, E]), sb2("same", [P, NT, E, E])
            lower, rank = sb2("lower", [P, E, E]), sb2("rank", [P, NT, E])

            def flat(a):
                return a if len(a.shape) == 1 else a.rearrange("h e -> (h e)")
            with nc.allow_non_contiguous_dma(reason="short columns"):
                load(nc, "gat_load", [(w[:], chunks(A["L0_ffn_W_gat"])), (b2s[:], A["L0_ffn_b2"])]
                     + [(b1s[:, e, :], column(A["L0_ffn_b1"][e], fc)) for e in range(E)]
                     + [(t[:], row_to_all(flat(A[f"L0_ffn_{n}"]))) for n, t in rows_in.items()])
            add_projection(nc, "gat_h", b2, w, tmp[:], fresh=True)

            def node_scores(link):
                link(nc.vector.tensor_copy(h[:, :, 0:HE], tmp[:]))
                for n, at in (("att_src", HE), ("att_dst", HE + H)):
                    link(nc.vector.tensor_tensor(tmp[:], h[:, :, 0:HE],
                                                 rows_in[n][:, None, :].broadcast_to([P, NT, HE]), ALU.mult))
                    link(nc.vector.tensor_reduce(h[:, :, at:at + H], tmp[:].rearrange("p t (h e) -> p t h e", h=H),
                                                 AX_X, ALU.add))
                link(nc.vector.tensor_copy(top[:], h[:, :, HE + H:]))
            on_vector(nc, "gat_v1", node_scores)
            load(nc, "gat_store", [(table.rearrange("(t p) w -> p t w", p=P), h[:])])
            own_dst = sb2("own_dst", [P, NT, H])
            on_vector(nc, "gat_v2", lambda link: link(nc.vector.tensor_copy(own_dst[:], top[:])))
            at = EdgeAttention(own, own.src, table, table, own_dst, H, E, dots=False, spare=b3, score_at=HE, held=held)
            edge_scores(nc, kit, "gat_s", at, scores, top[:])
            edge_sums(nc, kit, "gat_a", at, scores, top[:], acc[:])
            with ExitStack() as c3:
                step, ready, rooted = sems(nc, c3, "gat_score", "step ready rooted")
                with nc.Block() as block:
                    @block.vector
                    def _(dve):
                        link = link_on(dve, step)
                        agg, den = acc[:, :, H:], acc[:, :, 0:H]
                        agg_h = agg.rearrange("p t (h e) -> p t h e", h=H)
                        link(nc.vector.tensor_scalar(den, den, 1e-16, None, ALU.add))
                        link(nc.vector.reciprocal(den, den))
                        link(nc.vector.tensor_tensor(agg_h, agg_h, den[:, :, :, None].broadcast_to([P, NT, H, E]),
                                                     ALU.mult))
                        link(nc.vector.tensor_tensor(tmp[:], agg, rows_in["b_gat"][:, None, :].broadcast_to([P, NT, HE]),
                                                     ALU.add))
                        link(nc.vector.tensor_reduce(mean[:], tmp[:], AX_X, ALU.add))
                        link(nc.vector.tensor_scalar(mean[:], mean[:], 1.0 / HE, None, ALU.mult))
                        link(nc.vector.tensor_tensor(tmp[:], tmp[:], per_node(mean[:], HE), ALU.subtract))
                        link(nc.vector.tensor_tensor(agg, tmp[:], tmp[:], ALU.mult))
                        link(nc.vector.tensor_reduce(var[:], agg, AX_X, ALU.add))
                        nc.vector.tensor_scalar(var[:], var[:], 1.0 / HE, EPS, ALU.mult, ALU.add).then_inc(ready, 1)
                        dve.wait_ge(rooted, 1)
                        link(nc.vector.reciprocal(std[:], std[:]))
                        link(nc.vector.tensor_tensor(tmp[:], tmp[:], per_node(std[:], HE), ALU.mult))
                        for n, op in (("ln_gamma", ALU.mult), ("ln_beta", ALU.add)):
                            link(nc.vector.tensor_tensor(tmp[:], tmp[:],
                                                         rows_in[n][:, None, :].broadcast_to([P, NT, HE]), op))
                        link(nc.vector.tensor_reduce(score[:], tmp[:].rearrange("p t (h e) -> p t e h", h=H), AX_X,
                                                     ALU.add))
                        link(nc.vector.tensor_scalar(score[:], score[:], 1.0 / H, None, ALU.mult))
                        rank_rows(nc, kit, link, score[:], E, above[:], same[:], lower[:], rank[:])
                        link(nc.vector.tensor_scalar(rank[:], rank[:], 2.0, None, ALU.is_lt))
                        link(nc.vector.tensor_tensor(gates[:], score[:], rank[:], ALU.mult))
                        link(nc.vector.tensor_scalar(rank[:], rank[:], 1.0, BIG, ALU.subtract, ALU.mult))
                        link(nc.vector.tensor_tensor(gates[:], gates[:], rank[:], ALU.add))

                    @block.scalar
                    def _(act):
                        act.wait_ge(ready, 1)
                        nc.scalar.activation(std[:], var[:], ACT.Sqrt).then_inc(rooted, 1)
            softmax_rows(nc, "gat_sm", gates[:], E)
        add_gated_bias(nc, kit, "gat_b2", gates, b2s[:], x)
        of = lambda name: lambda e: A[name][ds(e, 1), :, :]
        expert_mlps(nc, "gatx", b2, E, [Mid(of("L0_ffn_W1"), 2, fc, ACT.Gelu, b1s)], of("L0_ffn_W2"), gates, x)


def hgt_stage(nc, kit, A, x, bufs, e):
    b1, b2, b3, b4 = bufs
    TYPES = A["L1_gnn_k_linears"].shape[0]
    RELS, H, DK, _ = A["L1_gnn_relation_att"].shape
    KC = TYPES * 2
    HP = H // 2
    keys = nc.dram_tensor("hgt_keys", (RELS * NP, D), F32).ap()
    values = nc.dram_tensor("hgt_values", (RELS * NP, D), F32).ap()
    q = nat(b2)
    w_k, w_q, w_v = (b3[:, n * KC * D:(n + 1) * KC * D].rearrange("p (k n) -> p k n", k=KC) for n in range(3))
    raw, rel_k, rel_v = (b4[:, n * HP * RELS * P:(n + 1) * HP * RELS * P].rearrange("p (h r n) -> p h r n", h=HP, r=RELS)
                         for n in range(3))
    with ExitStack() as c:
        def sb(name, shape, dt=F32):
            return c.enter_context(nc.sbuf_tensor(f"hgt_{name}", shape, dt))
        kind_i, kind, is_kind = sb("kind_i", [P, NT], I32), sb("kind", [P, NT]), sb("is_kind", [P, TYPES, NT])
        skip = sb("skip", [P, TYPES])
        layer_norm(nc, kit, "hgt_ln", x, b1)
        with ExitStack() as cc:
            pri = cc.enter_context(nc.sbuf_tensor("hgt_pri", [P, RELS, H], F32))
            step, zeroed, loaded, turned, squashed = sems(nc, cc, "hgt_w", "step zeroed loaded turned squashed")
            pt = cc.enter_context(nc.psum_tensor("hgt_pt", [P, HP * RELS * P], F32))
            with nc.Block() as block, nc.allow_non_contiguous_dma(reason="short rows"):
                @block.sync
                def _(sp):
                    for t, n in ((w_k, "k"), (w_q, "q"), (w_v, "v")):
                        sp.dma_start(t, A[f"L1_gnn_{n}_linears"].rearrange("t (k p) n -> p (t k) n", p=P)).then_inc(loaded, 16)
                    sp.dma_start(skip[:], row_to_all(A["L1_gnn_skip"])).then_inc(loaded, 16)
                    sp.dma_start(pri[:].rearrange("p r h -> p (r h)"),
                                 row_to_all(A["L1_gnn_relation_pri"].rearrange("r h -> (r h)"))).then_inc(loaded, 16)
                    sp.wait_ge(zeroed, 3)
                    sp.dma_start(kind_i[:, 0:NT - 1],
                                 A["node_type_4"][0:(NT - 1) * P].rearrange("(t p) -> p t", p=P)).then_inc(loaded, 16)
                    sp.dma_start(kind_i[0:LAST, NT - 1:NT],
                                 A["node_type_4"][(NT - 1) * P:N].rearrange("(p o) -> p o", o=1)).then_inc(loaded, 16)
                    for t, n in ((raw, "att"), (rel_v, "msg")):
                        for hp in range(HP):
                            for h2 in range(2):
                                at = slice(h2 * DK, (h2 + 1) * DK)
                                sp.dma_start(t[at, hp, :, at],
                                             A[f"L1_gnn_relation_{n}"][:, hp * 2 + h2, :, :].rearrange("r d e -> d r e")
                                             ).then_inc(loaded, 16)
                    sp.wait_ge(loaded, 16 * (7 + 2 * HP * 2))

                @block.vector
                def _(dve):
                    nc.vector.memset(raw, 0.0).then_inc(zeroed, 1)
                    nc.vector.memset(rel_v, 0.0).then_inc(zeroed, 1)
                    nc.vector.memset(kind_i[:], 0).then_inc(zeroed, 1)
                    dve.wait_ge(loaded, 16 * (7 + 2 * HP * 2))
                    link = link_on(dve, step)
                    link(nc.vector.tensor_copy(kind[:], kind_i[:]))
                    for t in range(TYPES):
                        link(nc.vector.tensor_scalar(is_kind[:, t, :], kind[:], float(t), None, ALU.is_equal))
                    link(nc.vector.tensor_scalar(pri[:], pri[:], 1.0 / DK ** 0.5, None, ALU.mult))
                    dve.wait_ge(turned, 1)
                    pt_v = pt[:].rearrange("p (h r n) -> p h r n", h=HP, r=RELS)
                    for hp in range(HP):
                        for h2 in range(2):
                            at = slice(h2 * DK, (h2 + 1) * DK)
                            link(nc.vector.tensor_tensor(rel_k[:, hp, :, at], pt_v[:, hp, :, at],
                                                         pri[:, :, hp * 2 + h2:hp * 2 + h2 + 1].broadcast_to([P, RELS, DK]),
                                                         ALU.mult))

                @block.tensor
                def _(pe):
                    pe.wait_ge(loaded, 16 * (7 + 2 * HP * 2))
                    for hp in range(HP):
                        for r in range(RELS):
                            n = hp * RELS + r
                            mm = nc.tensor.transpose(pt[:, n * P:(n + 1) * P], raw[:, hp, r, :], kit.ident[:])
                    mm.then_inc(turned, 1)

                @block.scalar
                def _(act):
                    act.wait_ge(loaded, 16 * (7 + 2 * HP * 2))
                    nc.scalar.activation(skip[:], skip[:], ACT.Sigmoid).then_inc(squashed, 1)
                    act.wait_ge(squashed, 1)
        hgt_tables(nc, kit, nat(b1), is_kind, w_k, w_q, w_v, rel_k, rel_v, q, keys, values, TYPES, RELS, HP)
        with ExitStack() as cc:
            groups = e.groups
            scores = cc.enter_context(nc.sbuf_tensor("hgt_scores", [P, groups, H], F32))
            top = cc.enter_context(nc.sbuf_tensor("hgt_top", [P, NT, H], F32))
            at = EdgeAttention(e, e.key, keys, values, q, H, DK, dots=True, spare=b3)
            edge_scores(nc, kit, "hgt_s", at, scores, top[:])
            acc = cc.enter_context(nc.sbuf_tensor("hgt_acc", [P, NT, H + D], F32))
            edge_sums(nc, kit, "hgt_a", at, scores, top[:], acc[:])

            def divide(link):
                link(nc.vector.tensor_scalar(acc[:, :, 0:H], acc[:, :, 0:H], 1e-30, None, ALU.max))
                link(nc.vector.reciprocal(acc[:, :, 0:H], acc[:, :, 0:H]))
                link(nc.vector.tensor_tensor(nat(b1).rearrange("p t (h d) -> p t h d", h=H),
                                             acc[:, :, H:].rearrange("p t (h d) -> p t h d", h=H),
                                             acc[:, :, 0:H][:, :, :, None].broadcast_to([P, NT, H, DK]), ALU.mult))
                for t in range(TYPES):
                    link(nc.vector.tensor_scalar(is_kind[:, t, :], is_kind[:, t, :], skip[:, t:t + 1], None, ALU.mult))
            on_vector(nc, "hgt_v1", divide)
        turn(nc, kit, "hgt_turn", nat(b1), tr(b2))
        load(nc, "hgt_load_a", [(w_k, A["L1_gnn_a_linears"].rearrange("t (k p) n -> p (t k) n", p=P))])
        for t in range(TYPES):
            add_projection(nc, f"hgt_out{t}", b2, w_k[:, 2 * t:2 * t + 2, :], nat(x), gate=is_kind[:, t, :])


def hgt_tables(nc, kit, xn, is_kind, w_k, w_q, w_v, rel_k, rel_v, q, keys, values, TYPES, RELS, HP):
    KC = TYPES * 2
    with ExitStack() as c:
        def sb(name, shape, dt=F32):
            return c.enter_context(nc.sbuf_tensor(f"hgtt_{name}", shape, dt))
        xm, xmt, kvt = sb("xm", [P, TYPES, D]), sb("xmt", [P, KC, P]), sb("kvt", [P, 2 * HP, P])
        out_k, out_v = sb("out_k", [P, RELS, D]), sb("out_v", [P, RELS, D])
        pt = c.enter_context(nc.psum_tensor("hgtt_pt", [P, KC * P], F32))
        pkv = c.enter_context(nc.psum_tensor("hgtt_pkv", [P, 512], F32))
        pq = c.enter_context(nc.psum_tensor("hgtt_pq", [P, 512], F32))
        pr = [c.enter_context(nc.psum_tensor(f"hgtt_pr{n}", [P, 512], F32)) for n in range(4)]
        (masked, turned, copied, projected, kv_copied, q_copied, related, out_k_ready, out_v_ready, k_free,
         v_free) = sems(nc, c, "hgtt", "masked turned copied projected kv_copied q_copied related out_k_ready "
                        "out_v_ready k_free v_free")
        stored_k, stored_v = sems(nc, c, "hgtt", "stored_k stored_v")
        half = RELS // 2
        parts = [(v, g, hp) for g in range(2) for hp in range(HP) for v in range(2)]

        def tiles(eng, step):
            with eng.Fori(0, NT - 1) as t:
                step(t, True)
            step(NT - 1, False)

        with nc.Block() as block:
            @block.vector
            def _(dve):
                def mask(t):
                    for k in range(TYPES):
                        ins = nc.vector.tensor_scalar(xm[:, k, :], xn[:, ds(t, 1), :].rearrange("p o d -> p (o d)"),
                                                      is_kind[:, k, ds(t, 1)], None, ALU.mult)
                    ins.then_inc(masked, 1)
                mask(0)
                dve.sem_inc(kv_copied, 1)
                dve.sem_inc(out_v_ready, 2)

                def step(t, more):
                    if more:
                        dve.wait_ge(turned, t + 1)
                        mask(t + 1)
                    dve.wait_ge(projected, t + 1)
                    dve.wait_ge(related, t * 8 + 8)
                    nc.vector.tensor_copy(kvt[:], pkv[:].rearrange("p (c n) -> p c n", n=P)).then_inc(kv_copied, 1)
                    dve.wait_ge(v_free, t + 1)
                    for n, (v, g, hp) in enumerate(parts):
                        if v:
                            dve.wait_ge(related, t * 8 + 8 + n + 1)
                            nc.vector.tensor_copy(out_v[:, g * half:(g + 1) * half, hp * P:(hp + 1) * P],
                                                  pr[n % 4][:].rearrange("p (r n) -> p r n", r=half)).then_inc(out_v_ready, 1)
                tiles(dve, step)

            @block.tensor
            def _(pe):
                pe.sem_inc(related, 8)

                def turn_masked():
                    for k in range(KC):
                        mm = nc.tensor.transpose(pt[:, k * P:(k + 1) * P], xm[:, k // 2, (k % 2) * P:(k % 2 + 1) * P],
                                                 kit.ident[:])
                    mm.then_inc(turned, 1)
                pe.wait_ge(masked, 1)
                turn_masked()

                def step(t, more):
                    pe.wait_ge(copied, t + 1)
                    pe.wait_ge(kv_copied, t + 1)
                    for n, w in enumerate((w_k, w_v)):
                        for f in range(HP):
                            for k in range(KC):
                                nc.tensor.matmul(pkv[:, (n * HP + f) * P:(n * HP + f + 1) * P], w[:, k, f * P:(f + 1) * P],
                                                 xmt[:, k, :], start=(k == 0), stop=(k == KC - 1))
                    pe.wait_ge(q_copied, t + 1)
                    for k in range(KC):
                        mm = nc.tensor.matmul(pq[:, 0:D], xmt[:, k, :], w_q[:, k, :], start=(k == 0), stop=(k == KC - 1))
                    mm.then_inc(projected, 1)
                    if more:
                        pe.wait_ge(masked, t + 2)
                        turn_masked()
                    pe.wait_ge(kv_copied, t + 2)
                    for n, (v, g, hp) in enumerate(parts):
                        pe.wait_ge(out_v_ready if v else out_k_ready, t * 4 + n // 2 + 1)
                        nc.tensor.matmul(pr[n % 4][:], kvt[:, v * HP + hp, :],
                                         (rel_v if v else rel_k)[:, hp, g * half:(g + 1) * half, :].rearrange(
                                             "p r n -> p (r n)"), start=True, stop=True).then_inc(related, 1)
                tiles(pe, step)

            @block.scalar
            def _(act):
                act.sem_inc(q_copied, 1)
                act.sem_inc(out_k_ready, 2)

                def copy_turned(t):
                    act.wait_ge(turned, t + 1)
                    nc.scalar.copy(xmt[:], pt[:].rearrange("p (k n) -> p k n", k=KC)).then_inc(copied, 1)
                copy_turned(0)

                def step(t, more):
                    wait_alone(act, projected, t + 1)
                    nc.scalar.copy(q[:, ds(t, 1), :].rearrange("p o d -> p (o d)"), pq[:, 0:D]).then_inc(q_copied, 1)
                    if more:
                        copy_turned(t + 1)
                    act.wait_ge(k_free, t + 1)
                    for n, (v, g, hp) in enumerate(parts):
                        if not v:
                            act.wait_ge(related, t * 8 + 8 + n + 1)
                            nc.scalar.copy(out_k[:, g * half:(g + 1) * half, hp * P:(hp + 1) * P],
                                           pr[n % 4][:].rearrange("p (r n) -> p r n", r=half)).then_inc(out_k_ready, 1)
                tiles(act, step)

            @block.sync
            def _(sp):
                sp.sem_inc(k_free, 1)
                sp.sem_inc(v_free, 1)
                by_node = [a.rearrange("(r t p) d -> t p r d", r=RELS, p=P) for a in (keys, values)]
                with sp.Fori(0, NT) as t:
                    for ready, out, table, stored in ((out_k_ready, out_k, by_node[0], stored_k),
                                                      (out_v_ready, out_v, by_node[1], stored_v)):
                        sp.wait_ge(ready, t * 4 + 2 + 4)
                        sp.dma_start(table[ds(t, 1), :, :, :].rearrange("o p r d -> p (o r) d"), out[:]).then_inc(stored, 16)
                    sp.wait_ge(stored_k, t * 16 + 16)
                    sp.sem_inc(k_free, 1)
                    sp.wait_ge(stored_v, t * 16 + 16)
                    sp.sem_inc(v_free, 1)


def column(ap1d, k):
    return ap1d.rearrange("(k p) -> p k", k=k)


def sage_stage(nc, kit, A, x, bufs, e, table):
    b1, b2, b3, b4 = bufs
    with ExitStack() as c:
        def sb(name, shape, dt=F32):
            return c.enter_context(nc.sbuf_tensor(f"sage_{name}", shape, dt))
        layers = A["L2_gnn_W_agg"].shape[0]
        w_in, w_out = sb("w_in", [P, 2, D]), sb("w_out", [P, 2, D])
        w_agg = [sb(f"w_agg{i}", [P, 2, D]) for i in range(layers)]
        w_self = [sb(f"w_self{i}", [P, 2, D]) for i in range(layers)]
        bias_in, bias_out = sb("b_in", [P, 2]), sb("b_out", [P, D])
        bias = [sb(f"b_hid{i}", [P, 2]) for i in range(layers)]
        rdeg, rall = sb("rdeg", [P, NT]), sb("rall", [P, NP])
        with nc.allow_non_contiguous_dma(reason="short bias columns"):
            load(nc, "sage_load",
                 [(w_in[:], chunks(A["L2_gnn_W_in"])), (w_out[:], chunks(A["L2_gnn_W_out"])),
                  (bias_in[:], column(A["L2_gnn_b_in"], 2)), (bias_out[:], row_to_all(A["L2_gnn_b_out"]))]
                 + [(w_agg[i][:], chunks(A["L2_gnn_W_agg"][i])) for i in range(layers)]
                 + [(w_self[i][:], chunks(A["L2_gnn_W_self"][i])) for i in range(layers)]
                 + [(bias[i][:], column(A["L2_gnn_b_hid"][i], 2)) for i in range(layers)])
        layer_norm(nc, kit, "sage_ln", x, b1, b2)

        def mean_factor(link):
            link(nc.vector.tensor_scalar(rdeg[:], kit.deg[:], 1.0, None, ALU.max))
            link(nc.vector.reciprocal(rdeg[:], rdeg[:]))
        on_vector(nc, "sage_v0", mean_factor)
        rows_to_all(nc, kit, "sage_rall", rdeg, rall)
        project_t(nc, "sage_in", [(b2, 2, w_in)], b3, 2, bias=bias_in)
        h, free = b3, b2
        for i in range(layers):
            write_table(nc, kit, f"sage_t{i}", h, 2, b1, table)
            aggregate_t(nc, kit, f"sage_a{i}", e, table, 2, b4)
            on_vector(nc, f"sage_v{i + 1}", lambda link: link(nc.vector.tensor_tensor(
                tr(b4), tr(b4), rall[:, None, :].broadcast_to([P, 2, NP]), ALU.mult)))
            project_t(nc, f"sage_p{i}", [(b4, 2, w_agg[i]), (h, 2, w_self[i])], free, 2, ACT.Relu, bias[i])
            h, free = free, h
        add_projection(nc, "sage_out", h, w_out, nat(x), bias_out)


def weighted_stage(nc, kit, A, x, bufs, e, table):
    b1, b2, b3, b4 = bufs
    with ExitStack() as c:
        def sb(name, shape, dt=F32):
            return c.enter_context(nc.sbuf_tensor(f"wsum_{name}", shape, dt))
        w, wt = sb("w", [P, 2, D]), sb("wt", [P, 2, D])
        ln_w, ln_b = sb("ln_w", [P, 2]), sb("ln_b", [P, 2])
        bias, gamma, beta = sb("b", [P, D]), sb("gamma", [P, D]), sb("beta", [P, D])
        with nc.allow_non_contiguous_dma(reason="short columns"):
            load(nc, "wsum_load",
                 [(w[:], chunks(A["L3_gnn_W"])), (ln_w[:], column(A["L3_gnn_ln_w"], 2)),
                  (ln_b[:], column(A["L3_gnn_ln_b"], 2)), (bias[:], row_to_all(A["L3_gnn_b"])),
                  (gamma[:], row_to_all(A["L3_gnn_gamma"])), (beta[:], row_to_all(A["L3_gnn_beta"]))])
        layer_norm(nc, kit, "wsum_ln", x, b1, b2)
        layer_norm(nc, kit, "wsum_ln2", b1, b3, b2)
        with ExitStack() as cc:
            step, squashed, turned = sems(nc, cc, "wsum_silu", "step squashed turned")
            ps = cc.enter_context(nc.psum_tensor("wsum_ps", [P, 512], F32))
            with nc.Block() as block:
                @block.tensor
                def _(pe):
                    for k in range(2):
                        for o in range(2):
                            mm = nc.tensor.transpose(ps[:, k * D + o * P:k * D + (o + 1) * P],
                                                     w[:, o, k * P:(k + 1) * P], kit.ident[:])
                    mm.then_inc(turned, 1)

                @block.vector
                def _(dve):
                    link = link_on(dve, step)
                    for k in range(2):
                        link(nc.vector.tensor_scalar(tr(b2)[:, k, :], tr(b2)[:, k, :], ln_w[:, k:k + 1],
                                                     ln_b[:, k:k + 1], ALU.mult, ALU.add))
                    dve.wait_ge(turned, 1)
                    link(nc.vector.tensor_tensor(wt[:], ps[:].rearrange("p (k n) -> p k n", k=2),
                                                 gamma[:, None, :].broadcast_to([P, 2, D]), ALU.mult))
                    link(nc.vector.tensor_tensor(bias[:], bias[:], gamma[:], ALU.mult))
                    link(nc.vector.tensor_tensor(bias[:], bias[:], beta[:], ALU.add))
                    link(nc.vector.tensor_tensor(x[:], x[:], b1[:], ALU.add))
                    for k in range(2):
                        dve.wait_ge(squashed, k + 1)
                        link(nc.vector.tensor_tensor(tr(b2)[:, k, :], tr(b2)[:, k, :], tr(b4)[:, k, :], ALU.mult))

                @block.scalar
                def _(act):
                    for k in range(2):
                        act.wait_ge(step, k + 1)
                        nc.scalar.activation(tr(b4)[:, k, :], tr(b2)[:, k, :], ACT.Sigmoid).then_inc(squashed, 1)
        write_table(nc, kit, "wsum_t", b2, 2, b3, table)
        aggregate_t(nc, kit, "wsum_a", e, table, 2, b4, weighted=True)
        add_projection(nc, "wsum_out", b4, wt, nat(x), bias)


def rank_rows(nc, kit, link, z, n, above, same, lower, rank):
    T = z.shape[1]
    each = z[:, :, :, None].broadcast_to([P, T, n, n])
    other = z[:, :, None, :].broadcast_to([P, T, n, n])
    link(nc.vector.tensor_tensor(lower, kit.iota[:, None, 0:n].broadcast_to([P, n, n]),
                                 kit.iota[:, 0:n, None].broadcast_to([P, n, n]), ALU.is_lt))
    link(nc.vector.tensor_tensor(above, other, each, ALU.is_gt))
    link(nc.vector.tensor_tensor(same, other, each, ALU.is_equal))
    link(nc.vector.tensor_tensor(same, same, lower[:, None, :, :].broadcast_to([P, T, n, n]), ALU.mult))
    link(nc.vector.tensor_tensor(above, above, same, ALU.add))
    link(nc.vector.tensor_reduce(rank, above, AX_X, ALU.add))


def shared_moe_stage(nc, kit, A, x, bufs):
    b1, b2, b3, b4 = bufs
    E, F = A["L3_ffn_b1"].shape
    fc = F // P
    K = 2
    CAPACITY = float(-(-N * 5 // (4 * E)))
    with ExitStack() as c:
        def sb(name, shape, dt=F32):
            return c.enter_context(nc.sbuf_tensor(f"shared_{name}", shape, dt))
        wr, br = sb("wr", [P, 2, E]), sb("br", [P, E])
        gamma, beta = sb("gamma", [P, D]), sb("beta", [P, D])
        mean, mean_all = sb("mean", [P, 2]), sb("mean_all", [P, 2, P])
        z, load_, pick_w = sb("z", [P, 1, E]), sb("load", [P, 1, E]), sb("pick_w", [P, 1, K])
        above, same, lower = sb("above", [P, 1, E, E]), sb("same", [P, 1, E, E]), sb("lower", [P, E, E])
        rank, is_r, pick_f = sb("rank", [P, 1, E]), sb("is_r", [P, 1, E]), sb("pick_f", [P, K])
        pick_i = sb("pick_i", [P, K], I32)
        gates = sb("gates", [P, NT, K])
        b1s, b2s = sb("b1s", [P, K, fc]), sb("b2s", [K, D])
        layer_norm(nc, kit, "shared_ln", x, b1, b2)
        load(nc, "shared_load", [(wr[:], chunks(A["L3_ffn_Wr"])), (br[:], row_to_all(A["L3_ffn_br"])),
                                 (gamma[:], row_to_all(A["L3_ffn_gamma"])), (beta[:], row_to_all(A["L3_ffn_beta"]))])
        with ExitStack() as cc:
            step, multiplied = sems(nc, cc, "shared_logit", "step multiplied")
            ps = cc.enter_context(nc.psum_tensor("shared_ps", [P, 512], F32))
            with nc.Block() as block:
                @block.vector
                def _(dve):
                    link = link_on(dve, step)
                    link(nc.vector.tensor_reduce(mean[:], tr(b2)[:, :, 0:N], AX_X, ALU.add))
                    link(nc.vector.tensor_scalar(mean[:], mean[:], 1.0 / N, None, ALU.mult))
                    link(nc.vector.tensor_copy(mean_all[:], mean[:, :, None].broadcast_to([P, 2, P])))
                    link(nc.vector.tensor_copy(b3[:], b1[:]))
                    dve.wait_ge(multiplied, 1)
                    link(nc.vector.tensor_tensor(z[:, 0, :], ps[:, 0:E], br[:], ALU.add))

                @block.tensor
                def _(pe):
                    pe.wait_ge(step, 3)
                    for k in range(2):
                        mm = nc.tensor.matmul(ps[:, 0:E], mean_all[:, k, :], wr[:, k, :], start=(k == 0), stop=(k == 1))
                    mm.then_inc(multiplied, 1)
        softmax_rows(nc, "shared_sm1", z[:], E)

        def scale_loads(link):
            link(nc.vector.tensor_scalar(load_[:], z[:], float(N), 1.0, ALU.mult, ALU.max))
            link(nc.vector.reciprocal(load_[:], load_[:]))
            link(nc.vector.tensor_scalar(load_[:], load_[:], CAPACITY, 1.0, ALU.mult, ALU.min))
            link(nc.vector.tensor_tensor(z[:], z[:], load_[:], ALU.mult))
        on_vector(nc, "shared_v1", scale_loads)
        softmax_rows(nc, "shared_sm2", z[:], E)

        def choose(link):
            rank_rows(nc, kit, link, z[:], E, above[:], same[:], lower[:], rank[:])
            for r in range(K):
                link(nc.vector.tensor_scalar(is_r[:], rank[:], float(r), None, ALU.is_equal))
                link(nc.vector.tensor_tensor(load_[:], is_r[:], kit.iota[:, None, 0:E], ALU.mult))
                link(nc.vector.tensor_reduce(pick_f[:, r:r + 1], load_[:], AX_X, ALU.add))
                link(nc.vector.tensor_tensor(load_[:], is_r[:], z[:], ALU.mult))
                link(nc.vector.tensor_reduce(pick_w[:, :, r:r + 1], load_[:], AX_X, ALU.add))
            link(nc.vector.tensor_copy(pick_i[:], pick_f[:]))
        on_vector(nc, "shared_v2", choose)
        softmax_rows(nc, "shared_sm3", pick_w[:], K)
        on_vector(nc, "shared_v3", lambda link: link(nc.vector.tensor_copy(
            gates[:], pick_w[:].broadcast_to([P, NT, K]))))
        pick = lambda eng, e: eng.value_load(pick_i[0:1, ds(e, 1)], min_val=0, max_val=E - 1)
        with ExitStack() as cc:
            loaded, = sems(nc, cc, "shared_b", "loaded")
            with nc.Block() as block:
                @block.sync
                def _(sp):
                    for r in range(K):
                        at = pick(sp, r)
                        for f in range(fc):
                            sp.dma_start(b1s[:, r, f:f + 1],
                                         A["L3_ffn_b1"][ds(at, 1), f * P:(f + 1) * P].rearrange("o p -> p o")
                                         ).then_inc(loaded, 16)
                        sp.dma_start(b2s[r:r + 1, :], A["L3_ffn_b2"][ds(at, 1), :]).then_inc(loaded, 16)
                    sp.wait_ge(loaded, 16 * K * (fc + 1))
        add_gated_bias(nc, kit, "shared_b2", gates, b2s[:], b3)
        of = lambda name: lambda e: A[name][ds(e, 1), :, :]
        expert_mlps(nc, "shared", b2, K, [Mid(of("L3_ffn_W1"), 2, fc, ACT.Gelu, b1s)], of("L3_ffn_W2"), gates, b3, pick)
        layer_norm(nc, kit, "shared_ln2", b3, b4)

        def after(link):
            link(nc.vector.tensor_tensor(nat(b4), nat(b4), gamma[:, None, :].broadcast_to([P, NT, D]), ALU.mult))
            link(nc.vector.tensor_tensor(nat(b4), nat(b4), beta[:, None, :].broadcast_to([P, NT, D]), ALU.add))
            link(nc.vector.tensor_tensor(x[:], x[:], b4[:], ALU.add))
        on_vector(nc, "shared_v4", after)


FLT_MAX = 3.4028234663852886e38


def switch_stage(nc, kit, A, x, bufs):
    b1, b2, b3, b4 = bufs
    E, F = A["L2_ffn_b1"].shape
    fc = F // P
    C = -(-N * 5 // (4 * E))
    ST = -(-C // P)
    S = ST * P
    slots = nc.dram_tensor("switch_slots", (E * S + NP, D), F32).ap()
    answers = nc.dram_tensor("switch_answers", (E * S, D), F32).ap()
    with ExitStack() as c:
        def sb(name, shape, dt=F32):
            return c.enter_context(nc.sbuf_tensor(f"switch_{name}", shape, dt))
        slot_i, back_i = sb("slot_i", [P, NT], I32), sb("back_i", [P, NT], I32)
        factor = sb("factor", [P, NT])
        layer_norm(nc, kit, "switch_ln", x, b1, b2)
        with ExitStack() as cc:
            def sb2(name, shape, dt=F32):
                return cc.enter_context(nc.sbuf_tensor(f"switch_{name}", shape, dt))
            gw, gb, z = sb2("gw", [P, 2, E]), sb2("gb", [P, E]), sb2("z", [P, NT, E])
            above, same = sb2("above", [P, NT, E, E]), sb2("same", [P, NT, E, E])
            lower, rank = sb2("lower", [P, E, E]), sb2("rank", [P, NT, E])
            hot, ahead, total = sb2("hot", [P, NT, E]), sb2("ahead", [P, NT, E]), sb2("total", [P, NT, E])
            pos, kept, first, valid, spare = (sb2(n, [P, NT]) for n in ("pos", "kept", "first", "valid", "spare"))
            load(nc, "switch_load", [(gw[:], chunks(A["L2_ffn_gate_w"])), (gb[:], row_to_all(A["L2_ffn_gate_b"]))])
            add_projection(nc, "switch_gate", b2, gw, z[:], gb, fresh=True)
            softmax_rows(nc, "switch_sm", z[:], E)
            step, chosen, summed, placed, zeroed = sems(nc, cc, "switch_route", "step chosen summed placed zeroed")
            sent, = gather_sems(nc, "switch_route", "sent", 1)
            ps = cc.enter_context(nc.psum_tensor("switch_ps", [P, 512], F32))
            with nc.Block() as block:
                @block.vector
                def _(dve):
                    link = link_on(dve, step)
                    link(nc.vector.memset(b3[:, 0:E * S * D // P // 2], 0.0))
                    link(nc.vector.tensor_reduce(factor[:], z[:], AX_X, ALU.max))
                    rank_rows(nc, kit, link, z[:], E, above[:], same[:], lower[:], rank[:])
                    link(nc.vector.tensor_scalar(valid[:], kit.node[:], float(N), None, ALU.is_lt))
                    link(nc.vector.tensor_scalar(hot[:], rank[:], 0.0, None, ALU.is_equal))
                    nc.vector.tensor_tensor(hot[:], hot[:], per_node(valid[:], E), ALU.mult).then_inc(chosen, 1)
                    dve.wait_ge(summed, 1)
                    link(nc.vector.tensor_copy(ahead[:], ps[:, 0:NT * E].rearrange("p (t e) -> p t e", e=E)))
                    link(nc.vector.tensor_copy(total[:], ps[:, 256:256 + NT * E].rearrange("p (t e) -> p t e", e=E)))
                    for e in range(E):
                        link(nc.vector.tensor_tensor_scan(rank[:, :, e], kit.ones[:, 0:NT], total[:, :, e], 0.0,
                                                          ALU.mult, ALU.add))
                    link(nc.vector.tensor_tensor(ahead[:], ahead[:], rank[:], ALU.add))
                    link(nc.vector.tensor_tensor(ahead[:], ahead[:], total[:], ALU.subtract))
                    link(nc.vector.tensor_tensor(ahead[:], ahead[:], hot[:], ALU.mult))
                    link(nc.vector.tensor_reduce(pos[:], ahead[:], AX_X, ALU.add))
                    link(nc.vector.tensor_tensor(total[:], hot[:], kit.iota[:, None, 0:E].broadcast_to([P, NT, E]),
                                                 ALU.mult))
                    link(nc.vector.tensor_reduce(first[:], total[:], AX_X, ALU.add))
                    link(nc.vector.tensor_scalar(first[:], first[:], float(S), None, ALU.mult))
                    link(nc.vector.tensor_scalar(kept[:], pos[:], float(C), None, ALU.is_lt))
                    link(nc.vector.tensor_tensor(kept[:], kept[:], valid[:], ALU.mult))
                    link(nc.vector.tensor_tensor(factor[:], factor[:], kept[:], ALU.mult))
                    link(nc.vector.scalar_tensor_tensor(out=spare[:], in0=pos[:], scalar=float(C - 1), in1=first[:],
                                                        op0=ALU.min, op1=ALU.add))
                    link(nc.vector.tensor_copy(back_i[:], spare[:]))
                    link(nc.vector.tensor_scalar(valid[:], kit.node[:], float(E * S), None, ALU.add))
                    link(nc.vector.tensor_tensor(spare[:], spare[:], valid[:], ALU.subtract))
                    link(nc.vector.tensor_tensor(spare[:], spare[:], kept[:], ALU.mult))
                    link(nc.vector.tensor_tensor(spare[:], spare[:], valid[:], ALU.add))
                    nc.vector.tensor_copy(slot_i[:], spare[:]).then_inc(placed, 1)

                @block.tensor
                def _(pe):
                    pe.wait_ge(chosen, 1)
                    flat = hot[:].rearrange("p t e -> p (t e)")
                    nc.tensor.matmul(ps[:, 0:NT * E], kit.tri[:], flat, start=True, stop=True)
                    nc.tensor.matmul(ps[:, 256:256 + NT * E], kit.ones[:], flat, start=True, stop=True).then_inc(summed, 1)

                @block.sync
                def _(sp):
                    half = E * S // 2
                    sp.wait_ge(step, 1)
                    for n in range(2):
                        sp.dma_start(slots[n * half:(n + 1) * half, :].rearrange("(p r) d -> p (r d)", p=P),
                                     b3[:, 0:half * D // P]).then_inc(zeroed, 16)

                @block.gpsimd
                def _(pool):
                    pool.wait_ge(zeroed, 32)
                    pool.wait_ge(placed, 1)
                    for t in range(NT):
                        nc.gpsimd.indirect_dma_start(slots, bass.IndirectOffsetOnAxis(ap=slot_i[:, t:t + 1], axis=0),
                                                     nat(b1)[:, t, :], None).then_inc(sent, 16)
                    pool.wait_ge(sent, 16 * NT)
        switch_experts(nc, kit, A, slots, answers, E, fc, ST, bufs)
        with ExitStack() as cc:
            fetched = gather_sems(nc, "switch_back", "fetched", ROUNDS)
            scaled, step = sems(nc, cc, "switch_back", "scaled step")
            limit = [cc.enter_context(nc.sbuf_tensor(f"switch_limit{n}", [P, 1], F32)) for n in range(3)]
            with nc.Block() as block:
                @block.gpsimd
                def _(pool):
                    for t in range(NT):
                        nc.gpsimd.indirect_dma_start(nat(b3)[:, t, :], None, answers,
                                                     bass.IndirectOffsetOnAxis(ap=back_i[:, t:t + 1], axis=0)
                                                     ).then_inc(fetched[t // U], 16)

                @block.vector
                def _(dve):
                    for r in range(ROUNDS):
                        dve.wait_ge(fetched[r], 16 * U)
                        part = nat(b3)[:, r * U:(r + 1) * U, :]
                        nc.vector.tensor_tensor(part, part, per_node(factor[:, r * U:(r + 1) * U], D),
                                                ALU.mult).then_inc(scaled, 1)
                    dve.wait_ge(scaled, ROUNDS)
                    link = link_on(dve, step)
                    mask = b4[:].bitcast(I32)
                    for n, (to, op, than) in enumerate(((1e4, ALU.is_gt, FLT_MAX), (-1e4, ALU.is_lt, -FLT_MAX),
                                                        (0.0, ALU.not_equal, None))):
                        link(nc.vector.memset(limit[n][:], to))
                        link(nc.vector.tensor_scalar(mask, b3[:], than, None, op) if than is not None
                             else nc.vector.tensor_tensor(mask, b3[:], b3[:], op))
                        link(nc.vector.copy_predicated(b3[:], mask, limit[n][:].broadcast_to([P, NT * D])))
                    link(nc.vector.tensor_tensor(x[:], x[:], b3[:], ALU.add))


def switch_experts(nc, kit, A, slots, answers, E, fc, ST, big):
    S = ST * P
    with ExitStack() as c:
        def sb(name, shape, dt=F32):
            return c.enter_context(nc.sbuf_tensor(f"swx_{name}", shape, dt))
        b1s = sb("b1s", [P, E, fc])

        def carve(buf, *shapes):
            at, parts = 0, []
            for n, m in shapes:
                parts.append(buf[:, at:at + n * m].rearrange("p (n m) -> p n m", n=n))
                at += n * m
            return parts
        h, = carve(big[0], (fc, S))
        w1_0, w1_1, w2_0 = carve(big[1], (2, fc * P), (2, fc * P), (fc, D))
        w2_1, rows_0, rows_1, y_0, y_1 = carve(big[2], (fc, D), (ST, D), (ST, D), (ST, D), (ST, D))
        b2s, xt = carve(big[3], (E, D), (2, S))
        w1, w2, rows, y = (w1_0, w1_1), (w2_0, w2_1), (rows_0, rows_1), (y_0, y_1)
        with nc.allow_non_contiguous_dma(reason="short columns"):
            load(nc, "swx_load", [(b1s[:, e, :], column(A["L2_ffn_b1"][e], fc)) for e in range(E)]
                 + [(b2s[:, e, :], row_to_all(A["L2_ffn_b2"][e])) for e in range(E)])
        ps = [c.enter_context(nc.psum_tensor(f"swx_ps{r}", [P, 512], F32)) for r in range(4)]
        py = [c.enter_context(nc.psum_tensor(f"swx_py{r}", [P, 512], F32)) for r in range(4)]
        loaded = sems(nc, c, "swx", "loaded0 loaded1")
        stored = gather_sems(nc, "swx", "stored", 2)
        turned, copied, multiplied, read, finished, added, left, y_free = sems(
            nc, c, "swx", "turned copied multiplied read finished added left y_free")
        with nc.Block() as block:
            def pairs(eng, body):
                with eng.Fori(0, E // 2) as i:
                    for q in range(2):
                        body(i, q, i * 2 + q)

            @block.sync
            def _(sp):
                def body(i, q, e):
                    sp.wait_ge(left, e + 1)
                    sp.dma_start(rows[q], slots[ds(e * S, S), :].rearrange("(s p) d -> p s d", p=P)).then_inc(loaded[q], 16)
                    sp.dma_start(w1[q], A["L2_ffn_w1"][ds(e, 1), :, :].rearrange("o (k p) f -> p (o k) f", p=P)
                                 ).then_inc(loaded[q], 16)
                    sp.dma_start(w2[q], A["L2_ffn_w2"][ds(e, 1), :, :].rearrange("o (k p) f -> p (o k) f", p=P)
                                 ).then_inc(loaded[q], 16)
                pairs(sp, body)

            @block.tensor
            def _(pe):
                pe.sem_inc(left, 2)

                def body(i, q, e):
                    wait_alone(pe, loaded[q], i * 48 + 48)
                    for k in range(2):
                        pe.wait_ge(read, e * fc + 4)
                        for s in range(ST):
                            mm = nc.tensor.transpose(ps[k][:, s * P:(s + 1) * P], rows[q][:, s, k * P:(k + 1) * P],
                                                     kit.ident[:])
                        mm.then_inc(turned, 1)
                    for g in range(fc):
                        pe.wait_ge(copied, e * 2 + 2)
                        pe.wait_ge(read, e * fc + g + 1)
                        for k in range(2):
                            mm = nc.tensor.matmul(ps[g % 4][:, 0:S], w1[q][:, k, g * P:(g + 1) * P], xt[:, k, :],
                                                  start=(k == 0), stop=(k == 1))
                        mm.then_inc(multiplied, 1)
                    pe.wait_ge(read, e * fc + fc + 4)
                    for s in range(ST):
                        pe.wait_ge(added, e * ST + s + 1)
                        for k in range(fc):
                            mm = nc.tensor.matmul(py[s][:, 0:D], h[:, k, s * P:(s + 1) * P], w2[q][:, k, :],
                                                  start=(k == 0), stop=(k == fc - 1))
                        mm.then_inc(finished, 1)
                    pe.drain().then_inc(left, 1)
                pairs(pe, body)

            @block.scalar
            def _(act):
                act.sem_inc(read, 4)

                def body(i, q, e):
                    for k in range(2):
                        act.wait_ge(turned, e * 2 + k + 1)
                        nc.scalar.copy(xt[:, k, :], ps[k][:, 0:S]).then_inc(copied, 1)
                    for g in range(fc):
                        wait_alone(act, multiplied, e * fc + g + 1)
                        nc.scalar.activation(h[:, g, :], ps[g % 4][:, 0:S], ACT.Relu,
                                             bias=b1s[:, ds(e, 1), g:g + 1].rearrange("p o f -> p (o f)")
                                             ).then_inc(read, 1)
                pairs(act, body)

            @block.vector
            def _(dve):
                dve.sem_inc(added, ST)

                def body(i, q, e):
                    dve.wait_ge(y_free, e + 1)
                    for s in range(ST):
                        dve.wait_ge(finished, e * ST + s + 1)
                        nc.vector.tensor_tensor(y[q][:, s, :], py[s][:, 0:D],
                                                b2s[:, ds(e, 1), :].rearrange("p o d -> p (o d)"), ALU.add).then_inc(added, 1)
                pairs(dve, body)

            @block.gpsimd
            def _(pool):
                pool.sem_inc(y_free, 2)

                def body(i, q, e):
                    wait_alone(pool, added, e * ST + ST + ST)
                    nc.gpsimd.dma_start(answers[ds(e * S, S), :].rearrange("(s p) d -> p s d", p=P), y[q]
                                        ).then_inc(stored[q], 16)
                    wait_alone(pool, stored[q], i * 16 + 16)
                    pool.sem_inc(y_free, 1)
                pairs(pool, body)


def program(nc, A, out, stages=range(8)):
    with ExitStack() as ctx:
        kit = Kit()
        make_constants(nc, ctx, kit)
        x, *bufs = [ctx.enter_context(nc.sbuf_tensor(n, [P, NT * D], F32)) for n in ("x", "big1", "big2", "big3", "big4")]
        kit.deg = ctx.enter_context(nc.sbuf_tensor("deg", [P, NT], F32))
        table = nc.dram_tensor("table", (NP, D), F32).ap()
        table_half = nc.dram_tensor("table_half", (NP, P), F32).ap()
        load_x(nc, A["x"], x)
        edges = alloc_edges(nc, ctx, "edge", 416)
        if 0 in stages or 2 in stages:
            sort_edges(nc, kit, edges, 125, A["src"], A["dst"], etype=A["edge_type_8"])
        if 0 in stages:
            gcn_stage(nc, kit, A, x, bufs, edges, table_half)
        if 1 in stages:
            gat_moe_stage(nc, kit, A, x, bufs)
        if 2 in stages:
            hgt_stage(nc, kit, A, x, bufs, edges)
        if 3 in stages:
            soft_moe_stage(nc, kit, A, x, bufs)
        if 4 in stages or 6 in stages:
            edges.name = "back"
            sort_edges(nc, kit, edges, 125, A["dst"], A["src"], weight=A["edge_weight"])
        if 4 in stages:
            in_degrees(nc, kit, "deg", A["src"], 125, kit.deg)
            sage_stage(nc, kit, A, x, bufs, edges, table)
        if 5 in stages:
            switch_stage(nc, kit, A, x, bufs)
        if 6 in stages:
            weighted_stage(nc, kit, A, x, bufs, edges, table)
        if 7 in stages:
            shared_moe_stage(nc, kit, A, x, bufs)
        store_x(nc, x, out)


def load_x(nc, src, x):
    with ExitStack() as c:
        loaded, cleared = sems(nc, c, "load_x", "loaded cleared")
        with nc.Block() as block:
            @block.vector
            def _(dve):
                nc.vector.memset(nat(x)[:, NT - 1, :], 0.0).then_inc(cleared, 1)

            @block.sync
            def _(sp):
                sp.dma_start(nat(x)[:, 0:NT - 1, :],
                             src[0:(NT - 1) * P, :].rearrange("(t p) d -> p t d", p=P)).then_inc(loaded, 16)
                sp.wait_ge(cleared, 1)
                sp.dma_start(nat(x)[0:LAST, NT - 1, :], src[(NT - 1) * P:N, :]).then_inc(loaded, 16)
                sp.wait_ge(loaded, 32)


def store_x(nc, x, out):
    with ExitStack() as c:
        stored, = sems(nc, c, "store_x", "stored")
        with nc.Block() as block:
            @block.sync
            def _(sp):
                sp.dma_start(out[0:(NT - 1) * P, :].rearrange("(t p) d -> p t d", p=P),
                             nat(x)[:, 0:NT - 1, :]).then_inc(stored, 16)
                sp.dma_start(out[(NT - 1) * P:N, :], nat(x)[0:LAST, NT - 1, :]).then_inc(stored, 16)
                sp.wait_ge(stored, 32)


_INS = ['x', 'src', 'dst', 'edge_type_8', 'edge_weight', 'node_type_4', 'L0_gnn_W1', 'L0_gnn_b1',
        'L0_gnn_W2', 'L0_gnn_b2', 'L0_ffn_W_gat', 'L0_ffn_att_src', 'L0_ffn_att_dst',
        'L0_ffn_b_gat', 'L0_ffn_ln_gamma', 'L0_ffn_ln_beta', 'L0_ffn_W1', 'L0_ffn_b1', 'L0_ffn_W2',
        'L0_ffn_b2', 'L0_ffn_edge_index', 'L1_gnn_k_linears', 'L1_gnn_q_linears',
        'L1_gnn_v_linears', 'L1_gnn_a_linears', 'L1_gnn_relation_att', 'L1_gnn_relation_msg',
        'L1_gnn_relation_pri', 'L1_gnn_skip', 'L1_ffn_Wr', 'L1_ffn_br', 'L1_ffn_W1', 'L1_ffn_b1',
        'L1_ffn_g1', 'L1_ffn_be1', 'L1_ffn_m1', 'L1_ffn_v1', 'L1_ffn_W2', 'L1_ffn_b2', 'L1_ffn_g2',
        'L1_ffn_be2', 'L1_ffn_m2', 'L1_ffn_v2', 'L1_ffn_Wo', 'L1_ffn_bo', 'L2_gnn_W_in',
        'L2_gnn_b_in', 'L2_gnn_W_agg', 'L2_gnn_W_self', 'L2_gnn_b_hid', 'L2_gnn_W_out',
        'L2_gnn_b_out', 'L2_ffn_gate_w', 'L2_ffn_gate_b', 'L2_ffn_w1', 'L2_ffn_b1', 'L2_ffn_w2',
        'L2_ffn_b2', 'L3_gnn_ln_w', 'L3_gnn_ln_b', 'L3_gnn_W', 'L3_gnn_b', 'L3_gnn_gamma',
        'L3_gnn_beta', 'L3_ffn_Wr', 'L3_ffn_br', 'L3_ffn_W1', 'L3_ffn_b1', 'L3_ffn_W2', 'L3_ffn_b2',
        'L3_ffn_gamma', 'L3_ffn_beta']
_OUTS = [((3125, 256), 'float32')]


def kernel(**inputs):
    import numpy as _np
    import concourse.bacc as _bacc
    from concourse import mybir as _mybir
    from concourse.bass_utils import run_bass_kernel_spmd as _run

    nc = _bacc.Bacc("TRN2", target_bir_lowering=False, num_devices=1)
    arrays, named = {}, {}
    for name in _INS:
        a = _np.ascontiguousarray(inputs[name])
        arrays[f"in_{name}_dram"] = a
        named[name] = nc.dram_tensor(f"in_{name}_dram", a.shape, _mybir.dt.from_np(a.dtype), kind="ExternalInput").ap()
    shape, dtype = _OUTS[0]
    out = nc.dram_tensor("out_0_dram", shape, _mybir.dt.from_np(_np.dtype(dtype)), kind="ExternalOutput").ap()
    program(nc, named, out)
    r = _run(nc, [arrays], core_ids=[0])
    return r.results[0]["out_0_dram"]
```

```python
from contextlib import ExitStack


import concourse.bass as bass
from concourse import mybir

F32 = mybir.dt.float32
BF16 = mybir.dt.bfloat16
I32 = mybir.dt.int32
ALU = mybir.AluOpType
ACT = mybir.ActivationFunctionType
AX_X = mybir.AxisListType.X
ds = bass.ds

P = 128
N = 3125
D = 256
NT = -(-N // P)
NP = NT * P
U = 5
ROUNDS = NT // U
LAST = N - (NT - 1) * P
EPS = 1e-5
CHUNK = 320
R = 4
GROUPS_MAX = 424
DEEP = 4


class Kit:
    pass


def sems(nc, ctx, stage, names):
    taken = [nc.alloc_semaphore(f"{stage}_{n}") for n in names.split()]

    def give_back():
        for sem in taken:
            nc.gpsimd.sem_clear(sem)
            nc.release_semaphore(sem)
    ctx.callback(give_back)
    return taken


def gather_sems(nc, stage, what, n):
    return [nc.alloc_semaphore(f"{stage}_{what}{u}") for u in range(n)]


def wait_alone(eng, sem, value):
    eng.wait_ge(sem, value)
    eng.nop(nofuse=True)


def link_on(eng, sem):
    count = {"base": 0, "k": 0}

    def link(ins):
        count["k"] += 1
        ins.then_inc(sem, 1)
        eng.wait_ge(sem, count["base"] + count["k"])

    def begin(i, n):
        count["start"], count["n"] = count["base"] + count["k"], n
        count["base"], count["k"] = count["start"] + i * n, 0

    def end(rounds):
        assert count["k"] == count["n"], (count["k"], count["n"])
        count["base"], count["k"] = count["start"] + rounds * count["n"], 0

    link.begin, link.end = begin, end
    return link


def nat(buf):
    return buf[:, :].rearrange("p (t d) -> p t d", t=NT)


def tr(buf, k=2):
    return buf[:, 0:k * NP].rearrange("p (k n) -> p k n", k=k)


def row_to_all(ap1d, n=P):
    return bass.AP(tensor=ap1d.tensor, offset=ap1d.offset, ap=[[0, n], list(ap1d.ap[0])])


def make_constants(nc, ctx, kit, x):
    def sb(name, shape, dt=F32):
        return ctx.enter_context(nc.sbuf_tensor(name, shape, dt))
    kit.ident = sb("ident", [P, P])
    kit.tri = sb("tri_strict", [P, P])
    kit.ones = sb("ones", [P, P])
    kit.iota = sb("iota_row", [P, P])
    kit.iota_t = sb("iota_tiles", [P, GROUPS_MAX])
    kit.node = sb("node_number", [P, NT])
    with ExitStack() as c:
        made, = sems(nc, c, "const", "made")
        ints = c.enter_context(nc.sbuf_tensor("iota_int", [P, P], I32))
        ints_t = c.enter_context(nc.sbuf_tensor("iota_t_int", [P, GROUPS_MAX], I32))
        node_i = c.enter_context(nc.sbuf_tensor("node_int", [P, NT], I32))
        with nc.Block() as block:
            @block.gpsimd
            def _(pool):
                link = link_on(pool, made)
                link(nc.gpsimd.memset(nat(x)[:, NT - 1, :], 0.0))
                link(nc.gpsimd.memset(kit.ident[:], 0.0))
                link(nc.gpsimd.affine_select(out=kit.ident[:], in_=kit.ident[:], compare_op=ALU.not_equal,
                                             fill=1.0, base=0, pattern=[[-1, P]], channel_multiplier=1))
                link(nc.gpsimd.memset(kit.ones[:], 1.0))
                link(nc.gpsimd.affine_select(out=kit.tri[:], in_=kit.ones[:], compare_op=ALU.is_gt,
                                             fill=0.0, base=0, pattern=[[1, P]], channel_multiplier=-1))
                link(nc.gpsimd.iota(ints[:], pattern=[[1, P]], base=0, channel_multiplier=0))
                link(nc.gpsimd.tensor_copy(kit.iota[:], ints[:]))
                link(nc.gpsimd.iota(ints_t[:], pattern=[[1, GROUPS_MAX]], base=0, channel_multiplier=0))
                link(nc.gpsimd.tensor_copy(kit.iota_t[:], ints_t[:]))
                link(nc.gpsimd.iota(node_i[:], pattern=[[P, NT]], base=0, channel_multiplier=1))
                link(nc.gpsimd.tensor_copy(kit.node[:], node_i[:]))


class EdgeList:
    pass


def alloc_edges(nc, ctx, name, n_edges, first=0):
    groups = -(-(first + (n_edges + NT * (P - 1)) // P) // (R * DEEP)) * R * DEEP
    e = EdgeList()
    e.name, e.groups = name, groups
    e.rec = ctx.enter_context(nc.sbuf_tensor(f"{name}_rec", [P, groups, 4], F32))
    e.src = ctx.enter_context(nc.sbuf_tensor(f"{name}_src", [P, groups], I32))
    e.key = ctx.enter_context(nc.sbuf_tensor(f"{name}_key", [P, groups], I32))
    e.tile = ctx.enter_context(nc.sbuf_tensor(f"{name}_tile", [P, groups], F32))
    e.blk = ctx.enter_context(nc.sbuf_tensor(f"{name}_blk", [1, groups], I32))
    e.dram = nc.dram_tensor(f"{name}_sorted", (P * groups, 4), F32).ap()
    return e


class EdgeSort:

    S = 16

    def __init__(self, nc, kit, name, e, rows, dst, rec, adr, first=0):
        self.nc, self.kit, self.name, self.e, self.rows, self.first = nc, kit, name, e, rows, first
        self.dst, self.C = dst, dst.shape[0] // rows
        self.hold(rec, adr)

    def hold(self, rec, adr):
        self.rec = rec[0:self.rows, 0:self.C * 4].rearrange("p (c w) -> p c w", w=4)
        self.adr = adr[0:self.rows, 0:self.C].bitcast(I32)

    def buffers(self, ctx):
        nc, name, rows = self.nc, self.name, self.rows
        self.st_rec = [ctx.enter_context(nc.sbuf_tensor(f"{name}_st_rec{u}", [rows, 4], F32)) for u in range(self.S)]
        self.st_adr = [ctx.enter_context(nc.sbuf_tensor(f"{name}_st_adr{u}", [rows, 1], I32)) for u in range(self.S)]
        self.staged, = sems(nc, ctx, name, "staged")
        self.sent = gather_sems(nc, name, "sent", self.S)

    def prepare(self, src, etype=None, weight=None, beside=None, loads=()):
        nc, kit, e, rows, first, C, groups = self.nc, self.kit, self.e, self.rows, self.first, self.C, self.e.groups
        view = lambda a: a.rearrange("(p c) -> p c", p=rows)
        nm, rec, adr = self.name, self.rec, self.adr
        with ExitStack() as c:
            def sb(name, shape, dt=F32):
                return c.enter_context(nc.sbuf_tensor(f"{nm}_{name}", shape, dt))
            dst_i, src_i, type_i, work_i, col = (sb(x, [rows, C], I32) for x in ("dsti", "srci", "typei", "worki", "col"))
            hi, eq, inc, pos, ones_row, wt = (sb(x, [rows, C]) for x in ("hi", "eq", "inc", "pos", "ones_row", "wt"))
            tot, before = sb("tot", [rows, NT]), sb("before", [rows, NT])
            n_grp, end = sb("n_grp", [P, NT]), sb("end", [P, NT])
            n_int = sb("n_int", [P, NT], I32)
            tile, shifted = e.tile, sb("shifted", [P, groups])
            empty = sb("empty", [P, groups, 4])
            ps = c.enter_context(nc.psum_tensor(f"{nm}_ps", [P, 512], F32))
            loaded, cleared, emptied, step, counted, summed, loaded_too = sems(
                nc, c, nm, "loaded cleared emptied step counted summed loaded_too")
            n_loads = 2 + (etype is not None) + (weight is not None)
            with nc.Block() as block:
                @block.sync
                def _(sp):
                    sp.dma_start(dst_i[:], view(self.dst)).then_inc(loaded, 16)
                    sp.dma_start(src_i[:], view(src)).then_inc(loaded, 16)
                    if etype is not None:
                        sp.dma_start(type_i[:], view(etype)).then_inc(loaded, 16)
                    if weight is not None:
                        sp.dma_start(wt[:], view(weight)).then_inc(loaded, 16)
                    sp.wait_ge(cleared, 3)
                    sp.dma_start(e.dram.rearrange("(p g) w -> p (g w)", p=P),
                                 empty[:].rearrange("p g w -> p (g w)")).then_inc(emptied, 16)
                    for to, what in loads:
                        sp.dma_start(to, what).then_inc(loaded_too, 16)
                    sp.wait_ge(emptied, 16)
                    if loads:
                        sp.wait_ge(loaded_too, 16 * len(loads))

                @block.vector
                def _(dve):
                    nc.vector.memset(empty[:], 0.0).then_inc(cleared, 1)
                    dve.wait_ge(cleared, 1)
                    nc.vector.memset(empty[:, :, 1:2], 999.0).then_inc(cleared, 1)
                    nc.vector.memset(tile[:], 0.0).then_inc(cleared, 1)
                    dve.wait_ge(cleared, 3)
                    dve.wait_ge(loaded, 16 * n_loads)
                    link = link_on(dve, step)
                    link(nc.vector.tensor_scalar(work_i[:], dst_i[:], 7, None, ALU.arith_shift_right))
                    link(nc.vector.tensor_copy(hi[:], work_i[:]))
                    link(nc.vector.tensor_scalar(col[:], dst_i[:], 127, None, ALU.bitwise_and))
                    link(nc.vector.tensor_copy(rec[:, :, 1], col[:]))
                    link(nc.vector.tensor_copy(rec[:, :, 0], src_i[:]))
                    if weight is not None:
                        link(nc.vector.tensor_copy(rec[:, :, 2], wt[:]))
                    else:
                        link(nc.vector.memset(rec[:, :, 2], 1.0))
                    if etype is not None:
                        link(nc.vector.scalar_tensor_tensor(out=rec[:, :, 3], in0=type_i[:], scalar=float(NP),
                                                            in1=src_i[:], op0=ALU.mult, op1=ALU.add))
                    else:
                        link(nc.vector.tensor_copy(rec[:, :, 3], src_i[:]))
                    link(nc.vector.memset(pos[:], float(first * P - 1)))
                    with dve.Fori(0, NT) as b:
                        link.begin(b, 2)
                        link(nc.vector.tensor_scalar(eq[:], hi[:], kit.iota[0:rows, ds(b, 1)], None, ALU.is_equal))
                        link(nc.vector.tensor_reduce(tot[:, ds(b, 1)], eq[:], AX_X, ALU.add))
                    link.end(NT)
                    nc.vector.memset(ones_row[:], 1.0).then_inc(counted, 1)
                    dve.wait_ge(counted, 1)
                    dve.wait_ge(summed, 1)
                    link(nc.vector.tensor_scalar(n_int[:], ps[:, 64:64 + NT], 127.0, None, ALU.add))
                    link(nc.vector.tensor_scalar(n_int[:], n_int[:], 7, None, ALU.arith_shift_right))
                    link(nc.vector.tensor_copy(n_grp[:], n_int[:]))
                    link(nc.vector.tensor_tensor_scan(end[:], kit.ones[:, 0:NT], n_grp[:], 0.0, ALU.mult, ALU.add))
                    link(nc.vector.tensor_tensor(n_grp[:], end[:], n_grp[:], ALU.subtract))
                    link(nc.vector.scalar_tensor_tensor(out=before[:], in0=n_grp[0:rows, :], scalar=128.0,
                                                        in1=ps[0:rows, 0:NT], op0=ALU.mult, op1=ALU.add))
                    with dve.Fori(0, NT) as b:
                        link.begin(b, 4)
                        link(nc.vector.tensor_scalar(eq[:], hi[:], kit.iota[0:rows, ds(b, 1)], None, ALU.is_equal))
                        link(nc.vector.tensor_tensor_scan(inc[:], ones_row[:], eq[:], 0.0, ALU.mult, ALU.add))
                        link(nc.vector.scalar_tensor_tensor(out=wt[:], in0=inc[:], scalar=before[:, ds(b, 1)],
                                                            in1=eq[:], op0=ALU.add, op1=ALU.mult))
                        link(nc.vector.tensor_tensor(pos[:], pos[:], wt[:], ALU.add))
                    link.end(NT)
                    link(nc.vector.tensor_copy(work_i[:], pos[:]))
                    link(nc.vector.tensor_scalar(col[:], work_i[:], 127, None, ALU.bitwise_and))
                    link(nc.vector.tensor_scalar(work_i[:], work_i[:], 7, None, ALU.arith_shift_right))
                    link(nc.vector.scalar_tensor_tensor(out=adr, in0=col[:], scalar=float(groups), in1=work_i[:],
                                                        op0=ALU.mult, op1=ALU.add))
                    with dve.Fori(0, NT) as b:
                        link.begin(b, 1)
                        link(nc.vector.scalar_tensor_tensor(out=tile[:], in0=kit.iota_t[:, 0:groups],
                                                            scalar=end[:, ds(b, 1)], in1=tile[:],
                                                            op0=ALU.is_ge, op1=ALU.add))
                    link.end(NT)
                    if first:
                        link(nc.vector.tensor_copy(shifted[:, first:groups], tile[:, 0:groups - first]))
                        link(nc.vector.tensor_copy(tile[:, first:groups], shifted[:, first:groups]))
                        link(nc.vector.tensor_copy(tile[:, 0:first], kit.iota_t[:, 0:first]))
                    link(nc.vector.tensor_scalar(tile[:], tile[:], float(NT - 1), None, ALU.min))
                    link(nc.vector.tensor_copy(e.blk[:], tile[0:1, :]))

                @block.tensor
                def _(pe):
                    pe.wait_ge(counted, 1)
                    nc.tensor.matmul(ps[0:rows, 0:NT], kit.tri[0:rows, 0:rows], tot[:], start=True, stop=True)
                    nc.tensor.matmul(ps[:, 64:64 + NT], kit.ones[0:rows, :], tot[:], start=True, stop=True)\
                        .then_inc(summed, 1)

                if beside is not None:
                    beside[0].part(block, *beside[1:])

    def send(self, u):
        self.nc.gpsimd.indirect_dma_start(self.e.dram, bass.IndirectOffsetOnAxis(ap=self.st_adr[u][:, :1], axis=0),
                                          self.st_rec[u][:], None).then_inc(self.sent[u], 16)

    def stage(self, copy, i, u):
        at = i * self.S + u
        copy(self.st_rec[u][:], self.rec[:, ds(at, 1), :].rearrange("p o w -> p (o w)"))
        copy(self.st_adr[u][:], self.adr[:, ds(at, 1)]).then_inc(self.staged, 1)

    def part(self, block, lo, hi):
        @block.scalar
        def _(act):
            if lo == 0:
                for u in range(self.S):
                    self.stage(self.nc.scalar.copy, 0, u)
            with act.Fori(max(lo, 1), hi) as i:
                for u in range(self.S):
                    wait_alone(act, self.sent[u], i * 16)
                    self.stage(self.nc.scalar.copy, i, u)

        @block.gpsimd
        def _(pool):
            with pool.Fori(lo, hi) as i:
                for u in range(self.S):
                    wait_alone(pool, self.staged, i * self.S + u + 1)
                    self.send(u)
            for u in range(self.S):
                pool.wait_ge(self.sent[u], 16 * hi)

    def scatter(self, pool):
        def column(i, u):
            self.stage(self.nc.gpsimd.tensor_copy, i, u)
            wait_alone(pool, self.staged, i * self.S + u + 1)
            self.send(u)
        for u in range(self.S):
            column(0, u)
        with pool.Fori(1, self.C // self.S) as i:
            for u in range(self.S):
                pool.wait_ge(self.sent[u], i * 16)
                column(i, u)
        for u in range(self.S):
            pool.wait_ge(self.sent[u], 16 * (self.C // self.S))

    def fetch(self):
        nc, kit, e, first = self.nc, self.kit, self.e, self.first
        with ExitStack() as c:
            fetched, step, addressed = sems(nc, c, self.name, "fetched looped addressed")
            with nc.Block() as block:
                @block.sync
                def _(sp):
                    sp.dma_start(e.rec[:], e.dram.rearrange("(p g) w -> p g w", p=P)).then_inc(fetched, 16)

                @block.vector
                def _(dve):
                    dve.wait_ge(fetched, 16)
                    if first:
                        link = link_on(dve, step)
                        link(nc.vector.tensor_copy(e.rec[:, 0:first, 0], kit.node[:]))
                        link(nc.vector.tensor_copy(e.rec[:, 0:first, 3], kit.node[:]))
                        link(nc.vector.tensor_copy(e.rec[:, 0:first, 1], kit.node[:, 0:1].broadcast_to([P, first])))
                    nc.vector.tensor_copy(e.src[:], e.rec[:, :, 0]).then_inc(addressed, 1)
                    nc.vector.tensor_copy(e.key[:], e.rec[:, :, 3]).then_inc(addressed, 1)
                    dve.wait_ge(addressed, 2)


class Round:

    def __init__(self, j, c, rounds, looped):
        self.j, self.c, self.rounds, self.looped = j, c, rounds, looped
        self.n, self.slot, self.turn = j * DEEP + c, c % DEEP, j + c // DEEP
        self.there = looped or 0 <= c < rounds

    def off(self, o):
        return Round(self.j, self.c + o, self.rounds, self.looped)


def rolling(eng, step, rounds):
    for c in range(-2, 3):
        step(Round(0, c, rounds, False))
    with eng.Fori(0, rounds // DEEP - 2) as j:
        for k in range(DEEP):
            step(Round(j, 3 + k, rounds, True))
    for c in range(rounds - 5, rounds + 3):
        step(Round(0, c, rounds, False))


def layer_norm(nc, kit, nm, x, xn=None, xt=None):
    with ExitStack() as c:
        st = [c.enter_context(nc.sbuf_tensor(f"{nm}_st{u}", [P, D], F32)) for u in range(U)]
        stats = c.enter_context(nc.sbuf_tensor(f"{nm}_stats", [P, NT, 6], F32))
        mean, var, tmp, std, rstd, shift = (c.enter_context(nc.sbuf_tensor(f"{nm}_{x_}", [P, NT], F32))
                                            for x_ in ("mean", "var", "tmp", "std", "rstd", "shift"))
        ps = [c.enter_context(nc.psum_tensor(f"{nm}_ps{u}", [P, 512], F32)) for u in range(U)]
        measured, step, rooted, normed, turned, kept = sems(nc, c, nm, "measured step rooted normed turned kept")
        with nc.Block() as block:
            @block.vector
            def _(dve):
                with dve.Fori(0, NT) as t:
                    nc.vector.bn_stats(stats[:, ds(t, 1), :].rearrange("p o s -> p (o s)"),
                                       nat(x)[:, ds(t, 1), :].rearrange("p o d -> p (o d)")).then_inc(measured, 1)
                dve.wait_ge(measured, NT)
                link = link_on(dve, step)
                link(nc.vector.tensor_tensor(mean[:], stats[:, :, 1], stats[:, :, 4], ALU.add))
                link(nc.vector.tensor_scalar(mean[:], mean[:], 0.5, None, ALU.mult))
                link(nc.vector.tensor_tensor(tmp[:], stats[:, :, 1], stats[:, :, 4], ALU.subtract))
                link(nc.vector.tensor_tensor(tmp[:], tmp[:], tmp[:], ALU.mult))
                link(nc.vector.tensor_tensor(var[:], stats[:, :, 2], stats[:, :, 5], ALU.add))
                link(nc.vector.tensor_scalar(var[:], var[:], 1.0 / D, EPS, ALU.mult, ALU.add))
                link(nc.vector.scalar_tensor_tensor(out=var[:], in0=tmp[:], scalar=0.25, in1=var[:],
                                                    op0=ALU.mult, op1=ALU.add))
                dve.wait_ge(rooted, 1)
                link(nc.vector.reciprocal(rstd[:], std[:]))
                link(nc.vector.scalar_tensor_tensor(out=shift[:], in0=mean[:], scalar=-1.0, in1=rstd[:],
                                                    op0=ALU.mult, op1=ALU.mult))
                with dve.Fori(0, ROUNDS) as i:
                    for u in range(U):
                        t = i * U + u
                        dve.wait_ge(kept, i * U + u + 1)
                        nc.vector.tensor_scalar(st[u][:], nat(x)[:, ds(t, 1), :].rearrange("p o d -> p (o d)"),
                                                rstd[:, ds(t, 1)], shift[:, ds(t, 1)],
                                                ALU.mult, ALU.add).then_inc(normed, 1)

            @block.scalar
            def _(act):
                act.wait_ge(step, 7)
                nc.scalar.activation(std[:], var[:], ACT.Sqrt).then_inc(rooted, 1)
                act.sem_inc(kept, U)
                with act.Fori(0, ROUNDS) as i:
                    for u in range(U):
                        t = i * U + u
                        wait_alone(act, turned, i * U + u + 1)
                        if xn is not None:
                            ins = nc.scalar.copy(nat(xn)[:, ds(t, 1), :].rearrange("p o d -> p (o d)"), st[u][:])
                        if xt is not None:
                            ins = nc.scalar.copy(tr(xt)[:, :, ds(t * P, P)],
                                                 ps[u][:, 0:D].rearrange("p (k n) -> p k n", k=2))
                        ins.then_inc(kept, 1)

            @block.tensor
            def _(pe):
                with pe.Fori(0, ROUNDS) as i:
                    for u in range(U):
                        pe.wait_ge(normed, i * U + u + 1)
                        if xt is None:
                            pe.nop(nofuse=True).then_inc(turned, 1)
                            continue
                        nc.tensor.transpose(ps[u][:, 0:P], st[u][:, 0:P], kit.ident[:])
                        nc.tensor.transpose(ps[u][:, P:D], st[u][:, P:D], kit.ident[:]).then_inc(turned, 1)


def project_t(nc, nm, sources, dst, fc, func=ACT.Identity, bias=None):
    terms = [(src, kc, w, k) for src, kc, w in sources for k in range(kc)]
    with ExitStack() as c:
        ps = [[c.enter_context(nc.psum_tensor(f"{nm}_ps{h}{f}", [P, 512], F32)) for f in range(fc)] for h in range(2)]
        multiplied, read = sems(nc, c, nm, "multiplied read")
        with nc.Block() as block:
            @block.tensor
            def _(pe):
                with pe.Fori(0, NP // CHUNK // 2) as i:
                    for h in range(2):
                        for f in range(fc):
                            pe.wait_ge(read, (i * 2 + h) * fc + f + 1)
                            for n, (src, kc, w, k) in enumerate(terms):
                                mm = nc.tensor.matmul(ps[h][f][:, 0:CHUNK], w[:, k, f * P:(f + 1) * P],
                                                      tr(src, kc)[:, k, ds((i * 2 + h) * CHUNK, CHUNK)],
                                                      start=(n == 0), stop=(n == len(terms) - 1))
                            mm.then_inc(multiplied, 1)

            @block.scalar
            def _(act):
                act.sem_inc(read, 2 * fc)
                with act.Fori(0, NP // CHUNK // 2) as i:
                    for h in range(2):
                        for f in range(fc):
                            act.wait_ge(multiplied, (i * 2 + h) * fc + f + 1)
                            nc.scalar.activation(tr(dst, fc)[:, f, ds((i * 2 + h) * CHUNK, CHUNK)],
                                                 ps[h][f][:, 0:CHUNK], func,
                                                 bias=(bias[:, f:f + 1] if bias is not None else 0.0)).then_inc(read, 1)


def write_table(nc, kit, nm, src, kc, scratch, table):
    W = kc * P
    rows = scratch[:, 0:NT * W].rearrange("p (t d) -> p t d", t=NT)
    with ExitStack() as c:
        st = [c.enter_context(nc.sbuf_tensor(f"{nm}_st{u}", [P, kc, P], F32)) for u in range(U)]
        ps = [c.enter_context(nc.psum_tensor(f"{nm}_ps{u}", [P, 512], F32)) for u in range(U)]
        staged, turned, copied, stored = sems(nc, c, nm, "staged turned copied stored")
        with nc.Block() as block:
            @block.vector
            def _(dve):
                with dve.Fori(0, ROUNDS) as i:
                    for u in range(U):
                        dve.wait_ge(turned, i * U + u + 1)
                        nc.vector.tensor_copy(st[u][:], tr(src, kc)[:, :, ds((i * U + u) * P, P)]).then_inc(staged, 1)

            @block.tensor
            def _(pe):
                pe.sem_inc(turned, U)
                with pe.Fori(0, ROUNDS) as i:
                    for u in range(U):
                        pe.wait_ge(staged, i * U + u + 1)
                        pe.wait_ge(copied, i * U + u + 1)
                        for k in range(kc):
                            mm = nc.tensor.transpose(ps[u][:, k * P:(k + 1) * P], st[u][:, k, :], kit.ident[:])
                        mm.then_inc(turned, 1)

            @block.scalar
            def _(act):
                act.sem_inc(copied, U)
                with act.Fori(0, ROUNDS) as i:
                    for u in range(U):
                        act.wait_ge(turned, i * U + u + 1 + U)
                        nc.scalar.copy(rows[:, ds(i * U + u, 1), :].rearrange("p o d -> p (o d)"),
                                       ps[u][:, 0:W]).then_inc(copied, 1)

            @block.sync
            def _(sp):
                with sp.Fori(0, ROUNDS) as i:
                    sp.wait_ge(copied, i * U + 2 * U)
                    sp.dma_start(table.rearrange("(t p) d -> p t d", p=P)[:, ds(i * U, U), :],
                                 rows[:, ds(i * U, U), :]).then_inc(stored, 16)
                sp.wait_ge(stored, 16 * ROUNDS)


def aggregate_t(nc, kit, nm, e, table, kc, acc, weighted=False):
    W = kc * P
    rounds = e.groups // R
    with ExitStack() as c:
        idx = [c.enter_context(nc.sbuf_tensor(f"{nm}_idx{a}", [P, R], I32)) for a in range(DEEP)]
        rows = [c.enter_context(nc.sbuf_tensor(f"{nm}_rows{a}", [P, R, W], F32)) for a in range(DEEP)]
        hot = [c.enter_context(nc.sbuf_tensor(f"{nm}_hot{a}", [P, R, P], F32)) for a in range(2)]
        ps = [[c.enter_context(nc.psum_tensor(f"{nm}_ps{a}{u}", [P, 512], F32)) for u in range(R)] for a in range(2)]
        indexed, selected, matched, multiplied, added = sems(nc, c, nm, "indexed selected matched multiplied added")
        gathered = gather_sems(nc, nm, "gathered", DEEP)
        with nc.Block() as block:
            @block.scalar
            def _(act):
                def step(r):
                    m = r.off(2)
                    if m.there:
                        if m.looped or m.c >= DEEP:
                            wait_alone(act, multiplied, (m.n + 1 - DEEP) * R)
                        nc.scalar.copy(idx[m.slot][:], e.src[:, ds(m.n * R, R)]).then_inc(indexed, 1)
                rolling(act, step, rounds)

            @block.gpsimd
            def _(pool):
                def step(r):
                    m = r.off(2)
                    if m.there:
                        wait_alone(pool, indexed, m.n + 1)
                        for u in range(R):
                            nc.gpsimd.indirect_dma_start(rows[m.slot][:, u, :], None, table,
                                                         bass.IndirectOffsetOnAxis(ap=idx[m.slot][:, u:u + 1], axis=0)
                                                         ).then_inc(gathered[m.slot], 16)
                rolling(pool, step, rounds)

            @block.tensor
            def _(pe):
                def step(r):
                    if r.there:
                        pe.wait_ge(gathered[r.slot], (r.turn + 1) * 16 * R)
                        pe.wait_ge(matched, r.n + 1)
                        if r.looped or r.c >= 2:
                            pe.wait_ge(added, (r.n - 1) * R + 1)
                        for u in range(R):
                            for k in range(kc):
                                mm = nc.tensor.matmul(ps[r.slot % 2][u][:, k * P:(k + 1) * P],
                                                      rows[r.slot][:, u, k * P:(k + 1) * P], hot[r.slot % 2][:, u, :],
                                                      start=True, stop=True)
                            mm.then_inc(multiplied, 1)
                rolling(pe, step, rounds)

            @block.vector
            def _(dve):
                nc.vector.memset(acc[:, 0:kc * NP], 0.0).then_inc(added, 1)

                def step(r):
                    old, nxt = r.off(-1), r.off(1)
                    if nxt.there:
                        if nxt.looped or nxt.c >= 2:
                            dve.wait_ge(multiplied, (nxt.n - 1) * R)
                        nc.vector.tensor_tensor(hot[nxt.slot % 2][:], kit.iota[:, None, :].broadcast_to([P, R, P]),
                                                e.rec[:, ds(nxt.n * R, R), 1:2].broadcast_to([P, R, P]),
                                                ALU.is_equal).then_inc(selected if weighted else matched, 1)
                    for u in range(R):
                        if old.there:
                            blk = dve.value_load(e.blk[0:1, ds(old.n * R + u, 1)], min_val=0, max_val=NT - 1)
                            to = tr(acc, kc)[:, :, ds(blk * P, P)]
                            if u == 0:
                                dve.wait_ge(multiplied, (old.n + 1) * R)
                            dve.wait_ge(added, old.n * R + u + 1)
                            nc.vector.tensor_tensor(to, to, ps[old.slot % 2][u][:, 0:W].rearrange(
                                "p (k n) -> p k n", k=kc), ALU.add).then_inc(added, 1)
                        if weighted and u == 0 and nxt.there:
                            dve.wait_ge(selected, nxt.n + 1)
                            nc.vector.tensor_tensor(hot[nxt.slot % 2][:], hot[nxt.slot % 2][:],
                                                    e.rec[:, ds(nxt.n * R, R), 2:3].broadcast_to([P, R, P]),
                                                    ALU.mult).then_inc(matched, 1)
                rolling(dve, step, rounds)


def turn(nc, kit, nm, src, dst):
    with ExitStack() as c:
        st = [c.enter_context(nc.sbuf_tensor(f"{nm}_st{u}", [P, D], F32)) for u in range(U)]
        ps = [c.enter_context(nc.psum_tensor(f"{nm}_ps{u}", [P, 512], F32)) for u in range(U)]
        staged, turned, copied = sems(nc, c, nm, "staged turned copied")
        with nc.Block() as block:
            @block.vector
            def _(dve):
                with dve.Fori(0, ROUNDS) as i:
                    for u in range(U):
                        dve.wait_ge(turned, i * U + u + 1)
                        nc.vector.tensor_copy(st[u][:], src[:, ds(i * U + u, 1), :].rearrange("p o d -> p (o d)")
                                              ).then_inc(staged, 1)

            @block.tensor
            def _(pe):
                pe.sem_inc(turned, U)
                with pe.Fori(0, ROUNDS) as i:
                    for u in range(U):
                        pe.wait_ge(staged, i * U + u + 1)
                        pe.wait_ge(copied, i * U + u + 1)
                        nc.tensor.transpose(ps[u][:, 0:P], st[u][:, 0:P], kit.ident[:])
                        nc.tensor.transpose(ps[u][:, P:D], st[u][:, P:D], kit.ident[:]).then_inc(turned, 1)

            @block.scalar
            def _(act):
                act.sem_inc(copied, U)
                with act.Fori(0, ROUNDS) as i:
                    for u in range(U):
                        wait_alone(act, turned, i * U + u + 1 + U)
                        nc.scalar.copy(dst[:, :, ds((i * U + u) * P, P)],
                                       ps[u][:, 0:D].rearrange("p (k n) -> p k n", k=2)).then_inc(copied, 1)


def add_projection(nc, nm, src, w, to, bias=None, fresh=False, gate=None):
    kc, width = w.shape[1], w.shape[2]
    with ExitStack() as c:
        st = [c.enter_context(nc.sbuf_tensor(f"{nm}_st{u}", [P, kc, P], F32)) for u in range(U)]
        ps = [c.enter_context(nc.psum_tensor(f"{nm}_ps{u}", [P, 512], F32)) for u in range(U)]
        staged, multiplied, added, biased = sems(nc, c, nm, "staged multiplied added biased")
        with nc.Block() as block:
            @block.scalar
            def _(act):
                with act.Fori(0, ROUNDS) as i:
                    for u in range(U):
                        act.wait_ge(multiplied, i * U + u + 1)
                        nc.scalar.copy(st[u][:], tr(src, kc)[:, :, ds((i * U + u) * P, P)]).then_inc(staged, 1)

            @block.tensor
            def _(pe):
                pe.sem_inc(multiplied, U)
                with pe.Fori(0, ROUNDS) as i:
                    for u in range(U):
                        pe.wait_ge(staged, i * U + u + 1)
                        pe.wait_ge(added, i * U + u + 1)
                        for k in range(kc):
                            mm = nc.tensor.matmul(ps[u][:, 0:width], st[u][:, k, :], w[:, k, :],
                                                  start=(k == 0), stop=(k == kc - 1))
                        mm.then_inc(multiplied, 1)

            @block.vector
            def _(dve):
                if fresh and bias is None:
                    nc.vector.memset(to, 0.0).then_inc(biased, 1)
                elif fresh:
                    nc.vector.tensor_copy(to, bias[:, None, :].broadcast_to([P, NT, width])).then_inc(biased, 1)
                elif bias is not None:
                    nc.vector.tensor_tensor(to, to, bias[:, None, :].broadcast_to([P, NT, width]),
                                            ALU.add).then_inc(biased, 1)
                if fresh or bias is not None:
                    dve.wait_ge(biased, 1)
                dve.sem_inc(added, U)
                with dve.Fori(0, ROUNDS) as i:
                    for u in range(U):
                        dve.wait_ge(multiplied, i * U + u + 1 + U)
                        part = to[:, ds(i * U + u, 1), :].rearrange("p o d -> p (o d)")
                        if gate is None:
                            nc.vector.tensor_tensor(part, part, ps[u][:, 0:width], ALU.add).then_inc(added, 1)
                        else:
                            nc.vector.scalar_tensor_tensor(out=part, in0=ps[u][:, 0:width],
                                                           scalar=gate[:, ds(i * U + u, 1)], in1=part,
                                                           op0=ALU.mult, op1=ALU.add).then_inc(added, 1)


def in_degrees(nc, kit, nm, counts, rows, beside):
    C = counts[0][0].shape[0] // rows
    B = 16
    with ExitStack() as c:
        def sb(name, shape, dt=F32):
            return c.enter_context(nc.sbuf_tensor(f"{nm}_{name}", shape, dt))
        dst_i = [sb(f"dst{n}", [rows, C], I32) for n in range(len(counts))]
        work_i = sb("work", [rows, C], I32)
        lo, hi = sb("lo", [rows, C]), sb("hi", [rows, C])
        is_lo = [sb(f"is_lo{h}", [rows, B, P], BF16) for h in range(2)]
        is_hi = [sb(f"is_hi{h}", [rows, B, NT], BF16) for h in range(2)]
        ps = c.enter_context(nc.psum_tensor(f"{nm}_ps", [P, 512], F32))
        zero = sb("zero", [P, P])
        loaded, step, split, matched, used = sems(nc, c, nm, "loaded step split matched used")
        rounds = C // B
        assert rounds % 2 == 1
        with nc.Block() as block:
            beside[0].part(block, *beside[1:])

            @block.sync
            def _(sp):
                for to, (dst, _) in zip(dst_i, counts):
                    sp.dma_start(to[:], dst.rearrange("(p c) -> p c", p=rows)).then_inc(loaded, 16)

            @block.vector
            def _(dve):
                dve.wait_ge(loaded, 16 * len(counts))
                link = link_on(dve, step)
                link(nc.vector.memset(zero[:], 0.0))
                for n, (dst, deg) in enumerate(counts):
                    base = n * rounds
                    link(nc.vector.tensor_scalar(work_i[:], dst_i[n][:], 7, None, ALU.arith_shift_right))
                    link(nc.vector.tensor_copy(hi[:], work_i[:]))
                    link(nc.vector.tensor_scalar(work_i[:], dst_i[n][:], 127, None, ALU.bitwise_and))
                    link(nc.vector.tensor_copy(lo[:], work_i[:]))
                    nc.vector.nop(nofuse=True).then_inc(split, 1)

                    def match(i, h):
                        for part, width, to in ((lo, P, is_lo[h]), (hi, NT, is_hi[h])):
                            ins = nc.vector.tensor_tensor(
                                to[:], part[:, ds(i * B, B)][:, :, None].broadcast_to([rows, B, width]),
                                kit.iota[0:rows, None, 0:width].broadcast_to([rows, B, width]), ALU.is_equal)
                        ins.then_inc(matched, 1)
                    match(0, 0)
                    with dve.Fori(0, (rounds - 1) // 2) as i:
                        for h in (1, 0):
                            j = i * 2 + (2 - h)
                            dve.wait_ge(used, base + j)
                            match(j, h)
                    dve.wait_ge(used, base + rounds + 1)
                    link(nc.vector.tensor_copy(deg[:], ps[:, 0:NT]))

            @block.tensor
            def _(pe):
                pe.sem_inc(used, 1)
                for n in range(len(counts)):
                    pe.wait_ge(split, n + 1)
                    nc.tensor.matmul(ps[:, 0:NT], zero[:], zero[:, 0:NT], start=True, stop=False)

                    def count(i, h, last=False):
                        pe.wait_ge(matched, n * rounds + i + 1)
                        for b in range(B):
                            mm = nc.tensor.matmul(ps[:, 0:NT], is_lo[h][:, b, :], is_hi[h][:, b, :], start=False,
                                                  stop=(last and b == B - 1))
                        mm.then_inc(used, 1)
                    with pe.Fori(0, (rounds - 1) // 2) as i:
                        for h in range(2):
                            count(i * 2 + h, h)
                    count(rounds - 1, 0, last=True)


def rows_to_all(nc, kit, nm, col, out):
    with ExitStack() as c:
        diag = [c.enter_context(nc.sbuf_tensor(f"{nm}_diag{u}", [P, P], F32)) for u in range(U)]
        ps = [c.enter_context(nc.psum_tensor(f"{nm}_ps{u}", [P, 512], F32)) for u in range(U)]
        made, multiplied, copied = sems(nc, c, nm, "made multiplied copied")
        with nc.Block() as block:
            @block.vector
            def _(dve):
                with dve.Fori(0, ROUNDS) as i:
                    for u in range(U):
                        dve.wait_ge(multiplied, i * U + u + 1)
                        nc.vector.tensor_scalar(diag[u][:], kit.ident[:], col[:, ds(i * U + u, 1)], None,
                                                ALU.mult).then_inc(made, 1)

            @block.tensor
            def _(pe):
                pe.sem_inc(multiplied, U)
                with pe.Fori(0, ROUNDS) as i:
                    for u in range(U):
                        pe.wait_ge(made, i * U + u + 1)
                        pe.wait_ge(copied, i * U + u + 1)
                        nc.tensor.matmul(ps[u][:, 0:P], kit.ones[:], diag[u][:], start=True,
                                         stop=True).then_inc(multiplied, 1)

            @block.scalar
            def _(act):
                act.sem_inc(copied, U)
                with act.Fori(0, ROUNDS) as i:
                    for u in range(U):
                        act.wait_ge(multiplied, i * U + u + 1 + U)
                        nc.scalar.copy(out[:, ds((i * U + u) * P, P)], ps[u][:, 0:P]).then_inc(copied, 1)


def load(nc, nm, pairs):
    with ExitStack() as c:
        loaded, = sems(nc, c, nm, "loaded")
        with nc.Block() as block:
            @block.sync
            def _(sp):
                for to, src in pairs:
                    sp.dma_start(to, src).then_inc(loaded, 16)
                sp.wait_ge(loaded, 16 * len(pairs))


def on_vector(nc, nm, steps):
    with ExitStack() as c:
        step, = sems(nc, c, nm, "step")
        with nc.Block() as block:
            @block.vector
            def _(dve):
                steps(link_on(dve, step))


def chunks(ap):
    return ap.rearrange("(k p) n -> p k n", p=P)


def gcn_stage(nc, kit, A, x, bufs, e, table):
    _, b2, b3, b4 = bufs
    with ExitStack() as c:
        def sb(name, shape, dt=F32):
            return c.enter_context(nc.sbuf_tensor(f"gcn_{name}", shape, dt))
        w1, w2 = sb("w1", [P, 2, P]), sb("w2", [P, 1, D])
        bias1, bias2 = sb("b1", [P, 1]), sb("b2", [P, D])
        deg, dinv, dall = kit.deg_in, sb("dinv", [P, NT]), sb("dall", [P, NP])
        load(nc, "gcn_load", [(w1[:], chunks(A["L0_gnn_W1"])), (w2[:], chunks(A["L0_gnn_W2"])),
                              (bias1[:], A["L0_gnn_b1"].rearrange("(p o) -> p o", o=1)),
                              (bias2[:], row_to_all(A["L0_gnn_b2"]))])
        layer_norm(nc, kit, "gcn_ln", x, xt=b2)
        with ExitStack() as cc:
            step, rooted = sems(nc, cc, "gcn_dinv", "step rooted")
            with nc.Block() as block:
                @block.vector
                def _(dve):
                    nc.vector.tensor_scalar(dinv[:], deg[:], 1.0, None, ALU.add).then_inc(step, 1)
                    dve.wait_ge(rooted, 1)
                    nc.vector.reciprocal(dinv[:], dinv[:]).then_inc(step, 1)
                    dve.wait_ge(step, 2)

                @block.scalar
                def _(act):
                    act.wait_ge(step, 1)
                    nc.scalar.activation(dinv[:], dinv[:], ACT.Sqrt).then_inc(rooted, 1)
        rows_to_all(nc, kit, "gcn_dall", dinv, dall)
        one, agg = b3[:, 0:NP], b4[:, 0:NP]
        project_t(nc, "gcn_h", [(b2, 2, w1)], b3, 1)
        on_vector(nc, "gcn_v1", lambda link: link(nc.vector.tensor_tensor(one, one, dall[:], ALU.mult)))
        write_table(nc, kit, "gcn_t1", b3, 1, b4, table)
        aggregate_t(nc, kit, "gcn_a1", e, table, 1, b4)

        def between(link):
            link(nc.vector.tensor_tensor(one, one, agg, ALU.add))
            link(nc.vector.tensor_tensor(one, one, dall[:], ALU.mult))
            link(nc.vector.tensor_scalar(one, one, bias1[:], 0.0, ALU.add, ALU.max))
            link(nc.vector.tensor_tensor(one, one, dall[:], ALU.mult))
        on_vector(nc, "gcn_v2", between)
        write_table(nc, kit, "gcn_t2", b3, 1, b4, table)
        aggregate_t(nc, kit, "gcn_a2", e, table, 1, b4)

        def after(link):
            link(nc.vector.tensor_tensor(one, one, agg, ALU.add))
            link(nc.vector.tensor_tensor(one, one, dall[:], ALU.mult))
        on_vector(nc, "gcn_v3", after)
        add_projection(nc, "gcn_out", b3, w2, nat(x), bias2)


def per_node(ap, n):
    return ap[:, :, None].broadcast_to([P, ap.shape[1], n])


def softmax_rows(nc, nm, z, n):
    tiles = z.shape[1]
    with ExitStack() as c:
        m, s = (c.enter_context(nc.sbuf_tensor(f"{nm}_{x}", [P, tiles], F32)) for x in "ms")
        step, raised = sems(nc, c, nm, "step raised")
        with nc.Block() as block:
            @block.vector
            def _(dve):
                link = link_on(dve, step)
                link(nc.vector.tensor_reduce(m[:], z, AX_X, ALU.max))
                link(nc.vector.tensor_tensor(z, z, per_node(m[:], n), ALU.subtract))
                dve.wait_ge(raised, 1)
                link(nc.vector.tensor_reduce(s[:], z, AX_X, ALU.add))
                link(nc.vector.reciprocal(s[:], s[:]))
                link(nc.vector.tensor_tensor(z, z, per_node(s[:], n), ALU.mult))

            @block.scalar
            def _(act):
                act.wait_ge(step, 2)
                nc.scalar.activation(z, z, ACT.Exp).then_inc(raised, 1)


def add_gated_bias(nc, kit, nm, gates, b, x):
    E = b.shape[0]
    with ExitStack() as c:
        gt = [c.enter_context(nc.sbuf_tensor(f"{nm}_gt{u}", [E, P], F32)) for u in range(U)]
        st = [c.enter_context(nc.sbuf_tensor(f"{nm}_st{u}", [P, E], F32)) for u in range(U)]
        ps = [c.enter_context(nc.psum_tensor(f"{nm}_ps{u}", [P, 512], F32)) for u in range(U)]
        staged, turned, copied, multiplied, added = sems(nc, c, nm, "staged turned copied multiplied added")
        with nc.Block() as block:
            @block.vector
            def _(dve):
                dve.sem_inc(added, U)
                with dve.Fori(0, ROUNDS) as i:
                    for u in range(U):
                        dve.wait_ge(multiplied, i * U + u + 1)
                        nc.vector.tensor_copy(st[u][:], gates[:, ds(i * U + u, 1), :].rearrange("p o e -> p (o e)")
                                              ).then_inc(staged, 1)
                    for u in range(U):
                        dve.wait_ge(multiplied, i * U + u + 1 + U)
                        part = nat(x)[:, ds(i * U + u, 1), :].rearrange("p o d -> p (o d)")
                        nc.vector.tensor_tensor(part, part, ps[u][:, 0:D], ALU.add).then_inc(added, 1)

            @block.tensor
            def _(pe):
                pe.sem_inc(multiplied, U)
                with pe.Fori(0, ROUNDS) as i:
                    for u in range(U):
                        pe.wait_ge(staged, i * U + u + 1)
                        pe.wait_ge(added, i * U + u + 1)
                        nc.tensor.transpose(ps[u][0:E, D:D + P], st[u][:], kit.ident[:]).then_inc(turned, 1)
                    for u in range(U):
                        pe.wait_ge(copied, i * U + u + 1)
                        nc.tensor.matmul(ps[u][:, 0:D], gt[u][:], b, start=True, stop=True).then_inc(multiplied, 1)

            @block.scalar
            def _(act):
                with act.Fori(0, ROUNDS) as i:
                    for u in range(U):
                        act.wait_ge(turned, i * U + u + 1)
                        nc.scalar.copy(gt[u][:], ps[u][0:E, D:D + P]).then_inc(copied, 1)


class Mid:

    def __init__(self, w, kc, fc, func, bias, scale=None):
        self.w, self.kc, self.fc, self.func, self.bias, self.scale = w, kc, fc, func, bias, scale


def expert_mlps(nc, nm, src, experts, mids, last, gates, x, pick=None, beside=None):
    SPAN = U * P
    kl = mids[-1].fc
    groups = sum(2 * m.fc for m in mids)
    RING = 4
    assert groups % RING == 0
    with ExitStack() as c:
        wm = [[c.enter_context(nc.sbuf_tensor(f"{nm}_w{n}_{q}", [P, m.kc, m.fc * P], F32)) for n, m in enumerate(mids)]
              for q in range(2)]
        wl = [c.enter_context(nc.sbuf_tensor(f"{nm}_wl_{q}", [P, kl, D], F32)) for q in range(2)]
        h = [c.enter_context(nc.sbuf_tensor(f"{nm}_h{n}", [P, m.fc, SPAN], F32)) for n, m in enumerate(mids)]
        ps = [c.enter_context(nc.psum_tensor(f"{nm}_ps{r}", [P, 512], F32)) for r in range(RING)]
        py = [c.enter_context(nc.psum_tensor(f"{nm}_py{r}", [P, 512], F32)) for r in range(4)]
        out_ps = [py[u % 4][:, 0:D] for u in range(U)]
        loaded = sems(nc, c, nm, "loaded0 loaded1")
        multiplied, read, finished, added, left = sems(nc, c, nm, "multiplied read finished added left")

        def experts_loop(eng, body):
            if experts == 2:
                for q in range(2):
                    body(0, q)
            else:
                with eng.Fori(0, experts // 2) as i:
                    for q in range(2):
                        body(i, q)

        with nc.Block() as block:
            if beside is not None:
                block.gpsimd(beside)

            @block.sync
            def _(sp):
                def body(i, q):
                    e = i * 2 + q
                    at = pick(sp, e) if pick else e
                    sp.wait_ge(left, e + 1)
                    for n, m in enumerate(mids):
                        sp.dma_start(wm[q][n][:], m.w(at).rearrange("o (k p) f -> p (o k) f", p=P)).then_inc(loaded[q], 16)
                    sp.dma_start(wl[q][:], last(at).rearrange("o (k p) f -> p (o k) f", p=P)).then_inc(loaded[q], 16)
                experts_loop(sp, body)

            @block.tensor
            def _(pe):
                pe.sem_inc(left, 2)

                def body(i, q):
                    wait_alone(pe, loaded[q], (i + 1) * 16 * (len(mids) + 1))
                    with pe.Fori(0, ROUNDS) as j:
                        r = (i * 2 + q) * ROUNDS + j
                        g = 0
                        for n, m in enumerate(mids):
                            for half in range(2):
                                if n:
                                    pe.wait_ge(read, r * groups + RING + g0 + (half + 1) * mids[n - 1].fc)
                                for f in range(m.fc):
                                    pe.wait_ge(read, r * groups + g + 1)
                                    for k in range(m.kc):
                                        rhs = (tr(src)[:, k, ds((j * 2 + half) * CHUNK, CHUNK)] if n == 0
                                               else h[n - 1][:, k, half * CHUNK:(half + 1) * CHUNK])
                                        mm = nc.tensor.matmul(ps[g % RING][:, 0:CHUNK],
                                                              wm[q][n][:, k, f * P:(f + 1) * P], rhs,
                                                              start=(k == 0), stop=(k == m.kc - 1))
                                    mm.then_inc(multiplied, 1)
                                    g += 1
                            g0 = g - 2 * m.fc
                        for u in range(U):
                            half = 0 if (u + 1) * P <= CHUNK else 1
                            pe.wait_ge(read, r * groups + RING + g0 + (half + 1) * kl)
                            pe.wait_ge(added, r * U + (U if u == 0 else U + 1 if u == 4 else u + 1))
                            for k in range(kl):
                                mm = nc.tensor.matmul(out_ps[u], h[-1][:, k, u * P:(u + 1) * P], wl[q][:, k, :],
                                                      start=(k == 0), stop=(k == kl - 1))
                            mm.then_inc(finished, 1)
                    pe.drain().then_inc(left, 1)
                experts_loop(pe, body)

            @block.scalar
            def _(act):
                act.sem_inc(read, RING)

                def body(i, q):
                    with act.Fori(0, ROUNDS) as j:
                        r = (i * 2 + q) * ROUNDS + j
                        g = 0
                        for n, m in enumerate(mids):
                            for half in range(2):
                                for f in range(m.fc):
                                    wait_alone(act, multiplied, r * groups + g + 1)
                                    e = i * 2 + q
                                    bias = m.bias[:, ds(e, 1), f:f + 1].rearrange("p o f -> p (o f)")
                                    scale = (m.scale[:, ds(e, 1), f:f + 1].rearrange("p o f -> p (o f)")
                                             if m.scale is not None else 1.0)
                                    nc.scalar.activation(h[n][:, f, half * CHUNK:(half + 1) * CHUNK],
                                                         ps[g % RING][:, 0:CHUNK], m.func, bias=bias,
                                                         scale=scale).then_inc(read, 1)
                                    g += 1
                experts_loop(act, body)

            @block.vector
            def _(dve):
                dve.sem_inc(added, U)

                def body(i, q):
                    with dve.Fori(0, ROUNDS) as j:
                        r = (i * 2 + q) * ROUNDS + j
                        e = i * 2 + q
                        for u in range(U):
                            t = j * U + u
                            dve.wait_ge(finished, r * U + u + 1)
                            dve.wait_ge(added, r * U + u + 1)
                            part = nat(x)[:, ds(t, 1), :].rearrange("p o d -> p (o d)")
                            gate = gates[:, ds(t, 1), ds(e, 1)].rearrange("p o e -> p (o e)")
                            nc.vector.scalar_tensor_tensor(out=part, in0=out_ps[u], scalar=gate, in1=part,
                                                           op0=ALU.mult, op1=ALU.add).then_inc(added, 1)
                experts_loop(dve, body)


def expert_columns(ap2d, fc):
    return ap2d.rearrange("e (f p) -> p e f", f=fc)


def soft_moe_stage(nc, kit, A, x, bufs, beside):
    b2 = bufs[1]
    E, F = A["L1_ffn_b1"].shape
    fc = F // P
    BN_EPS = 0.001
    with ExitStack() as c:
        def sb(name, shape, dt=F32):
            return c.enter_context(nc.sbuf_tensor(f"soft_{name}", shape, dt))
        wr, br, bo = sb("wr", [P, 2, E]), sb("br", [P, E]), sb("bo", [E, D])
        gates = sb("gates", [P, NT, E])
        par = {n: sb(n, [P, E, fc]) for n in "b1 g1 be1 m1 v1 b2 g2 be2 m2 v2".split()}
        layer_norm(nc, kit, "soft_ln", x, xt=b2)
        with nc.allow_non_contiguous_dma(reason="short columns"):
            load(nc, "soft_load",
                 [(wr[:], chunks(A["L1_ffn_Wr"])), (br[:], row_to_all(A["L1_ffn_br"])), (bo[:], A["L1_ffn_bo"])]
                 + [(t[:, e, :], column(A[f"L1_ffn_{n}"][e], fc)) for n, t in par.items() for e in range(E)])
        with ExitStack() as cc:
            step, rooted = sems(nc, cc, "soft_bn", "step rooted")
            with nc.Block() as block:
                @block.vector
                def _(dve):
                    link = link_on(dve, step)
                    for n in "12":
                        v = par["v" + n]
                        link(nc.vector.tensor_scalar(v[:], v[:], BN_EPS, None, ALU.add))
                    dve.wait_ge(rooted, 2)
                    for n in "12":
                        v, g, b, m, be = (par[k + n] for k in ("v", "g", "b", "m", "be"))
                        link(nc.vector.reciprocal(v[:], v[:]))
                        link(nc.vector.tensor_tensor(v[:], v[:], g[:], ALU.mult))
                        link(nc.vector.tensor_tensor(b[:], b[:], m[:], ALU.subtract))
                        link(nc.vector.tensor_tensor(b[:], b[:], v[:], ALU.mult))
                        link(nc.vector.tensor_tensor(b[:], b[:], be[:], ALU.add))

                @block.scalar
                def _(act):
                    for k, n in enumerate("12"):
                        act.wait_ge(step, k + 1)
                        nc.scalar.activation(par["v" + n][:], par["v" + n][:], ACT.Sqrt).then_inc(rooted, 1)
        add_projection(nc, "soft_gate", b2, wr, gates[:], br, fresh=True)
        softmax_rows(nc, "soft_sm", gates[:], E)
        add_gated_bias(nc, kit, "soft_bo", gates, bo[:], x)
        of = lambda name: lambda e: A[name][ds(e, 1), :, :]
        expert_mlps(nc, "soft", b2, E, [Mid(of("L1_ffn_W1"), 2, fc, ACT.Relu, par["b1"], par["v1"]),
                                        Mid(of("L1_ffn_W2"), fc, fc, ACT.Relu, par["b2"], par["v2"])],
                    of("L1_ffn_Wo"), gates, x, beside=beside)


BIG = 1e30


class EdgeAttention:

    def __init__(self, edges, index, keys, values, q, heads, dv, dots, spare, score_at=0, held=None):
        self.edges, self.index, self.keys, self.values, self.q = edges, index, keys, values, q
        self.heads, self.dv, self.dots, self.score_at, self.held = heads, dv, dots, score_at, held
        self.spare = spare

    def rows(self, width):
        return [self.spare[:, a * R * width:(a + 1) * R * width].rearrange("p (r w) -> p r w", r=R)
                for a in range(DEEP)]


def edge_scores(nc, kit, nm, at, scores, top):
    e, H, dv = at.edges, at.heads, at.dv
    WQ, WK = at.q.shape[2], at.keys.shape[1]
    rounds = e.groups // R
    assert rounds % DEEP == 0
    with ExitStack() as c:
        def many(count, name, shape, dt=F32):
            return [c.enter_context(nc.sbuf_tensor(f"{nm}_{name}{a}", shape, dt)) for a in range(count)]
        idx, rows = many(DEEP, "idx", [P, R], I32), at.rows(WK)
        hot, hot_t = many(DEEP, "hot", [P, R, P]), many(2, "hot_t", [P, R, P])
        off, sc = many(DEEP, "off", [P, R, P], BF16), many(DEEP, "sc", [P, R, H])
        qs, tmp = many(2, "qs", [P, R, WQ]), many(2, "tmp", [P, R, WQ])
        big, = many(1, "big", [P, H, P], BF16)
        row_max, = many(1, "row_max", [P, R, H])
        is_tile, = many(1, "is_tile", [P, R, NT])
        by_tile, = many(1, "by_tile", [P, NT, H, R])
        round_max, = many(1, "round_max", [P, NT, H])
        pt = [c.enter_context(nc.psum_tensor(f"{nm}_pt{a}", [P, 512], F32)) for a in range(2)]
        pq = c.enter_context(nc.psum_tensor(f"{nm}_pq", [P, max(512, R * WQ)], F32))
        pm = [c.enter_context(nc.psum_tensor(f"{nm}_pm{u}", [P, 512], F32)) for u in range(R)]
        pq_v = pq[:, 0:R * WQ].rearrange("p (r w) -> p r w", r=R)
        (indexed, matched, turned, copied, shifted, spread, q_copied, part, scored, kept, broadcast, reduced, selected,
         limited, clipped, folded, raised, chain) = sems(
             nc, c, nm, "indexed matched turned copied shifted spread q_copied part scored kept broadcast reduced "
             "selected limited clipped folded raised chain")
        gathered = gather_sems(nc, nm, "gathered", DEEP)
        with nc.Block() as block:
            @block.scalar
            def _(act):
                act.sem_inc(kept, DEEP)

                def step(r):
                    m = r.off(-1)
                    if m.there:
                        act.wait_ge(spread, m.n + 1)
                        nc.scalar.activation(qs[m.slot % 2][:], pq_v, ACT.Copy).then_inc(q_copied, 1)
                    m = r.off(1)
                    if m.there:
                        act.wait_ge(turned, DEEP + m.n + 1)
                        nc.scalar.copy(hot_t[m.slot % 2][:], pt[m.slot % 2][:].rearrange("p (r n) -> p r n", r=R)
                                       ).then_inc(copied, 1)
                        act.wait_ge(broadcast, (m.n + 1) * R)
                        nc.scalar.activation(off[m.slot][:], hot[m.slot][:], ACT.Copy, bias=-1.0
                                             ).then_inc(shifted, 1)
                    m = r.off(-2)
                    if m.there:
                        wait_alone(act, scored, m.n + 1)
                        if at.held is not None:
                            nc.scalar.copy(at.held[:, ds(m.n * R, R), :], rows[m.slot][:, :, 0:H * dv])
                        nc.scalar.copy(scores[:, ds(m.n * R, R), :], sc[m.slot][:]).then_inc(kept, 1)
                    m = r.off(2)
                    if m.there:
                        nc.scalar.copy(idx[m.slot][:], at.index[:, ds(m.n * R, R)]).then_inc(indexed, 1)
                rolling(act, step, rounds)

            @block.gpsimd
            def _(pool):
                def step(r):
                    m = r.off(2)
                    if m.there:
                        wait_alone(pool, indexed, m.n + 1)
                        if at.held is not None:
                            wait_alone(pool, kept, m.n + 1)
                        for u in range(R):
                            nc.gpsimd.indirect_dma_start(rows[m.slot][:, u, :], None, at.keys,
                                                         bass.IndirectOffsetOnAxis(ap=idx[m.slot][:, u:u + 1], axis=0)
                                                         ).then_inc(gathered[m.slot], 16)
                rolling(pool, step, rounds)

            @block.tensor
            def _(pe):
                pe.sem_inc(turned, DEEP)
                pe.sem_inc(broadcast, DEEP * R)

                def step(r):
                    nxt, old = r.off(1), r.off(-2)
                    if nxt.there:
                        pe.wait_ge(matched, nxt.n + 1)
                        for u in range(R):
                            mm = nc.tensor.transpose(pt[nxt.slot % 2][:, u * P:(u + 1) * P], hot[nxt.slot][:, u, :],
                                                     kit.ident[:])
                        mm.then_inc(turned, 1)
                    for u in range(R):
                        if r.there:
                            blk = pe.value_load(e.blk[0:1, ds(r.n * R + u, 1)], min_val=0, max_val=NT - 1)
                        if old.there:
                            if u == 0:
                                pe.wait_ge(scored, old.n + 1)
                                pe.wait_ge(shifted, old.n + 1)
                            pe.wait_ge(reduced, old.n * R + u + 1)
                            nc.tensor.matmul(pm[u][:, 0:H * P], off[old.slot][:, u, :],
                                             big[:].rearrange("p h n -> p (h n)"), start=True, stop=False)
                            for h in range(H):
                                mm = nc.tensor.matmul(pm[u][:, h * P:(h + 1) * P],
                                                      sc[old.slot][:, u, h:h + 1].broadcast_to([P, P]), kit.ident[:],
                                                      start=False, stop=(h == H - 1))
                            mm.then_inc(broadcast, 1)
                        if r.there:
                            if u == 0:
                                pe.wait_ge(copied, r.n + 1)
                                pe.wait_ge(q_copied, r.n + 1)
                            mm = nc.tensor.matmul(pq_v[:, u, :], hot_t[r.slot % 2][:, u, :],
                                                  at.q[:, ds(blk, 1), :].rearrange("p o w -> p (o w)"),
                                                  start=True, stop=True)
                            if u == R - 1:
                                mm.then_inc(spread, 1)
                rolling(pe, step, rounds)

            @block.vector
            def _(dve):
                link = link_on(dve, chain)
                for h in range(H):
                    link(nc.vector.tensor_scalar(big[:, h, :], kit.ident[:], BIG, None, ALU.mult))
                nc.vector.memset(top, -3e38).then_inc(raised, 1)
                dve.sem_inc(reduced, R)
                dve.sem_inc(q_copied, 1)

                def step(r):
                    old, cur, far = r.off(-3), r.off(-1), r.off(2)

                    def combine(us):
                        for u in us:
                            q = qs[cur.slot % 2][:, u, :]
                            if at.dots:
                                ins = nc.vector.tensor_tensor(tmp[cur.slot % 2][:, u, :], rows[cur.slot][:, u, :], q,
                                                              ALU.mult)
                            else:
                                ins = nc.vector.tensor_tensor(tmp[cur.slot % 2][:, u, :],
                                                              rows[cur.slot][:, u, at.score_at:at.score_at + H], q,
                                                              ALU.add)
                        return ins
                    if old.there:
                        if old.looped or old.c >= 1:
                            dve.wait_ge(clipped, old.n)
                        nc.vector.tensor_tensor(is_tile[:], kit.iota[:, None, 0:NT].broadcast_to([P, R, NT]),
                                                e.tile[:, ds(old.n * R, R), None].broadcast_to([P, R, NT]),
                                                ALU.is_equal).then_inc(selected, 1)
                        for u in range(R):
                            dve.wait_ge(broadcast, (DEEP + old.n) * R + u + 1)
                            nc.vector.tensor_reduce(row_max[:, u, :], pm[u][:, 0:H * P].rearrange(
                                "p (h n) -> p h n", h=H), AX_X, ALU.max).then_inc(reduced, 1)
                        dve.wait_ge(selected, old.n + 1)
                        nc.vector.tensor_scalar(is_tile[:], is_tile[:], 2 * BIG, BIG, ALU.mult, ALU.subtract
                                                ).then_inc(limited, 1)
                    if cur.there:
                        dve.wait_ge(q_copied, cur.n + 2)
                        dve.wait_ge(gathered[cur.slot], (cur.turn + 1) * 16 * R)
                        if cur.looped or cur.c >= 2:
                            dve.wait_ge(scored, cur.n - 1)
                        combine(range(R // 2))
                    if old.there:
                        dve.wait_ge(reduced, (old.n + 2) * R)
                        dve.wait_ge(limited, old.n + 1)
                        nc.vector.tensor_tensor(
                            by_tile[:], row_max[:].rearrange("p r h -> p h r")[:, None, :, :].broadcast_to([P, NT, H, R]),
                            is_tile[:].rearrange("p r t -> p t r")[:, :, None, :].broadcast_to([P, NT, H, R]),
                            ALU.min).then_inc(clipped, 1)
                    if cur.there:
                        combine(range(R // 2, R)).then_inc(part, 1)
                    if old.there:
                        dve.wait_ge(clipped, old.n + 1)
                        dve.wait_ge(raised, old.n + 1)
                        nc.vector.tensor_reduce(round_max[:], by_tile[:], AX_X, ALU.max).then_inc(folded, 1)
                    if far.there:
                        dve.wait_ge(turned, far.n + 1)
                        if far.looped or far.c >= DEEP:
                            dve.wait_ge(shifted, far.n + 1 - DEEP)
                        nc.vector.tensor_tensor(hot[far.slot][:], kit.iota[:, None, :].broadcast_to([P, R, P]),
                                                e.rec[:, ds(far.n * R, R), 1:2].broadcast_to([P, R, P]),
                                                ALU.is_equal).then_inc(matched, 1)
                    if old.there:
                        dve.wait_ge(folded, old.n + 1)
                        nc.vector.tensor_tensor(top, top, round_max[:], ALU.max).then_inc(raised, 1)
                    if cur.there:
                        dve.wait_ge(part, cur.n + 1)
                        dve.wait_ge(kept, cur.n + 1)
                        if at.dots:
                            nc.vector.tensor_reduce(sc[cur.slot][:], tmp[cur.slot % 2][:].rearrange(
                                "p r (h d) -> p r h d", h=H), AX_X, ALU.add).then_inc(scored, 1)
                        else:
                            nc.vector.scalar_tensor_tensor(out=sc[cur.slot][:], in0=tmp[cur.slot % 2][:], scalar=0.2,
                                                           in1=tmp[cur.slot % 2][:], op0=ALU.mult, op1=ALU.max
                                                           ).then_inc(scored, 1)
                rolling(dve, step, rounds)


def edge_sums(nc, kit, nm, at, scores, top, acc):
    e, H, dv = at.edges, at.heads, at.dv
    WV = at.values.shape[1]
    W = H + H * dv
    rounds = e.groups // R
    PARTS = R if at.held is None else 1
    with ExitStack() as c:
        def many(count, name, shape, dt=F32):
            return [c.enter_context(nc.sbuf_tensor(f"{nm}_{name}{a}", shape, dt)) for a in range(count)]
        if at.held is None:
            idx, rows = many(DEEP, "idx", [P, R], I32), at.rows(WV)
            gathered = gather_sems(nc, nm, "gathered", DEEP)
        hot, hot_t = many(DEEP, "hot", [P, R, P]), many(2, "hot_t", [P, R, P])
        z, val = many(2, "z", [P, R, H]), many(2, "val", [P, R, W])
        pt = [c.enter_context(nc.psum_tensor(f"{nm}_pt{a}", [P, 512], F32)) for a in range(2)]
        pd = [c.enter_context(nc.psum_tensor(f"{nm}_pd{a}", [P, 512], F32)) for a in range(2)]
        pa = [c.enter_context(nc.psum_tensor(f"{nm}_pa{u}", [P, 512], F32)) for u in range(R)]
        pd_v = [p[:, 0:R * H].rearrange("p (r h) -> p r h", r=R) for p in pd]
        (indexed, matched, turned, copied, spread, part, shifted, raised, weighted, multiplied, added) = sems(
            nc, c, nm, "indexed matched turned copied spread part shifted raised weighted multiplied added")

        with nc.Block() as block:
            @block.scalar
            def _(act):
                def step(r):
                    m = r.off(-1)
                    if m.there:
                        act.wait_ge(shifted, m.n + 1)
                        nc.scalar.activation(val[m.slot % 2][:, :, 0:H], z[m.slot % 2][:], ACT.Exp).then_inc(raised, 1)
                    m = r.off(2)
                    if m.there and at.held is None:
                        if m.looped or m.c >= DEEP:
                            wait_alone(act, weighted, (m.n + 1 - DEEP) * PARTS)
                        nc.scalar.copy(idx[m.slot][:], at.index[:, ds(m.n * R, R)]).then_inc(indexed, 1)
                    m = r.off(1)
                    if m.there:
                        act.wait_ge(turned, m.n + 1)
                        nc.scalar.copy(hot_t[m.slot % 2][:], pt[m.slot % 2][:].rearrange("p (r n) -> p r n", r=R)
                                       ).then_inc(copied, 1)
                rolling(act, step, rounds)

            if at.held is None:
                @block.gpsimd
                def _(pool):
                    def step(r):
                        m = r.off(2)
                        if m.there:
                            wait_alone(pool, indexed, m.n + 1)
                            for u in range(R):
                                nc.gpsimd.indirect_dma_start(
                                    rows[m.slot][:, u, :], None, at.values,
                                    bass.IndirectOffsetOnAxis(ap=idx[m.slot][:, u:u + 1], axis=0)
                                ).then_inc(gathered[m.slot], 16)
                    rolling(pool, step, rounds)

            @block.tensor
            def _(pe):
                def step(r):
                    old, nxt = r.off(-2), r.off(1)
                    for u in range(R):
                        if r.there:
                            blk = pe.value_load(e.blk[0:1, ds(r.n * R + u, 1)], min_val=0, max_val=NT - 1)
                        if old.there:
                            if u < PARTS:
                                pe.wait_ge(weighted, old.n * PARTS + u + 1)
                            pe.wait_ge(added, old.n * R + u + 1)
                            nc.tensor.matmul(pa[u][:, 0:W], hot[old.slot][:, u, :], val[old.slot % 2][:, u, :],
                                             start=True, stop=True).then_inc(multiplied, 1)
                        if r.there:
                            if u == 0:
                                pe.wait_ge(copied, r.n + 1)
                                if r.looped or r.c >= 2:
                                    pe.wait_ge(shifted, r.n - 1)
                            mm = nc.tensor.matmul(pd_v[r.slot % 2][:, u, :], hot_t[r.slot % 2][:, u, :],
                                                  top[:, ds(blk, 1), :].rearrange("p o w -> p (o w)"),
                                                  start=True, stop=True)
                            if u == R - 1:
                                mm.then_inc(spread, 1)
                        if nxt.there and u == R - 1:
                            pe.wait_ge(matched, nxt.n + 1)
                            for v in range(R):
                                mm = nc.tensor.transpose(pt[nxt.slot % 2][:, v * P:(v + 1) * P], hot[nxt.slot][:, v, :],
                                                         kit.ident[:])
                            mm.then_inc(turned, 1)
                rolling(pe, step, rounds)

            @block.vector
            def _(dve):
                nc.vector.memset(acc, 0.0).then_inc(added, R)

                def step(r):
                    cur, mid, old, nxt = r.off(-1), r.off(-2), r.off(-3), r.off(1)
                    for u in range(R):
                        if old.there:
                            blk = dve.value_load(e.blk[0:1, ds(old.n * R + u, 1)], min_val=0, max_val=NT - 1)
                        if mid.there and u < PARTS:
                            if u == 0:
                                if at.held is None:
                                    dve.wait_ge(gathered[mid.slot], (mid.turn + 1) * 16 * R)
                                dve.wait_ge(raised, mid.n + 1)
                            us = slice(u, u + 1) if PARTS == R else slice(0, R)
                            v = rows[mid.slot][:, us, 0:H * dv] if at.held is None else at.held[:, ds(mid.n * R, R), :]
                            into = val[mid.slot % 2][:, us, :]
                            n = us.stop - us.start
                            nc.vector.tensor_tensor(into[:, :, H:].rearrange("p r (h d) -> p r h d", h=H),
                                                    v.rearrange("p r (h d) -> p r h d", h=H),
                                                    into[:, :, 0:H][:, :, :, None].broadcast_to([P, n, H, dv]),
                                                    ALU.mult).then_inc(weighted, 1)
                        if old.there:
                            to = acc[:, ds(blk, 1), :].rearrange("p o w -> p (o w)")
                            dve.wait_ge(multiplied, old.n * R + u + 1)
                            dve.wait_ge(added, (old.n + 1) * R + u)
                            nc.vector.tensor_tensor(to, to, pa[u][:, 0:W], ALU.add).then_inc(added, 1)
                        if cur.there and u == 1:
                            dve.wait_ge(spread, cur.n + 1)
                            nc.vector.tensor_tensor(z[cur.slot % 2][:], scores[:, ds(cur.n * R, R), :], pd_v[cur.slot % 2],
                                                    ALU.subtract).then_inc(part, 1)
                        if cur.there and u == 2:
                            dve.wait_ge(part, cur.n + 1)
                            nc.vector.tensor_scalar(z[cur.slot % 2][:], z[cur.slot % 2][:], 0.0, None, ALU.min
                                                    ).then_inc(shifted, 1)
                        if nxt.there and u == R - 1:
                            nc.vector.tensor_tensor(hot[nxt.slot][:], kit.iota[:, None, :].broadcast_to([P, R, P]),
                                                    e.rec[:, ds(nxt.n * R, R), 1:2].broadcast_to([P, R, P]),
                                                    ALU.is_equal).then_inc(matched, 1)
                rolling(dve, step, rounds)


def gat_moe_stage(nc, kit, A, x, bufs, own):
    _, b2, b3, b4 = bufs
    E, F = A["L0_ffn_b1"].shape
    H = A["L0_ffn_att_src"].shape[0]
    fc, HE = F // P, H * E
    groups = own.groups
    table = nc.dram_tensor("gat_table", (NP, HE + 2 * H), F32).ap()
    with ExitStack() as c:
        def sb(name, shape, dt=F32):
            return c.enter_context(nc.sbuf_tensor(f"gat_{name}", shape, dt))
        gates = sb("gates", [P, NT, E])
        b1s, b2s = sb("b1s", [P, E, fc]), sb("b2s", [E, D])
        layer_norm(nc, kit, "gat_ln", x, xt=b2)
        with ExitStack() as cc:
            def sb2(name, shape, dt=F32):
                return cc.enter_context(nc.sbuf_tensor(f"gat_{name}", shape, dt))
            w = sb2("w", [P, 2, HE])
            rows_in = {n: sb2(n, [P, HE]) for n in ("att_src", "att_dst", "b_gat", "ln_gamma", "ln_beta")}
            h = sb2("h", [P, NT, HE + 2 * H])
            tmp, score = sb2("tmp", [P, NT, HE]), sb2("score", [P, NT, E])
            scores, top = sb2("scores", [P, groups, H]), sb2("top", [P, NT, H])
            acc = sb2("acc", [P, NT, H + HE])
            held = b4[:, 0:groups * HE].rearrange("p (g w) -> p g w", g=groups)
            mean, var, std = sb2("mean", [P, NT]), sb2("var", [P, NT]), sb2("std", [P, NT])
            above, same = sb2("above", [P, NT, E, E]), sb2("same", [P, NT, E, E])
            lower, rank = sb2("lower", [P, E, E]), sb2("rank", [P, NT, E])

            def flat(a):
                return a if len(a.shape) == 1 else a.rearrange("h e -> (h e)")
            with nc.allow_non_contiguous_dma(reason="short columns"):
                load(nc, "gat_load", [(w[:], chunks(A["L0_ffn_W_gat"])), (b2s[:], A["L0_ffn_b2"])]
                     + [(b1s[:, e, :], column(A["L0_ffn_b1"][e], fc)) for e in range(E)]
                     + [(t[:], row_to_all(flat(A[f"L0_ffn_{n}"]))) for n, t in rows_in.items()])
            add_projection(nc, "gat_h", b2, w, tmp[:], fresh=True)

            def node_scores(link):
                link(nc.vector.tensor_copy(h[:, :, 0:HE], tmp[:]))
                for n, at in (("att_src", HE), ("att_dst", HE + H)):
                    link(nc.vector.tensor_tensor(tmp[:], h[:, :, 0:HE],
                                                 rows_in[n][:, None, :].broadcast_to([P, NT, HE]), ALU.mult))
                    link(nc.vector.tensor_reduce(h[:, :, at:at + H], tmp[:].rearrange("p t (h e) -> p t h e", h=H),
                                                 AX_X, ALU.add))
                link(nc.vector.tensor_copy(top[:], h[:, :, HE + H:]))
            on_vector(nc, "gat_v1", node_scores)
            load(nc, "gat_store", [(table.rearrange("(t p) w -> p t w", p=P), h[:])])
            own_dst = sb2("own_dst", [P, NT, H])
            on_vector(nc, "gat_v2", lambda link: link(nc.vector.tensor_copy(own_dst[:], top[:])))
            at = EdgeAttention(own, own.src, table, table, own_dst, H, E, dots=False, spare=b3, score_at=HE, held=held)
            edge_scores(nc, kit, "gat_s", at, scores, top[:])
            edge_sums(nc, kit, "gat_a", at, scores, top[:], acc[:])
            with ExitStack() as c3:
                step, ready, rooted = sems(nc, c3, "gat_score", "step ready rooted")
                with nc.Block() as block:
                    @block.vector
                    def _(dve):
                        link = link_on(dve, step)
                        agg, den = acc[:, :, H:], acc[:, :, 0:H]
                        agg_h = agg.rearrange("p t (h e) -> p t h e", h=H)
                        link(nc.vector.tensor_scalar(den, den, 1e-16, None, ALU.add))
                        link(nc.vector.reciprocal(den, den))
                        link(nc.vector.tensor_tensor(agg_h, agg_h, den[:, :, :, None].broadcast_to([P, NT, H, E]),
                                                     ALU.mult))
                        link(nc.vector.tensor_tensor(tmp[:], agg, rows_in["b_gat"][:, None, :].broadcast_to([P, NT, HE]),
                                                     ALU.add))
                        link(nc.vector.tensor_reduce(mean[:], tmp[:], AX_X, ALU.add))
                        link(nc.vector.tensor_scalar(mean[:], mean[:], 1.0 / HE, None, ALU.mult))
                        link(nc.vector.tensor_tensor(tmp[:], tmp[:], per_node(mean[:], HE), ALU.subtract))
                        link(nc.vector.tensor_tensor(agg, tmp[:], tmp[:], ALU.mult))
                        link(nc.vector.tensor_reduce(var[:], agg, AX_X, ALU.add))
                        nc.vector.tensor_scalar(var[:], var[:], 1.0 / HE, EPS, ALU.mult, ALU.add).then_inc(ready, 1)
                        dve.wait_ge(rooted, 1)
                        link(nc.vector.reciprocal(std[:], std[:]))
                        link(nc.vector.tensor_tensor(tmp[:], tmp[:], per_node(std[:], HE), ALU.mult))
                        for n, op in (("ln_gamma", ALU.mult), ("ln_beta", ALU.add)):
                            link(nc.vector.tensor_tensor(tmp[:], tmp[:],
                                                         rows_in[n][:, None, :].broadcast_to([P, NT, HE]), op))
                        link(nc.vector.tensor_reduce(score[:], tmp[:].rearrange("p t (h e) -> p t e h", h=H), AX_X,
                                                     ALU.add))
                        link(nc.vector.tensor_scalar(score[:], score[:], 1.0 / H, None, ALU.mult))
                        rank_rows(nc, kit, link, score[:], E, above[:], same[:], lower[:], rank[:])
                        link(nc.vector.tensor_scalar(rank[:], rank[:], 2.0, None, ALU.is_lt))
                        link(nc.vector.tensor_tensor(gates[:], score[:], rank[:], ALU.mult))
                        link(nc.vector.tensor_scalar(rank[:], rank[:], 1.0, BIG, ALU.subtract, ALU.mult))
                        link(nc.vector.tensor_tensor(gates[:], gates[:], rank[:], ALU.add))

                    @block.scalar
                    def _(act):
                        act.wait_ge(ready, 1)
                        nc.scalar.activation(std[:], var[:], ACT.Sqrt).then_inc(rooted, 1)
            softmax_rows(nc, "gat_sm", gates[:], E)
        add_gated_bias(nc, kit, "gat_b2", gates, b2s[:], x)
        of = lambda name: lambda e: A[name][ds(e, 1), :, :]
        expert_mlps(nc, "gatx", b2, E, [Mid(of("L0_ffn_W1"), 2, fc, ACT.Gelu, b1s)], of("L0_ffn_W2"), gates, x)


def hgt_stage(nc, kit, A, x, bufs, e):
    b1, b2, b3, b4 = bufs
    TYPES = A["L1_gnn_k_linears"].shape[0]
    RELS, H, DK, _ = A["L1_gnn_relation_att"].shape
    KC = TYPES * 2
    HP = H // 2
    keys = nc.dram_tensor("hgt_keys", (RELS * NP, D), F32).ap()
    values = nc.dram_tensor("hgt_values", (RELS * NP, D), F32).ap()
    q = nat(b2)
    w_k, w_q, w_v = (b3[:, n * KC * D:(n + 1) * KC * D].rearrange("p (k n) -> p k n", k=KC) for n in range(3))
    raw, rel_k, rel_v = (b4[:, n * HP * RELS * P:(n + 1) * HP * RELS * P].rearrange("p (h r n) -> p h r n", h=HP, r=RELS)
                         for n in range(3))
    with ExitStack() as c:
        def sb(name, shape, dt=F32):
            return c.enter_context(nc.sbuf_tensor(f"hgt_{name}", shape, dt))
        kind_i, kind, is_kind = sb("kind_i", [P, NT], I32), sb("kind", [P, NT]), sb("is_kind", [P, TYPES, NT])
        skip = sb("skip", [P, TYPES])
        layer_norm(nc, kit, "hgt_ln", x, b1)
        with ExitStack() as cc:
            pri = cc.enter_context(nc.sbuf_tensor("hgt_pri", [P, RELS, H], F32))
            step, zeroed, loaded, turned, squashed = sems(nc, cc, "hgt_w", "step zeroed loaded turned squashed")
            pt = cc.enter_context(nc.psum_tensor("hgt_pt", [P, HP * RELS * P], F32))
            with nc.Block() as block, nc.allow_non_contiguous_dma(reason="short rows"):
                @block.sync
                def _(sp):
                    for t, n in ((w_k, "k"), (w_q, "q"), (w_v, "v")):
                        sp.dma_start(t, A[f"L1_gnn_{n}_linears"].rearrange("t (k p) n -> p (t k) n", p=P)).then_inc(loaded, 16)
                    sp.dma_start(skip[:], row_to_all(A["L1_gnn_skip"])).then_inc(loaded, 16)
                    sp.dma_start(pri[:].rearrange("p r h -> p (r h)"),
                                 row_to_all(A["L1_gnn_relation_pri"].rearrange("r h -> (r h)"))).then_inc(loaded, 16)
                    sp.wait_ge(zeroed, 3)
                    sp.dma_start(kind_i[:, 0:NT - 1],
                                 A["node_type_4"][0:(NT - 1) * P].rearrange("(t p) -> p t", p=P)).then_inc(loaded, 16)
                    sp.dma_start(kind_i[0:LAST, NT - 1:NT],
                                 A["node_type_4"][(NT - 1) * P:N].rearrange("(p o) -> p o", o=1)).then_inc(loaded, 16)
                    for t, n in ((raw, "att"), (rel_v, "msg")):
                        for hp in range(HP):
                            for h2 in range(2):
                                at = slice(h2 * DK, (h2 + 1) * DK)
                                sp.dma_start(t[at, hp, :, at],
                                             A[f"L1_gnn_relation_{n}"][:, hp * 2 + h2, :, :].rearrange("r d e -> d r e")
                                             ).then_inc(loaded, 16)
                    sp.wait_ge(loaded, 16 * (7 + 2 * HP * 2))

                @block.vector
                def _(dve):
                    nc.vector.memset(raw, 0.0).then_inc(zeroed, 1)
                    nc.vector.memset(rel_v, 0.0).then_inc(zeroed, 1)
                    nc.vector.memset(kind_i[:], 0).then_inc(zeroed, 1)
                    dve.wait_ge(loaded, 16 * (7 + 2 * HP * 2))
                    link = link_on(dve, step)
                    link(nc.vector.tensor_copy(kind[:], kind_i[:]))
                    for t in range(TYPES):
                        link(nc.vector.tensor_scalar(is_kind[:, t, :], kind[:], float(t), None, ALU.is_equal))
                    link(nc.vector.tensor_scalar(pri[:], pri[:], 1.0 / DK ** 0.5, None, ALU.mult))
                    dve.wait_ge(turned, 1)
                    pt_v = pt[:].rearrange("p (h r n) -> p h r n", h=HP, r=RELS)
                    for hp in range(HP):
                        for h2 in range(2):
                            at = slice(h2 * DK, (h2 + 1) * DK)
                            link(nc.vector.tensor_tensor(rel_k[:, hp, :, at], pt_v[:, hp, :, at],
                                                         pri[:, :, hp * 2 + h2:hp * 2 + h2 + 1].broadcast_to([P, RELS, DK]),
                                                         ALU.mult))

                @block.tensor
                def _(pe):
                    pe.wait_ge(loaded, 16 * (7 + 2 * HP * 2))
                    for hp in range(HP):
                        for r in range(RELS):
                            n = hp * RELS + r
                            mm = nc.tensor.transpose(pt[:, n * P:(n + 1) * P], raw[:, hp, r, :], kit.ident[:])
                    mm.then_inc(turned, 1)

                @block.scalar
                def _(act):
                    act.wait_ge(loaded, 16 * (7 + 2 * HP * 2))
                    nc.scalar.activation(skip[:], skip[:], ACT.Sigmoid).then_inc(squashed, 1)
                    act.wait_ge(squashed, 1)
        hgt_tables(nc, kit, nat(b1), is_kind, w_k, w_q, w_v, rel_k, rel_v, q, keys, values, TYPES, RELS, HP)
        with ExitStack() as cc:
            groups = e.groups
            scores = cc.enter_context(nc.sbuf_tensor("hgt_scores", [P, groups, H], F32))
            top = cc.enter_context(nc.sbuf_tensor("hgt_top", [P, NT, H], F32))
            at = EdgeAttention(e, e.key, keys, values, q, H, DK, dots=True, spare=b3)
            edge_scores(nc, kit, "hgt_s", at, scores, top[:])
            acc = cc.enter_context(nc.sbuf_tensor("hgt_acc", [P, NT, H + D], F32))
            edge_sums(nc, kit, "hgt_a", at, scores, top[:], acc[:])

            def divide(link):
                link(nc.vector.tensor_scalar(acc[:, :, 0:H], acc[:, :, 0:H], 1e-30, None, ALU.max))
                link(nc.vector.reciprocal(acc[:, :, 0:H], acc[:, :, 0:H]))
                link(nc.vector.tensor_tensor(nat(b1).rearrange("p t (h d) -> p t h d", h=H),
                                             acc[:, :, H:].rearrange("p t (h d) -> p t h d", h=H),
                                             acc[:, :, 0:H][:, :, :, None].broadcast_to([P, NT, H, DK]), ALU.mult))
                for t in range(TYPES):
                    link(nc.vector.tensor_scalar(is_kind[:, t, :], is_kind[:, t, :], skip[:, t:t + 1], None, ALU.mult))
            on_vector(nc, "hgt_v1", divide)
        turn(nc, kit, "hgt_turn", nat(b1), tr(b2))
        load(nc, "hgt_load_a", [(w_k, A["L1_gnn_a_linears"].rearrange("t (k p) n -> p (t k) n", p=P))])
        for t in range(TYPES):
            add_projection(nc, f"hgt_out{t}", b2, w_k[:, 2 * t:2 * t + 2, :], nat(x), gate=is_kind[:, t, :])


def hgt_tables(nc, kit, xn, is_kind, w_k, w_q, w_v, rel_k, rel_v, q, keys, values, TYPES, RELS, HP):
    KC = TYPES * 2
    with ExitStack() as c:
        def sb(name, shape, dt=F32):
            return c.enter_context(nc.sbuf_tensor(f"hgtt_{name}", shape, dt))
        xm, xmt, kvt = sb("xm", [P, TYPES, D]), sb("xmt", [P, KC, P]), sb("kvt", [P, 2 * HP, P])
        out_k, out_v = sb("out_k", [P, RELS, D]), sb("out_v", [P, RELS, D])
        pt = c.enter_context(nc.psum_tensor("hgtt_pt", [P, KC * P], F32))
        pkv = c.enter_context(nc.psum_tensor("hgtt_pkv", [P, 512], F32))
        pq = c.enter_context(nc.psum_tensor("hgtt_pq", [P, 512], F32))
        pr = [c.enter_context(nc.psum_tensor(f"hgtt_pr{n}", [P, 512], F32)) for n in range(4)]
        (masked, turned, copied, projected, kv_copied, q_copied, related, out_k_ready, out_v_ready, k_free,
         v_free) = sems(nc, c, "hgtt", "masked turned copied projected kv_copied q_copied related out_k_ready "
                        "out_v_ready k_free v_free")
        stored_k, stored_v = sems(nc, c, "hgtt", "stored_k stored_v")
        half = RELS // 2
        parts = [(v, g, hp) for g in range(2) for hp in range(HP) for v in range(2)]

        def tiles(eng, step):
            with eng.Fori(0, NT - 1) as t:
                step(t, True)
            step(NT - 1, False)

        with nc.Block() as block:
            @block.vector
            def _(dve):
                def mask(t):
                    for k in range(TYPES):
                        ins = nc.vector.tensor_scalar(xm[:, k, :], xn[:, ds(t, 1), :].rearrange("p o d -> p (o d)"),
                                                      is_kind[:, k, ds(t, 1)], None, ALU.mult)
                    ins.then_inc(masked, 1)
                mask(0)
                dve.sem_inc(kv_copied, 1)
                dve.sem_inc(out_v_ready, 2)

                def step(t, more):
                    if more:
                        dve.wait_ge(turned, t + 1)
                        mask(t + 1)
                    dve.wait_ge(projected, t + 1)
                    dve.wait_ge(related, t * 8 + 8)
                    nc.vector.tensor_copy(kvt[:], pkv[:].rearrange("p (c n) -> p c n", n=P)).then_inc(kv_copied, 1)
                    dve.wait_ge(v_free, t + 1)
                    for n, (v, g, hp) in enumerate(parts):
                        if v:
                            dve.wait_ge(related, t * 8 + 8 + n + 1)
                            nc.vector.tensor_copy(out_v[:, g * half:(g + 1) * half, hp * P:(hp + 1) * P],
                                                  pr[n % 4][:].rearrange("p (r n) -> p r n", r=half)).then_inc(out_v_ready, 1)
                tiles(dve, step)

            @block.tensor
            def _(pe):
                pe.sem_inc(related, 8)

                def turn_masked():
                    for k in range(KC):
                        mm = nc.tensor.transpose(pt[:, k * P:(k + 1) * P], xm[:, k // 2, (k % 2) * P:(k % 2 + 1) * P],
                                                 kit.ident[:])
                    mm.then_inc(turned, 1)
                pe.wait_ge(masked, 1)
                turn_masked()

                def step(t, more):
                    pe.wait_ge(copied, t + 1)
                    pe.wait_ge(kv_copied, t + 1)
                    for n, w in enumerate((w_k, w_v)):
                        for f in range(HP):
                            for k in range(KC):
                                nc.tensor.matmul(pkv[:, (n * HP + f) * P:(n * HP + f + 1) * P], w[:, k, f * P:(f + 1) * P],
                                                 xmt[:, k, :], start=(k == 0), stop=(k == KC - 1))
                    pe.wait_ge(q_copied, t + 1)
                    for k in range(KC):
                        mm = nc.tensor.matmul(pq[:, 0:D], xmt[:, k, :], w_q[:, k, :], start=(k == 0), stop=(k == KC - 1))
                    mm.then_inc(projected, 1)
                    if more:
                        pe.wait_ge(masked, t + 2)
                        turn_masked()
                    pe.wait_ge(kv_copied, t + 2)
                    for n, (v, g, hp) in enumerate(parts):
                        pe.wait_ge(out_v_ready if v else out_k_ready, t * 4 + n // 2 + 1)
                        nc.tensor.matmul(pr[n % 4][:], kvt[:, v * HP + hp, :],
                                         (rel_v if v else rel_k)[:, hp, g * half:(g + 1) * half, :].rearrange(
                                             "p r n -> p (r n)"), start=True, stop=True).then_inc(related, 1)
                tiles(pe, step)

            @block.scalar
            def _(act):
                act.sem_inc(q_copied, 1)
                act.sem_inc(out_k_ready, 2)

                def copy_turned(t):
                    act.wait_ge(turned, t + 1)
                    nc.scalar.copy(xmt[:], pt[:].rearrange("p (k n) -> p k n", k=KC)).then_inc(copied, 1)
                copy_turned(0)

                def step(t, more):
                    wait_alone(act, projected, t + 1)
                    nc.scalar.copy(q[:, ds(t, 1), :].rearrange("p o d -> p (o d)"), pq[:, 0:D]).then_inc(q_copied, 1)
                    if more:
                        copy_turned(t + 1)
                    act.wait_ge(k_free, t + 1)
                    for n, (v, g, hp) in enumerate(parts):
                        if not v:
                            act.wait_ge(related, t * 8 + 8 + n + 1)
                            nc.scalar.copy(out_k[:, g * half:(g + 1) * half, hp * P:(hp + 1) * P],
                                           pr[n % 4][:].rearrange("p (r n) -> p r n", r=half)).then_inc(out_k_ready, 1)
                tiles(act, step)

            @block.sync
            def _(sp):
                sp.sem_inc(k_free, 1)
                sp.sem_inc(v_free, 1)
                by_node = [a.rearrange("(r t p) d -> t p r d", r=RELS, p=P) for a in (keys, values)]
                with sp.Fori(0, NT) as t:
                    for ready, out, table, stored in ((out_k_ready, out_k, by_node[0], stored_k),
                                                      (out_v_ready, out_v, by_node[1], stored_v)):
                        sp.wait_ge(ready, t * 4 + 2 + 4)
                        sp.dma_start(table[ds(t, 1), :, :, :].rearrange("o p r d -> p (o r) d"), out[:]).then_inc(stored, 16)
                    sp.wait_ge(stored_k, t * 16 + 16)
                    sp.sem_inc(k_free, 1)
                    sp.wait_ge(stored_v, t * 16 + 16)
                    sp.sem_inc(v_free, 1)


def column(ap1d, k):
    return ap1d.rearrange("(k p) -> p k", k=k)


def sage_stage(nc, kit, A, x, bufs, e, table):
    b1, b2, b3, b4 = bufs
    with ExitStack() as c:
        def sb(name, shape, dt=F32):
            return c.enter_context(nc.sbuf_tensor(f"sage_{name}", shape, dt))
        layers = A["L2_gnn_W_agg"].shape[0]
        w_in, w_out = sb("w_in", [P, 2, D]), sb("w_out", [P, 2, D])
        w_agg = [sb(f"w_agg{i}", [P, 2, D]) for i in range(layers)]
        w_self = [sb(f"w_self{i}", [P, 2, D]) for i in range(layers)]
        bias_in, bias_out = sb("b_in", [P, 2]), sb("b_out", [P, D])
        bias = [sb(f"b_hid{i}", [P, 2]) for i in range(layers)]
        rdeg, rall = sb("rdeg", [P, NT]), sb("rall", [P, NP])
        with nc.allow_non_contiguous_dma(reason="short bias columns"):
            load(nc, "sage_load",
                 [(w_in[:], chunks(A["L2_gnn_W_in"])), (w_out[:], chunks(A["L2_gnn_W_out"])),
                  (bias_in[:], column(A["L2_gnn_b_in"], 2)), (bias_out[:], row_to_all(A["L2_gnn_b_out"]))]
                 + [(w_agg[i][:], chunks(A["L2_gnn_W_agg"][i])) for i in range(layers)]
                 + [(w_self[i][:], chunks(A["L2_gnn_W_self"][i])) for i in range(layers)]
                 + [(bias[i][:], column(A["L2_gnn_b_hid"][i], 2)) for i in range(layers)])
        layer_norm(nc, kit, "sage_ln", x, xt=b2)

        def mean_factor(link):
            link(nc.vector.tensor_scalar(rdeg[:], kit.deg_out[:], 1.0, None, ALU.max))
            link(nc.vector.reciprocal(rdeg[:], rdeg[:]))
        on_vector(nc, "sage_v0", mean_factor)
        rows_to_all(nc, kit, "sage_rall", rdeg, rall)
        project_t(nc, "sage_in", [(b2, 2, w_in)], b3, 2, bias=bias_in)
        h, free = b3, b2
        for i in range(layers):
            write_table(nc, kit, f"sage_t{i}", h, 2, b1, table)
            aggregate_t(nc, kit, f"sage_a{i}", e, table, 2, b4)
            on_vector(nc, f"sage_v{i + 1}", lambda link: link(nc.vector.tensor_tensor(
                tr(b4), tr(b4), rall[:, None, :].broadcast_to([P, 2, NP]), ALU.mult)))
            project_t(nc, f"sage_p{i}", [(b4, 2, w_agg[i]), (h, 2, w_self[i])], free, 2, ACT.Relu, bias[i])
            h, free = free, h
        add_projection(nc, "sage_out", h, w_out, nat(x), bias_out)


def weighted_stage(nc, kit, A, x, bufs, e, table):
    b1, b2, b3, b4 = bufs
    with ExitStack() as c:
        def sb(name, shape, dt=F32):
            return c.enter_context(nc.sbuf_tensor(f"wsum_{name}", shape, dt))
        w, wt = sb("w", [P, 2, D]), sb("wt", [P, 2, D])
        ln_w, ln_b = sb("ln_w", [P, 2]), sb("ln_b", [P, 2])
        bias, gamma, beta = sb("b", [P, D]), sb("gamma", [P, D]), sb("beta", [P, D])
        with nc.allow_non_contiguous_dma(reason="short columns"):
            load(nc, "wsum_load",
                 [(w[:], chunks(A["L3_gnn_W"])), (ln_w[:], column(A["L3_gnn_ln_w"], 2)),
                  (ln_b[:], column(A["L3_gnn_ln_b"], 2)), (bias[:], row_to_all(A["L3_gnn_b"])),
                  (gamma[:], row_to_all(A["L3_gnn_gamma"])), (beta[:], row_to_all(A["L3_gnn_beta"]))])
        layer_norm(nc, kit, "wsum_ln", x, b1, b2)
        layer_norm(nc, kit, "wsum_ln2", b1, b3, b2)
        with ExitStack() as cc:
            step, squashed, turned = sems(nc, cc, "wsum_silu", "step squashed turned")
            ps = cc.enter_context(nc.psum_tensor("wsum_ps", [P, 512], F32))
            with nc.Block() as block:
                @block.tensor
                def _(pe):
                    for k in range(2):
                        for o in range(2):
                            mm = nc.tensor.transpose(ps[:, k * D + o * P:k * D + (o + 1) * P],
                                                     w[:, o, k * P:(k + 1) * P], kit.ident[:])
                    mm.then_inc(turned, 1)

                @block.vector
                def _(dve):
                    link = link_on(dve, step)
                    for k in range(2):
                        link(nc.vector.tensor_scalar(tr(b2)[:, k, :], tr(b2)[:, k, :], ln_w[:, k:k + 1],
                                                     ln_b[:, k:k + 1], ALU.mult, ALU.add))
                    dve.wait_ge(turned, 1)
                    link(nc.vector.tensor_tensor(wt[:], ps[:].rearrange("p (k n) -> p k n", k=2),
                                                 gamma[:, None, :].broadcast_to([P, 2, D]), ALU.mult))
                    link(nc.vector.tensor_tensor(bias[:], bias[:], gamma[:], ALU.mult))
                    link(nc.vector.tensor_tensor(bias[:], bias[:], beta[:], ALU.add))
                    link(nc.vector.tensor_tensor(x[:], x[:], b1[:], ALU.add))
                    for k in range(2):
                        dve.wait_ge(squashed, k + 1)
                        link(nc.vector.tensor_tensor(tr(b2)[:, k, :], tr(b2)[:, k, :], tr(b4)[:, k, :], ALU.mult))

                @block.scalar
                def _(act):
                    for k in range(2):
                        act.wait_ge(step, k + 1)
                        nc.scalar.activation(tr(b4)[:, k, :], tr(b2)[:, k, :], ACT.Sigmoid).then_inc(squashed, 1)
        write_table(nc, kit, "wsum_t", b2, 2, b3, table)
        aggregate_t(nc, kit, "wsum_a", e, table, 2, b4, weighted=True)
        add_projection(nc, "wsum_out", b4, wt, nat(x), bias)


def rank_rows(nc, kit, link, z, n, above, same, lower, rank):
    T = z.shape[1]
    each = z[:, :, :, None].broadcast_to([P, T, n, n])
    other = z[:, :, None, :].broadcast_to([P, T, n, n])
    link(nc.vector.tensor_tensor(lower, kit.iota[:, None, 0:n].broadcast_to([P, n, n]),
                                 kit.iota[:, 0:n, None].broadcast_to([P, n, n]), ALU.is_lt))
    link(nc.vector.tensor_tensor(above, other, each, ALU.is_gt))
    link(nc.vector.tensor_tensor(same, other, each, ALU.is_equal))
    link(nc.vector.tensor_tensor(same, same, lower[:, None, :, :].broadcast_to([P, T, n, n]), ALU.mult))
    link(nc.vector.tensor_tensor(above, above, same, ALU.add))
    link(nc.vector.tensor_reduce(rank, above, AX_X, ALU.add))


def shared_moe_stage(nc, kit, A, x, bufs):
    b1, b2, b3, b4 = bufs
    E, F = A["L3_ffn_b1"].shape
    fc = F // P
    K = 2
    CAPACITY = float(-(-N * 5 // (4 * E)))
    with ExitStack() as c:
        def sb(name, shape, dt=F32):
            return c.enter_context(nc.sbuf_tensor(f"shared_{name}", shape, dt))
        wr, br = sb("wr", [P, 2, E]), sb("br", [P, E])
        gamma, beta = sb("gamma", [P, D]), sb("beta", [P, D])
        mean, mean_all = sb("mean", [P, 2]), sb("mean_all", [P, 2, P])
        z, load_, pick_w = sb("z", [P, 1, E]), sb("load", [P, 1, E]), sb("pick_w", [P, 1, K])
        above, same, lower = sb("above", [P, 1, E, E]), sb("same", [P, 1, E, E]), sb("lower", [P, E, E])
        rank, is_r, pick_f = sb("rank", [P, 1, E]), sb("is_r", [P, 1, E]), sb("pick_f", [P, K])
        pick_i = sb("pick_i", [P, K], I32)
        gates = sb("gates", [P, NT, K])
        b1s, b2s = sb("b1s", [P, K, fc]), sb("b2s", [K, D])
        layer_norm(nc, kit, "shared_ln", x, b1, b2)
        load(nc, "shared_load", [(wr[:], chunks(A["L3_ffn_Wr"])), (br[:], row_to_all(A["L3_ffn_br"])),
                                 (gamma[:], row_to_all(A["L3_ffn_gamma"])), (beta[:], row_to_all(A["L3_ffn_beta"]))])
        with ExitStack() as cc:
            step, multiplied = sems(nc, cc, "shared_logit", "step multiplied")
            ps = cc.enter_context(nc.psum_tensor("shared_ps", [P, 512], F32))
            with nc.Block() as block:
                @block.vector
                def _(dve):
                    link = link_on(dve, step)
                    link(nc.vector.tensor_reduce(mean[:], tr(b2)[:, :, 0:N], AX_X, ALU.add))
                    link(nc.vector.tensor_scalar(mean[:], mean[:], 1.0 / N, None, ALU.mult))
                    link(nc.vector.tensor_copy(mean_all[:], mean[:, :, None].broadcast_to([P, 2, P])))
                    link(nc.vector.tensor_copy(b3[:], b1[:]))
                    dve.wait_ge(multiplied, 1)
                    link(nc.vector.tensor_tensor(z[:, 0, :], ps[:, 0:E], br[:], ALU.add))

                @block.tensor
                def _(pe):
                    pe.wait_ge(step, 3)
                    for k in range(2):
                        mm = nc.tensor.matmul(ps[:, 0:E], mean_all[:, k, :], wr[:, k, :], start=(k == 0), stop=(k == 1))
                    mm.then_inc(multiplied, 1)
        softmax_rows(nc, "shared_sm1", z[:], E)

        def scale_loads(link):
            link(nc.vector.tensor_scalar(load_[:], z[:], float(N), 1.0, ALU.mult, ALU.max))
            link(nc.vector.reciprocal(load_[:], load_[:]))
            link(nc.vector.tensor_scalar(load_[:], load_[:], CAPACITY, 1.0, ALU.mult, ALU.min))
            link(nc.vector.tensor_tensor(z[:], z[:], load_[:], ALU.mult))
        on_vector(nc, "shared_v1", scale_loads)
        softmax_rows(nc, "shared_sm2", z[:], E)

        def choose(link):
            rank_rows(nc, kit, link, z[:], E, above[:], same[:], lower[:], rank[:])
            for r in range(K):
                link(nc.vector.tensor_scalar(is_r[:], rank[:], float(r), None, ALU.is_equal))
                link(nc.vector.tensor_tensor(load_[:], is_r[:], kit.iota[:, None, 0:E], ALU.mult))
                link(nc.vector.tensor_reduce(pick_f[:, r:r + 1], load_[:], AX_X, ALU.add))
                link(nc.vector.tensor_tensor(load_[:], is_r[:], z[:], ALU.mult))
                link(nc.vector.tensor_reduce(pick_w[:, :, r:r + 1], load_[:], AX_X, ALU.add))
            link(nc.vector.tensor_copy(pick_i[:], pick_f[:]))
        on_vector(nc, "shared_v2", choose)
        softmax_rows(nc, "shared_sm3", pick_w[:], K)
        on_vector(nc, "shared_v3", lambda link: link(nc.vector.tensor_copy(
            gates[:], pick_w[:].broadcast_to([P, NT, K]))))
        pick = lambda eng, e: eng.value_load(pick_i[0:1, ds(e, 1)], min_val=0, max_val=E - 1)
        with ExitStack() as cc:
            loaded, = sems(nc, cc, "shared_b", "loaded")
            with nc.Block() as block:
                @block.sync
                def _(sp):
                    for r in range(K):
                        at = pick(sp, r)
                        for f in range(fc):
                            sp.dma_start(b1s[:, r, f:f + 1],
                                         A["L3_ffn_b1"][ds(at, 1), f * P:(f + 1) * P].rearrange("o p -> p o")
                                         ).then_inc(loaded, 16)
                        sp.dma_start(b2s[r:r + 1, :], A["L3_ffn_b2"][ds(at, 1), :]).then_inc(loaded, 16)
                    sp.wait_ge(loaded, 16 * K * (fc + 1))
        add_gated_bias(nc, kit, "shared_b2", gates, b2s[:], b3)
        of = lambda name: lambda e: A[name][ds(e, 1), :, :]
        expert_mlps(nc, "shared", b2, K, [Mid(of("L3_ffn_W1"), 2, fc, ACT.Gelu, b1s)], of("L3_ffn_W2"), gates, b3, pick)
        layer_norm(nc, kit, "shared_ln2", b3, b4)

        def after(link):
            link(nc.vector.tensor_tensor(nat(b4), nat(b4), gamma[:, None, :].broadcast_to([P, NT, D]), ALU.mult))
            link(nc.vector.tensor_tensor(nat(b4), nat(b4), beta[:, None, :].broadcast_to([P, NT, D]), ALU.add))
            link(nc.vector.tensor_tensor(x[:], x[:], b4[:], ALU.add))
        on_vector(nc, "shared_v4", after)


FLT_MAX = 3.4028234663852886e38


def switch_stage(nc, kit, A, x, bufs):
    b1, b2, b3, b4 = bufs
    E, F = A["L2_ffn_b1"].shape
    fc = F // P
    C = -(-N * 5 // (4 * E))
    ST = -(-C // P)
    S = ST * P
    slots = nc.dram_tensor("switch_slots", (E * S + NP, D), F32).ap()
    answers = nc.dram_tensor("switch_answers", (E * S, D), F32).ap()
    with ExitStack() as c:
        def sb(name, shape, dt=F32):
            return c.enter_context(nc.sbuf_tensor(f"switch_{name}", shape, dt))
        slot_i, back_i = sb("slot_i", [P, NT], I32), sb("back_i", [P, NT], I32)
        factor = sb("factor", [P, NT])
        layer_norm(nc, kit, "switch_ln", x, b1, b2)
        with ExitStack() as cc:
            def sb2(name, shape, dt=F32):
                return cc.enter_context(nc.sbuf_tensor(f"switch_{name}", shape, dt))
            gw, gb, z = sb2("gw", [P, 2, E]), sb2("gb", [P, E]), sb2("z", [P, NT, E])
            above, same = sb2("above", [P, NT, E, E]), sb2("same", [P, NT, E, E])
            lower, rank = sb2("lower", [P, E, E]), sb2("rank", [P, NT, E])
            hot, ahead, total = sb2("hot", [P, NT, E]), sb2("ahead", [P, NT, E]), sb2("total", [P, NT, E])
            pos, kept, first, valid, spare = (sb2(n, [P, NT]) for n in ("pos", "kept", "first", "valid", "spare"))
            load(nc, "switch_load", [(gw[:], chunks(A["L2_ffn_gate_w"])), (gb[:], row_to_all(A["L2_ffn_gate_b"]))])
            add_projection(nc, "switch_gate", b2, gw, z[:], gb, fresh=True)
            softmax_rows(nc, "switch_sm", z[:], E)
            step, chosen, summed, placed, zeroed = sems(nc, cc, "switch_route", "step chosen summed placed zeroed")
            sent, = gather_sems(nc, "switch_route", "sent", 1)
            ps = cc.enter_context(nc.psum_tensor("switch_ps", [P, 512], F32))
            with nc.Block() as block:
                @block.vector
                def _(dve):
                    link = link_on(dve, step)
                    link(nc.vector.memset(b3[:, 0:E * S * D // P // 2], 0.0))
                    link(nc.vector.tensor_reduce(factor[:], z[:], AX_X, ALU.max))
                    rank_rows(nc, kit, link, z[:], E, above[:], same[:], lower[:], rank[:])
                    link(nc.vector.tensor_scalar(valid[:], kit.node[:], float(N), None, ALU.is_lt))
                    link(nc.vector.tensor_scalar(hot[:], rank[:], 0.0, None, ALU.is_equal))
                    nc.vector.tensor_tensor(hot[:], hot[:], per_node(valid[:], E), ALU.mult).then_inc(chosen, 1)
                    dve.wait_ge(summed, 1)
                    link(nc.vector.tensor_copy(ahead[:], ps[:, 0:NT * E].rearrange("p (t e) -> p t e", e=E)))
                    link(nc.vector.tensor_copy(total[:], ps[:, 256:256 + NT * E].rearrange("p (t e) -> p t e", e=E)))
                    for e in range(E):
                        link(nc.vector.tensor_tensor_scan(rank[:, :, e], kit.ones[:, 0:NT], total[:, :, e], 0.0,
                                                          ALU.mult, ALU.add))
                    link(nc.vector.tensor_tensor(ahead[:], ahead[:], rank[:], ALU.add))
                    link(nc.vector.tensor_tensor(ahead[:], ahead[:], total[:], ALU.subtract))
                    link(nc.vector.tensor_tensor(ahead[:], ahead[:], hot[:], ALU.mult))
                    link(nc.vector.tensor_reduce(pos[:], ahead[:], AX_X, ALU.add))
                    link(nc.vector.tensor_tensor(total[:], hot[:], kit.iota[:, None, 0:E].broadcast_to([P, NT, E]),
                                                 ALU.mult))
                    link(nc.vector.tensor_reduce(first[:], total[:], AX_X, ALU.add))
                    link(nc.vector.tensor_scalar(first[:], first[:], float(S), None, ALU.mult))
                    link(nc.vector.tensor_scalar(kept[:], pos[:], float(C), None, ALU.is_lt))
                    link(nc.vector.tensor_tensor(kept[:], kept[:], valid[:], ALU.mult))
                    link(nc.vector.tensor_tensor(factor[:], factor[:], kept[:], ALU.mult))
                    link(nc.vector.scalar_tensor_tensor(out=spare[:], in0=pos[:], scalar=float(C - 1), in1=first[:],
                                                        op0=ALU.min, op1=ALU.add))
                    link(nc.vector.tensor_copy(back_i[:], spare[:]))
                    link(nc.vector.tensor_scalar(valid[:], kit.node[:], float(E * S), None, ALU.add))
                    link(nc.vector.tensor_tensor(spare[:], spare[:], valid[:], ALU.subtract))
                    link(nc.vector.tensor_tensor(spare[:], spare[:], kept[:], ALU.mult))
                    link(nc.vector.tensor_tensor(spare[:], spare[:], valid[:], ALU.add))
                    nc.vector.tensor_copy(slot_i[:], spare[:]).then_inc(placed, 1)

                @block.tensor
                def _(pe):
                    pe.wait_ge(chosen, 1)
                    flat = hot[:].rearrange("p t e -> p (t e)")
                    nc.tensor.matmul(ps[:, 0:NT * E], kit.tri[:], flat, start=True, stop=True)
                    nc.tensor.matmul(ps[:, 256:256 + NT * E], kit.ones[:], flat, start=True, stop=True).then_inc(summed, 1)

                @block.sync
                def _(sp):
                    half = E * S // 2
                    sp.wait_ge(step, 1)
                    for n in range(2):
                        sp.dma_start(slots[n * half:(n + 1) * half, :].rearrange("(p r) d -> p (r d)", p=P),
                                     b3[:, 0:half * D // P]).then_inc(zeroed, 16)

                @block.gpsimd
                def _(pool):
                    pool.wait_ge(zeroed, 32)
                    pool.wait_ge(placed, 1)
                    for t in range(NT):
                        nc.gpsimd.indirect_dma_start(slots, bass.IndirectOffsetOnAxis(ap=slot_i[:, t:t + 1], axis=0),
                                                     nat(b1)[:, t, :], None).then_inc(sent, 16)
                    pool.wait_ge(sent, 16 * NT)
        switch_experts(nc, kit, A, slots, answers, E, fc, ST, bufs)
        with ExitStack() as cc:
            fetched = gather_sems(nc, "switch_back", "fetched", ROUNDS)
            scaled, step = sems(nc, cc, "switch_back", "scaled step")
            limit = [cc.enter_context(nc.sbuf_tensor(f"switch_limit{n}", [P, 1], F32)) for n in range(3)]
            with nc.Block() as block:
                @block.gpsimd
                def _(pool):
                    for t in range(NT):
                        nc.gpsimd.indirect_dma_start(nat(b3)[:, t, :], None, answers,
                                                     bass.IndirectOffsetOnAxis(ap=back_i[:, t:t + 1], axis=0)
                                                     ).then_inc(fetched[t // U], 16)

                @block.vector
                def _(dve):
                    for r in range(ROUNDS):
                        dve.wait_ge(fetched[r], 16 * U)
                        part = nat(b3)[:, r * U:(r + 1) * U, :]
                        nc.vector.tensor_tensor(part, part, per_node(factor[:, r * U:(r + 1) * U], D),
                                                ALU.mult).then_inc(scaled, 1)
                    dve.wait_ge(scaled, ROUNDS)
                    link = link_on(dve, step)
                    mask = b4[:].bitcast(I32)
                    for n, (to, op, than) in enumerate(((1e4, ALU.is_gt, FLT_MAX), (-1e4, ALU.is_lt, -FLT_MAX),
                                                        (0.0, ALU.not_equal, None))):
                        link(nc.vector.memset(limit[n][:], to))
                        link(nc.vector.tensor_scalar(mask, b3[:], than, None, op) if than is not None
                             else nc.vector.tensor_tensor(mask, b3[:], b3[:], op))
                        link(nc.vector.copy_predicated(b3[:], mask, limit[n][:].broadcast_to([P, NT * D])))
                    link(nc.vector.tensor_tensor(x[:], x[:], b3[:], ALU.add))


def switch_experts(nc, kit, A, slots, answers, E, fc, ST, big):
    S = ST * P
    with ExitStack() as c:
        def sb(name, shape, dt=F32):
            return c.enter_context(nc.sbuf_tensor(f"swx_{name}", shape, dt))
        b1s = sb("b1s", [P, E, fc])

        def carve(buf, *shapes):
            at, parts = 0, []
            for n, m in shapes:
                parts.append(buf[:, at:at + n * m].rearrange("p (n m) -> p n m", n=n))
                at += n * m
            return parts
        h, = carve(big[0], (fc, S))
        w1_0, w1_1, w2_0 = carve(big[1], (2, fc * P), (2, fc * P), (fc, D))
        w2_1, rows_0, rows_1, y_0, y_1 = carve(big[2], (fc, D), (ST, D), (ST, D), (ST, D), (ST, D))
        b2s, xt = carve(big[3], (E, D), (2, S))
        w1, w2, rows, y = (w1_0, w1_1), (w2_0, w2_1), (rows_0, rows_1), (y_0, y_1)
        with nc.allow_non_contiguous_dma(reason="short columns"):
            load(nc, "swx_load", [(b1s[:, e, :], column(A["L2_ffn_b1"][e], fc)) for e in range(E)]
                 + [(b2s[:, e, :], row_to_all(A["L2_ffn_b2"][e])) for e in range(E)])
        ps = [c.enter_context(nc.psum_tensor(f"swx_ps{r}", [P, 512], F32)) for r in range(4)]
        py = [c.enter_context(nc.psum_tensor(f"swx_py{r}", [P, 512], F32)) for r in range(4)]
        loaded = sems(nc, c, "swx", "loaded0 loaded1")
        stored = gather_sems(nc, "swx", "stored", 2)
        turned, copied, multiplied, read, finished, added, left, y_free = sems(
            nc, c, "swx", "turned copied multiplied read finished added left y_free")
        with nc.Block() as block:
            def pairs(eng, body):
                with eng.Fori(0, E // 2) as i:
                    for q in range(2):
                        body(i, q, i * 2 + q)

            @block.sync
            def _(sp):
                def body(i, q, e):
                    sp.wait_ge(left, e + 1)
                    sp.dma_start(rows[q], slots[ds(e * S, S), :].rearrange("(s p) d -> p s d", p=P)).then_inc(loaded[q], 16)
                    sp.dma_start(w1[q], A["L2_ffn_w1"][ds(e, 1), :, :].rearrange("o (k p) f -> p (o k) f", p=P)
                                 ).then_inc(loaded[q], 16)
                    sp.dma_start(w2[q], A["L2_ffn_w2"][ds(e, 1), :, :].rearrange("o (k p) f -> p (o k) f", p=P)
                                 ).then_inc(loaded[q], 16)
                pairs(sp, body)

            @block.tensor
            def _(pe):
                pe.sem_inc(left, 2)

                def body(i, q, e):
                    wait_alone(pe, loaded[q], i * 48 + 48)
                    for k in range(2):
                        pe.wait_ge(read, e * fc + 4)
                        for s in range(ST):
                            mm = nc.tensor.transpose(ps[k][:, s * P:(s + 1) * P], rows[q][:, s, k * P:(k + 1) * P],
                                                     kit.ident[:])
                        mm.then_inc(turned, 1)
                    for g in range(fc):
                        pe.wait_ge(copied, e * 2 + 2)
                        pe.wait_ge(read, e * fc + g + 1)
                        for k in range(2):
                            mm = nc.tensor.matmul(ps[g % 4][:, 0:S], w1[q][:, k, g * P:(g + 1) * P], xt[:, k, :],
                                                  start=(k == 0), stop=(k == 1))
                        mm.then_inc(multiplied, 1)
                    pe.wait_ge(read, e * fc + fc + 4)
                    for s in range(ST):
                        pe.wait_ge(added, e * ST + s + 1)
                        for k in range(fc):
                            mm = nc.tensor.matmul(py[s][:, 0:D], h[:, k, s * P:(s + 1) * P], w2[q][:, k, :],
                                                  start=(k == 0), stop=(k == fc - 1))
                        mm.then_inc(finished, 1)
                    pe.drain().then_inc(left, 1)
                pairs(pe, body)

            @block.scalar
            def _(act):
                act.sem_inc(read, 4)

                def body(i, q, e):
                    for k in range(2):
                        act.wait_ge(turned, e * 2 + k + 1)
                        nc.scalar.copy(xt[:, k, :], ps[k][:, 0:S]).then_inc(copied, 1)
                    for g in range(fc):
                        wait_alone(act, multiplied, e * fc + g + 1)
                        nc.scalar.activation(h[:, g, :], ps[g % 4][:, 0:S], ACT.Relu,
                                             bias=b1s[:, ds(e, 1), g:g + 1].rearrange("p o f -> p (o f)")
                                             ).then_inc(read, 1)
                pairs(act, body)

            @block.vector
            def _(dve):
                dve.sem_inc(added, ST)

                def body(i, q, e):
                    dve.wait_ge(y_free, e + 1)
                    for s in range(ST):
                        dve.wait_ge(finished, e * ST + s + 1)
                        nc.vector.tensor_tensor(y[q][:, s, :], py[s][:, 0:D],
                                                b2s[:, ds(e, 1), :].rearrange("p o d -> p (o d)"), ALU.add).then_inc(added, 1)
                pairs(dve, body)

            @block.gpsimd
            def _(pool):
                pool.sem_inc(y_free, 2)

                def body(i, q, e):
                    wait_alone(pool, added, e * ST + ST + ST)
                    nc.gpsimd.dma_start(answers[ds(e * S, S), :].rearrange("(s p) d -> p s d", p=P), y[q]
                                        ).then_inc(stored[q], 16)
                    wait_alone(pool, stored[q], i * 16 + 16)
                    pool.sem_inc(y_free, 1)
                pairs(pool, body)


def program(nc, A, out):
    with ExitStack() as ctx:
        kit = Kit()
        x, *bufs = [ctx.enter_context(nc.sbuf_tensor(n, [P, NT * D], F32)) for n in ("x", "big1", "big2", "big3", "big4")]
        make_constants(nc, ctx, kit, x)
        kit.deg_in, kit.deg_out = (ctx.enter_context(nc.sbuf_tensor(n, [P, NT], F32)) for n in ("deg_in", "deg_out"))
        table = nc.dram_tensor("table", (NP, D), F32).ap()
        table_half = nc.dram_tensor("table_half", (NP, P), F32).ap()
        edges = alloc_edges(nc, ctx, "edge", A["src"].shape[0])
        with ExitStack() as c:
            own_src, own_dst = A["L0_ffn_edge_index"][0], A["L0_ffn_edge_index"][1]
            own = alloc_edges(nc, c, "own", own_dst.shape[0], first=NT)
            with ExitStack() as cc:
                sort = EdgeSort(nc, kit, "edge", edges, 125, A["dst"], bufs[0], bufs[1])
                own_sort = EdgeSort(nc, kit, "own", own, P, own_dst, bufs[2], bufs[3], first=NT)
                sort.buffers(cc)
                own_sort.buffers(cc)
                sort.prepare(A["src"], etype=A["edge_type_8"], loads=[
                    (nat(x)[:, 0:NT - 1, :], A["x"][0:(NT - 1) * P, :].rearrange("(t p) d -> p t d", p=P)),
                    (nat(x)[0:LAST, NT - 1, :], A["x"][(NT - 1) * P:N, :])])
                rounds, own_rounds = sort.C // sort.S, own_sort.C // own_sort.S
                own_sort.prepare(own_src, beside=(sort, 0, rounds // 2))
                in_degrees(nc, kit, "deg", [(A["dst"], kit.deg_in), (A["src"], kit.deg_out)], 125,
                           beside=(sort, rounds // 2, rounds))
                sort.fetch()
                back = EdgeList()
                back.groups = edges.groups
                back.tile = cc.enter_context(nc.sbuf_tensor("back_tile", [P, back.groups], F32))
                back.blk = cc.enter_context(nc.sbuf_tensor("back_blk", [1, back.groups], I32))
                back.dram = nc.dram_tensor("back_sorted", (P * back.groups, 4), F32).ap()
                back_sort = EdgeSort(nc, kit, "back", back, 125, A["src"], bufs[0], bufs[1])
                back_sort.prepare(A["dst"], weight=A["edge_weight"], beside=(own_sort, 0, own_rounds))
                kept = [nc.dram_tensor(f"back_kept{n}", shape, dt).ap() for n, (shape, dt) in enumerate(
                    (((125, back_sort.C, 4), F32), ((125, back_sort.C), I32), ((P, back.groups), F32), ((1, back.groups), I32)))]
                load(nc, "back_keep", list(zip(kept, (back_sort.rec, back_sort.adr, back.tile[:], back.blk[:]))))
                own_sort.fetch()
            gcn_stage(nc, kit, A, x, bufs, edges, table_half)
            gat_moe_stage(nc, kit, A, x, bufs, own)
        hgt_stage(nc, kit, A, x, bufs, edges)
        with ExitStack() as c:
            edges.dram = back.dram
            back_sort.e = edges
            back_sort.hold(bufs[2], bufs[3])
            back_sort.buffers(c)
            load(nc, "back_again", list(zip((back_sort.rec, back_sort.adr, edges.tile[:], edges.blk[:]), kept)))
            soft_moe_stage(nc, kit, A, x, bufs, beside=back_sort.scatter)
            back_sort.fetch()
        sage_stage(nc, kit, A, x, bufs, edges, table)
        switch_stage(nc, kit, A, x, bufs)
        weighted_stage(nc, kit, A, x, bufs, edges, table)
        shared_moe_stage(nc, kit, A, x, bufs)
        store_x(nc, x, out)


def store_x(nc, x, out):
    with ExitStack() as c:
        stored, = sems(nc, c, "store_x", "stored")
        with nc.Block() as block:
            @block.sync
            def _(sp):
                sp.dma_start(out[0:(NT - 1) * P, :].rearrange("(t p) d -> p t d", p=P),
                             nat(x)[:, 0:NT - 1, :]).then_inc(stored, 16)
                sp.dma_start(out[(NT - 1) * P:N, :], nat(x)[0:LAST, NT - 1, :]).then_inc(stored, 16)
                sp.wait_ge(stored, 32)


_INS = ['x', 'src', 'dst', 'edge_type_8', 'edge_weight', 'node_type_4', 'L0_gnn_W1', 'L0_gnn_b1',
        'L0_gnn_W2', 'L0_gnn_b2', 'L0_ffn_W_gat', 'L0_ffn_att_src', 'L0_ffn_att_dst',
        'L0_ffn_b_gat', 'L0_ffn_ln_gamma', 'L0_ffn_ln_beta', 'L0_ffn_W1', 'L0_ffn_b1', 'L0_ffn_W2',
        'L0_ffn_b2', 'L0_ffn_edge_index', 'L1_gnn_k_linears', 'L1_gnn_q_linears',
        'L1_gnn_v_linears', 'L1_gnn_a_linears', 'L1_gnn_relation_att', 'L1_gnn_relation_msg',
        'L1_gnn_relation_pri', 'L1_gnn_skip', 'L1_ffn_Wr', 'L1_ffn_br', 'L1_ffn_W1', 'L1_ffn_b1',
        'L1_ffn_g1', 'L1_ffn_be1', 'L1_ffn_m1', 'L1_ffn_v1', 'L1_ffn_W2', 'L1_ffn_b2', 'L1_ffn_g2',
        'L1_ffn_be2', 'L1_ffn_m2', 'L1_ffn_v2', 'L1_ffn_Wo', 'L1_ffn_bo', 'L2_gnn_W_in',
        'L2_gnn_b_in', 'L2_gnn_W_agg', 'L2_gnn_W_self', 'L2_gnn_b_hid', 'L2_gnn_W_out',
        'L2_gnn_b_out', 'L2_ffn_gate_w', 'L2_ffn_gate_b', 'L2_ffn_w1', 'L2_ffn_b1', 'L2_ffn_w2',
        'L2_ffn_b2', 'L3_gnn_ln_w', 'L3_gnn_ln_b', 'L3_gnn_W', 'L3_gnn_b', 'L3_gnn_gamma',
        'L3_gnn_beta', 'L3_ffn_Wr', 'L3_ffn_br', 'L3_ffn_W1', 'L3_ffn_b1', 'L3_ffn_W2', 'L3_ffn_b2',
        'L3_ffn_gamma', 'L3_ffn_beta']
_OUTS = [((3125, 256), 'float32')]


def kernel(**inputs):
    import numpy as _np
    import concourse.bacc as _bacc
    from concourse import mybir as _mybir
    from concourse.bass_utils import run_bass_kernel_spmd as _run

    nc = _bacc.Bacc("TRN2", target_bir_lowering=False, num_devices=1)
    arrays, named = {}, {}
    for name in _INS:
        a = _np.ascontiguousarray(inputs[name])
        arrays[f"in_{name}_dram"] = a
        named[name] = nc.dram_tensor(f"in_{name}_dram", a.shape, _mybir.dt.from_np(a.dtype), kind="ExternalInput").ap()
    shape, dtype = _OUTS[0]
    out = nc.dram_tensor("out_0_dram", shape, _mybir.dt.from_np(_np.dtype(dtype)), kind="ExternalOutput").ap()
    program(nc, named, out)
    r = _run(nc, [arrays], core_ids=[0])
    return r.results[0]["out_0_dram"]
```
